# Optimizing a Trainium2 kernel written in Bass

```python
import numpy as np
import jax
import jax.numpy as jnp

def _softmax(x, axis=-1):
    return jax.nn.softmax(x, axis=axis)

def _gelu(x):
    return jax.nn.gelu(x, approximate=True)

def _silu(x):
    return jax.nn.silu(x)

def _sigmoid(x):
    return jax.nn.sigmoid(x)

def _layernorm(x, axis=-1, eps=1e-05):
    m = jnp.mean(x, axis=axis, keepdims=True)
    v = jnp.var(x, axis=axis, keepdims=True)
    return (x - m) / jnp.sqrt(v + eps)

def _scatter_add(tgt, idx, src, axis=0):
    return tgt.at[idx].add(src)

def _segment_sum(src, seg, n):
    return jax.ops.segment_sum(src, seg, n)
kernel_name = 'mk_gps_d2_gnn_r8_bd33a9'

def setup_inputs(seed: int=0):
    np.random.seed(seed)
    _w = jnp.asarray

    def _rec_inputs():
        import jax
        import jax.numpy as jnp
        _gk = jax.random.key(seed)
        x = -0.0003713 + 1 * jax.random.normal(jax.random.fold_in(_gk, 1), (6250, 256), jnp.float32)
        src = jax.random.randint(jax.random.fold_in(_gk, 2), (200000,), 0, 6250, jnp.int32)
        dst = jax.random.randint(jax.random.fold_in(_gk, 3), (200000,), 0, 6250, jnp.int32)
        _o = jnp.argsort(dst, stable=True)
        src = src[_o]
        dst = dst[_o]
        edge_attr_64 = 1.36993e-05 + 0.999972 * jax.random.normal(jax.random.fold_in(_gk, 11), (200000, 64), jnp.float32)
        edge_weight = jax.random.uniform(jax.random.fold_in(_gk, 13), (200000,), jnp.float32, 0.0, 0.999998)
        return (x, src, dst, edge_attr_64, edge_weight)
    x, src, dst, edge_attr_64, edge_weight = _rec_inputs()

    def _L0_gnn_setup():
        import jax, jax.numpy as jnp
        import numpy as np
        N, IN_CH, HEADS, OUT_CH, E = (6250, 256, 4, 64, 100000)
        key = jax.random.key(seed)
        k1, k2, k3, k4, k5 = jax.random.split(key, 5)
        x = jax.random.normal(k1, (N, IN_CH), dtype=jnp.float32)
        edge_index = jax.random.randint(k2, (2, E), 0, N, dtype=jnp.int64)
        bw = float(np.sqrt(6.0 / (IN_CH + HEADS * OUT_CH)))
        ba = float(np.sqrt(6.0 / (HEADS + OUT_CH)))
        weight = jax.random.uniform(k3, (IN_CH, HEADS * OUT_CH), jnp.float32, -bw, bw)
        attn_l = jax.random.uniform(k4, (HEADS, OUT_CH), jnp.float32, -ba, ba)
        attn_r = jax.random.uniform(k5, (HEADS, OUT_CH), jnp.float32, -ba, ba)
        return {'x': x, 'edge_index': edge_index, 'weight': weight, 'attn_l': attn_l, 'attn_r': attn_r}
    _L0_gnn_all = _L0_gnn_setup()
    _L0_gnn_in = {k: v for k, v in _L0_gnn_all.items() if k in ('weight', 'attn_l', 'attn_r')}
    del _L0_gnn_all

    def _L0_mix_setup():
        import jax, jax.numpy as jnp
        import numpy as np
        C_CURV = 1.0
        MIN_NORM = 1e-15
        BALL_EPS = 1e-05
        ATT_EPS = 1e-15
        DIM = 32

        def _norm(x):
            return jnp.clip(jnp.linalg.norm(x, axis=-1, keepdims=True), MIN_NORM)

        def proj(x, c):
            maxnorm = (1.0 - BALL_EPS) / jnp.sqrt(c)
            n = _norm(x)
            return jnp.where(n > maxnorm, x / n * maxnorm, x)

        def expmap0(u, c):
            sc = jnp.sqrt(c)
            n = _norm(u)
            return jnp.tanh(sc * n) * u / (sc * n)

        def logmap0(p, c):
            sc = jnp.sqrt(c)
            n = _norm(p)
            return jnp.arctanh(jnp.clip(sc * n, -1.0 + 1e-07, 1.0 - 1e-07)) * p / (sc * n)

        def mobius_add(x, y, c):
            x2 = jnp.sum(x * x, -1, keepdims=True)
            y2 = jnp.sum(y * y, -1, keepdims=True)
            xy = jnp.sum(x * y, -1, keepdims=True)
            num = (1 + 2 * c * xy + c * y2) * x + (1 - c * x2) * y
            den = 1 + 2 * c * xy + c * c * x2 * y2
            return num / jnp.clip(den, MIN_NORM)

        def conv1d(x, w, pad, groups=1):
            return jax.lax.conv_general_dilated(x, w, (1,), [(pad, pad)], dimension_numbers=('NCH', 'OIH', 'NCH'), feature_group_count=groups)

        def batchnorm(x, gamma, beta):
            mean = jnp.mean(x, axis=(0, 2), keepdims=True)
            var = jnp.var(x, axis=(0, 2), keepdims=True)
            xn = (x - mean) * jax.lax.rsqrt(var + 1e-05)
            return gamma[None, :, None] * xn + beta[None, :, None]

        def _reference_tuple_inner(x, w_qkv, bn_gamma, bn_beta, w_dw, w_pw, w_res, b_res):
            c = C_CURV
            h = logmap0(proj(x, c), c)
            h = jnp.transpose(h, (1, 2, 0))
            h = conv1d(h, w_qkv, pad=2)
            h = batchnorm(h, bn_gamma, bn_beta)
            h = jax.nn.relu(jnp.transpose(h, (2, 0, 1)))
            qkv = proj(expmap0(h, c), c)
            t = jnp.transpose(logmap0(proj(qkv, c), c), (1, 2, 0))
            s = conv1d(t, w_dw, pad=2, groups=t.shape[1])
            s = conv1d(s, w_pw, pad=0, groups=t.shape[1] // DIM)
            cat = jnp.concatenate([t, s], axis=1)
            ai = proj(expmap0(jnp.transpose(cat, (2, 0, 1)), c), c)
            t2 = logmap0(proj(ai, c), c)
            L, N, C2 = t2.shape
            g = C2 // (3 * DIM)
            qkv3 = jnp.transpose(t2, (1, 2, 0)).reshape(N, g, 3 * DIM, L)
            q, k, v = jnp.split(qkv3, 3, axis=2)
            q = jax.nn.relu(q)
            k = jax.nn.relu(k)
            vk = jnp.einsum('ngdl,ngel->ngde', v, k)
            out = jnp.einsum('ngde,ngdl->ngdl', vk, q)
            out = out / (jnp.sum(v, -1, keepdims=True) + ATT_EPS)
            out = jnp.transpose(out.reshape(N, g * DIM, L), (2, 0, 1))
            fx_h = proj(expmap0(out, c), c)
            ft = jnp.transpose(logmap0(proj(fx_h, c), c), (1, 2, 0))
            ft = conv1d(ft, w_res, pad=0) + b_res[None, :, None]
            fx = proj(expmap0(jnp.transpose(ft, (2, 0, 1)), c), c)
            residual = mobius_add(fx, x, c)
            return (fx, residual)
        key = jax.random.key(seed)
        ks = jax.random.split(key, 6)
        L, N, C, TD = (256, 16, 256, 256)
        x = jax.random.normal(ks[0], (L, N, C), jnp.float32) * 0.05
        w_qkv = jax.random.normal(ks[1], (3 * TD, C, 5), jnp.float32) / np.sqrt(C * 5)
        bn_gamma = jnp.ones((3 * TD,), jnp.float32)
        bn_beta = jnp.zeros((3 * TD,), jnp.float32)
        w_dw = jax.random.normal(ks[2], (3 * TD, 1, 5), jnp.float32) / np.sqrt(5.0)
        w_pw = jax.random.normal(ks[3], (3 * TD, DIM, 1), jnp.float32) / np.sqrt(DIM)
        w_res = jax.random.normal(ks[4], (C, 2 * TD, 1), jnp.float32) / np.sqrt(2 * TD)
        b_res = jnp.zeros((C,), jnp.float32)
        return {'x': x, 'w_qkv': w_qkv, 'bn_gamma': bn_gamma, 'bn_beta': bn_beta, 'w_dw': w_dw, 'w_pw': w_pw, 'w_res': w_res, 'b_res': b_res}
    _L0_mix_all = _L0_mix_setup()
    _L0_mix_in = {k: v for k, v in _L0_mix_all.items() if k in ('w_qkv', 'bn_gamma', 'bn_beta', 'w_dw', 'w_pw', 'w_res', 'b_res')}
    del _L0_mix_all

    def _L0_ffn_setup():
        import jax, jax.numpy as jnp
        import numpy as np
        B, N, D = (16, 512, 256)
        NUM_EXPERTS, TOP_K, HEADS = (4, 2, 4)
        N_EDGES = 131072
        LN_EPS = 1e-05

        def _layernorm(x, g, b):
            mu = x.mean(-1, keepdims=True)
            var = ((x - mu) ** 2).mean(-1, keepdims=True)
            return (x - mu) * jax.lax.rsqrt(var + LN_EPS) * g + b

        def _forward(x, edge_index, W_gat, att_src, att_dst, b_gat, ln_gamma, ln_beta, W1, b1, W2, b2):
            Bc, Nc, Dc = x.shape
            M = Bc * Nc
            x_flat = x.reshape(M, Dc)
            h = (x_flat @ W_gat).reshape(M, HEADS, NUM_EXPERTS)
            loops = jnp.arange(M, dtype=edge_index.dtype)
            src = jnp.concatenate([edge_index[0], loops])
            dst = jnp.concatenate([edge_index[1], loops])
            a_src = (h * att_src).sum(-1)
            a_dst = (h * att_dst).sum(-1)
            e = jax.nn.leaky_relu(a_src[src] + a_dst[dst], negative_slope=0.2)
            e_max = jax.ops.segment_max(e, dst, num_segments=M)
            ee = jnp.exp(e - e_max[dst])
            denom = jax.ops.segment_sum(ee, dst, num_segments=M)
            alpha = ee / (denom[dst] + 1e-16)
            msg = h[src] * alpha[:, :, None]
            agg = jax.ops.segment_sum(msg, dst, num_segments=M).reshape(M, HEADS * NUM_EXPERTS) + b_gat
            scores = _layernorm(agg, ln_gamma, ln_beta).reshape(M, HEADS, NUM_EXPERTS).mean(1)
            scores = scores.reshape(Bc, Nc, NUM_EXPERTS)
            topk_s, topk_i = jax.lax.top_k(scores, TOP_K)
            w = jax.nn.softmax(topk_s, axis=-1)
            out = jnp.zeros_like(x)
            for ei in range(NUM_EXPERTS):
                g = jnp.where(topk_i == ei, w, 0.0).sum(-1)
                hh = jax.nn.gelu(x @ W1[ei] + b1[ei], approximate=False)
                out = out + g[..., None] * (hh @ W2[ei] + b2[ei])
            return out
        key = jax.random.key(seed)
        ks = jax.random.split(key, 8)
        s = 0.05
        return {'x': jax.random.normal(ks[0], (B, N, D), jnp.float32), 'W_gat': jax.random.normal(ks[1], (D, HEADS * NUM_EXPERTS), jnp.float32) * s, 'att_src': jax.random.normal(ks[2], (HEADS, NUM_EXPERTS), jnp.float32) * s, 'att_dst': jax.random.normal(ks[3], (HEADS, NUM_EXPERTS), jnp.float32) * s, 'b_gat': jnp.zeros((HEADS * NUM_EXPERTS,), jnp.float32), 'ln_gamma': jnp.ones((HEADS * NUM_EXPERTS,), jnp.float32), 'ln_beta': jnp.zeros((HEADS * NUM_EXPERTS,), jnp.float32), 'W1': jax.random.normal(ks[4], (NUM_EXPERTS, D, 2 * D), jnp.float32) * s, 'b1': jnp.zeros((NUM_EXPERTS, 2 * D), jnp.float32), 'W2': jax.random.normal(ks[5], (NUM_EXPERTS, 2 * D, D), jnp.float32) * s, 'b2': jnp.zeros((NUM_EXPERTS, D), jnp.float32), 'edge_index': jax.random.randint(ks[6], (2, N_EDGES), 0, B * N, jnp.int32)}
    _L0_ffn_all = _L0_ffn_setup()
    _L0_ffn_in = {k: v for k, v in _L0_ffn_all.items() if k in ('W_gat', 'att_src', 'att_dst', 'b_gat', 'ln_gamma', 'ln_beta', 'W1', 'b1', 'W2', 'b2', 'edge_index')}
    del _L0_ffn_all

    def _L1_gnn_setup():
        import jax, jax.numpy as jnp
        import numpy as np
        N = 2500
        E = 40000
        D = 256
        H = 8
        DH = D // H
        ED = 64
        FF = 4 * D
        EPS = 1e-05

        def _layernorm(x, g, b):
            m = jnp.mean(x, axis=-1, keepdims=True)
            v = jnp.var(x, axis=-1, keepdims=True)
            return (x - m) * jax.lax.rsqrt(v + EPS) * g + b

        def _edge_attention(xn, edge_index, ef, ew, Wq, bq, Wk, bk, Wv, bv, We, be, Wo, bo):
            n = xn.shape[0]
            scale = DH ** (-0.5)
            q = (xn @ Wq + bq).reshape(n, H, DH)
            k = (xn @ Wk + bk).reshape(n, H, DH)
            v = (xn @ Wv + bv).reshape(n, H, DH)
            src, dst = (edge_index[0], edge_index[1])
            ep = ef @ We + be
            scores = jnp.einsum('ehd,ehd->eh', q[dst], k[src] + ep[:, None, :]) * scale
            scores = scores * ew[:, None]
            m = jax.ops.segment_max(scores, dst, num_segments=n)
            m = jnp.where(jnp.isfinite(m), m, 0.0)
            ex = jnp.exp(scores - m[dst])
            s = jax.ops.segment_sum(ex, dst, num_segments=n)
            attn = ex / s[dst]
            out = jax.ops.segment_sum(attn[:, :, None] * v[src], dst, num_segments=n)
            out = out.reshape(n, D) @ Wo + bo
            return out
        key = jax.random.key(seed)
        ks = jax.random.split(key, 32)

        def lin_w(k, i, o):
            return (jax.random.normal(k, (i, o), jnp.float32) / np.sqrt(i)).astype(jnp.float32)
        return {'x': jax.random.normal(ks[0], (N, D), jnp.float32), 'edge_features': jax.random.normal(ks[1], (E, ED), jnp.float32), 'edge_weights': jax.random.uniform(ks[2], (E,), jnp.float32), 'edge_index': jax.random.randint(ks[3], (2, E), 0, N, dtype=jnp.int32), 'Wq': lin_w(ks[4], D, D), 'bq': jnp.zeros((D,), jnp.float32), 'Wk': lin_w(ks[5], D, D), 'bk': jnp.zeros((D,), jnp.float32), 'Wv': lin_w(ks[6], D, D), 'bv': jnp.zeros((D,), jnp.float32), 'We': lin_w(ks[7], ED, DH), 'be': jnp.zeros((DH,), jnp.float32), 'Wo': lin_w(ks[8], D, D), 'bo': jnp.zeros((D,), jnp.float32), 'ln1_g': jnp.ones((D,), jnp.float32), 'ln1_b': jnp.zeros((D,), jnp.float32), 'ln2_g': jnp.ones((D,), jnp.float32), 'ln2_b': jnp.zeros((D,), jnp.float32), 'W1': lin_w(ks[9], D, FF), 'b1': jnp.zeros((FF,), jnp.float32), 'W2': lin_w(ks[10], FF, D), 'b2': jnp.zeros((D,), jnp.float32), 'alpha': jnp.ones((1,), jnp.float32), 'beta': jnp.ones((1,), jnp.float32)}
    _L1_gnn_all = _L1_gnn_setup()
    _L1_gnn_in = {k: v for k, v in _L1_gnn_all.items() if k in ('Wq', 'bq', 'Wk', 'bk', 'Wv', 'bv', 'We', 'be', 'Wo', 'bo', 'ln1_g', 'ln1_b', 'ln2_g', 'ln2_b', 'W1', 'b1', 'W2', 'b2', 'alpha', 'beta')}
    del _L1_gnn_all

    def _L1_mix_setup():
        import jax, jax.numpy as jnp
        import numpy as np
        A, Bc, Cc = (0.5, 1.0, 1.0)
        H = 8
        EPS = 1e-12

        def _normalize(t):
            n = jnp.linalg.norm(t, axis=-1, keepdims=True)
            return t / jnp.maximum(n, EPS)
        key = jax.random.key(seed)
        ks = jax.random.split(key, 5)
        B, N, C = (8, 256, 256)
        D = C // H
        x = jax.random.normal(ks[0], (B, N, C), dtype=jnp.float32)
        Wqkv = jax.random.normal(ks[1], (3 * H * D, C), dtype=jnp.float32) * 0.02
        bqkv = jnp.zeros((3 * H * D,), dtype=jnp.float32)
        Wproj = jax.random.normal(ks[2], (C, H * D), dtype=jnp.float32) * 0.02
        bproj = jnp.zeros((C,), dtype=jnp.float32)
        temperature = jnp.ones((1, H, 1, 1), dtype=jnp.float32)
        return {'x': x, 'Wqkv': Wqkv, 'bqkv': bqkv, 'Wproj': Wproj, 'bproj': bproj, 'temperature': temperature}
    _L1_mix_all = _L1_mix_setup()
    _L1_mix_in = {k: v for k, v in _L1_mix_all.items() if k in ('Wqkv', 'bqkv', 'Wproj', 'bproj', 'temperature')}
    del _L1_mix_all

    def _L1_ffn_setup():
        import math
        import jax, jax.numpy as jnp
        import numpy as np
        CAPACITY_FACTOR = 1.25
        key = jax.random.key(seed)
        ks = jax.random.split(key, 5)
        B, L, D, F, E = (8, 1024, 256, 1024, 8)
        h = jax.random.normal(ks[0], (B, L, D), dtype=jnp.float32)
        gate_w = jax.random.normal(ks[1], (D, E), dtype=jnp.float32) * 0.02
        gate_b = jnp.zeros((E,), dtype=jnp.float32)
        w1 = jax.random.normal(ks[2], (E, D, F), dtype=jnp.float32) * (1.0 / math.sqrt(D))
        b1 = jnp.zeros((E, F), dtype=jnp.float32)
        w2 = jax.random.normal(ks[3], (E, F, D), dtype=jnp.float32) * (1.0 / math.sqrt(F))
        b2 = jnp.zeros((E, D), dtype=jnp.float32)
        return {'h': h, 'gate_w': gate_w, 'gate_b': gate_b, 'w1': w1, 'b1': b1, 'w2': w2, 'b2': b2}
    _L1_ffn_all = _L1_ffn_setup()
    _L1_ffn_in = {k: v for k, v in _L1_ffn_all.items() if k in ('gate_w', 'gate_b', 'w1', 'b1', 'w2', 'b2')}
    del _L1_ffn_all
    return {'x': x, 'src': src, 'dst': dst, 'edge_attr_64': edge_attr_64, 'edge_weight': edge_weight, 'L0_gnn_weight': _L0_gnn_in['weight'], 'L0_gnn_attn_l': _L0_gnn_in['attn_l'], 'L0_gnn_attn_r': _L0_gnn_in['attn_r'], 'L0_mix_w_qkv': _L0_mix_in['w_qkv'], 'L0_mix_bn_gamma': _L0_mix_in['bn_gamma'], 'L0_mix_bn_beta': _L0_mix_in['bn_beta'], 'L0_mix_w_dw': _L0_mix_in['w_dw'], 'L0_mix_w_pw': _L0_mix_in['w_pw'], 'L0_mix_w_res': _L0_mix_in['w_res'], 'L0_mix_b_res': _L0_mix_in['b_res'], 'L0_ffn_W_gat': _L0_ffn_in['W_gat'], 'L0_ffn_att_src': _L0_ffn_in['att_src'], 'L0_ffn_att_dst': _L0_ffn_in['att_dst'], 'L0_ffn_b_gat': _L0_ffn_in['b_gat'], 'L0_ffn_ln_gamma': _L0_ffn_in['ln_gamma'], 'L0_ffn_ln_beta': _L0_ffn_in['ln_beta'], 'L0_ffn_W1': _L0_ffn_in['W1'], 'L0_ffn_b1': _L0_ffn_in['b1'], 'L0_ffn_W2': _L0_ffn_in['W2'], 'L0_ffn_b2': _L0_ffn_in['b2'], 'L0_ffn_edge_index': _L0_ffn_in['edge_index'], 'L1_gnn_Wq': _L1_gnn_in['Wq'], 'L1_gnn_bq': _L1_gnn_in['bq'], 'L1_gnn_Wk': _L1_gnn_in['Wk'], 'L1_gnn_bk': _L1_gnn_in['bk'], 'L1_gnn_Wv': _L1_gnn_in['Wv'], 'L1_gnn_bv': _L1_gnn_in['bv'], 'L1_gnn_We': _L1_gnn_in['We'], 'L1_gnn_be': _L1_gnn_in['be'], 'L1_gnn_Wo': _L1_gnn_in['Wo'], 'L1_gnn_bo': _L1_gnn_in['bo'], 'L1_gnn_ln1_g': _L1_gnn_in['ln1_g'], 'L1_gnn_ln1_b': _L1_gnn_in['ln1_b'], 'L1_gnn_ln2_g': _L1_gnn_in['ln2_g'], 'L1_gnn_ln2_b': _L1_gnn_in['ln2_b'], 'L1_gnn_W1': _L1_gnn_in['W1'], 'L1_gnn_b1': _L1_gnn_in['b1'], 'L1_gnn_W2': _L1_gnn_in['W2'], 'L1_gnn_b2': _L1_gnn_in['b2'], 'L1_gnn_alpha': _L1_gnn_in['alpha'], 'L1_gnn_beta': _L1_gnn_in['beta'], 'L1_mix_Wqkv': _L1_mix_in['Wqkv'], 'L1_mix_bqkv': _L1_mix_in['bqkv'], 'L1_mix_Wproj': _L1_mix_in['Wproj'], 'L1_mix_bproj': _L1_mix_in['bproj'], 'L1_mix_temperature': _L1_mix_in['temperature'], 'L1_ffn_gate_w': _L1_ffn_in['gate_w'], 'L1_ffn_gate_b': _L1_ffn_in['gate_b'], 'L1_ffn_w1': _L1_ffn_in['w1'], 'L1_ffn_b1': _L1_ffn_in['b1'], 'L1_ffn_w2': _L1_ffn_in['w2'], 'L1_ffn_b2': _L1_ffn_in['b2']}

def reference(x, src, dst, edge_attr_64, edge_weight, L0_gnn_weight, L0_gnn_attn_l, L0_gnn_attn_r, L0_mix_w_qkv, L0_mix_bn_gamma, L0_mix_bn_beta, L0_mix_w_dw, L0_mix_w_pw, L0_mix_w_res, L0_mix_b_res, L0_ffn_W_gat, L0_ffn_att_src, L0_ffn_att_dst, L0_ffn_b_gat, L0_ffn_ln_gamma, L0_ffn_ln_beta, L0_ffn_W1, L0_ffn_b1, L0_ffn_W2, L0_ffn_b2, L0_ffn_edge_index, L1_gnn_Wq, L1_gnn_bq, L1_gnn_Wk, L1_gnn_bk, L1_gnn_Wv, L1_gnn_bv, L1_gnn_We, L1_gnn_be, L1_gnn_Wo, L1_gnn_bo, L1_gnn_ln1_g, L1_gnn_ln1_b, L1_gnn_ln2_g, L1_gnn_ln2_b, L1_gnn_W1, L1_gnn_b1, L1_gnn_W2, L1_gnn_b2, L1_gnn_alpha, L1_gnn_beta, L1_mix_Wqkv, L1_mix_bqkv, L1_mix_Wproj, L1_mix_bproj, L1_mix_temperature, L1_ffn_gate_w, L1_ffn_gate_b, L1_ffn_w1, L1_ffn_b1, L1_ffn_w2, L1_ffn_b2):
    import jax
    import jax.numpy as jnp

    def _L0_gnn_ref(x, edge_index, weight, attn_l, attn_r):
        import jax, jax.numpy as jnp
        import numpy as np
        N, IN_CH, HEADS, OUT_CH, E = (6250, 256, 4, 64, 100000)
        heads, out_ch = attn_l.shape
        n = x.shape[0]
        xt = jnp.matmul(x, weight).reshape(-1, heads, out_ch)
        row, col = (edge_index[0], edge_index[1])
        alpha_l = jnp.einsum('ehd,hd->eh', xt[row], attn_l)
        alpha_r = jnp.einsum('ehd,hd->eh', xt[col], attn_r)
        alpha = jax.nn.softmax(jax.nn.leaky_relu(alpha_l + alpha_r, 0.01), axis=1)
        tmp = jnp.einsum('nh,nhd->nd', alpha[:n], xt[col[:n]])
        out = jnp.broadcast_to(tmp[:, None, :], (n, heads, out_ch))
        return out.reshape(n, heads * out_ch)

    def _L0_mix_ref(x, w_qkv, bn_gamma, bn_beta, w_dw, w_pw, w_res, b_res):
        import jax, jax.numpy as jnp
        import numpy as np
        C_CURV = 1.0
        MIN_NORM = 1e-15
        BALL_EPS = 1e-05
        ATT_EPS = 1e-15
        DIM = 32

        def _norm(x):
            return jnp.clip(jnp.linalg.norm(x, axis=-1, keepdims=True), MIN_NORM)

        def proj(x, c):
            maxnorm = (1.0 - BALL_EPS) / jnp.sqrt(c)
            n = _norm(x)
            return jnp.where(n > maxnorm, x / n * maxnorm, x)

        def expmap0(u, c):
            sc = jnp.sqrt(c)
            n = _norm(u)
            return jnp.tanh(sc * n) * u / (sc * n)

        def logmap0(p, c):
            sc = jnp.sqrt(c)
            n = _norm(p)
            return jnp.arctanh(jnp.clip(sc * n, -1.0 + 1e-07, 1.0 - 1e-07)) * p / (sc * n)

        def mobius_add(x, y, c):
            x2 = jnp.sum(x * x, -1, keepdims=True)
            y2 = jnp.sum(y * y, -1, keepdims=True)
            xy = jnp.sum(x * y, -1, keepdims=True)
            num = (1 + 2 * c * xy + c * y2) * x + (1 - c * x2) * y
            den = 1 + 2 * c * xy + c * c * x2 * y2
            return num / jnp.clip(den, MIN_NORM)

        def conv1d(x, w, pad, groups=1):
            return jax.lax.conv_general_dilated(x, w, (1,), [(pad, pad)], dimension_numbers=('NCH', 'OIH', 'NCH'), feature_group_count=groups)

        def batchnorm(x, gamma, beta):
            mean = jnp.mean(x, axis=(0, 2), keepdims=True)
            var = jnp.var(x, axis=(0, 2), keepdims=True)
            xn = (x - mean) * jax.lax.rsqrt(var + 1e-05)
            return gamma[None, :, None] * xn + beta[None, :, None]

        def _reference_tuple_inner(x, w_qkv, bn_gamma, bn_beta, w_dw, w_pw, w_res, b_res):
            c = C_CURV
            h = logmap0(proj(x, c), c)
            h = jnp.transpose(h, (1, 2, 0))
            h = conv1d(h, w_qkv, pad=2)
            h = batchnorm(h, bn_gamma, bn_beta)
            h = jax.nn.relu(jnp.transpose(h, (2, 0, 1)))
            qkv = proj(expmap0(h, c), c)
            t = jnp.transpose(logmap0(proj(qkv, c), c), (1, 2, 0))
            s = conv1d(t, w_dw, pad=2, groups=t.shape[1])
            s = conv1d(s, w_pw, pad=0, groups=t.shape[1] // DIM)
            cat = jnp.concatenate([t, s], axis=1)
            ai = proj(expmap0(jnp.transpose(cat, (2, 0, 1)), c), c)
            t2 = logmap0(proj(ai, c), c)
            L, N, C2 = t2.shape
            g = C2 // (3 * DIM)
            qkv3 = jnp.transpose(t2, (1, 2, 0)).reshape(N, g, 3 * DIM, L)
            q, k, v = jnp.split(qkv3, 3, axis=2)
            q = jax.nn.relu(q)
            k = jax.nn.relu(k)
            vk = jnp.einsum('ngdl,ngel->ngde', v, k)
            out = jnp.einsum('ngde,ngdl->ngdl', vk, q)
            out = out / (jnp.sum(v, -1, keepdims=True) + ATT_EPS)
            out = jnp.transpose(out.reshape(N, g * DIM, L), (2, 0, 1))
            fx_h = proj(expmap0(out, c), c)
            ft = jnp.transpose(logmap0(proj(fx_h, c), c), (1, 2, 0))
            ft = conv1d(ft, w_res, pad=0) + b_res[None, :, None]
            fx = proj(expmap0(jnp.transpose(ft, (2, 0, 1)), c), c)
            residual = mobius_add(fx, x, c)
            return (fx, residual)
        return _reference_tuple_inner(x, w_qkv, bn_gamma, bn_beta, w_dw, w_pw, w_res, b_res)[0]

    def _L0_ffn_ref(x, W_gat, att_src, att_dst, b_gat, ln_gamma, ln_beta, W1, b1, W2, b2, edge_index):
        import jax, jax.numpy as jnp
        import numpy as np
        B, N, D = (16, 512, 256)
        NUM_EXPERTS, TOP_K, HEADS = (4, 2, 4)
        N_EDGES = 131072
        LN_EPS = 1e-05

        def _layernorm(x, g, b):
            mu = x.mean(-1, keepdims=True)
            var = ((x - mu) ** 2).mean(-1, keepdims=True)
            return (x - mu) * jax.lax.rsqrt(var + LN_EPS) * g + b

        def _forward(x, edge_index, W_gat, att_src, att_dst, b_gat, ln_gamma, ln_beta, W1, b1, W2, b2):
            Bc, Nc, Dc = x.shape
            M = Bc * Nc
            x_flat = x.reshape(M, Dc)
            h = (x_flat @ W_gat).reshape(M, HEADS, NUM_EXPERTS)
            loops = jnp.arange(M, dtype=edge_index.dtype)
            src = jnp.concatenate([edge_index[0], loops])
            dst = jnp.concatenate([edge_index[1], loops])
            a_src = (h * att_src).sum(-1)
            a_dst = (h * att_dst).sum(-1)
            e = jax.nn.leaky_relu(a_src[src] + a_dst[dst], negative_slope=0.2)
            e_max = jax.ops.segment_max(e, dst, num_segments=M)
            ee = jnp.exp(e - e_max[dst])
            denom = jax.ops.segment_sum(ee, dst, num_segments=M)
            alpha = ee / (denom[dst] + 1e-16)
            msg = h[src] * alpha[:, :, None]
            agg = jax.ops.segment_sum(msg, dst, num_segments=M).reshape(M, HEADS * NUM_EXPERTS) + b_gat
            scores = _layernorm(agg, ln_gamma, ln_beta).reshape(M, HEADS, NUM_EXPERTS).mean(1)
            scores = scores.reshape(Bc, Nc, NUM_EXPERTS)
            topk_s, topk_i = jax.lax.top_k(scores, TOP_K)
            w = jax.nn.softmax(topk_s, axis=-1)
            out = jnp.zeros_like(x)
            for ei in range(NUM_EXPERTS):
                g = jnp.where(topk_i == ei, w, 0.0).sum(-1)
                hh = jax.nn.gelu(x @ W1[ei] + b1[ei], approximate=False)
                out = out + g[..., None] * (hh @ W2[ei] + b2[ei])
            return out
        return _forward(x, edge_index, W_gat, att_src, att_dst, b_gat, ln_gamma, ln_beta, W1, b1, W2, b2)

    def _L1_gnn_ref(x, edge_features, edge_weights, edge_index, Wq, bq, Wk, bk, Wv, bv, We, be, Wo, bo, ln1_g, ln1_b, ln2_g, ln2_b, W1, b1, W2, b2, alpha, beta):
        import jax, jax.numpy as jnp
        import numpy as np
        N = 2500
        E = 40000
        D = 256
        H = 8
        DH = D // H
        ED = 64
        FF = 4 * D
        EPS = 1e-05

        def _layernorm(x, g, b):
            m = jnp.mean(x, axis=-1, keepdims=True)
            v = jnp.var(x, axis=-1, keepdims=True)
            return (x - m) * jax.lax.rsqrt(v + EPS) * g + b

        def _edge_attention(xn, edge_index, ef, ew, Wq, bq, Wk, bk, Wv, bv, We, be, Wo, bo):
            n = xn.shape[0]
            scale = DH ** (-0.5)
            q = (xn @ Wq + bq).reshape(n, H, DH)
            k = (xn @ Wk + bk).reshape(n, H, DH)
            v = (xn @ Wv + bv).reshape(n, H, DH)
            src, dst = (edge_index[0], edge_index[1])
            ep = ef @ We + be
            scores = jnp.einsum('ehd,ehd->eh', q[dst], k[src] + ep[:, None, :]) * scale
            scores = scores * ew[:, None]
            m = jax.ops.segment_max(scores, dst, num_segments=n)
            m = jnp.where(jnp.isfinite(m), m, 0.0)
            ex = jnp.exp(scores - m[dst])
            s = jax.ops.segment_sum(ex, dst, num_segments=n)
            attn = ex / s[dst]
            out = jax.ops.segment_sum(attn[:, :, None] * v[src], dst, num_segments=n)
            out = out.reshape(n, D) @ Wo + bo
            return out
        xn = _layernorm(x, ln1_g, ln1_b)
        attn_out = _edge_attention(xn, edge_index, edge_features, edge_weights, Wq, bq, Wk, bk, Wv, bv, We, be, Wo, bo)
        x = x + alpha * attn_out
        xn = _layernorm(x, ln2_g, ln2_b)
        ff = jax.nn.gelu(xn @ W1 + b1, approximate=False) @ W2 + b2
        x = x + beta * ff
        return x

    def _L1_mix_ref(x, Wqkv, bqkv, Wproj, bproj, temperature):
        import jax, jax.numpy as jnp
        import numpy as np
        A, Bc, Cc = (0.5, 1.0, 1.0)
        H = 8
        EPS = 1e-12

        def _normalize(t):
            n = jnp.linalg.norm(t, axis=-1, keepdims=True)
            return t / jnp.maximum(n, EPS)
        B, N, C = x.shape
        D = C // H
        scale = float(D) ** 0.25
        qkv = (x @ Wqkv.T + bqkv).reshape(B, N, 3, H, D)
        qkv = jnp.transpose(qkv, (2, 0, 3, 1, 4))
        q, k, v = (qkv[0], qkv[1], qkv[2])
        q = q * scale
        v1 = jnp.concatenate([jnp.ones((B, H, N, 1), dtype=v.dtype), v], axis=-1)
        qn = _normalize(q) * (scale * temperature)
        kn = _normalize(k) * scale
        vN = v1 / N
        kv_mod = jnp.einsum('bhni,bhnj,bhne->bhije', kn, kn, vN)
        kv = jnp.einsum('bhnd,bhne->bhde', kn, vN)
        vsum = jnp.sum(vN, axis=-2)[:, :, None, :]
        y = A * jnp.einsum('bhni,bhnj,bhije->bhne', qn, qn, kv_mod) + scale ** 2 * Bc * jnp.einsum('bhnd,bhde->bhne', qn, kv) + scale ** 4 * Cc * vsum
        y_norm, y = (y[..., :1], y[..., 1:])
        y = y / y_norm
        out = jnp.transpose(y, (0, 2, 1, 3)).reshape(B, N, H * D)
        return out @ Wproj.T + bproj

    def _L1_ffn_ref(h, gate_w, gate_b, w1, b1, w2, b2):
        import math
        import jax, jax.numpy as jnp
        import numpy as np
        CAPACITY_FACTOR = 1.25
        B, L, D = h.shape
        E = gate_w.shape[1]
        T = B * L
        C = max(1, math.ceil(CAPACITY_FACTOR * T / E))
        x = h.reshape(T, D)
        logits = x @ gate_w + gate_b
        probs = jax.nn.softmax(logits, axis=-1)
        idx = jnp.argmax(probs, axis=-1)
        prb = jnp.take_along_axis(probs, idx[:, None], axis=1)[:, 0]
        one_hot = jax.nn.one_hot(idx, E, dtype=jnp.float32)
        pos = (jnp.cumsum(one_hot, axis=0) * one_hot).sum(-1).astype(jnp.int32) - 1
        kept = pos < C
        pos_safe = jnp.where(kept, pos, C)
        buf = jnp.zeros((E, C, D), dtype=h.dtype).at[idx, pos_safe].set(x, mode='drop')
        hmid = jax.nn.relu(jnp.einsum('ecd,edf->ecf', buf, w1) + b1[:, None, :])
        ybuf = jnp.einsum('ecf,efd->ecd', hmid, w2) + b2[:, None, :]
        pos_g = jnp.minimum(pos, C - 1)
        y_tok = ybuf[idx, pos_g] * (prb * kept)[:, None]
        y = y_tok.reshape(B, L, D)
        y = jnp.nan_to_num(y, nan=0.0, posinf=10000.0, neginf=-10000.0)
        return y
    edge_index = jnp.stack([src, dst])
    xn = _layernorm(x, axis=-1)
    x = x + _L0_gnn_ref(xn, edge_index, L0_gnn_weight, L0_gnn_attn_l, L0_gnn_attn_r) + _L0_mix_ref(xn[None], L0_mix_w_qkv, L0_mix_bn_gamma, L0_mix_bn_beta, L0_mix_w_dw, L0_mix_w_pw, L0_mix_w_res, L0_mix_b_res)[0]
    x = x + _L0_ffn_ref(_layernorm(x, axis=-1)[None], L0_ffn_W_gat, L0_ffn_att_src, L0_ffn_att_dst, L0_ffn_b_gat, L0_ffn_ln_gamma, L0_ffn_ln_beta, L0_ffn_W1, L0_ffn_b1, L0_ffn_W2, L0_ffn_b2, L0_ffn_edge_index)[0]
    xn = _layernorm(x, axis=-1)
    x = x + _L1_gnn_ref(xn, edge_attr_64, edge_weight, edge_index, L1_gnn_Wq, L1_gnn_bq, L1_gnn_Wk, L1_gnn_bk, L1_gnn_Wv, L1_gnn_bv, L1_gnn_We, L1_gnn_be, L1_gnn_Wo, L1_gnn_bo, L1_gnn_ln1_g, L1_gnn_ln1_b, L1_gnn_ln2_g, L1_gnn_ln2_b, L1_gnn_W1, L1_gnn_b1, L1_gnn_W2, L1_gnn_b2, L1_gnn_alpha, L1_gnn_beta) + _L1_mix_ref(xn[None], L1_mix_Wqkv, L1_mix_bqkv, L1_mix_Wproj, L1_mix_bproj, L1_mix_temperature)[0]
    x = x + _L1_ffn_ref(_layernorm(x, axis=-1)[None], L1_ffn_gate_w, L1_ffn_gate_b, L1_ffn_w1, L1_ffn_b1, L1_ffn_w2, L1_ffn_b2)[0]
    return x

_drawn_inputs = setup_inputs


def setup_inputs(seed=0):
    import zlib

    import numpy as np

    out = dict(_drawn_inputs(seed))
    spreads = {'L0_mix_bn_gamma': (1.0, 0.6),
     'L0_mix_bn_beta': (0.0, 0.317),
     'L0_mix_b_res': (0.0, 0.1),
     'L0_ffn_b_gat': (0.0, 0.1),
     'L0_ffn_ln_gamma': (1.0, 0.2),
     'L0_ffn_ln_beta': (0.0, 0.1),
     'L0_ffn_b1': (0.0, 0.1),
     'L0_ffn_b2': (0.0, 0.1),
     'L1_gnn_bq': (0.0, 0.541),
     'L1_gnn_bk': (0.0, 0.8),
     'L1_gnn_bv': (0.0, 0.1),
     'L1_gnn_be': (0.0, 0.8),
     'L1_gnn_bo': (0.0, 0.1),
     'L1_gnn_ln1_g': (1.0, 0.2),
     'L1_gnn_ln1_b': (0.0, 0.1),
     'L1_gnn_ln2_g': (1.0, 0.2),
     'L1_gnn_ln2_b': (0.0, 0.268),
     'L1_gnn_b1': (0.0, 0.1),
     'L1_gnn_b2': (0.0, 0.1),
     'L1_mix_bqkv': (0.0, 0.525),
     'L1_mix_bproj': (0.0, 0.1),
     'L1_mix_temperature': (1.0, 0.6),
     'L1_ffn_gate_b': (0.0, 0.1),
     'L1_ffn_b1': (0.0, 0.8),
     'L1_ffn_b2': (0.0, 0.8)}
    factors = {'L0_mix_w_dw': 3.509, 'L0_mix_w_pw': 3.36, 'L1_mix_Wqkv': 7.969, 'L1_mix_Wproj': 3.995}
    for name, (base, spread) in spreads.items():
        noise = np.random.default_rng([zlib.crc32(name.encode()), seed]).standard_normal(out[name].shape)
        drawn = base * np.exp(spread * noise) if base else spread * noise
        out[name] = jnp.asarray(drawn.astype(out[name].dtype))
    for name, factor in factors.items():
        out[name] = (out[name] * factor).astype(out[name].dtype)
    return out
```

```python
import numpy as np
import concourse.bass as bass
from concourse import mybir
from concourse.alu_op_type import AluOpType as ALU
from contextlib import ExitStack

F32 = mybir.dt.float32
I32 = mybir.dt.int32
ACT = mybir.ActivationFunctionType
AX = mybir.AxisListType

P = 128
N = 6250
D = 256
KD = D // P
NT = -(-N // P)
GT = 7
NG = NT // GT
GC = GT * P
HC = GC // 2
NP = NT * P
BIG = 1.0e30
LN_EPS = 1e-05

H0, C0 = 4, 64
R0 = D + H0
QC = 6
MAXNORM = 1.0 - 1e-05
ATANH_MAX = float(np.arctanh(np.float64(np.float32(MAXNORM))))
MIN_NORM = 1e-15
ATT_EPS = 1e-15
E0, F0, GH = 4, 512, 4
GW = GH * E0
MW = GW + GH
E0_EDGES = 131072
S0 = E0_EDGES // P
U0 = 8

E_EDGES = 200000
H1, D1, ED = 8, 32, 64
U1 = 8
S1 = -(-E_EDGES // (P * U1)) * U1
EP = S1 * P
AW = D + 2 * H1
FF = 1024
VW = D1 + 1
PD = D1 // 2 + 1
PR = PD * D1
PC = -(-PR // P)
E1, F1 = 8, 1024
CAP = -(-5 * N // (4 * E1))
CS = 1024
CT = CS // P


class Chain:

    def __init__(self, eng, sem):
        self.eng, self.sem, self.n = eng, sem, 0

    def __call__(self, ins):
        self.n += 1
        ins.then_inc(self.sem, 1)
        self.eng.wait_ge(self.sem, self.n)

    def fresh(self):
        self.eng.sem_clear(self.sem)
        self.n = 0


class Tally:

    held = None

    def __init__(self, sem, per_pass, credit=1):
        self.sem, self.per_pass, self.credit = sem, per_pass, credit

    def open(self, eng):
        eng.sem_inc(self.sem, self.credit)

    def wait(self, eng, i, n=0):
        eng.wait_ge(self.sem, i * self.per_pass + (self.credit + n))

    def hold(self, eng, i, n=0):
        self.wait(eng, i, n)
        eng.sem_inc(self.held, 1)


class Scope:

    lasting = None

    def __init__(self, nc, es, name):
        self.nc, self.es, self.name, self.sems = nc, es, name, []
        es.callback(self.clear)

    def clear(self):
        if self.sems:
            with self.nc.Block() as block:
                @block.sync
                def _(sp):
                    for sem in self.sems:
                        sp.sem_clear(sem)

    def sb(self, name, shape, dt=F32):
        return self.es.enter_context(self.nc.sbuf_tensor(f"{self.name}_{name}", shape, dt))

    def ps(self, name, shape):
        return self.es.enter_context(self.nc.psum_tensor(f"{self.name}_{name}", shape, F32))

    def sem(self, name):
        self.sems.append(self.es.enter_context(self.nc.semaphore(f"{self.name}_{name}")))
        return self.sems[-1]

    def pool_dma_sem(self, name):
        return Scope.lasting.enter_context(self.nc.semaphore(f"{self.name}_{name}"))

    def tally(self, name, per_pass, credit=1):
        return Tally(self.sem(name), per_pass, credit)

    def pool_dma_tally(self, name, per_pass):
        return Tally(self.pool_dma_sem(name), per_pass, 0)


def tile_of(x, t):
    return x[:, bass.ds(t, 1), :].rearrange("p o c -> p (o c)")


def setup_phase(nc, a, k):
    with ExitStack() as es:
        s = Scope(nc, es, "setup")
        loaded, made = s.sem("loaded"), s.sem("made")
        with nc.Block() as block:
            @block.sync
            def _(sp):
                sp.dma_start(k.X[:], a["x"].rearrange("(t p) c -> p t c", p=P)).then_inc(loaded, 16)
                sp.wait_ge(loaded, 16)

            @block.gpsimd
            def _(pool):
                chain = Chain(pool, made)
                nc.gpsimd.memset(k.ones[:], 1.0)
                nc.gpsimd.memset(k.eps[:], LN_EPS)
                nc.gpsimd.memset(k.valid[:], 1.0)
                chain(nc.gpsimd.memset(k.ident[:], 0.0))
                nc.gpsimd.affine_select(out=k.ident[:], in_=k.ident[:], compare_op=ALU.not_equal, fill=1.0,
                                        base=0, pattern=[[-1, P]], channel_multiplier=1)
                chain(nc.gpsimd.affine_select(out=k.valid[:], in_=k.valid[:], compare_op=ALU.is_ge, fill=0.0,
                                              base=N - 1, pattern=[[-P, NT]], channel_multiplier=-1))


def layernorm_phase(nc, k, name, src, keep=None, scale=None, shift=None, ball=None):
    with ExitStack() as es:
        s = Scope(nc, es, name)
        stats = s.sb("stats", [P, GT, 6])
        mv = s.sb("mv", [P, GT, 2])
        sd = s.sb("sd", [P, GT])
        rows = s.sb("rows", [P, GT, D])
        pt = s.ps("pt", [P, KD, 1024])
        nsets = 2 if ball is not None else 1
        stats_ready = s.tally("stats_ready", 1)
        sd_ready = s.tally("sd_ready", 1)
        rows_ready = s.tally("rows_ready", nsets)
        transposed = s.tally("transposed", KD * nsets)
        evacuated = s.tally("evacuated", KD * nsets)
        kept = s.tally("kept", 1)
        order = s.sem("order")
        aorder = s.sem("aorder")
        if ball is not None:
            sq = s.sb("sq", [P, D])
            n2 = s.sb("n2", [P, GT])
            nrm = s.sb("nrm", [P, GT])
            z = s.sb("z", [P, 8, GT])
            norms_ready = s.tally("norms_ready", 2)
            ratio_ready = s.tally("ratio_ready", 1)

        with nc.Block() as block:
            @block.vector
            def _(dve):
                stats_ready.open(dve)
                rows_ready.open(dve)
                chain = Chain(dve, order)
                if ball is not None:
                    ratio_ready.open(dve)
                with dve.Fori(0, NG) as i:
                    chain.fresh()
                    for t in range(GT):
                        last = nc.vector.bn_stats(stats[:, t, :], tile_of(src, i * GT + t))
                    chain(last)
                    for t in range(GT):
                        last = nc.vector.bn_aggr(mv[:, t, :], stats[:, t, :])
                    last.then_inc(stats_ready.sem, 1)
                    sd_ready.wait(dve, i, 1)
                    chain(nc.vector.reciprocal(sd[:], sd[:]))
                    transposed.wait(dve, i)
                    if keep is not None:
                        kept.wait(dve, i)
                    for t in range(GT):
                        last = nc.vector.tensor_scalar(rows[:, t, :], tile_of(src, i * GT + t), mv[:, t, 0:1],
                                                       sd[:, t:t + 1], ALU.subtract, ALU.mult)
                    last.then_inc(rows_ready.sem, 1)
                    if ball is not None:
                        c, c2, top, r, ser, m = (z[:, j, :] for j in range(6))
                        norms_ready.wait(dve, i, 1)
                        chain(nc.vector.tensor_scalar_min(c, nrm[:], MAXNORM))
                        chain(nc.vector.tensor_scalar(r, c, -1.0, 1.0, ALU.mult, ALU.add))
                        chain(nc.vector.reciprocal(r, r))
                        chain(nc.vector.scalar_tensor_tensor(top, c, 1.0, r, ALU.add, ALU.mult))
                        nc.vector.tensor_tensor(c2, c, c, ALU.mult).then_inc(ratio_ready.sem, 1)
                        norms_ready.wait(dve, i, 2)
                        chain(nc.vector.tensor_scalar_max(r, nrm[:], MIN_NORM))
                        chain(nc.vector.reciprocal(r, r))
                        chain(nc.vector.scalar_tensor_tensor(top, z[:, 6, :], 0.5, r, ALU.mult, ALU.mult))
                        chain(nc.vector.tensor_scalar(ser, c2, 1.0 / 7, 1.0 / 5, ALU.mult, ALU.add))
                        chain(nc.vector.tensor_tensor(ser, ser, c2, ALU.mult))
                        chain(nc.vector.scalar_tensor_tensor(ser, ser, 1.0 / 3, c2, ALU.add, ALU.mult))
                        chain(nc.vector.tensor_scalar(m, c, 0.05, None, ALU.is_lt))
                        chain(nc.vector.scalar_tensor_tensor(ser, ser, 1.0, top, ALU.add, ALU.subtract))
                        chain(nc.vector.tensor_tensor(ser, ser, m, ALU.mult))
                        chain(nc.vector.tensor_tensor(top, ser, top, ALU.add))
                        transposed.wait(dve, i, KD)
                        for t in range(GT):
                            last = nc.vector.tensor_scalar(rows[:, t, :], rows[:, t, :], top[:, t:t + 1], None, ALU.mult)
                        last.then_inc(rows_ready.sem, 1)

            @block.scalar
            def _(act):
                sd_ready.open(act)
                evacuated.open(act)
                if ball is not None:
                    norms_ready.open(act)
                chain = Chain(act, aorder)
                with act.Fori(0, NG) as i:
                    chain.fresh()
                    stats_ready.wait(act, i, 1)
                    nc.scalar.activation(sd[:], mv[:, :, 1], ACT.Sqrt, bias=k.eps[:, 0:1]).then_inc(sd_ready.sem, 1)
                    if ball is not None:
                        rows_ready.wait(act, i, 1)
                        for t in range(GT):
                            chain(nc.scalar.activation(sq[:], rows[:, t, :], ACT.Square, accum_out=n2[:, t:t + 1]))
                        nc.scalar.activation(nrm[:], n2[:], ACT.Sqrt).then_inc(norms_ready.sem, 1)
                    for j in range(nsets):
                        if j:
                            ratio_ready.wait(act, i, 1)
                            nc.scalar.activation(z[:, 6, :], z[:, 2, :], ACT.Ln).then_inc(norms_ready.sem, 1)
                        for c in range(KD):
                            transposed.wait(act, i, KD * j + c + 1)
                            out = (ball if j else k.XT)[:, c, bass.ds(i * GC, GC)]
                            if scale is not None:
                                ins = nc.scalar.activation(out, pt[:, c, 0:GC], ACT.Identity,
                                                           bias=shift[:, c:c + 1], scale=scale[:, c:c + 1])
                            else:
                                ins = nc.scalar.activation(out, pt[:, c, 0:GC], ACT.Copy)
                            ins.then_inc(evacuated.sem, 1)

            @block.tensor
            def _(pe):
                transposed.open(pe)
                with pe.Fori(0, NG) as i:
                    for j in range(nsets):
                        rows_ready.wait(pe, i, j + 1)
                        for c in range(KD):
                            evacuated.wait(pe, i, c + 1 if j else 0)
                            for t in range(GT):
                                last = nc.tensor.transpose(pt[:, c, t * P:(t + 1) * P], rows[:, t, c * P:(c + 1) * P],
                                                           k.ident[:])
                            last.then_inc(transposed.sem, 1)

            if keep is not None:
                @block.gpsimd
                def _(pool):
                    kept.open(pool)
                    with pool.Fori(0, NG) as i:
                        rows_ready.hold(pool, i, 1)
                        nc.gpsimd.tensor_copy(keep[:, bass.ds(i * GT, GT), :], rows[:]).then_inc(kept.sem, 1)


def gather_phase(nc, k, a):
    with ExitStack() as es:
        s = Scope(nc, es, "g0")
        w = s.sb("w", [P, KD, D])
        at = s.sb("at", [P, 2, D])
        xs = s.sb("xs", [P, KD, GC])
        pr = s.ps("pr", [P, 8, D])
        row = s.sb("row", [P, GT, R0])
        left = s.sb("left", [P, GT, H0])
        prod = s.sb("prod", [P, GT, D])
        iall = s.sb("iall", [P, 2, NT], I32)
        table, ltable = k.dram("g0_table", (NP, R0)), k.dram("g0_left_logits", (NP, H0))
        weights = s.sem("weights")
        copied = s.tally("copied", 1)
        projected = s.tally("projected", 1)
        rows_ready = s.tally("rows_ready", 1)
        stored = s.tally("stored", 32)
        order = s.sem("order")
        with nc.Block() as block:
            @block.sync
            def _(sp):
                sp.dma_start(w[:], a["L0_gnn_weight"].rearrange("(k p) c -> p k c", p=P)).then_inc(weights, 16)
                sp.dma_start(at[:, 0, :], a["L0_gnn_attn_l"].rearrange("h c -> (h c)").partition_broadcast(P)).then_inc(weights, 16)
                sp.dma_start(at[:, 1, :], a["L0_gnn_attn_r"].rearrange("h c -> (h c)").partition_broadcast(P)).then_inc(weights, 16)
                sp.dma_start(iall[:, 0, :], a["first_src"]).then_inc(weights, 16)
                sp.dma_start(iall[:, 1, :], a["first_dst"]).then_inc(weights, 16)
                sp.wait_ge(weights, 80)
                stored.open(sp)
                with sp.Fori(0, NG) as i:
                    rows_ready.hold(sp, i, 1)
                    sp.dma_start(table[bass.ds(i * GC, GC), :].rearrange("(t p) c -> p t c", p=P), row[:]).then_inc(stored.sem, 16)
                    sp.dma_start(ltable[bass.ds(i * GC, GC), :].rearrange("(t p) c -> p t c", p=P), left[:]).then_inc(stored.sem, 16)
                    stored.hold(sp, i, 32)

            @block.scalar
            def _(act):
                copied.open(act)
                with act.Fori(0, NG) as i:
                    projected.wait(act, i)
                    nc.scalar.activation(xs[:], k.XT[:, :, bass.ds(i * GC, GC)], ACT.Copy).then_inc(copied.sem, 1)

            @block.tensor
            def _(pe):
                projected.open(pe)
                pe.wait_ge(weights, 80)
                with pe.Fori(0, NG) as i:
                    copied.wait(pe, i, 1)
                    rows_ready.wait(pe, i)
                    for t in range(GT):
                        for c in range(KD):
                            last = nc.tensor.matmul(pr[:, t, :], xs[:, c, t * P:(t + 1) * P], w[:, c, :],
                                                    start=c == 0, stop=c == KD - 1)
                    last.then_inc(projected.sem, 1)

            @block.vector
            def _(dve):
                rows_ready.open(dve)
                dve.wait_ge(weights, 80)
                chain = Chain(dve, order)
                with dve.Fori(0, NG) as i:
                    chain.fresh()
                    projected.wait(dve, i, 1)
                    stored.wait(dve, i)
                    for side, out in ((0, left[:]), (1, row[:, :, D:R0])):
                        chain(nc.vector.tensor_tensor(prod[:], pr[:, 0:GT, :], at[:, side:side + 1, :].to_broadcast((P, GT, D)), ALU.mult))
                        chain(nc.vector.tensor_reduce(out, prod[:].rearrange("p t (h c) -> p t h c", h=H0), AX.X, ALU.add))
                    nc.vector.tensor_copy(row[:, :, 0:D], pr[:, 0:GT, :]).then_inc(rows_ready.sem, 1)

        idx = s.sb("idx", [P, 2, GT], I32)
        got = s.sb("got", [P, GT, R0])
        gotl = s.sb("gotl", [P, GT, H0])
        al = s.sb("al", [P, 2, GT, H0])
        mx = s.sb("mx", [P, 2, GT])
        mix = s.sb("mix", [P, GT, C0])
        indexed = s.tally("indexed", 1)
        gathered = [s.pool_dma_tally(f"gathered{t}", 32) for t in range(GT)]
        consumed = s.tally("consumed", 1)
        logits = s.tally("logits", 1)
        exps = s.tally("exps", 1)
        with nc.Block() as block:
            @block.gpsimd
            def _(pool):
                with pool.Fori(0, NG) as i:
                    indexed.hold(pool, i, 1)
                    for t in range(GT):
                        nc.gpsimd.indirect_dma_start(got[:, t, :], None, table, bass.IndirectOffsetOnAxis(ap=idx[:, 1, t:t + 1], axis=0)).then_inc(gathered[t].sem, 16)
                        nc.gpsimd.indirect_dma_start(gotl[:, t, :], None, ltable, bass.IndirectOffsetOnAxis(ap=idx[:, 0, t:t + 1], axis=0)).then_inc(gathered[t].sem, 16)

            @block.scalar
            def _(act):
                exps.open(act)
                with act.Fori(0, NG) as i:
                    logits.wait(act, i, 1)
                    nc.scalar.activation(al[:, 0], al[:, 0], ACT.Exp).then_inc(exps.sem, 1)

            @block.vector
            def _(dve):
                indexed.open(dve)
                logits.open(dve)
                chain = Chain(dve, order)
                chain.fresh()
                with dve.Fori(0, NG) as i:
                    chain.fresh()
                    nc.vector.tensor_copy(idx[:], iall[:, :, bass.ds(i * GT, GT)]).then_inc(indexed.sem, 1)
                    for t in range(GT):
                        gathered[t].wait(dve, i, 32)
                    v, wt = al[:, 0], al[:, 1]
                    chain(nc.vector.tensor_tensor(v, gotl[:], got[:, :, D:R0], ALU.add))
                    chain(nc.vector.scalar_tensor_tensor(v, v, 0.01, v, ALU.mult, ALU.max))
                    chain(nc.vector.tensor_reduce(mx[:, 0, :], v, AX.X, ALU.max))
                    nc.vector.tensor_tensor(v, v, mx[:, 0, :].unsqueeze(2).to_broadcast((P, GT, H0)), ALU.subtract).then_inc(logits.sem, 1)
                    exps.wait(dve, i, 1)
                    chain(nc.vector.tensor_reduce(mx[:, 1, :], v, AX.X, ALU.add))
                    chain(nc.vector.reciprocal(mx[:, 1, :], mx[:, 1, :]))
                    chain(nc.vector.tensor_tensor(wt, v, mx[:, 1, :].unsqueeze(2).to_broadcast((P, GT, H0)), ALU.mult))
                    chain(nc.vector.tensor_tensor(prod[:].rearrange("p t (h c) -> p t h c", h=H0),
                                                  got[:, :, 0:D].rearrange("p t (h c) -> p t h c", h=H0),
                                                  wt.unsqueeze(3).to_broadcast((P, GT, H0, C0)), ALU.mult))
                    chain(nc.vector.tensor_reduce(mix[:], prod[:].rearrange("p t (h c) -> p t c h", h=H0), AX.X, ALU.add))
                    x = k.X[:, bass.ds(i * GT, GT), :].rearrange("p t (h c) -> p t h c", h=H0)
                    chain(nc.vector.tensor_tensor(x, x, mix[:].unsqueeze(2).to_broadcast((P, GT, H0, C0)), ALU.add))


def mixer_phase(nc, k, a, ball):
    with ExitStack() as es:
        s = Scope(nc, es, "mix")
        wq = s.sb("wq", [P, KD, QC * P])
        col = s.sb("col", [P, 3, QC])
        pw = s.sb("pw", [P, QC, P])
        stats = s.sb("stats", [P, QC, 2 * NG, 6])
        mv = s.sb("mv", [P, QC, 2])
        bn = s.sb("bn", [P, 6, QC])
        ph = s.ps("ph", [P, 8, 512])
        loaded, order, aorder = s.sem("loaded"), s.sem("order"), s.sem("aorder")
        zeroed = s.sem("zeroed")
        product = s.tally("product", QC)
        counted = s.tally("counted", QC)
        var_ready, sd_ready = s.sem("var_ready"), s.sem("sd_ready")
        with nc.Block() as block:
            @block.sync
            def _(sp):
                sp.dma_start(wq[:], a["mix_wq"].rearrange("(k p) c -> p k c", p=P)).then_inc(loaded, 16)
                sp.dma_start(col[:], a["mix_col"].rearrange("j (c p) -> p j c", p=P), allow_slow_non_contiguous=True).then_inc(loaded, 16)
                sp.wait_ge(zeroed, 1)
                for b in range(4):
                    sp.dma_start(pw[b * 32:(b + 1) * 32, :, b * 32:(b + 1) * 32],
                                 a["mix_pw"].rearrange("(c b i) o -> b i c o", b=4, i=32)[b]).then_inc(loaded, 16)
                sp.wait_ge(loaded, 96)

            @block.gpsimd
            def _(pool):
                nc.gpsimd.memset(pw[:], 0.0).then_inc(zeroed, 1)

            @block.tensor
            def _(pe):
                product.open(pe)
                pe.wait_ge(loaded, 96)
                with pe.Fori(0, 2 * NG) as i:
                    for c in range(QC):
                        counted.wait(pe, i)
                        for kk in range(KD):
                            last = nc.tensor.matmul(ph[:, c, 0:HC], wq[:, kk, c * P:(c + 1) * P],
                                                    ball[:, kk, bass.ds(i * HC, HC)], start=kk == 0, stop=kk == KD - 1)
                        last.then_inc(product.sem, 1)

            @block.vector
            def _(dve):
                counted.open(dve)
                chain = Chain(dve, order)
                with dve.Fori(0, 2 * NG) as i:
                    for c in range(QC):
                        product.wait(dve, i, c + 1)
                        nc.vector.bn_stats(stats[:, c, bass.ds(i, 1), :].rearrange("p o s -> p (o s)"), ph[:, c, 0:HC]).then_inc(counted.sem, 1)
                dve.wait_ge(loaded, 96)
                counted.wait(dve, 2 * NG)
                for c in range(QC):
                    last = nc.vector.bn_aggr(mv[:, c, :], stats[:, c].rearrange("p i s -> p (i s)"))
                chain(last)
                mean, ex2, m2, var = (bn[:, j, :] for j in range(4))
                ratio = float(NP) / N
                chain(nc.vector.tensor_tensor(ex2, mv[:, :, 0], mv[:, :, 0], ALU.mult))
                chain(nc.vector.tensor_tensor(ex2, ex2, mv[:, :, 1], ALU.add))
                chain(nc.vector.tensor_scalar(mean, mv[:, :, 0], ratio, None, ALU.mult))
                chain(nc.vector.tensor_tensor(m2, mean, mean, ALU.mult))
                chain(nc.vector.scalar_tensor_tensor(var, ex2, ratio, m2, ALU.mult, ALU.subtract))
                nc.vector.tensor_scalar_max(var, var, 0.0).then_inc(var_ready, 1)
                dve.wait_ge(sd_ready, 1)
                chain(nc.vector.reciprocal(bn[:, 4, :], bn[:, 4, :]))
                chain(nc.vector.tensor_tensor(bn[:, 4, :], bn[:, 4, :], col[:, 0, :], ALU.mult))
                chain(nc.vector.tensor_tensor(mean, mean, bn[:, 4, :], ALU.mult))
                chain(nc.vector.tensor_tensor(bn[:, 5, :], col[:, 1, :], mean, ALU.subtract))
                chain(nc.vector.tensor_tensor(pw[:], pw[:], col[:, 2, :].unsqueeze(2).to_broadcast((P, QC, P)), ALU.mult))

            @block.scalar
            def _(act):
                act.wait_ge(var_ready, 1)
                nc.scalar.activation(bn[:, 4, :], bn[:, 3, :], ACT.Sqrt, bias=k.eps[:, 0:1]).then_inc(sd_ready, 1)

        wr = s.sb("wr", [P, 4, D])
        br = s.sb("br", [P, D])
        blk = s.sb("blk", [P, P])
        work = k.XT[:].rearrange("p k n -> p (k n)")[:, 0:(3 * QC + 4) * HC].rearrange("p (c n) -> p c n", n=HC)
        U, V, sq, tmp = work[:, 0:QC], work[:, QC:2 * QC], work[:, 2 * QC:3 * QC], work[:, 3 * QC:]
        O = s.sb("O", [P, 4, GC])
        g = s.sb("g", [P, 6, HC])
        node = s.sb("node", [P, 4, GT])
        ft = s.sb("ft", [P, GT, D])
        junk = s.sb("junk", [P, D])
        made = s.sem("made")
        h_done = s.tally("h_done", 2)
        s_done = s.tally("s_done", 2)
        sums_done = s.tally("sums_done", 2)
        onorm_done = s.tally("onorm_done", 2)
        ft_done = s.tally("ft_done", 1)
        u_ready = s.tally("u_ready", 2)
        s_ready = s.tally("s_ready", 2)
        roots = s.tally("roots", 6)
        row_norms = s.tally("row_norms", 1)
        u2_ready = s.tally("u2_ready", 2)
        squares = s.tally("squares", 6)
        o_ready = s.tally("o_ready", 2)
        o_scaled = s.tally("o_scaled", 2)
        ft_ready = s.tally("ft_ready", 1)
        with nc.Block() as block:
            @block.sync
            def _(sp):
                sp.dma_start(wr[:], a["L0_mix_w_res"]).then_inc(loaded, 16)
                sp.dma_start(br[:], a["L0_mix_b_res"].partition_broadcast(P)).then_inc(loaded, 16)
                sp.wait_ge(loaded, 128)

            @block.gpsimd
            def _(pool):
                nc.gpsimd.memset(blk[:], 0.0).then_inc(made, 1)
                pool.wait_ge(made, 1)
                for b in range(4):
                    nc.gpsimd.memset(blk[32 * b:32 * b + 32, 32 * b:32 * b + 32], 1.0).then_inc(made, 1)

            @block.tensor
            def _(pe):
                for x in (h_done, s_done, sums_done, onorm_done, ft_done):
                    x.open(pe)
                pe.wait_ge(loaded, 128)
                pe.wait_ge(made, 5)
                with pe.Fori(0, NG) as i:
                    for j in range(2):
                        o_ready.wait(pe, i, j)
                        ft_ready.wait(pe, i)
                        for c in range(QC):
                            for kk in range(KD):
                                last = nc.tensor.matmul(ph[:, c, 0:HC], wq[:, kk, c * P:(c + 1) * P],
                                                        ball[:, kk, bass.ds(i * GC + j * HC, HC)], start=kk == 0, stop=kk == KD - 1)
                        last.then_inc(h_done.sem, 1)
                        u_ready.wait(pe, i, j + 1)
                        for c in range(QC):
                            nc.tensor.matmul(ph[:, c, 0:HC], pw[:, c, :], U[:, c, :], start=True, stop=True)
                        u2_ready.wait(pe, i, j + 1)
                        squares.wait(pe, i, 3 * j)
                        for c in range(QC):
                            last = nc.tensor.matmul(ph[:, 6, 0:HC], k.ones[:], sq[:, c, :], start=c == 0, stop=c == QC - 1)
                        last.then_inc(s_done.sem, 1)
                        s_ready.wait(pe, i, j + 1)
                        for c in range(QC):
                            nc.tensor.matmul(ph[:, 7, 0:HC], k.ones[:], sq[:, c, :], start=c == 0, stop=c == QC - 1)
                        for m in range(4):
                            last = nc.tensor.matmul(ph[:, m, 0:HC], blk[:], U[:, 2 + m, :] if m < 2 else V[:, m, :],
                                                    start=True, stop=True)
                        last.then_inc(sums_done.sem, 1)
                        o_ready.wait(pe, i, j + 1)
                        for m in range(4):
                            last = nc.tensor.matmul(ph[:, 6, 0:HC], k.ones[:], sq[:, m, :], start=m == 0, stop=m == 3)
                        last.then_inc(onorm_done.sem, 1)
                    o_scaled.wait(pe, i, 2)
                    for t in range(GT):
                        for m in range(4):
                            last = nc.tensor.matmul(ph[:, t // 2, (t % 2) * D:(t % 2 + 1) * D], O[:, m, t * P:(t + 1) * P],
                                                    wr[:, m, :], start=m == 0, stop=m == 3)
                    last.then_inc(ft_done.sem, 1)

            @block.scalar
            def _(act):
                for x in (u_ready, s_ready, roots, row_norms):
                    x.open(act)
                chain = Chain(act, aorder)
                with act.Fori(0, NG) as i:
                    chain.fresh()
                    for j in range(2):
                        h_done.wait(act, i, j + 1)
                        for c in range(QC):
                            last = nc.scalar.activation(U[:, c, :], ph[:, c, 0:HC], ACT.Relu, bias=bn[:, 5, c:c + 1], scale=bn[:, 4, c:c + 1])
                        last.then_inc(u_ready.sem, 1)
                        s_done.wait(act, i, j + 1)
                        nc.scalar.activation(V[:, 0:4, :], ph[:, 0:4, 0:HC], ACT.Relu)
                        nc.scalar.activation(V[:, 4:6, :], ph[:, 4:6, 0:HC], ACT.Copy)
                        nc.scalar.activation(sq, ph[:, 0:6, 0:HC], ACT.Square).then_inc(s_ready.sem, 1)
                        squares.wait(act, i, 3 * j + 1)
                        nc.scalar.activation(g[:, 1, :], g[:, 0, :], ACT.Sqrt).then_inc(roots.sem, 1)
                        squares.wait(act, i, 3 * j + 2)
                        nc.scalar.activation(g[:, 3, :], g[:, 2, :], ACT.Sqrt).then_inc(roots.sem, 1)
                        squares.wait(act, i, 3 * j + 3)
                        nc.scalar.activation(g[:, 1, :], g[:, 0, :], ACT.Sqrt).then_inc(roots.sem, 1)
                    ft_ready.wait(act, i, 1)
                    for t in range(GT):
                        chain(nc.scalar.activation(junk[:], ft[:, t, :], ACT.Square, accum_out=node[:, 0, t:t + 1]))
                    chain(nc.scalar.activation(node[:, 1, :], node[:, 0, :], ACT.Sqrt))
                    nc.scalar.activation(node[:, 2, :], node[:, 1, :], ACT.Tanh).then_inc(row_norms.sem, 1)

            @block.vector
            def _(dve):
                for x in (u2_ready, squares, o_ready, o_scaled, ft_ready):
                    x.open(dve)
                chain = Chain(dve, order)
                chain.fresh()
                dve.wait_ge(loaded, 128)
                with dve.Fori(0, NG) as i:
                    chain.fresh()
                    for j in range(2):
                        u_ready.wait(dve, i, j + 1)
                        onorm_done.wait(dve, i, j)
                        nc.vector.tensor_tensor(sq, U, U, ALU.mult).then_inc(u2_ready.sem, 1)
                        sums_done.wait(dve, i, j + 1)
                        nc.vector.tensor_scalar_max(g[:, 0, :], ph[:, 6, 0:HC], MIN_NORM ** 2).then_inc(squares.sem, 1)
                        roots.wait(dve, i, 3 * j + 1)
                        chain(nc.vector.reciprocal(g[:, 1, :], g[:, 1, :]))
                        chain(nc.vector.tensor_scalar(g[:, 1, :], g[:, 1, :], ATANH_MAX, 1.0, ALU.mult, ALU.min))
                        chain(nc.vector.tensor_tensor(g[:, 2, :], g[:, 0, :], ph[:, 7, 0:HC], ALU.add))
                        chain(nc.vector.tensor_tensor(g[:, 2, :], g[:, 2, :], g[:, 1, :], ALU.mult))
                        chain(nc.vector.tensor_tensor(g[:, 2, :], g[:, 2, :], g[:, 1, :], ALU.mult))
                        nc.vector.tensor_scalar_max(g[:, 2, :], g[:, 2, :], MIN_NORM ** 2).then_inc(squares.sem, 1)
                        roots.wait(dve, i, 3 * j + 2)
                        chain(nc.vector.reciprocal(g[:, 3, :], g[:, 3, :]))
                        chain(nc.vector.tensor_scalar(g[:, 3, :], g[:, 3, :], ATANH_MAX, 1.0, ALU.mult, ALU.min))
                        chain(nc.vector.tensor_tensor(g[:, 4, :], g[:, 1, :], g[:, 3, :], ALU.mult))
                        chain(nc.vector.reciprocal(g[:, 5, :], g[:, 4, :]))
                        chain(nc.vector.tensor_scalar(g[:, 5, :], g[:, 5, :], ATT_EPS, None, ALU.mult))
                        eps2 = g[:, 5:6, :].to_broadcast((P, 2, HC))
                        nc.vector.tensor_tensor(tmp[:, 0:2], U[:, 4:6], eps2, ALU.add)
                        chain(nc.vector.tensor_tensor(tmp[:, 2:4], V[:, 4:6], eps2, ALU.add))
                        chain(nc.vector.reciprocal(tmp, tmp))
                        nc.vector.tensor_tensor(tmp[:, 0:2], tmp[:, 0:2], U[:, 4:6], ALU.mult)
                        chain(nc.vector.tensor_tensor(tmp[:, 2:4], tmp[:, 2:4], V[:, 4:6], ALU.mult))
                        nc.vector.tensor_tensor(tmp[:, 0:2], tmp[:, 0:2], U[:, 0:2], ALU.mult)
                        chain(nc.vector.tensor_tensor(tmp[:, 2:4], tmp[:, 2:4], V[:, 0:2], ALU.mult))
                        chain(nc.vector.tensor_tensor(tmp, tmp, ph[:, 0:4, 0:HC], ALU.mult))
                        nc.vector.tensor_tensor(sq[:, 0:4], tmp, tmp, ALU.mult).then_inc(o_ready.sem, 1)
                        onorm_done.wait(dve, i, j + 1)
                        nc.vector.tensor_scalar_max(g[:, 0, :], ph[:, 6, 0:HC], MIN_NORM ** 2).then_inc(squares.sem, 1)
                        chain(nc.vector.tensor_tensor(g[:, 4, :], g[:, 4, :], g[:, 4, :], ALU.mult))
                        roots.wait(dve, i, 3 * j + 3)
                        chain(nc.vector.reciprocal(g[:, 1, :], g[:, 1, :]))
                        chain(nc.vector.scalar_tensor_tensor(g[:, 1, :], g[:, 1, :], ATANH_MAX, g[:, 4, :], ALU.mult, ALU.min))
                        ft_done.wait(dve, i)
                        nc.vector.tensor_tensor(O[:, :, j * HC:(j + 1) * HC], tmp, g[:, 1:2, :].to_broadcast((P, 4, HC)), ALU.mult).then_inc(o_scaled.sem, 1)
                        o_scaled.wait(dve, i, j + 1)
                    ft_done.wait(dve, i, 1)
                    nc.vector.tensor_tensor(ft[:], ph[:, 0:4, :].rearrange("p b c -> p (b c)")[:, 0:GT * D].rearrange("p (t c) -> p t c", c=D),
                                            br[:].unsqueeze(1).to_broadcast((P, GT, D)), ALU.add).then_inc(ft_ready.sem, 1)
                    row_norms.wait(dve, i, 1)
                    chain(nc.vector.tensor_scalar_max(node[:, 1, :], node[:, 1, :], MIN_NORM))
                    chain(nc.vector.reciprocal(node[:, 1, :], node[:, 1, :]))
                    chain(nc.vector.scalar_tensor_tensor(node[:, 3, :], node[:, 2, :], MAXNORM, node[:, 1, :], ALU.min, ALU.mult))
                    for t in range(GT):
                        x = tile_of(k.X, i * GT + t)
                        last = nc.vector.scalar_tensor_tensor(x, ft[:, t, :], node[:, 3, t:t + 1], x, ALU.mult, ALU.add)
                    chain(last)


def leaky(chain, dve, x, slope):
    chain(dve.scalar_tensor_tensor(x, x, slope, x, ALU.mult, ALU.max))


def gate_phase(nc, k, a, gates):
    with ExitStack() as es:
        s = Scope(nc, es, "gate")
        wg = s.sb("wg", [P, KD, GW])
        att = s.sb("att", [P, 4, GW])
        bg = s.sb("bg", [P, GW])
        hs = s.sb("hs", [P, NT, MW])
        td = s.sb("td", [P, NT, 2 * GH])
        own = s.sb("own", [P, NT, MW])
        ew = s.sb("ew", [P, NT, GW])
        si = s.sb("si", [P, S0 + 2 * U0], I32)
        di = s.sb("di", [P, S0 + 2 * U0], I32)
        lo = s.sb("lo", [P, S0])
        hi = s.sb("hi", [P, S0])
        ti = s.sb("ti", [P, S0], I32)
        small = s.sb("small", [P, 16])
        stable, dtable = k.dram("gate_stable", (NP, MW)), k.dram("gate_dtable", (NP, 2 * GH))
        loaded, order = s.sem("loaded"), s.sem("order")
        tables_ready, stored = s.sem("tables_ready"), s.sem("stored")
        top = s.sem("top")
        es2 = ExitStack()
        with es2:
            s2 = Scope(nc, es2, "gate1")
            xs = s2.sb("xs", [P, KD, GC])
            pg = s2.ps("pg", [P, 3, 512])
            copied, projected, taken = s2.tally("copied", 1), s2.tally("projected", 1), s2.tally("taken", 1)
            logits, exps = s2.sem("logits"), s2.sem("exps")
            with nc.Block() as block:
                @block.sync
                def _(sp):
                    sp.dma_start(wg[:], a["L0_ffn_W_gat"].rearrange("(k p) c -> p k c", p=P)).then_inc(loaded, 16)
                    sp.dma_start(att[:, 0, :], a["L0_ffn_att_src"].rearrange("h e -> (h e)").partition_broadcast(P)).then_inc(loaded, 16)
                    sp.dma_start(att[:, 1, :], a["L0_ffn_att_dst"].rearrange("h e -> (h e)").partition_broadcast(P)).then_inc(loaded, 16)
                    sp.dma_start(att[:, 2, :], a["L0_ffn_ln_gamma"].partition_broadcast(P)).then_inc(loaded, 16)
                    sp.dma_start(att[:, 3, :], a["L0_ffn_ln_beta"].partition_broadcast(P)).then_inc(loaded, 16)
                    sp.dma_start(bg[:], a["L0_ffn_b_gat"].partition_broadcast(P)).then_inc(loaded, 16)
                    sp.dma_start(si[:, 0:S0], a["L0_ffn_edge_index"][0]).then_inc(loaded, 16)
                    sp.dma_start(di[:, 0:S0], a["L0_ffn_edge_index"][1]).then_inc(loaded, 16)
                    sp.wait_ge(loaded, 128)
                    sp.wait_ge(tables_ready, 1)
                    sp.dma_start(stable.rearrange("(t p) c -> p t c", p=P), hs[:]).then_inc(stored, 16)
                    sp.dma_start(dtable.rearrange("(t p) c -> p t c", p=P), td[:]).then_inc(stored, 16)
                    sp.wait_ge(stored, 32)

                @block.scalar
                def _(act):
                    copied.open(act)
                    with act.Fori(0, NG) as i:
                        projected.wait(act, i)
                        nc.scalar.activation(xs[:], k.XT[:, :, bass.ds(i * GC, GC)], ACT.Copy).then_inc(copied.sem, 1)
                    act.wait_ge(logits, 1)
                    nc.scalar.activation(own[:, :, GW:MW], own[:, :, GW:MW], ACT.Exp).then_inc(exps, 1)

                @block.tensor
                def _(pe):
                    projected.open(pe)
                    pe.wait_ge(loaded, 128)
                    with pe.Fori(0, NG) as i:
                        copied.wait(pe, i, 1)
                        taken.wait(pe, i)
                        for t in range(GT):
                            for c in range(KD):
                                last = nc.tensor.matmul(pg[:, 0, t * GW:(t + 1) * GW], xs[:, c, t * P:(t + 1) * P], wg[:, c, :],
                                                        start=c == 0, stop=c == KD - 1)
                        last.then_inc(projected.sem, 1)
                    pe.wait_ge(top, 1)
                    nc.tensor.transpose(pg[0:GH, 1, 0:P], small[:, 0:GH], k.ident[:]).then_inc(top, 1)
                    pe.wait_ge(top, 3)
                    nc.tensor.matmul(pg[:, 2, 0:GH], k.ones[0:GH, :], small[0:GH, 8:8 + GH], start=True, stop=True).then_inc(top, 1)

                @block.vector
                def _(dve):
                    taken.open(dve)
                    chain = Chain(dve, order)
                    dve.wait_ge(loaded, 128)
                    with dve.Fori(0, NG) as i:
                        projected.wait(dve, i, 1)
                        nc.vector.tensor_copy(hs[:, bass.ds(i * GT, GT), 0:GW], pg[:, 0, 0:GT * GW].rearrange("p (t c) -> p t c", c=GW)).then_inc(taken.sem, 1)
                    taken.wait(dve, NG)
                    h = hs[:, :, 0:GW]
                    for side, out in ((0, hs[:, :, GW:MW]), (1, td[:, :, 0:GH])):
                        chain(nc.vector.tensor_tensor(ew[:], h, att[:, side:side + 1, :].to_broadcast((P, NT, GW)), ALU.mult))
                        chain(nc.vector.tensor_reduce(out, ew[:].rearrange("p t (h e) -> p t h e", e=E0), AX.X, ALU.add))
                    chain(nc.vector.tensor_scalar(ew[:, :, 4], k.valid[:], BIG, -BIG, ALU.mult, ALU.add))
                    chain(nc.vector.tensor_tensor(ew[:, :, 0:GH], hs[:, :, GW:MW], ew[:, :, 4:5].to_broadcast((P, NT, GH)), ALU.add))
                    nc.vector.tensor_reduce(small[:, 0:GH], ew[:, :, 0:GH].rearrange("p t h -> p h t"), AX.X, ALU.max).then_inc(top, 1)
                    chain(nc.vector.tensor_single_scalar(ti[:], di[:, 0:S0], 7, ALU.arith_shift_right))
                    chain(nc.vector.tensor_copy(hi[:], ti[:]))
                    chain(nc.vector.tensor_single_scalar(ti[:], di[:, 0:S0], P - 1, ALU.bitwise_and))
                    chain(nc.vector.tensor_copy(lo[:], ti[:]))
                    nc.vector.memset(si[:, S0:], 0)
                    nc.vector.memset(di[:, S0:], 0)
                    chain(nc.vector.tensor_scalar_min(si[:, 0:S0], si[:, 0:S0], N - 1))
                    chain(nc.vector.tensor_scalar_min(di[:, 0:S0], di[:, 0:S0], N - 1))
                    dve.wait_ge(top, 2)
                    chain(nc.vector.tensor_reduce(small[0:GH, 4:5], pg[0:GH, 1, 0:P], AX.X, ALU.max))
                    nc.vector.tensor_scalar(small[0:GH, 8:8 + GH], k.ident[0:GH, 0:GH], small[0:GH, 4:5], None, ALU.mult).then_inc(top, 1)
                    dve.wait_ge(top, 4)
                    shift, e = td[:, :, GH:2 * GH], own[:, :, GW:MW]
                    chain(nc.vector.tensor_copy(small[:, 12:16], pg[:, 2, 0:GH]))
                    chain(nc.vector.tensor_tensor(shift, td[:, :, 0:GH], small[:, 12:16].unsqueeze(1).to_broadcast((P, NT, GH)), ALU.add))
                    leaky(chain, nc.vector, shift, 0.2)
                    dve.sem_inc(tables_ready, 1)
                    chain(nc.vector.tensor_tensor(e, hs[:, :, GW:MW], td[:, :, 0:GH], ALU.add))
                    leaky(chain, nc.vector, e, 0.2)
                    nc.vector.tensor_tensor(e, e, shift, ALU.subtract).then_inc(logits, 1)
                    dve.wait_ge(exps, 1)
                    chain(nc.vector.tensor_tensor(own[:, :, 0:GW].rearrange("p t (h e) -> p t h e", e=E0),
                                                  h.rearrange("p t (h e) -> p t h e", e=E0),
                                                  e.unsqueeze(3).to_broadcast((P, NT, GH, E0)), ALU.mult))

        B0 = (NT // 2 + 1) * MW
        iota_lo = s.sb("iota_lo", [P, P])
        iota_hi = s.sb("iota_hi", [P, NT])
        zero = s.sb("zero", [P, 512])
        sums = s.ps("sums", [P, 2, 512])
        with ExitStack() as es2:
            s2 = Scope(nc, es2, "gate2")
            idx = s2.sb("idx", [P, 2, 2, U0], I32)
            gs = s2.sb("gs", [P, 2, U0, MW])
            gd = s2.sb("gd", [P, 2, U0, 2 * GH])
            msg = s2.sb("msg", [P, U0, MW])
            hot = s2.sb("hot", [P, U0, NT])
            pick = s2.sb("pick", [P, 2, 4, P])
            wide = s2.sb("wide", [P, 2, 4, NT * MW])
            made = s2.sem("made")
            indexed = s2.tally("indexed", 2)
            gathered = [s2.pool_dma_tally(f"gathered{b}", 32 * U0) for b in range(2)]
            logits, exps = s2.tally("logits", 2), s2.tally("exps", 2)
            expanded, summed = s2.tally("expanded", 4), s2.tally("summed", 4)
            with nc.Block() as block:
                @block.gpsimd
                def _(pool):
                    nc.gpsimd.memset(zero[:], 0.0).then_inc(made, 1)
                    nc.gpsimd.iota(iota_lo[:], pattern=[[1, P]], base=0, channel_multiplier=0, allow_small_or_imprecise_dtypes=True).then_inc(made, 1)
                    nc.gpsimd.iota(iota_hi[:], pattern=[[1, NT]], base=0, channel_multiplier=0, allow_small_or_imprecise_dtypes=True).then_inc(made, 1)
                    with pool.Fori(0, S0 // (2 * U0)) as i:
                        for b in range(2):
                            indexed.hold(pool, i, b + 1)
                            for u in range(U0):
                                nc.gpsimd.indirect_dma_start(gs[:, b, u, :], None, stable, bass.IndirectOffsetOnAxis(ap=idx[:, 0, b, u:u + 1], axis=0)).then_inc(gathered[b].sem, 16)
                                nc.gpsimd.indirect_dma_start(gd[:, b, u, :], None, dtable, bass.IndirectOffsetOnAxis(ap=idx[:, 1, b, u:u + 1], axis=0)).then_inc(gathered[b].sem, 16)

                @block.scalar
                def _(act):
                    exps.open(act)
                    with act.Fori(0, S0 // (2 * U0)) as i:
                        for b in range(2):
                            logits.wait(act, i, b + 1)
                            nc.scalar.activation(msg[:, :, GW:MW], msg[:, :, GW:MW], ACT.Exp).then_inc(exps.sem, 1)

                @block.vector
                def _(dve):
                    for x in (indexed, logits, expanded):
                        x.open(dve)
                    dve.wait_ge(made, 3)
                    chain = Chain(dve, order)
                    chain.fresh()

                    def index(step, b):
                        nc.vector.tensor_copy(idx[:, 0, b, :], si[:, bass.ds(step, U0)])
                        nc.vector.tensor_copy(idx[:, 1, b, :], di[:, bass.ds(step, U0)]).then_inc(indexed.sem, 1)

                    index(0, 0)
                    index(U0, 1)
                    with dve.Fori(0, S0 // (2 * U0)) as i:
                        chain.fresh()
                        for b in range(2):
                            step = i * (2 * U0) + b * U0
                            gathered[b].wait(dve, i, 32 * U0)
                            e = msg[:, :, GW:MW]
                            chain(nc.vector.tensor_tensor(e, gs[:, b, :, GW:MW], gd[:, b, :, 0:GH], ALU.add))
                            leaky(chain, nc.vector, e, 0.2)
                            nc.vector.tensor_tensor(e, e, gd[:, b, :, GH:2 * GH], ALU.subtract).then_inc(logits.sem, 1)
                            chain(nc.vector.tensor_tensor(hot[:], iota_hi[:].unsqueeze(1).to_broadcast((P, U0, NT)),
                                                          hi[:, bass.ds(step, U0)].unsqueeze(2).to_broadcast((P, U0, NT)), ALU.is_equal))
                            exps.wait(dve, i, b + 1)
                            chain(nc.vector.tensor_tensor(msg[:, :, 0:GW].rearrange("p u (h e) -> p u h e", e=E0),
                                                          gs[:, b, :, 0:GW].rearrange("p u (h e) -> p u h e", e=E0),
                                                          e.unsqueeze(3).to_broadcast((P, U0, GH, E0)), ALU.mult))
                            nc.vector.tensor_copy(idx[:, 0, b, :], si[:, bass.ds((i * (2 * U0) + (b + 2) * U0), U0)])
                            nc.vector.tensor_copy(idx[:, 1, b, :], di[:, bass.ds((i * (2 * U0) + (b + 2) * U0), U0)]).then_inc(indexed.sem, 1)
                            for q in range(2):
                                summed.wait(dve, i, 2 * b + q - 1)
                                u0 = 4 * q
                                nc.vector.tensor_tensor(pick[:, q], iota_lo[:].unsqueeze(1).to_broadcast((P, 4, P)),
                                                        lo[:, bass.ds(step + u0, 4)].unsqueeze(2).to_broadcast((P, 4, P)), ALU.is_equal)
                                nc.vector.tensor_tensor(wide[:, q].rearrange("p u (n c) -> p u n c", c=MW),
                                                        hot[:, u0:u0 + 4, :].unsqueeze(3).to_broadcast((P, 4, NT, MW)),
                                                        msg[:, u0:u0 + 4, :].unsqueeze(2).to_broadcast((P, 4, NT, MW)), ALU.mult).then_inc(expanded.sem, 1)
                            expanded.wait(dve, i, 2 * b + 2)

                @block.tensor
                def _(pe):
                    summed.open(pe)
                    pe.wait_ge(made, 3)
                    for c, w in ((0, B0), (1, NT * MW - B0)):
                        nc.tensor.matmul(sums[:, c, 0:w], zero[:, 0:P], zero[:, 0:w], start=True, stop=False)
                    with pe.Fori(0, S0 // (2 * U0)) as i:
                        for j in range(4):
                            expanded.wait(pe, i, j + 1)
                            for u in range(4):
                                nc.tensor.matmul(sums[:, 0, 0:B0], pick[:, j % 2, u, :], wide[:, j % 2, u, 0:B0], start=False, stop=False)
                                last = nc.tensor.matmul(sums[:, 1, 0:NT * MW - B0], pick[:, j % 2, u, :], wide[:, j % 2, u, B0:], start=False, stop=False)
                            last.then_inc(summed.sem, 1)
                    for c, w in ((0, B0), (1, NT * MW - B0)):
                        nc.tensor.matmul(sums[:, c, 0:w], zero[:, 0:P], zero[:, 0:w], start=False, stop=True)

        with ExitStack() as es2:
            s2 = Scope(nc, es2, "gate3")
            agg = s2.sb("agg", [P, NT, GW])
            t4 = s2.sb("t4", [P, 6, NT, E0])
            t1 = s2.sb("t1", [P, 3, NT])
            steps, asteps = s2.sem("steps"), s2.sem("asteps")
            with nc.Block() as block:
                @block.vector
                def _(dve):
                    chain = Chain(dve, order)
                    chain.fresh()

                    def over(x, w):
                        return x.unsqueeze(2).to_broadcast((P, NT, w))

                    n0 = B0 // MW
                    nc.vector.tensor_tensor(own[:, 0:n0, :], own[:, 0:n0, :], sums[:, 0, 0:B0].rearrange("p (t c) -> p t c", c=MW), ALU.add)
                    chain(nc.vector.tensor_tensor(own[:, n0:, :], own[:, n0:, :], sums[:, 1, 0:NT * MW - B0].rearrange("p (t c) -> p t c", c=MW), ALU.add))
                    chain(nc.vector.reciprocal(own[:, :, GW:MW], own[:, :, GW:MW]))
                    chain(nc.vector.tensor_tensor(agg[:].rearrange("p t (h e) -> p t h e", e=E0),
                                                  own[:, :, 0:GW].rearrange("p t (h e) -> p t h e", e=E0),
                                                  own[:, :, GW:MW].unsqueeze(3).to_broadcast((P, NT, GH, E0)), ALU.mult))
                    chain(nc.vector.tensor_tensor(agg[:], agg[:], bg[:].unsqueeze(1).to_broadcast((P, NT, GW)), ALU.add))
                    mean, var, r = (t1[:, j, :] for j in range(3))
                    chain(nc.vector.tensor_reduce(mean, agg[:], AX.X, ALU.add))
                    chain(nc.vector.tensor_scalar(mean, mean, 1.0 / GW, None, ALU.mult))
                    chain(nc.vector.tensor_tensor(agg[:], agg[:], over(mean, GW), ALU.subtract))
                    chain(nc.vector.tensor_tensor(ew[:], agg[:], agg[:], ALU.mult))
                    chain(nc.vector.tensor_reduce(var, ew[:], AX.X, ALU.add))
                    nc.vector.tensor_scalar(var, var, 1.0 / GW, None, ALU.mult).then_inc(steps, 1)
                    dve.wait_ge(asteps, 1)
                    chain(nc.vector.reciprocal(r, r))
                    chain(nc.vector.tensor_tensor(agg[:], agg[:], over(r, GW), ALU.mult))
                    chain(nc.vector.tensor_tensor(agg[:], agg[:], att[:, 2:3, :].to_broadcast((P, NT, GW)), ALU.mult))
                    chain(nc.vector.tensor_tensor(agg[:], agg[:], att[:, 3:4, :].to_broadcast((P, NT, GW)), ALU.add))
                    score, rank, ge, ex = (t4[:, j] for j in range(4))
                    chain(nc.vector.tensor_reduce(score, agg[:].rearrange("p t (h e) -> p t e h", e=E0), AX.X, ALU.add))
                    chain(nc.vector.tensor_scalar(score, score, 1.0 / GH, None, ALU.mult))
                    chain(nc.vector.memset(rank, 0.0))
                    for e in range(E0):
                        for o in range(E0):
                            if o != e:
                                chain(nc.vector.tensor_tensor(ge[:, :, 0], score[:, :, o], score[:, :, e], ALU.is_ge if o < e else ALU.is_gt))
                                chain(nc.vector.tensor_tensor(rank[:, :, e], rank[:, :, e], ge[:, :, 0], ALU.add))
                    chain(nc.vector.tensor_scalar(rank, rank, 1.5, None, ALU.is_lt))
                    chain(nc.vector.tensor_reduce(mean, score, AX.X, ALU.max))
                    nc.vector.tensor_tensor(ex, score, over(mean, E0), ALU.subtract).then_inc(steps, 1)
                    dve.wait_ge(asteps, 2)
                    chain(nc.vector.tensor_tensor(ex, ex, rank, ALU.mult))
                    chain(nc.vector.tensor_reduce(var, ex, AX.X, ALU.add))
                    chain(nc.vector.reciprocal(var, var))
                    chain(nc.vector.tensor_tensor(gates[:], ex, over(var, E0), ALU.mult))

                @block.scalar
                def _(act):
                    act.wait_ge(steps, 1)
                    nc.scalar.activation(t1[:, 2, :], t1[:, 1, :], ACT.Sqrt, bias=k.eps[:, 0:1]).then_inc(asteps, 1)
                    act.wait_ge(steps, 2)
                    nc.scalar.activation(t4[:, 3], t4[:, 3], ACT.Exp).then_inc(asteps, 1)


def experts_phase(nc, k, name, w1d, b1d, w2d, b2d, parts, gate, dst):
    FC = F0 // P
    with ExitStack() as es:
        s = Scope(nc, es, name)
        w1 = s.sb("w1", [P, parts, KD, F0])
        w2 = s.sb("w2", [P, parts, FC, D])
        b1 = s.sb("b1", [P, parts, FC])
        b2 = s.sb("b2", [1, parts, D])
        hid = s.sb("hid", [P, 2, FC, GC])
        ph = s.ps("ph", [P, FC, 512])
        py = s.ps("py", [P, 8, D])
        loaded = s.sem("loaded")
        h_done, gelus = s.tally("h_done", parts * 2 * FC), s.tally("gelus", parts * 2 * FC)
        y_done, added = s.tally("y_done", parts), s.tally("added", parts)
        with nc.Block() as block:
            @block.sync
            def _(sp):
                for e in range(parts):
                    sp.dma_start(w1[:, e], w1d[e].rearrange("(k p) f -> p k f", p=P)).then_inc(loaded, 16)
                    sp.dma_start(w2[:, e], w2d[e].rearrange("(k p) f -> p k f", p=P)).then_inc(loaded, 16)
                sp.dma_start(b1[:], b1d.rearrange("e (f p) -> p e f", p=P), allow_slow_non_contiguous=True).then_inc(loaded, 16)
                sp.dma_start(b2[:], b2d.rearrange("(o e) d -> o e d", o=1)).then_inc(loaded, 16)
                sp.wait_ge(loaded, 32 * parts + 32)

            @block.tensor
            def _(pe):
                h_done.open(pe)
                y_done.open(pe)
                pe.wait_ge(loaded, 32 * parts + 32)
                with pe.Fori(0, NG) as i:
                    def hidden(e):
                        for j in range(2):
                            for f in range(FC):
                                gelus.wait(pe, i, max((e * 2 + j - 1) * FC + f + 1, 0))
                                for c in range(KD):
                                    last = nc.tensor.matmul(ph[:, f, 0:HC], w1[:, e, c, f * P:(f + 1) * P],
                                                            k.XT[:, c, bass.ds(i * GC + j * HC, HC)], start=c == 0, stop=c == KD - 1)
                                last.then_inc(h_done.sem, 1)

                    def down(e):
                        gelus.wait(pe, i, (e + 1) * 2 * FC)
                        added.wait(pe, i, e)
                        for t in range(GT):
                            nc.tensor.matmul(py[:, t, :], k.ones[0:1, :], b2[0:1, e, :], start=True, stop=False)
                            for f in range(FC):
                                last = nc.tensor.matmul(py[:, t, :], hid[:, e % 2, f, t * P:(t + 1) * P], w2[:, e, f, :],
                                                        start=False, stop=f == FC - 1)
                        last.then_inc(y_done.sem, 1)

                    hidden(0)
                    for e in range(1, parts):
                        hidden(e)
                        down(e - 1)
                    down(parts - 1)

            @block.scalar
            def _(act):
                gelus.open(act)
                act.wait_ge(loaded, 32 * parts + 32)
                with act.Fori(0, NG) as i:
                    for e in range(parts):
                        y_done.wait(act, i, max(e - 1, 0))
                        for j in range(2):
                            for f in range(FC):
                                h_done.wait(act, i, (e * 2 + j) * FC + f + 1)
                                nc.scalar.activation(hid[:, e % 2, f, j * HC:(j + 1) * HC], ph[:, f, 0:HC], ACT.Gelu,
                                                     bias=b1[:, e, f:f + 1]).then_inc(gelus.sem, 1)

            @block.vector
            def _(dve):
                added.open(dve)
                with dve.Fori(0, NG) as i:
                    for e in range(parts):
                        y_done.wait(dve, i, e + 1)
                        for t in range(GT):
                            x = tile_of(dst, i * GT + t)
                            last = nc.vector.scalar_tensor_tensor(x, py[:, t, :], gate(e, i * GT + t), x, ALU.mult, ALU.add)
                        last.then_inc(added.sem, 1)
                        added.wait(dve, i, e + 1)


def tables_phase(nc, k, a, qtable, ktable, atable):
    KW = D + H1 * VW
    with ExitStack() as es:
        s = Scope(nc, es, "tab")
        w = s.sb("w", [P, KD, 3 * D])
        b = s.sb("b", [P, 3 * D])
        be = s.sb("be", [P, D1])
        xs = s.sb("xs", [P, KD, GC])
        qrow = s.sb("qrow", [P, D])
        krow = s.sb("krow", [P, KW])
        blank = s.sb("blank", [P, AW])
        pr = s.ps("pr", [P, 2, 1024])
        loaded, order, made = s.sem("loaded"), s.sem("order"), s.sem("made")
        copied = s.tally("copied", 1)
        projected, rows_ready = s.tally("projected", GT), s.tally("rows_ready", GT)
        stored = s.tally("stored", 48 * GT)
        with nc.Block() as block:
            @block.gpsimd
            def _(pool):
                nc.gpsimd.memset(blank[:, 0:H1 * VW], 0.0)
                nc.gpsimd.memset(blank[:, H1 * VW:], -BIG)
                nc.gpsimd.memset(krow[:], 1.0).then_inc(made, 1)

            @block.sync
            def _(sp):
                for j, n in enumerate("qkv"):
                    sp.dma_start(w[:, :, j * D:(j + 1) * D], a[f"L1_gnn_W{n}"].rearrange("(k p) c -> p k c", p=P)).then_inc(loaded, 16)
                    sp.dma_start(b[:, j * D:(j + 1) * D], a[f"L1_gnn_b{n}"].partition_broadcast(P)).then_inc(loaded, 16)
                sp.dma_start(be[:], a["L1_gnn_be"].partition_broadcast(P)).then_inc(loaded, 16)
                sp.wait_ge(loaded, 112)
                sp.wait_ge(made, 1)
                stored.open(sp)
                with sp.Fori(0, NG) as i:
                    for t in range(GT):
                        rows_ready.hold(sp, i, t + 1)
                        sp.dma_start(qtable[bass.ds(i * GC + t * P, P), :], qrow[:]).then_inc(stored.sem, 16)
                        sp.dma_start(ktable[bass.ds(i * GC + t * P, P), :], krow[:]).then_inc(stored.sem, 16)
                        sp.dma_start(atable[bass.ds(i * GC + t * P, P), :], blank[:]).then_inc(stored.sem, 16)
                        stored.hold(sp, i, 48 * (t + 1))

            @block.scalar
            def _(act):
                copied.open(act)
                with act.Fori(0, NG) as i:
                    projected.wait(act, i)
                    nc.scalar.activation(xs[:], k.XT[:, :, bass.ds(i * GC, GC)], ACT.Copy).then_inc(copied.sem, 1)

            @block.tensor
            def _(pe):
                projected.open(pe)
                pe.wait_ge(loaded, 112)
                with pe.Fori(0, NG) as i:
                    copied.wait(pe, i, 1)
                    for t in range(GT):
                        rows_ready.wait(pe, i, max(t - 1, 0))
                        for n0, n1 in ((0, 512), (512, 3 * D)):
                            for c in range(KD):
                                last = nc.tensor.matmul(pr[:, t % 2, n0:n1], xs[:, c, t * P:(t + 1) * P], w[:, c, n0:n1],
                                                        start=c == 0, stop=c == KD - 1)
                        last.then_inc(projected.sem, 1)

            @block.vector
            def _(dve):
                rows_ready.open(dve)
                dve.wait_ge(loaded, 112)
                dve.wait_ge(made, 1)
                chain = Chain(dve, order)
                chain(nc.vector.tensor_tensor(b[:, D:2 * D].rearrange("p (h c) -> p h c", h=H1), b[:, D:2 * D].rearrange("p (h c) -> p h c", h=H1),
                                              be[:].unsqueeze(1).to_broadcast((P, H1, D1)), ALU.add))
                with dve.Fori(0, NG) as i:
                    for t in range(GT):
                        projected.wait(dve, i, t + 1)
                        stored.wait(dve, i, 48 * t)
                        nc.vector.tensor_tensor(qrow[:], pr[:, t % 2, 0:D], b[:, 0:D], ALU.add)
                        nc.vector.tensor_tensor(krow[:, 0:D], pr[:, t % 2, D:2 * D], b[:, D:2 * D], ALU.add)
                        nc.vector.tensor_tensor(krow[:, D:].rearrange("p (h c) -> p h c", c=VW)[:, :, 0:D1],
                                                pr[:, t % 2, 2 * D:3 * D].rearrange("p (h c) -> p h c", c=D1),
                                                b[:, 2 * D:].rearrange("p (h c) -> p h c", c=D1), ALU.add).then_inc(rows_ready.sem, 1)


def edges_and_linear_phase(nc, k, a, qtable, ktable, atable, xtable, dst):
    KW = D + H1 * VW
    HALF = U1 // 2
    VS = H1 * VW
    NOWHERE = 1 << 20
    NPASS = S1 // U1
    MID = NPASS // 2
    assert MID == 2 * NT
    scale = float(D1) ** 0.25
    NCH = (PD - 1) * D1 // P
    Q4 = H1 // 4
    NB = H1 + 1
    with ExitStack() as es:
        s = Scope(nc, es, "edge")
        flat = k.XT[:].rearrange("p k n -> p (k n)")
        kv = flat[:, 0:2 * HALF * KW].rearrange("p (b u c) -> p b u c", b=2, c=KW)
        o = 2 * HALF * KW
        df, free = flat[:, 0:S1], flat[:, S1:2 * S1 - 1]
        q = flat[:, o:o + 2 * HALF * D].rearrange("p (b u c) -> p b u c", b=2, c=D)
        o += 2 * HALF * D
        hist = flat[:, o:o + 2 * HALF * AW].rearrange("p (b u c) -> p b u c", b=2, c=AW)
        o += 2 * HALF * AW
        prod = flat[:, o:o + HALF * D].rearrange("p (u c) -> p u c", c=D)
        o += HALF * D
        assert o <= KD * NP
        si = s.sb("si", [P, S1 + U1], I32)
        di = s.sb("di", [P, S1 + U1], I32)
        ends = s.sb("ends", [P, S1], I32)
        reset = s.sb("reset", [P, S1])
        ew = s.sb("ew", [P, S1])
        last_dst = s.sb("last_dst", [P, 1])
        we = s.sb("we", [ED, D1])
        attr = s.sb("attr", [ED, 2, HALF, P])
        idx = s.sb("idx", [P, 2, 2, HALF], I32)
        eidx = s.sb("eidx", [P, 2, HALF], I32)
        sc = s.sb("sc", [P, HALF, H1])
        ex = s.sb("ex", [P, 2, HALF, H1])
        tmp = s.sb("tmp", [P, VS])
        loaded, order, ready, made = s.sem("loaded"), s.sem("order"), s.sem("ready"), s.sem("made")
        indexed = s.tally("indexed", 2)
        gathered = [s.pool_dma_tally(f"gathered{b}", 32 * HALF) for b in range(2)]
        scattered = [s.pool_dma_tally(f"scattered{b}", 16 * HALF) for b in range(2)]
        features = [s.tally(f"features{b}", 16) for b in range(2)]
        projected, logits = s.tally("projected", 2), s.tally("logits", 2)
        shifted, exps, summed = s.tally("shifted", 2), s.tally("exps", 2), s.tally("summed", 2)

        eq = ExitStack()
        es.enter_context(eq)
        sl = Scope(nc, eq, "lin")
        w = sl.sb("w", [P, KD, 3 * D])
        bias = sl.sb("bias", [P, 3 * D])
        wp = sl.sb("wp", [P, KD, D])
        bp = sl.sb("bp", [P, D])
        temp = sl.sb("temp", [P, H1])
        blk = sl.sb("blk", [P, 4, VW])
        coef = sl.sb("coef", [P, 1])
        xs = sl.sb("xs", [P, KD, P])
        row = sl.sb("row", [P, 2 * D])
        sqr = sl.sb("sqr", [P, D])
        nrm = sl.sb("nrm", [P, 3, H1])
        twice = sl.sb("twice", [P, H1, 2 * D1])
        feat = sl.sb("feat", [P, H1, (PD - 1) * D1])
        last_d = sl.sb("last_d", [P, H1 * D1])
        once = sl.sb("once", [P, H1 * D1])
        v1 = sl.sb("v1", [P, VS])
        S = sl.sb("S", [P, H1, NCH, VW])
        Sl = sl.sb("Sl", [P, 2, Q4, 4, VW])
        Sf = sl.sb("Sf", [P, VS])
        xs_loaded = sl.tally("xs_loaded", 16)
        window = bass.AP(tensor=twice[:].tensor, offset=twice[:].offset,
                         ap=[list(twice[:].ap[0]), [2 * D1, H1], [1, PD - 1], [1, D1]])
        pe_ = s.ps("ep", [P, 512])

        def pair_features(chain, x, factor):
            f3 = x.rearrange("p (h c) -> p h c", c=D1)
            chain(nc.vector.tensor_tensor(twice[:, :, 0:D1], f3, factor, ALU.mult))
            nc.vector.tensor_copy(twice[:, :, D1:], twice[:, :, 0:D1])
            chain(nc.vector.tensor_copy(once[:].rearrange("p (h c) -> p h c", c=D1), twice[:, :, 0:D1]))
            nc.vector.tensor_tensor(last_d[:].rearrange("p (h c) -> p h c", c=D1), twice[:, :, 0:D1], twice[:, :, D1 // 2:D1 // 2 + D1], ALU.mult)
            return nc.vector.tensor_tensor(feat[:].rearrange("p h (d c) -> p h d c", c=D1),
                                           twice[:, :, 0:D1].unsqueeze(2).to_broadcast((P, H1, PD - 1, D1)), window, ALU.mult)


        def load_features(sp, first):
            with sp.Fori(first, first + MID) as i:
                for b in range(2):
                    projected.hold(sp, i, b)
                    if b == 0:
                        features[0].hold(sp, i)
                    sp.dma_start(attr[:, b], a["edge_attr"][:, bass.ds(i * U1 + b * HALF, HALF), :]).then_inc(features[b].sem, 16)

        def project_features(pe, i, b):
            features[b].wait(pe, i, 16)
            logits.wait(pe, i, b)
            for u in range(HALF):
                last = nc.tensor.matmul(pe_[:, (b * HALF + u) * D1:(b * HALF + u + 1) * D1], attr[:, b, u, :], we[:], start=True, stop=True)
            last.then_inc(projected.sem, 1)

        def gathers(b):
            for u in range(HALF):
                nc.gpsimd.indirect_dma_start(kv[:, b, u, :], None, ktable, bass.IndirectOffsetOnAxis(ap=idx[:, 0, b, u:u + 1], axis=0)).then_inc(gathered[b].sem, 16)
                nc.gpsimd.indirect_dma_start(q[:, b, u, :], None, qtable, bass.IndirectOffsetOnAxis(ap=idx[:, 1, b, u:u + 1], axis=0)).then_inc(gathered[b].sem, 16)

        def scatters(b):
            for u in range(HALF):
                nc.gpsimd.indirect_dma_start(atable, bass.IndirectOffsetOnAxis(ap=eidx[:, b, u:u + 1], axis=0), hist[:, b, u, :], None,
                                             bounds_check=NP - 1, oob_is_err=False).then_inc(scattered[b].sem, 16)

        def move_rows(pool, first):
            with pool.Fori(first, first + MID) as i:
                for b in range(2):
                    indexed.hold(pool, i, b + 2)
                    gathers(1 - b)
                    summed.hold(pool, i, b + 1)
                    scatters(b)

        def exponentials(act, i, b):
            shifted.wait(act, i, b + 1)
            nc.scalar.activation(ex[:], ex[:], ACT.Exp).then_inc(exps.sem, 1)

        def edge_set(dve, chain, i, b):
            step = i * U1 + b * HALF
            gathered[b].wait(dve, i, 32 * HALF)
            projected.wait(dve, i, b + 1)
            p4 = prod.rearrange("p u (h c) -> p u h c", c=D1)
            chain(nc.vector.tensor_tensor(p4, kv[:, b, :, 0:D].rearrange("p u (h c) -> p u h c", c=D1),
                                          pe_[:, b * HALF * D1:(b + 1) * HALF * D1].rearrange("p (u c) -> p u c", c=D1).unsqueeze(2).to_broadcast((P, HALF, H1, D1)), ALU.add))
            dve.sem_inc(logits.sem, 1)
            chain(nc.vector.tensor_tensor(prod, prod, q[:, b], ALU.mult))
            chain(nc.vector.tensor_reduce(sc[:], p4, AX.X, ALU.add))
            chain(nc.vector.tensor_tensor(sc[:], sc[:], ew[:, bass.ds(step, HALF)].unsqueeze(2).to_broadcast((P, HALF, H1)), ALU.mult))
            scattered[b].wait(dve, i, 16 * HALF)
            nc.vector.tensor_copy(eidx[:, b, :], ends[:, bass.ds(step, HALF)])
            for u in range(HALF):
                before = hist[:, b, u - 1, VS:] if u else hist[:, 1 - b, HALF - 1, VS:]
                now = hist[:, b, u, VS:]
                r = reset[:, bass.ds(step + u, 1)]
                chain(nc.vector.scalar_tensor_tensor(now, before, r, sc[:, u, :], ALU.add, ALU.max))
                nc.vector.scalar_tensor_tensor(ex[:, 0, u, :], before, r, now, ALU.add, ALU.subtract)
            nc.vector.tensor_tensor(ex[:, 1], sc[:], hist[:, b, :, VS:], ALU.subtract).then_inc(shifted.sem, 1)
            exps.wait(dve, i, b + 1)
            chain(nc.vector.tensor_tensor(hist[:, b, :, 0:VS].rearrange("p u (h c) -> p u h c", c=VW),
                                          kv[:, b, :, D:].rearrange("p u (h c) -> p u h c", c=VW),
                                          ex[:, 1].unsqueeze(3).to_broadcast((P, HALF, H1, VW)), ALU.mult))
            nc.vector.tensor_copy(idx[:, 0, b, :], si[:, bass.ds(step + U1, HALF)])
            nc.vector.tensor_copy(idx[:, 1, b, :], di[:, bass.ds(step + U1, HALF)]).then_inc(indexed.sem, 1)
            for u in range(HALF):
                before = hist[:, b, u - 1, 0:VS] if u else hist[:, 1 - b, HALF - 1, 0:VS]
                now = hist[:, b, u, 0:VS]
                chain(nc.vector.tensor_tensor(tmp[:].rearrange("p (h c) -> p h c", c=VW), before.rearrange("p (h c) -> p h c", c=VW),
                                              ex[:, 0, u, :].unsqueeze(2).to_broadcast((P, H1, VW)), ALU.mult))
                chain(nc.vector.tensor_tensor(now, now, tmp[:], ALU.add))
            dve.sem_inc(summed.sem, 1)

        es2 = ExitStack()
        with es2:
            s2 = Scope(nc, es2, "kv")
            pk = s2.ps("pk", [P, 512])
            pS = s2.ps("pS", [P, 3, 512])
            pL = s2.ps("pL", [P, 2, 512])
            pF = s2.ps("pF", [P, 512])
            k_done, norms, roots, pairs, sums_done = (s2.tally(n, 1) for n in ("k_done", "norms", "roots", "pairs", "sums_done"))
            zero = feat[:].rearrange("p h c -> p (h c)")
            banks = [pS[:, 0], pS[:, 1], pS[:, 2], pL[:, 0], pL[:, 1], pF[:]]
            with nc.Block() as block:
                @block.sync
                def _(sp):
                    sp.dma_start(si[:, 0:S1], a["edge_src"]).then_inc(loaded, 16)
                    sp.dma_start(di[:, 0:S1], a["edge_dst"]).then_inc(loaded, 16)
                    sp.dma_start(ew[:], a["edge_weight"]).then_inc(loaded, 16)
                    sp.dma_start(we[:], a["L1_gnn_We"]).then_inc(loaded, 16)
                    sp.dma_start(w[:], a["lin_w"].rearrange("(k p) c -> p k c", p=P)).then_inc(loaded, 16)
                    sp.dma_start(bias[:], a["L1_mix_bqkv"].partition_broadcast(P)).then_inc(loaded, 16)
                    sp.dma_start(wp[:], a["lin_wp"].rearrange("(k p) c -> p k c", p=P)).then_inc(loaded, 16)
                    sp.dma_start(bp[:], a["L1_mix_bproj"].partition_broadcast(P)).then_inc(loaded, 16)
                    sp.dma_start(temp[:], a["lin_temp"].partition_broadcast(P)).then_inc(loaded, 16)
                    sp.wait_ge(loaded, 144)
                    for f in features:
                        f.open(sp)
                    load_features(sp, 0)

                @block.tensor
                def _(pe):
                    for x in (projected, k_done, sums_done):
                        x.open(pe)
                    pe.wait_ge(loaded, 144)
                    pe.wait_ge(made, 1)
                    for bank in banks:
                        nc.tensor.matmul(bank, zero[:, 0:P], zero[:, 0:512], start=True, stop=False)
                    with pe.Fori(0, NT) as i:
                        project_features(pe, i * 2, 0)
                        xs_loaded.wait(pe, i, 16)
                        pairs.wait(pe, i)
                        for c in range(KD):
                            last = nc.tensor.matmul(pk[:], xs[:, c, :], w[:, c, D:3 * D], start=c == 0, stop=c == KD - 1)
                        last.then_inc(k_done.sem, 1)
                        project_features(pe, i * 2, 1)
                        project_features(pe, i * 2 + 1, 0)
                        project_features(pe, i * 2 + 1, 1)
                        pairs.wait(pe, i, 1)
                        for h in range(H1):
                            for c in range(NCH):
                                o = (h % 3) * NCH * VW + c * VW
                                nc.tensor.matmul(pS[:, h // 3, o:o + VW], feat[:, h, c * P:(c + 1) * P], v1[:, h * VW:(h + 1) * VW], start=False, stop=False)
                        for g in range(Q4):
                            vg = v1[:, 4 * g * VW:4 * (g + 1) * VW]
                            nc.tensor.matmul(pL[:, 0, 4 * g * VW:4 * (g + 1) * VW], once[:, g * P:(g + 1) * P], vg, start=False, stop=False)
                            nc.tensor.matmul(pL[:, 1, 4 * g * VW:4 * (g + 1) * VW], last_d[:, g * P:(g + 1) * P], vg, start=False, stop=False)
                        nc.tensor.matmul(pF[:, 0:VS], k.ones[:], v1[:], start=False, stop=False).then_inc(sums_done.sem, 1)
                    pe.wait_ge(made, 7)
                    for bank in banks:
                        last = nc.tensor.matmul(bank, zero[:, 0:P], zero[:, 0:512], start=False, stop=True)
                    last.then_inc(made, 1)

                @block.gpsimd
                def _(pool):
                    nc.gpsimd.memset(feat[:], 0.0).then_inc(made, 1)
                    nc.gpsimd.memset(blk[:], 1.0).then_inc(made, 1)
                    nc.gpsimd.memset(coef[:], 1.0).then_inc(made, 1)
                    pool.wait_ge(made, 3)
                    nc.gpsimd.affine_select(out=blk[:], in_=blk[:], compare_op=ALU.is_ge, fill=0.0, base=0,
                                            pattern=[[-D1, 4], [0, VW]], channel_multiplier=1).then_inc(made, 1)
                    pool.wait_ge(made, 4)
                    nc.gpsimd.affine_select(out=blk[:], in_=blk[:], compare_op=ALU.is_ge, fill=0.0, base=D1 - 1,
                                            pattern=[[D1, 4], [0, VW]], channel_multiplier=-1).then_inc(made, 1)
                    nc.gpsimd.affine_select(out=coef[:], in_=coef[:], compare_op=ALU.is_ge, fill=0.5, base=-D1,
                                            pattern=[[0, 1]], channel_multiplier=1).then_inc(made, 1)
                    pool.wait_ge(ready, 1)
                    scatters(0)
                    scatters(1)
                    indexed.hold(pool, 0, 1)
                    gathers(0)
                    move_rows(pool, 0)

                @block.scalar
                def _(act):
                    for x in (exps, roots, xs_loaded):
                        x.open(act)
                    act.dma_start(xs[:], xtable[0]).then_inc(xs_loaded.sem, 16)
                    with act.Fori(0, NT) as i:
                        exponentials(act, i * 2, 0)
                        exponentials(act, i * 2, 1)
                        k_done.hold(act, i, 1)
                        act.dma_start(xs[:], xtable[bass.ds(i + 1, 1)].rearrange("o p k n -> p (o k) n")).then_inc(xs_loaded.sem, 16)
                        norms.wait(act, i, 1)
                        nc.scalar.activation(nrm[:, 1, :], nrm[:, 0, :], ACT.Sqrt).then_inc(roots.sem, 1)
                        exponentials(act, i * 2 + 1, 0)
                        exponentials(act, i * 2 + 1, 1)
                    xs_loaded.wait(act, NT, 16)

                @block.vector
                def _(dve):
                    for x in (indexed, logits, shifted, summed, norms, pairs):
                        x.open(dve)
                    chain = Chain(dve, order)
                    chain(nc.vector.memset(eidx[:], NOWHERE))
                    nc.vector.memset(hist[:, :, :, 0:VS], 0.0)
                    nc.vector.memset(hist[:, :, :, VS:], -BIG).then_inc(ready, 1)
                    dve.wait_ge(loaded, 144)
                    nc.vector.memset(si[:, S1:], 0)
                    chain(nc.vector.memset(di[:, S1:], 0))
                    chain(nc.vector.tensor_copy(df, di[:, 0:S1]))
                    chain(nc.vector.tensor_copy(last_dst[:], df[:, S1 - 1:S1]))
                    chain(nc.vector.tensor_scalar(ew[:], ew[:], float(D1) ** -0.5, None, ALU.mult))
                    chain(nc.vector.memset(reset[:, 0:1], -BIG))
                    chain(nc.vector.tensor_tensor(reset[:, 1:], df[:, 1:], df[:, 0:S1 - 1], ALU.not_equal))
                    chain(nc.vector.tensor_scalar(free, reset[:, 1:], -float(NOWHERE), float(NOWHERE), ALU.mult, ALU.add))
                    chain(nc.vector.tensor_tensor(free, free, df[:, 0:S1 - 1], ALU.add))
                    chain(nc.vector.tensor_copy(ends[:, 0:S1 - 1], free))
                    chain(nc.vector.memset(ends[:, S1 - 1:], NOWHERE))
                    chain(nc.vector.tensor_scalar(reset[:, 1:], reset[:, 1:], -BIG, None, ALU.mult))
                    for b in range(2):
                        nc.vector.tensor_copy(idx[:, 0, b, :], si[:, b * HALF:(b + 1) * HALF])
                        nc.vector.tensor_copy(idx[:, 1, b, :], di[:, b * HALF:(b + 1) * HALF]).then_inc(indexed.sem, 1)
                    dve.wait_ge(made, 6)
                    with dve.Fori(0, NT) as i:
                        chain.fresh()
                        edge_set(dve, chain, i * 2, 0)
                        edge_set(dve, chain, i * 2, 1)
                        k_done.wait(dve, i, 1)
                        chain(nc.vector.tensor_tensor(row[:], pk[:], bias[:, D:3 * D], ALU.add))
                        chain(nc.vector.tensor_tensor(sqr[:], row[:, 0:D], row[:, 0:D], ALU.mult))
                        nc.vector.tensor_reduce(nrm[:, 0, :], sqr[:].rearrange("p (h c) -> p h c", c=D1), AX.X, ALU.add).then_inc(norms.sem, 1)
                        edge_set(dve, chain, i * 2 + 1, 0)
                        roots.wait(dve, i, 1)
                        chain(nc.vector.tensor_scalar_max(nrm[:, 1, :], nrm[:, 1, :], 1e-12))
                        chain(nc.vector.reciprocal(nrm[:, 1, :], nrm[:, 1, :]))
                        chain(nc.vector.tensor_scalar(nrm[:, 2, :], nrm[:, 1, :], scale, None, ALU.mult))
                        sums_done.wait(dve, i)
                        m = k.valid[:, bass.ds(i, 1)]
                        v3 = v1[:].rearrange("p (h c) -> p h c", c=VW)
                        nc.vector.tensor_copy(v3[:, :, 0], m.to_broadcast((P, H1)))
                        nc.vector.tensor_scalar(v3[:, :, 1:], row[:, D:2 * D].rearrange("p (h c) -> p h c", c=D1), m, None, ALU.mult)
                        pair_features(chain, row[:, 0:D], nrm[:, 2, :].unsqueeze(2).to_broadcast((P, H1, D1))).then_inc(pairs.sem, 1)
                        edge_set(dve, chain, i * 2 + 1, 1)
                    sums_done.wait(dve, NT)
                    chain.fresh()
                    nc.vector.memset(feat[:, 0, :], 0.0).then_inc(made, 1)
                    dve.wait_ge(made, 8)
                    for h in range(H1):
                        o = (h % 3) * NCH * VW
                        nc.vector.tensor_scalar(S[:, h].rearrange("p c e -> p (c e)"), pS[:, h // 3, o:o + NCH * VW], 1.0 / N, None, ALU.mult)
                    for g in range(Q4):
                        for j, f in ((0, scale ** 2 / N), (1, 0.5 / N)):
                            nc.vector.scalar_tensor_tensor(Sl[:, j, g].rearrange("p m e -> p (m e)"), pL[:, j, 4 * g * VW:4 * (g + 1) * VW],
                                                           f, blk[:].rearrange("p m e -> p (m e)"), ALU.mult, ALU.mult)
                    chain(nc.vector.tensor_scalar(Sf[:], pF[:, 0:VS], scale ** 4 / N, None, ALU.mult))
                    chain(nc.vector.tensor_scalar(S[:, :, 0, :], S[:, :, 0, :], coef[:, 0:1], None, ALU.mult))

        es2 = ExitStack()
        with es2:
            s2 = Scope(nc, es2, "q")
            pqp = s2.ps("pqp", [P, 2, D])
            pq, pp = pqp[:, 0], pqp[:, 1]
            pt = s2.ps("pt", [P, 4, 512])
            py = s2.ps("py", [P, 512])
            ppt = s2.ps("ppt", [P, 512])
            fT = s2.sb("fT", [P, 4, 512])
            y = s2.sb("y", [P, VS])
            r = s2.sb("r", [P, H1])
            on = s2.sb("on", [P, D])
            oT = s2.sb("oT", [P, D])
            res = s2.sb("res", [P, D])
            tq = s2.sb("tq", [P, H1])
            q_done, norms, roots, pairs = (s2.tally(n, 1) for n in ("q_done", "norms", "roots", "pairs"))
            turned, evacuated, met = (s2.tally(n, NB) for n in ("turned", "evacuated", "met"))
            normed, o_turned, o_evacuated, out_done, added = (s2.tally(n, 1) for n in ("normed", "o_turned", "o_evacuated", "out_done", "added"))
            xs_again = s2.tally("xs_again", 16)
            with nc.Block() as block:
                @block.sync
                def _(sp):
                    load_features(sp, MID)

                @block.gpsimd
                def _(pool):
                    move_rows(pool, MID)
                    gathered[0].wait(pool, NPASS, 32 * HALF)
                    for b in range(2):
                        scattered[b].wait(pool, NPASS, 16 * HALF)

                @block.scalar
                def _(act):
                    for x in (roots, evacuated, o_evacuated, xs_again):
                        x.open(act)

                    def evacuate(i, b):
                        turned.wait(act, i, b + 1)
                        met.wait(act, i, max(b - 3, 0))
                        nc.scalar.activation(fT[:, b % 4], pt[:, b % 4], ACT.Copy).then_inc(evacuated.sem, 1)

                    act.dma_start(xs[:], xtable[0]).then_inc(xs_again.sem, 16)
                    with act.Fori(0, NT) as i:
                        exponentials(act, i * 2 + MID, 0)
                        norms.wait(act, i, 1)
                        nc.scalar.activation(nrm[:, 1, :], nrm[:, 0, :], ACT.Sqrt).then_inc(roots.sem, 1)
                        q_done.hold(act, i, 1)
                        act.dma_start(xs[:], xtable[bass.ds(i + 1, 1)].rearrange("o p k n -> p (o k) n")).then_inc(xs_again.sem, 16)
                        exponentials(act, i * 2 + MID, 1)
                        for b in range(4):
                            evacuate(i, b)
                        exponentials(act, i * 2 + (MID + 1), 0)
                        for b in range(4, NB):
                            evacuate(i, b)
                        o_turned.wait(act, i, 1)
                        nc.scalar.activation(oT[:], ppt[:, 0:D], ACT.Copy).then_inc(o_evacuated.sem, 1)
                        exponentials(act, i * 2 + (MID + 1), 1)
                    xs_again.wait(act, NT, 16)

                @block.tensor
                def _(pe):
                    for x in (q_done, turned, met, o_turned, out_done):
                        x.open(pe)
                    with pe.Fori(0, NT) as i:
                        project_features(pe, i * 2 + MID, 0)
                        xs_again.wait(pe, i, 16)
                        added.wait(pe, i)
                        for c in range(KD):
                            last = nc.tensor.matmul(pq, xs[:, c, :], w[:, c, 0:D], start=c == 0, stop=c == KD - 1)
                        last.then_inc(q_done.sem, 1)
                        project_features(pe, i * 2 + MID, 1)
                        project_features(pe, i * 2 + (MID + 1), 0)
                        pairs.wait(pe, i, 1)

                        def turn(b):
                            evacuated.wait(pe, i, max(b - 3, 0))
                            for c in range(4):
                                if b:
                                    src = feat[:, b - 1, c * P:(c + 1) * P]
                                else:
                                    src = (once if c < Q4 else last_d)[:, (c % Q4) * P:(c % Q4 + 1) * P]
                                last = nc.tensor.transpose(pt[:, b % 4, c * P:(c + 1) * P], src, k.ident[:])
                            last.then_inc(turned.sem, 1)

                        def meet(b):
                            evacuated.wait(pe, i, b + 1)
                            part = fT[:, b % 4]
                            if b == 0:
                                normed.wait(pe, i)
                                for g in range(Q4):
                                    o = py[:, 4 * g * VW:4 * (g + 1) * VW]
                                    nc.tensor.matmul(o, part[:, g * P:(g + 1) * P], Sl[:, 0, g].rearrange("p m e -> p (m e)"),
                                                     start=g == 0, stop=False, skip_group_check=True)
                                    last = nc.tensor.matmul(o, part[:, (Q4 + g) * P:(Q4 + g + 1) * P], Sl[:, 1, g].rearrange("p m e -> p (m e)"),
                                                            start=False, stop=False, skip_group_check=True)
                            else:
                                for c in range(NCH):
                                    last = nc.tensor.matmul(py[:, (b - 1) * VW:b * VW], part[:, c * P:(c + 1) * P], S[:, b - 1, c, :],
                                                            start=False, stop=c == NCH - 1, skip_group_check=True)
                            last.then_inc(met.sem, 1)

                        for b in range(3):
                            turn(b)
                        for b in range(NB):
                            if b + 3 < NB:
                                turn(b + 3)
                            meet(b)
                        project_features(pe, i * 2 + (MID + 1), 1)
                        normed.wait(pe, i, 1)
                        for c in range(KD):
                            last = nc.tensor.transpose(ppt[:, c * P:(c + 1) * P], on[:, c * P:(c + 1) * P], k.ident[:])
                        last.then_inc(o_turned.sem, 1)
                        o_evacuated.wait(pe, i, 1)
                        added.wait(pe, i)
                        for c in range(KD):
                            last = nc.tensor.matmul(pp, oT[:, c * P:(c + 1) * P], wp[:, c, :], start=c == 0, stop=c == KD - 1)
                        last.then_inc(out_done.sem, 1)

                @block.vector
                def _(dve):
                    for x in (norms, pairs, normed, added):
                        x.open(dve)
                    chain = Chain(dve, order)
                    chain.fresh()
                    chain(nc.vector.tensor_scalar(tq[:], temp[:], scale * scale, None, ALU.mult))
                    with dve.Fori(0, NT) as i:
                        chain.fresh()
                        edge_set(dve, chain, i * 2 + MID, 0)
                        q_done.wait(dve, i, 1)
                        chain(nc.vector.tensor_tensor(row[:, 0:D], pq, bias[:, 0:D], ALU.add))
                        chain(nc.vector.tensor_tensor(sqr[:], row[:, 0:D], row[:, 0:D], ALU.mult))
                        nc.vector.tensor_reduce(nrm[:, 0, :], sqr[:].rearrange("p (h c) -> p h c", c=D1), AX.X, ALU.add).then_inc(norms.sem, 1)
                        edge_set(dve, chain, i * 2 + MID, 1)
                        roots.wait(dve, i, 1)
                        chain(nc.vector.tensor_scalar(nrm[:, 1, :], nrm[:, 1, :], scale, 1e-12, ALU.mult, ALU.max))
                        chain(nc.vector.reciprocal(nrm[:, 1, :], nrm[:, 1, :]))
                        chain(nc.vector.tensor_tensor(nrm[:, 2, :], nrm[:, 1, :], tq[:], ALU.mult))
                        turned.wait(dve, i)
                        pair_features(chain, row[:, 0:D], nrm[:, 2, :].unsqueeze(2).to_broadcast((P, H1, D1))).then_inc(pairs.sem, 1)
                        edge_set(dve, chain, i * 2 + (MID + 1), 0)
                        met.wait(dve, i, NB)
                        chain(nc.vector.tensor_tensor(y[:], py[:, 0:VS], Sf[:], ALU.add))
                        y3 = y[:].rearrange("p (h c) -> p h c", c=VW)
                        chain(nc.vector.reciprocal(r[:], y3[:, :, 0]))
                        nc.vector.tensor_tensor(on[:].rearrange("p (h c) -> p h c", c=D1), y3[:, :, 1:],
                                                r[:].unsqueeze(2).to_broadcast((P, H1, D1)), ALU.mult).then_inc(normed.sem, 1)
                        edge_set(dve, chain, i * 2 + (MID + 1), 1)
                        out_done.wait(dve, i, 1)
                        chain(nc.vector.tensor_tensor(res[:], pp, bp[:], ALU.add))
                        x = tile_of(dst, i)
                        nc.vector.tensor_tensor(x, x, res[:], ALU.add).then_inc(added.sem, 1)
                        added.wait(dve, i, 1)
        eq.close()

        tail = hist[:, 1, HALF - 1, :]
        es2 = ExitStack()
        with es2:
            s2 = Scope(nc, es2, "join")
            same = s2.sb("same", [P, P])
            off = s2.sb("off", [P, P])
            later = s2.sb("later", [P, P])
            diag = s2.sb("diag", [P, H1, P])
            col = s2.sb("col", [P, 4])
            ti = s2.sb("ti", [P, 1], I32)
            held = s2.sb("held", [P, AW])
            joined = s2.sb("joined", [P, AW])
            part = s2.sb("part", [P, VS])
            mx = s2.sb("mx", [P, 3, H1])
            pj = s2.ps("pj", [P, 4, 512])
            v, p_, e_, g_ = (s2.sem(n) for n in ("v", "p", "e", "g"))
            got, put = s2.pool_dma_sem("got"), s2.pool_dma_sem("put")
            with nc.Block() as block:
                @block.tensor
                def _(pe):
                    pe.wait_ge(v, 1)
                    nc.tensor.matmul(pj[:, 0, 0:P], k.ones[:], same[:], start=True, stop=True)
                    for c in range(2):
                        last = nc.tensor.matmul(pj[:, 1 + c, :], k.ones[:], diag[:, 4 * c:4 * c + 4, :].rearrange("p h c -> p (h c)"), start=True, stop=True)
                    last.then_inc(p_, 1)
                    pe.wait_ge(v, 3)
                    nc.tensor.matmul(pj[:, 3, 0:VS], same[:], part[:], start=True, stop=True).then_inc(p_, 1)

                @block.gpsimd
                def _(pool):
                    pool.wait_ge(v, 1)
                    nc.gpsimd.indirect_dma_start(held[:], None, atable, bass.IndirectOffsetOnAxis(ap=ti[:], axis=0)).then_inc(got, 16)
                    pool.wait_ge(v, 2)
                    nc.gpsimd.affine_select(out=later[:], in_=same[:], compare_op=ALU.is_gt, fill=0.0, base=0,
                                            pattern=[[1, P]], channel_multiplier=-1).then_inc(g_, 1)
                    pool.wait_ge(v, 4)
                    nc.gpsimd.indirect_dma_start(atable, bass.IndirectOffsetOnAxis(ap=ti[:], axis=0), joined[:], None,
                                                 bounds_check=NP - 1, oob_is_err=False).then_inc(put, 16)
                    pool.wait_ge(put, 16)

                @block.scalar
                def _(act):
                    act.wait_ge(v, 3 - 1)
                    act.wait_ge(e_, 1)
                    nc.scalar.activation(mx[:, 1:3, :], mx[:, 1:3, :], ACT.Exp).then_inc(e_, 1)

                @block.vector
                def _(dve):
                    chain = Chain(dve, order)
                    chain.fresh()
                    chain(nc.vector.tensor_copy(col[:, 0:1], last_dst[:]))
                    chain(nc.vector.tensor_copy(ti[:], di[:, S1 - 1:S1]))
                    nc.vector.tensor_scalar(same[:], k.ident[:], col[:, 0:1], None, ALU.mult)
                    nc.vector.tensor_tensor(diag[:], k.ident[:].unsqueeze(1).to_broadcast((P, H1, P)), tail[:, VS:].unsqueeze(2).to_broadcast((P, H1, P)), ALU.mult).then_inc(v, 1)
                    dve.wait_ge(p_, 1)
                    nc.vector.tensor_scalar(same[:], pj[:, 0, 0:P], col[:, 0:1], None, ALU.is_equal).then_inc(v, 1)
                    dve.wait_ge(v, 2)
                    chain(nc.vector.tensor_scalar(off[:], same[:], BIG, -BIG, ALU.mult, ALU.add))
                    for c in range(2):
                        last = nc.vector.tensor_tensor(diag[:, 4 * c:4 * c + 4, :], pj[:, 1 + c, :].rearrange("p (h c) -> p h c", c=P),
                                                       off[:].unsqueeze(1).to_broadcast((P, 4, P)), ALU.add)
                    chain(last)
                    chain(nc.vector.tensor_reduce(mx[:, 0, :], diag[:], AX.X, ALU.max))
                    dve.wait_ge(got, 16)
                    chain(nc.vector.tensor_tensor(mx[:, 0, :], mx[:, 0, :], held[:, VS:], ALU.max))
                    nc.vector.tensor_tensor(mx[:, 1, :], tail[:, VS:], mx[:, 0, :], ALU.subtract)
                    nc.vector.tensor_tensor(mx[:, 2, :], held[:, VS:], mx[:, 0, :], ALU.subtract).then_inc(e_, 1)
                    dve.wait_ge(e_, 2)
                    nc.vector.tensor_tensor(part[:].rearrange("p (h c) -> p h c", c=VW), tail[:, 0:VS].rearrange("p (h c) -> p h c", c=VW),
                                            mx[:, 1, :].unsqueeze(2).to_broadcast((P, H1, VW)), ALU.mult).then_inc(v, 1)
                    chain(nc.vector.tensor_tensor(joined[:, 0:VS].rearrange("p (h c) -> p h c", c=VW), held[:, 0:VS].rearrange("p (h c) -> p h c", c=VW),
                                                  mx[:, 2, :].unsqueeze(2).to_broadcast((P, H1, VW)), ALU.mult))
                    dve.wait_ge(g_, 1)
                    chain(nc.vector.tensor_reduce(col[:, 1:2], later[:], AX.X, ALU.max))
                    chain(nc.vector.scalar_tensor_tensor(col[:, 2:3], col[:, 1:2], float(NOWHERE), col[:, 0:1], ALU.mult, ALU.add))
                    chain(nc.vector.tensor_copy(joined[:, VS:], mx[:, 0, :]))
                    chain(nc.vector.tensor_copy(ti[:], col[:, 2:3]))
                    dve.wait_ge(p_, 2)
                    nc.vector.tensor_tensor(joined[:, 0:VS], joined[:, 0:VS], pj[:, 3, 0:VS], ALU.add).then_inc(v, 1)


def attention_out_phase(nc, k, a, atable, dst):
    VS = H1 * VW
    with ExitStack() as es:
        s = Scope(nc, es, "aout")
        wo = s.sb("wo", [P, KD, D])
        bo = s.sb("bo", [P, D])
        alpha = s.sb("alpha", [P, 1])
        rows = s.sb("rows", [P, GT, AW])
        r = s.sb("r", [P, GT, H1])
        on = s.sb("on", [P, GT, D])
        oT = s.sb("oT", [P, KD, GC])
        pt = s.ps("pt", [P, KD, 1024])
        py = s.ps("py", [P, 8, D])
        loaded, order = s.sem("loaded"), s.sem("order")
        fetched, normed, transposed, evacuated, projected, added = (s.tally(n, c) for n, c in (
            ("fetched", 16), ("normed", 1), ("transposed", 1), ("evacuated", 1), ("projected", 1), ("added", 1)))
        with nc.Block() as block:
            @block.sync
            def _(sp):
                sp.dma_start(wo[:], a["L1_gnn_Wo"].rearrange("(k p) c -> p k c", p=P)).then_inc(loaded, 16)
                sp.dma_start(bo[:], a["L1_gnn_bo"].partition_broadcast(P)).then_inc(loaded, 16)
                sp.dma_start(alpha[:], a["L1_gnn_alpha"].partition_broadcast(P)).then_inc(loaded, 16)
                sp.wait_ge(loaded, 48)
                fetched.open(sp)
                with sp.Fori(0, NG) as i:
                    normed.hold(sp, i)
                    sp.dma_start(rows[:], atable[bass.ds(i * GC, GC), :].rearrange("(t p) c -> p t c", p=P)).then_inc(fetched.sem, 16)

            @block.vector
            def _(dve):
                normed.open(dve)
                added.open(dve)
                dve.wait_ge(loaded, 48)
                chain = Chain(dve, order)
                chain.fresh()
                with dve.Fori(0, NG) as i:
                    chain.fresh()
                    fetched.wait(dve, i, 16)
                    acc = rows[:, :, 0:VS].rearrange("p t (h c) -> p t h c", c=VW)
                    chain(nc.vector.tensor_scalar_max(r[:], acc[:, :, :, D1], 1e-30))
                    chain(nc.vector.reciprocal(r[:], r[:]))
                    transposed.wait(dve, i)
                    nc.vector.tensor_tensor(on[:].rearrange("p t (h c) -> p t h c", c=D1), acc[:, :, :, 0:D1],
                                            r[:].unsqueeze(3).to_broadcast((P, GT, H1, D1)), ALU.mult).then_inc(normed.sem, 1)
                    normed.wait(dve, i, 1)
                    projected.wait(dve, i, 1)
                    chain(nc.vector.tensor_tensor(on[:], py[:, 0:GT, :], bo[:].unsqueeze(1).to_broadcast((P, GT, D)), ALU.add))
                    x = dst[:, bass.ds(i * GT, GT), :]
                    nc.vector.scalar_tensor_tensor(x, on[:], alpha[:, 0:1], x, ALU.mult, ALU.add).then_inc(added.sem, 1)
                    added.wait(dve, i, 1)

            @block.tensor
            def _(pe):
                transposed.open(pe)
                projected.open(pe)
                pe.wait_ge(loaded, 48)
                with pe.Fori(0, NG) as i:
                    normed.wait(pe, i, 1)
                    evacuated.wait(pe, i)
                    for c in range(KD):
                        for t in range(GT):
                            last = nc.tensor.transpose(pt[:, c, t * P:(t + 1) * P], on[:, t, c * P:(c + 1) * P], k.ident[:])
                    last.then_inc(transposed.sem, 1)
                    evacuated.wait(pe, i, 1)
                    added.wait(pe, i)
                    for t in range(GT):
                        for c in range(KD):
                            last = nc.tensor.matmul(py[:, t, :], oT[:, c, t * P:(t + 1) * P], wo[:, c, :], start=c == 0, stop=c == KD - 1)
                    last.then_inc(projected.sem, 1)

            @block.scalar
            def _(act):
                evacuated.open(act)
                with act.Fori(0, NG) as i:
                    transposed.wait(act, i, 1)
                    projected.wait(act, i)
                    nc.scalar.activation(oT[:], pt[:, :, 0:GC], ACT.Copy).then_inc(evacuated.sem, 1)


def top1_phase(nc, k, a, B, out):
    SLOTS = E1 * CS
    NOSLOT = 1 << 20
    buf, ybuf = k.dram("slots_in", (SLOTS, D)), k.dram("slots_out", (SLOTS, D))
    with ExitStack() as es:
        s = Scope(nc, es, "top1")
        slot = s.sb("slot", [P, 2, NT], I32)
        prob = s.sb("prob", [P, NT])
        loaded, order = s.sem("loaded"), s.sem("order")
        es2 = ExitStack()
        with es2:
            s2 = Scope(nc, es2, "route")
            gw = s2.sb("gw", [P, KD, E1])
            gb = s2.sb("gb", [P, E1])
            tri = s2.sb("tri", [P, P])
            zero = s2.sb("zero", [P, 2048])
            xs = s2.sb("xs", [P, KD, GC])
            L = s2.sb("L", [P, NT, E1])
            H = s2.sb("H", [P, NT, E1])
            C = s2.sb("C", [P, NT, E1])
            T = s2.sb("T", [P, NT + 1, E1])
            io = s2.sb("io", [P, E1])
            t1 = s2.sb("t1", [P, 6, NT])
            one = s2.sb("one", [P, NT])
            pl = s2.ps("pl", [P, 512])
            pc = s2.ps("pc", [P, 2, 512])
            made, steps, exps, counted, cleared = (s2.sem(n) for n in ("made", "steps", "exps", "counted", "cleared"))
            copied, projected, taken = (s2.tally(n, 1) for n in ("copied", "projected", "taken"))
            with nc.Block() as block:
                @block.gpsimd
                def _(pool):
                    nc.gpsimd.memset(zero[:], 0.0).then_inc(made, 1)
                    nc.gpsimd.iota(io[:], pattern=[[1, E1]], base=0, channel_multiplier=0, allow_small_or_imprecise_dtypes=True).then_inc(made, 1)
                    nc.gpsimd.memset(one[:], 1.0).then_inc(made, 1)
                    nc.gpsimd.affine_select(out=tri[:], in_=k.ones[:], compare_op=ALU.is_ge, fill=0.0, base=0,
                                            pattern=[[1, P]], channel_multiplier=-1).then_inc(made, 1)

                @block.sync
                def _(sp):
                    sp.dma_start(gw[:], a["L1_ffn_gate_w"].rearrange("(k p) c -> p k c", p=P)).then_inc(loaded, 16)
                    sp.dma_start(gb[:], a["L1_ffn_gate_b"].partition_broadcast(P)).then_inc(loaded, 16)
                    sp.wait_ge(made, 4)
                    for e in range(E1):
                        sp.dma_start(buf[e * CS:(e + 1) * CS, :].rearrange("(p r) c -> p (r c)", p=P), zero[:]).then_inc(cleared, 16)
                    sp.wait_ge(loaded, 32)
                    sp.wait_ge(cleared, 16 * E1)

                @block.scalar
                def _(act):
                    copied.open(act)
                    with act.Fori(0, NG) as i:
                        projected.wait(act, i)
                        nc.scalar.activation(xs[:], k.XT[:, :, bass.ds(i * GC, GC)], ACT.Copy).then_inc(copied.sem, 1)
                    act.wait_ge(steps, 1)
                    nc.scalar.activation(L[:], L[:], ACT.Exp).then_inc(exps, 1)

                @block.tensor
                def _(pe):
                    projected.open(pe)
                    pe.wait_ge(loaded, 32)
                    with pe.Fori(0, NG) as i:
                        copied.wait(pe, i, 1)
                        taken.wait(pe, i)
                        for t in range(GT):
                            for c in range(KD):
                                last = nc.tensor.matmul(pl[:, t * E1:(t + 1) * E1], xs[:, c, t * P:(t + 1) * P], gw[:, c, :],
                                                        start=c == 0, stop=c == KD - 1)
                        last.then_inc(projected.sem, 1)
                    pe.wait_ge(made, 4)
                    pe.wait_ge(steps, 2)
                    h = H[:].rearrange("p t e -> p (t e)")
                    nc.tensor.matmul(pc[:, 0, 0:NT * E1], tri[:], h, start=True, stop=True)
                    nc.tensor.matmul(pc[:, 1, 0:NT * E1], k.ones[:], h, start=True, stop=True).then_inc(counted, 1)

                @block.vector
                def _(dve):
                    taken.open(dve)
                    dve.wait_ge(loaded, 32)
                    dve.wait_ge(made, 4)
                    chain = Chain(dve, order)
                    with dve.Fori(0, NG) as i:
                        projected.wait(dve, i, 1)
                        nc.vector.tensor_tensor(L[:, bass.ds(i * GT, GT), :], pl[:, 0:GT * E1].rearrange("p (t e) -> p t e", e=E1),
                                                gb[:].unsqueeze(1).to_broadcast((P, GT, E1)), ALU.add).then_inc(taken.sem, 1)
                    taken.wait(dve, NG)
                    mx, tot, idx, pos, kept, base = (t1[:, j, :] for j in range(6))

                    def over(x):
                        return x.unsqueeze(2).to_broadcast((P, NT, E1))

                    iob = io[:].unsqueeze(1).to_broadcast((P, NT, E1))
                    chain(nc.vector.tensor_reduce(mx, L[:], AX.X, ALU.max))
                    nc.vector.tensor_tensor(L[:], L[:], over(mx), ALU.subtract).then_inc(steps, 1)
                    dve.wait_ge(exps, 1)
                    chain(nc.vector.tensor_reduce(tot, L[:], AX.X, ALU.add))
                    chain(nc.vector.reciprocal(tot, tot))
                    chain(nc.vector.tensor_tensor(L[:], L[:], over(tot), ALU.mult))
                    chain(nc.vector.tensor_reduce(mx, L[:], AX.X, ALU.max))
                    chain(nc.vector.tensor_tensor(H[:], L[:], over(mx), ALU.is_equal))
                    chain(nc.vector.tensor_scalar(io[:], io[:], -1.0, float(E1), ALU.mult, ALU.add))
                    chain(nc.vector.tensor_tensor(H[:], H[:], iob, ALU.mult))
                    chain(nc.vector.tensor_reduce(idx, H[:], AX.X, ALU.max))
                    chain(nc.vector.tensor_tensor(H[:], over(idx), iob, ALU.is_equal))
                    nc.vector.tensor_tensor(H[:], H[:], over(k.valid[:]), ALU.mult).then_inc(steps, 1)
                    dve.wait_ge(counted, 1)
                    chain(nc.vector.memset(T[:, 0, :], 0.0))
                    for e in range(E1):
                        last = nc.vector.tensor_tensor_scan(T[:, 1:, e], one[:], pc[:, 1, 0:NT * E1].rearrange("p (t e) -> p t e", e=E1)[:, :, e],
                                                            0.0, ALU.mult, ALU.add)
                    chain(last)
                    chain(nc.vector.tensor_tensor(C[:], pc[:, 0, 0:NT * E1].rearrange("p (t e) -> p t e", e=E1), T[:, 0:NT, :], ALU.add))
                    chain(nc.vector.tensor_tensor(C[:], C[:], H[:], ALU.mult))
                    chain(nc.vector.tensor_reduce(pos, C[:], AX.X, ALU.add))
                    chain(nc.vector.tensor_scalar(kept, pos, float(CAP), None, ALU.is_le))
                    chain(nc.vector.tensor_tensor(kept, kept, k.valid[:], ALU.mult))
                    chain(nc.vector.tensor_tensor(prob[:], mx, kept, ALU.mult))
                    chain(nc.vector.tensor_scalar(base, idx, -float(CS), float(E1 * CS - 1), ALU.mult, ALU.add))
                    chain(nc.vector.tensor_tensor(base, base, pos, ALU.add))
                    chain(nc.vector.tensor_tensor(base, base, kept, ALU.mult))
                    chain(nc.vector.tensor_copy(slot[:, 1, :], base))
                    chain(nc.vector.tensor_scalar(kept, kept, -float(NOSLOT), float(NOSLOT), ALU.mult, ALU.add))
                    chain(nc.vector.tensor_tensor(base, base, kept, ALU.add))
                    chain(nc.vector.tensor_copy(slot[:, 0, :], base))

        with ExitStack() as es2:
            s2 = Scope(nc, es2, "send")
            rows = s2.sb("rows", [P, GT, D])
            idx = s2.sb("idx", [P, GT], I32)
            sent = s2.pool_dma_tally("sent", 16 * GT)
            ready, free = s2.tally("ready", 1), s2.tally("free", 1)
            with nc.Block() as block:
                @block.vector
                def _(dve):
                    ready.open(dve)
                    with dve.Fori(0, NG) as i:
                        free.wait(dve, i)
                        nc.vector.tensor_copy(rows[:], B[:, bass.ds(i * GT, GT), :])
                        nc.vector.tensor_copy(idx[:], slot[:, 0, bass.ds(i * GT, GT)]).then_inc(ready.sem, 1)

                @block.gpsimd
                def _(pool):
                    free.open(pool)
                    with pool.Fori(0, NG) as i:
                        ready.hold(pool, i, 1)
                        for t in range(GT):
                            nc.gpsimd.indirect_dma_start(buf, bass.IndirectOffsetOnAxis(ap=idx[:, t:t + 1], axis=0), rows[:, t, :], None,
                                                         bounds_check=SLOTS - 1, oob_is_err=False).then_inc(sent.sem, 16)
                        sent.wait(pool, i, 16 * GT)
                        pool.sem_inc(free.sem, 1)

        with ExitStack() as es2:
            s2 = Scope(nc, es2, "ex1")
            FC = F1 // P
            w1 = s2.sb("w1", [P, KD, F1])
            w2 = s2.sb("w2", [P, FC, D])
            b1 = s2.sb("b1", [P, E1, FC])
            bias = s2.sb("bias", [P, FC])
            b2 = s2.sb("b2", [1, E1, D])
            rows = s2.sb("rows", [P, CT, D])
            flat = B[:].rearrange("p t c -> p (t c)")
            XE = flat[:, 0:KD * CS].rearrange("p (k n) -> p k n", k=KD)
            hid = flat[:, KD * CS:KD * CS + FC * CS].rearrange("p (f n) -> p f n", n=CS)
            Y = k.XT[:].rearrange("p k n -> p (k n)")[:, 0:CT * D].rearrange("p (t c) -> p t c", c=D)
            pa = s2.ps("pa", [P, 4, 512])
            py = s2.ps("py", [P, 8, D])
            biases, aorder = s2.sem("biases"), s2.sem("aorder")
            fetched = s2.tally("fetched", 48)
            turned, evacuated = s2.tally("turned", 4), s2.tally("evacuated", 4)
            h_done, relus = s2.tally("h_done", 2 * FC), s2.tally("relus", 2 * FC)
            y_done, copied = s2.tally("y_done", 1), s2.tally("copied", 1)
            stored, written = s2.pool_dma_tally("stored", 16), s2.tally("written", 1)
            with nc.Block() as block:
                @block.sync
                def _(sp):
                    sp.dma_start(b1[:], a["L1_ffn_b1"].rearrange("e (f p) -> p e f", p=P), allow_slow_non_contiguous=True).then_inc(biases, 16)
                    sp.dma_start(b2[:], a["L1_ffn_b2"].rearrange("(o e) d -> o e d", o=1)).then_inc(biases, 16)
                    sp.wait_ge(biases, 32)
                    fetched.open(sp)
                    with sp.Fori(0, E1) as i:
                        y_done.hold(sp, i)
                        sp.dma_start(w1[:], a["L1_ffn_w1"][bass.ds(i, 1)].rearrange("o (k p) f -> p (o k) f", p=P)).then_inc(fetched.sem, 16)
                        sp.dma_start(w2[:], a["L1_ffn_w2"][bass.ds(i, 1)].rearrange("o (k p) f -> p (o k) f", p=P)).then_inc(fetched.sem, 16)
                        sp.dma_start(rows[:], buf[bass.ds(i * CS, CS), :].rearrange("(t p) c -> p t c", p=P)).then_inc(fetched.sem, 16)

                @block.gpsimd
                def _(pool):
                    with pool.Fori(0, E1) as i:
                        copied.hold(pool, i, 1)
                        pool.dma_start(ybuf[bass.ds(i * CS, CS), :].rearrange("(t p) c -> p t c", p=P), Y).then_inc(stored.sem, 16)
                        stored.wait(pool, i, 16)
                        pool.sem_inc(written.sem, 1)

                @block.tensor
                def _(pe):
                    for x in (turned, h_done, y_done):
                        x.open(pe)
                    pe.wait_ge(biases, 32)
                    with pe.Fori(0, E1) as i:
                        fetched.wait(pe, i, 48)
                        for j in range(4):
                            if j == 0:
                                relus.wait(pe, i)
                            for t in range(4):
                                last = nc.tensor.transpose(pa[:, j, t * P:(t + 1) * P], rows[:, j % 2 * 4 + t, j // 2 * P:(j // 2 + 1) * P], k.ident[:])
                            last.then_inc(turned.sem, 1)
                        evacuated.wait(pe, i, 4)
                        for f in range(FC):
                            for j in range(2):
                                n = 2 * f + j
                                if n >= 4:
                                    relus.wait(pe, i, n - 3)
                                for c in range(KD):
                                    last = nc.tensor.matmul(pa[:, n % 4, :], w1[:, c, f * P:(f + 1) * P], XE[:, c, j * 512:(j + 1) * 512],
                                                            start=c == 0, stop=c == KD - 1)
                                last.then_inc(h_done.sem, 1)
                        relus.wait(pe, i, 2 * FC)
                        copied.wait(pe, i)
                        bb = b2[0:1, bass.ds(i, 1), :].rearrange("p o c -> p (o c)")
                        for t in range(CT):
                            nc.tensor.matmul(py[:, t, :], k.ones[0:1, :], bb, start=True, stop=False)
                            for f in range(FC):
                                last = nc.tensor.matmul(py[:, t, :], hid[:, f, t * P:(t + 1) * P], w2[:, f, :], start=False, stop=f == FC - 1)
                        last.then_inc(y_done.sem, 1)

                @block.scalar
                def _(act):
                    for x in (evacuated, relus):
                        x.open(act)
                    act.wait_ge(biases, 32)
                    chain = Chain(act, aorder)
                    with act.Fori(0, E1) as i:
                        chain.fresh()
                        relus.wait(act, i)
                        chain(nc.scalar.activation(bias[:], b1[:, bass.ds(i, 1), :].rearrange("p o f -> p (o f)"), ACT.Copy))
                        for j in range(4):
                            turned.wait(act, i, j + 1)
                            nc.scalar.activation(XE[:, j // 2, j % 2 * 512:(j % 2 + 1) * 512], pa[:, j, :], ACT.Copy).then_inc(evacuated.sem, 1)
                        y_done.wait(act, i)
                        for f in range(FC):
                            for j in range(2):
                                h_done.wait(act, i, 2 * f + j + 1)
                                nc.scalar.activation(hid[:, f, j * 512:(j + 1) * 512], pa[:, (2 * f + j) % 4, :], ACT.Relu,
                                                     bias=bias[:, f:f + 1]).then_inc(relus.sem, 1)


                @block.vector
                def _(dve):
                    copied.open(dve)
                    dve.sem_inc(written.sem, 1)
                    with dve.Fori(0, E1) as i:
                        y_done.wait(dve, i, 1)
                        written.wait(dve, i)
                        nc.vector.tensor_copy(Y, py[:]).then_inc(copied.sem, 1)

        with ExitStack() as es2:
            s2 = Scope(nc, es2, "back")
            idx = s2.sb("idx", [P, GT], I32)
            y = s2.sb("y", [P, GT, D])
            mask = s2.sb("mask", [P, GT * D], I32)
            const = s2.sb("const", [P, 3, 256])
            made = s2.sem("made")
            indexed = s2.tally("indexed", 1)
            got = s2.pool_dma_tally("got", 16 * GT)
            summed = s2.tally("summed", 1)
            stored = s2.sem("stored")
            with nc.Block() as block:
                @block.gpsimd
                def _(pool):
                    for j, v in enumerate((0.0, 1.0e4, -1.0e4)):
                        nc.gpsimd.memset(const[:, j], v).then_inc(made, 1)
                    with pool.Fori(0, NG) as i:
                        indexed.hold(pool, i, 1)
                        for t in range(GT):
                            nc.gpsimd.indirect_dma_start(y[:, t, :], None, ybuf, bass.IndirectOffsetOnAxis(ap=idx[:, t:t + 1], axis=0)).then_inc(got.sem, 16)

                @block.vector
                def _(dve):
                    indexed.open(dve)
                    summed.open(dve)
                    dve.wait_ge(made, 3)
                    chain = Chain(dve, order)
                    chain.fresh()
                    m3 = mask[:].rearrange("p (t c) -> p t c", c=D)

                    def filled(j):
                        return const[:, j:j + 1, 0:D].to_broadcast((P, GT, D))

                    with dve.Fori(0, NG) as i:
                        chain.fresh()
                        nc.vector.tensor_copy(idx[:], slot[:, 1, bass.ds(i * GT, GT)]).then_inc(indexed.sem, 1)
                        got.wait(dve, i, 16 * GT)
                        pr = prob[:, bass.ds(i * GT, GT)].unsqueeze(2).to_broadcast((P, GT, D))
                        chain(nc.vector.tensor_tensor(y[:], y[:], pr, ALU.mult))
                        chain(nc.vector.tensor_tensor(m3, y[:], y[:], ALU.not_equal))
                        chain(nc.vector.copy_predicated(y[:], m3, filled(0)))
                        chain(nc.vector.tensor_scalar(mask[:], y[:].rearrange("p t c -> p (t c)"), FLT_MAX, None, ALU.is_gt))
                        chain(nc.vector.copy_predicated(y[:], m3, filled(1)))
                        chain(nc.vector.tensor_scalar(mask[:], y[:].rearrange("p t c -> p (t c)"), -FLT_MAX, None, ALU.is_lt))
                        chain(nc.vector.copy_predicated(y[:], m3, filled(2)))
                        x = k.X[:, bass.ds(i * GT, GT), :]
                        nc.vector.tensor_tensor(x, x, y[:], ALU.add).then_inc(summed.sem, 1)
                        summed.wait(dve, i, 1)

                @block.sync
                def _(sp):
                    stored_t = Tally(stored, 16)
                    stored_t.open(sp)
                    with sp.Fori(0, NG) as i:
                        summed.hold(sp, i, 1)
                        sp.dma_start(out[bass.ds(i * GC, GC), :].rearrange("(t p) c -> p t c", p=P), k.X[:, bass.ds(i * GT, GT), :]).then_inc(stored, 16)
                    stored_t.wait(sp, NG)


FLT_MAX = float(np.finfo(np.float32).max)


def arrays(inputs):
    a = {n: np.asarray(v) for n, v in inputs.items()}
    out = {n: v for n, v in a.items() if n not in RESHAPED}

    def padded(v, n):
        return np.concatenate([v, np.zeros((n - v.shape[0],) + v.shape[1:], v.dtype)])

    def by_role(v):
        return v.reshape((8, 3, 32) + v.shape[1:]).transpose((1, 0, 2) + tuple(range(3, v.ndim + 2))).reshape(v.shape)

    out["x"] = padded(a["x"], NP)
    out["first_src"] = padded(a["src"][:N], NP).reshape(NT, P).T
    out["first_dst"] = padded(a["dst"][:N], NP).reshape(NT, P).T
    out["mix_wq"] = by_role(a["L0_mix_w_qkv"][:, :, 2]).T
    out["mix_col"] = np.stack([by_role(a["L0_mix_bn_gamma"]), by_role(a["L0_mix_bn_beta"]), by_role(a["L0_mix_w_dw"][:, 0, 2])])
    out["mix_pw"] = by_role(a["L0_mix_w_pw"][:, :, 0].reshape(24, 32, 32).transpose(0, 2, 1).reshape(QC * P, 32))
    for n in ("src", "dst", "weight"):
        v = a["edge_weight" if n == "weight" else n]
        fill = N if n == "dst" else 0
        out["edge_" + n] = np.concatenate([v, np.full(EP - E_EDGES, fill, v.dtype)]).reshape(P, S1)
    out["edge_attr"] = padded(a["edge_attr_64"], EP).reshape(P, S1, ED).transpose(2, 1, 0)
    out["ff_w1"] = a["L1_gnn_W1"].reshape(D, 2, F0).transpose(1, 0, 2)
    out["ff_b1"] = a["L1_gnn_b1"].reshape(2, F0)
    out["ff_w2"] = a["L1_gnn_W2"].reshape(2, F0, D)
    out["ff_b2"] = padded(a["L1_gnn_b2"][None], 2)
    out["lin_w"] = a["L1_mix_Wqkv"].T
    out["lin_wp"] = a["L1_mix_Wproj"].T
    out["lin_temp"] = a["L1_mix_temperature"].reshape(H1)
    out["L0_ffn_edge_index"] = a["L0_ffn_edge_index"].reshape(2, P, S0)
    out["L0_mix_w_res"] = a["L0_mix_w_res"][:, :, 0].T.reshape(4, P, D).transpose(1, 0, 2)
    return {n: np.ascontiguousarray(v) for n, v in out.items()}


RESHAPED = ("x", "src", "dst", "edge_attr_64", "edge_weight", "L0_mix_w_qkv", "L0_mix_bn_gamma", "L0_mix_bn_beta",
            "L0_mix_w_dw", "L0_mix_w_pw", "L0_mix_w_res", "L0_ffn_edge_index",
            "L1_gnn_W1", "L1_gnn_b1", "L1_gnn_W2", "L1_gnn_b2", "L1_mix_Wqkv", "L1_mix_Wproj", "L1_mix_temperature")


class Kept:

    def __init__(self, nc, es):
        self.nc = nc
        Scope.lasting = es
        s = Scope(nc, es, "kept")
        Tally.held = s.sem("held")
        self.X = s.sb("X", [P, NT, D])
        self.XT = s.sb("XT", [P, KD, NP])
        self.ident = s.sb("ident", [P, P])
        self.ones = s.sb("ones", [P, P])
        self.eps = s.sb("eps", [P, 1])
        self.valid = s.sb("valid", [P, NT])

    def dram(self, name, shape, dt=F32):
        return self.nc.dram_tensor(name, shape, dt, kind="Internal").ap()


def layer1_graph(nc, k, a):
    KW = D + H1 * VW
    qtable, ktable, atable = k.dram("qtable", (NP, D)), k.dram("ktable", (NP, KW)), k.dram("atable", (NP, AW))
    xtable = k.dram("xtable", (NT + 1, P, KD, P))
    xrows = k.dram("xrows", (P, NT, D))
    es = ExitStack()
    with es:
        s = Scope(nc, es, "l1")
        chan = s.sb("chan", [P, 4, KD])
        beta = s.sb("beta", [P, 1])
        loaded, order, kept = s.sem("loaded"), s.sem("order"), s.sem("kept")
        es2 = ExitStack()
        with es2:
            B = Scope(nc, es2, "rows").sb("B", [P, NT, D])
            layernorm_phase(nc, k, "ln2", k.X, keep=B)
            with nc.Block() as block:
                @block.sync
                def _(sp):
                    for j, n in enumerate(("ln1_g", "ln1_b", "ln2_g", "ln2_b")):
                        sp.dma_start(chan[:, j, :], a[f"L1_gnn_{n}"].rearrange("(k p) -> p k", p=P), allow_slow_non_contiguous=True).then_inc(loaded, 16)
                    sp.dma_start(beta[:], a["L1_gnn_beta"].partition_broadcast(P)).then_inc(loaded, 16)
                    for c in range(KD):
                        sp.dma_start(xtable[0:NT, :, c, :].rearrange("t p n -> p t n"), k.XT[:, c, :].rearrange("p (t n) -> p t n", n=P)).then_inc(kept, 16)
                    sp.dma_start(xtable[NT], k.XT[:, :, 0:P]).then_inc(kept, 16)
                    sp.dma_start(xrows, B[:]).then_inc(kept, 16)
                    sp.wait_ge(loaded, 80)
                    sp.wait_ge(kept, 16 * (KD + 2))
            layernorm_phase(nc, k, "ln3", B, scale=chan[:, 0, :], shift=chan[:, 1, :])
            tables_phase(nc, k, a, qtable, ktable, atable)
        edges_and_linear_phase(nc, k, a, qtable, ktable, atable, xtable, k.X)
        es2 = ExitStack()
        with es2:
            B = Scope(nc, es2, "rows2").sb("B", [P, NT, D])
            with nc.Block() as block:
                @block.sync
                def _(sp):
                    sp.dma_start(B[:], xrows).then_inc(loaded, 16)
                    sp.wait_ge(loaded, 96)
            attention_out_phase(nc, k, a, atable, B)
            layernorm_phase(nc, k, "ln4", B, scale=chan[:, 2, :], shift=chan[:, 3, :])
            experts_phase(nc, k, "ff1", a["ff_w1"], a["ff_b1"], a["ff_w2"], a["ff_b2"], 2, lambda e, t: beta[:, 0:1], B)
            with nc.Block() as block:
                @block.vector
                def _(dve):
                    nc.vector.tensor_tensor(k.X[:], k.X[:], B[:], ALU.add).then_inc(order, 1)
                    dve.wait_ge(order, 1)


def program(nc, a, out, phases=("L0a", "L0b", "L1a", "L1b")):
    with ExitStack() as es:
        k = Kept(nc, es)
        setup_phase(nc, a, k)
        if "L0a" in phases:
            with ExitStack() as es0:
                ball = Scope(nc, es0, "L0").sb("ball", [P, KD, NP])
                layernorm_phase(nc, k, "ln0", k.X, ball=ball)
                gather_phase(nc, k, a)
                mixer_phase(nc, k, a, ball)
        if "L0b" in phases:
            with ExitStack() as es0:
                gates = Scope(nc, es0, "L0").sb("gates", [P, NT, E0])
                layernorm_phase(nc, k, "ln1", k.X)
                gate_phase(nc, k, a, gates)
                experts_phase(nc, k, "moe0", a["L0_ffn_W1"], a["L0_ffn_b1"], a["L0_ffn_W2"], a["L0_ffn_b2"], E0,
                              lambda e, t: gates[:, bass.ds(t, 1), e], k.X)
        if "L1a" in phases:
            layer1_graph(nc, k, a)
        es1 = ExitStack()
        with es1:
            B = Scope(nc, es1, "last").sb("B", [P, NT, D])
            if "L1b" in phases:
                layernorm_phase(nc, k, "ln5", k.X, keep=B)
                top1_phase(nc, k, a, B, out)
                return
        with ExitStack() as es1:
            stored = Scope(nc, es1, "end").sem("stored")
            with nc.Block() as block:
                @block.sync
                def _(sp):
                    sp.dma_start(out.rearrange("(t p) c -> p t c", p=P), k.X[:]).then_inc(stored, 16)
                    sp.wait_ge(stored, 16)


def kernel(**inputs):
    import concourse.bacc as bacc
    from concourse.bass_utils import run_bass_kernel_spmd

    nc = bacc.Bacc("TRN2", target_bir_lowering=False, num_devices=1)
    host = arrays(inputs)
    a = {n: nc.dram_tensor(f"in_{n}", v.shape, mybir.dt.from_np(v.dtype), kind="ExternalInput").ap() for n, v in host.items()}
    out = nc.dram_tensor("out", (NP, D), F32, kind="ExternalOutput").ap()
    program(nc, a, out)
    r = run_bass_kernel_spmd(nc, [{f"in_{n}": v for n, v in host.items()}], core_ids=[0])
    return r.results[0]["out"][:N]
```

```python
import numpy as np
import concourse.bass as bass
from concourse import mybir
from concourse.alu_op_type import AluOpType as ALU
from contextlib import ExitStack

F32 = mybir.dt.float32
I32 = mybir.dt.int32
ACT = mybir.ActivationFunctionType
AX = mybir.AxisListType

P = 128
N = 6250
D = 256
KD = D // P
NT = -(-N // P)
GT = 7
NG = NT // GT
GC = GT * P
HC = GC // 2
NP = NT * P
BIG = 1.0e30
LN_EPS = 1e-05

H0, C0 = 4, 64
R0 = D + H0
QC = 6
MAXNORM = 1.0 - 1e-05
ATANH_MAX = float(np.arctanh(np.float64(np.float32(MAXNORM))))
MIN_NORM = 1e-15
ATT_EPS = 1e-15
E0, F0, GH = 4, 512, 4
GW = GH * E0
MW = GW + GH
E0_EDGES = 131072
S0 = E0_EDGES // P
U0 = 8

E_EDGES = 200000
H1, D1, ED = 8, 32, 64
U1 = 8
W = 2
S1 = -(-E_EDGES // (P * U1)) * U1
EP = S1 * P
AW = D + 2 * H1
FF = 1024
VW = D1 + 1
PD = D1 // 2 + 1
PR = PD * D1
PC = -(-PR // P)
E1, F1 = 8, 1024
CAP = -(-5 * N // (4 * E1))
CS = 1024
CT = CS // P


class Chain:

    def __init__(self, eng, sem):
        self.eng, self.sem, self.n = eng, sem, 0

    def __call__(self, ins):
        self.n += 1
        ins.then_inc(self.sem, 1)
        self.eng.wait_ge(self.sem, self.n)

    def fresh(self):
        self.eng.sem_clear(self.sem)
        self.n = 0


class Tally:

    held = None

    def __init__(self, sem, per_pass, credit=1):
        self.sem, self.per_pass, self.credit = sem, per_pass, credit

    def open(self, eng):
        eng.sem_inc(self.sem, self.credit)

    def wait(self, eng, i, n=0):
        eng.wait_ge(self.sem, i * self.per_pass + (self.credit + n))

    def hold(self, eng, i, n=0):
        self.wait(eng, i, n)
        eng.sem_inc(self.held, 1)


class Scope:

    lasting = None

    def __init__(self, nc, es, name):
        self.nc, self.es, self.name, self.sems = nc, es, name, []
        es.callback(self.clear)

    def clear(self):
        if self.sems:
            with self.nc.Block() as block:
                @block.sync
                def _(sp):
                    for sem in self.sems:
                        sp.sem_clear(sem)

    def sb(self, name, shape, dt=F32):
        return self.es.enter_context(self.nc.sbuf_tensor(f"{self.name}_{name}", shape, dt))

    def ps(self, name, shape):
        return self.es.enter_context(self.nc.psum_tensor(f"{self.name}_{name}", shape, F32))

    def sem(self, name):
        self.sems.append(self.es.enter_context(self.nc.semaphore(f"{self.name}_{name}")))
        return self.sems[-1]

    def pool_dma_sem(self, name):
        return Scope.lasting.enter_context(self.nc.semaphore(f"{self.name}_{name}"))

    def tally(self, name, per_pass, credit=1):
        return Tally(self.sem(name), per_pass, credit)

    def pool_dma_tally(self, name, per_pass):
        return Tally(self.pool_dma_sem(name), per_pass, 0)


def tile_of(x, t):
    return x[:, bass.ds(t, 1), :].rearrange("p o c -> p (o c)")


def setup_phase(nc, a, k):
    with ExitStack() as es:
        s = Scope(nc, es, "setup")
        loaded, made = s.sem("loaded"), s.sem("made")
        with nc.Block() as block:
            @block.sync
            def _(sp):
                sp.dma_start(k.X[:], a["x"].rearrange("(t p) c -> p t c", p=P)).then_inc(loaded, 16)
                sp.wait_ge(loaded, 16)

            @block.gpsimd
            def _(pool):
                chain = Chain(pool, made)
                nc.gpsimd.memset(k.ones[:], 1.0)
                nc.gpsimd.memset(k.eps[:], LN_EPS)
                nc.gpsimd.memset(k.valid[:], 1.0)
                chain(nc.gpsimd.memset(k.ident[:], 0.0))
                nc.gpsimd.affine_select(out=k.ident[:], in_=k.ident[:], compare_op=ALU.not_equal, fill=1.0,
                                        base=0, pattern=[[-1, P]], channel_multiplier=1)
                chain(nc.gpsimd.affine_select(out=k.valid[:], in_=k.valid[:], compare_op=ALU.is_ge, fill=0.0,
                                              base=N - 1, pattern=[[-P, NT]], channel_multiplier=-1))


def layernorm_phase(nc, k, name, src, keep=None, scale=None, shift=None, ball=None):
    with ExitStack() as es:
        s = Scope(nc, es, name)
        stats = s.sb("stats", [P, GT, 6])
        mv = s.sb("mv", [P, GT, 2])
        sd = s.sb("sd", [P, GT])
        rows = s.sb("rows", [P, GT, D])
        pt = s.ps("pt", [P, KD, 1024])
        nsets = 2 if ball is not None else 1
        stats_ready = s.tally("stats_ready", 1)
        sd_ready = s.tally("sd_ready", 1)
        rows_ready = s.tally("rows_ready", nsets)
        transposed = s.tally("transposed", KD * nsets)
        evacuated = s.tally("evacuated", KD * nsets)
        kept = s.tally("kept", 1)
        order = s.sem("order")
        aorder = s.sem("aorder")
        if ball is not None:
            sq = s.sb("sq", [P, D])
            n2 = s.sb("n2", [P, GT])
            nrm = s.sb("nrm", [P, GT])
            z = s.sb("z", [P, 8, GT])
            norms_ready = s.tally("norms_ready", 2)
            ratio_ready = s.tally("ratio_ready", 1)

        with nc.Block() as block:
            @block.vector
            def _(dve):
                stats_ready.open(dve)
                rows_ready.open(dve)
                chain = Chain(dve, order)
                if ball is not None:
                    ratio_ready.open(dve)
                with dve.Fori(0, NG) as i:
                    chain.fresh()
                    for t in range(GT):
                        last = nc.vector.bn_stats(stats[:, t, :], tile_of(src, i * GT + t))
                    chain(last)
                    for t in range(GT):
                        last = nc.vector.bn_aggr(mv[:, t, :], stats[:, t, :])
                    last.then_inc(stats_ready.sem, 1)
                    sd_ready.wait(dve, i, 1)
                    chain(nc.vector.reciprocal(sd[:], sd[:]))
                    transposed.wait(dve, i)
                    if keep is not None:
                        kept.wait(dve, i)
                    for t in range(GT):
                        last = nc.vector.tensor_scalar(rows[:, t, :], tile_of(src, i * GT + t), mv[:, t, 0:1],
                                                       sd[:, t:t + 1], ALU.subtract, ALU.mult)
                    last.then_inc(rows_ready.sem, 1)
                    if ball is not None:
                        c, c2, top, r, ser, m = (z[:, j, :] for j in range(6))
                        norms_ready.wait(dve, i, 1)
                        chain(nc.vector.tensor_scalar_min(c, nrm[:], MAXNORM))
                        chain(nc.vector.tensor_scalar(r, c, -1.0, 1.0, ALU.mult, ALU.add))
                        chain(nc.vector.reciprocal(r, r))
                        chain(nc.vector.scalar_tensor_tensor(top, c, 1.0, r, ALU.add, ALU.mult))
                        nc.vector.tensor_tensor(c2, c, c, ALU.mult).then_inc(ratio_ready.sem, 1)
                        norms_ready.wait(dve, i, 2)
                        chain(nc.vector.tensor_scalar_max(r, nrm[:], MIN_NORM))
                        chain(nc.vector.reciprocal(r, r))
                        chain(nc.vector.scalar_tensor_tensor(top, z[:, 6, :], 0.5, r, ALU.mult, ALU.mult))
                        chain(nc.vector.tensor_scalar(ser, c2, 1.0 / 7, 1.0 / 5, ALU.mult, ALU.add))
                        chain(nc.vector.tensor_tensor(ser, ser, c2, ALU.mult))
                        chain(nc.vector.scalar_tensor_tensor(ser, ser, 1.0 / 3, c2, ALU.add, ALU.mult))
                        chain(nc.vector.tensor_scalar(m, c, 0.05, None, ALU.is_lt))
                        chain(nc.vector.scalar_tensor_tensor(ser, ser, 1.0, top, ALU.add, ALU.subtract))
                        chain(nc.vector.tensor_tensor(ser, ser, m, ALU.mult))
                        chain(nc.vector.tensor_tensor(top, ser, top, ALU.add))
                        transposed.wait(dve, i, KD)
                        for t in range(GT):
                            last = nc.vector.tensor_scalar(rows[:, t, :], rows[:, t, :], top[:, t:t + 1], None, ALU.mult)
                        last.then_inc(rows_ready.sem, 1)

            @block.scalar
            def _(act):
                sd_ready.open(act)
                evacuated.open(act)
                if ball is not None:
                    norms_ready.open(act)
                chain = Chain(act, aorder)
                with act.Fori(0, NG) as i:
                    chain.fresh()
                    stats_ready.wait(act, i, 1)
                    nc.scalar.activation(sd[:], mv[:, :, 1], ACT.Sqrt, bias=k.eps[:, 0:1]).then_inc(sd_ready.sem, 1)
                    if ball is not None:
                        rows_ready.wait(act, i, 1)
                        for t in range(GT):
                            chain(nc.scalar.activation(sq[:], rows[:, t, :], ACT.Square, accum_out=n2[:, t:t + 1]))
                        nc.scalar.activation(nrm[:], n2[:], ACT.Sqrt).then_inc(norms_ready.sem, 1)
                    for j in range(nsets):
                        if j:
                            ratio_ready.wait(act, i, 1)
                            nc.scalar.activation(z[:, 6, :], z[:, 2, :], ACT.Ln).then_inc(norms_ready.sem, 1)
                        for c in range(KD):
                            transposed.wait(act, i, KD * j + c + 1)
                            out = (ball if j else k.XT)[:, c, bass.ds(i * GC, GC)]
                            if scale is not None:
                                ins = nc.scalar.activation(out, pt[:, c, 0:GC], ACT.Identity,
                                                           bias=shift[:, c:c + 1], scale=scale[:, c:c + 1])
                            else:
                                ins = nc.scalar.activation(out, pt[:, c, 0:GC], ACT.Copy)
                            ins.then_inc(evacuated.sem, 1)

            @block.tensor
            def _(pe):
                transposed.open(pe)
                with pe.Fori(0, NG) as i:
                    for j in range(nsets):
                        rows_ready.wait(pe, i, j + 1)
                        for c in range(KD):
                            evacuated.wait(pe, i, c + 1 if j else 0)
                            for t in range(GT):
                                last = nc.tensor.transpose(pt[:, c, t * P:(t + 1) * P], rows[:, t, c * P:(c + 1) * P],
                                                           k.ident[:])
                            last.then_inc(transposed.sem, 1)

            if keep is not None:
                @block.gpsimd
                def _(pool):
                    kept.open(pool)
                    with pool.Fori(0, NG) as i:
                        rows_ready.hold(pool, i, 1)
                        nc.gpsimd.tensor_copy(keep[:, bass.ds(i * GT, GT), :], rows[:]).then_inc(kept.sem, 1)


def gather_phase(nc, k, a):
    with ExitStack() as es:
        s = Scope(nc, es, "g0")
        w = s.sb("w", [P, KD, D])
        at = s.sb("at", [P, 2, D])
        xs = s.sb("xs", [P, KD, GC])
        pr = s.ps("pr", [P, 8, D])
        row = s.sb("row", [P, GT, R0])
        left = s.sb("left", [P, GT, H0])
        prod = s.sb("prod", [P, GT, D])
        iall = s.sb("iall", [P, 2, NT], I32)
        table, ltable = k.dram("g0_table", (NP, R0)), k.dram("g0_left_logits", (NP, H0))
        weights = s.sem("weights")
        copied = s.tally("copied", 1)
        projected = s.tally("projected", 1)
        rows_ready = s.tally("rows_ready", 1)
        stored = s.tally("stored", 32)
        order = s.sem("order")
        with nc.Block() as block:
            @block.sync
            def _(sp):
                sp.dma_start(w[:], a["L0_gnn_weight"].rearrange("(k p) c -> p k c", p=P)).then_inc(weights, 16)
                sp.dma_start(at[:, 0, :], a["L0_gnn_attn_l"].rearrange("h c -> (h c)").partition_broadcast(P)).then_inc(weights, 16)
                sp.dma_start(at[:, 1, :], a["L0_gnn_attn_r"].rearrange("h c -> (h c)").partition_broadcast(P)).then_inc(weights, 16)
                sp.dma_start(iall[:, 0, :], a["first_src"]).then_inc(weights, 16)
                sp.dma_start(iall[:, 1, :], a["first_dst"]).then_inc(weights, 16)
                sp.wait_ge(weights, 80)
                stored.open(sp)
                with sp.Fori(0, NG) as i:
                    rows_ready.hold(sp, i, 1)
                    sp.dma_start(table[bass.ds(i * GC, GC), :].rearrange("(t p) c -> p t c", p=P), row[:]).then_inc(stored.sem, 16)
                    sp.dma_start(ltable[bass.ds(i * GC, GC), :].rearrange("(t p) c -> p t c", p=P), left[:]).then_inc(stored.sem, 16)
                    stored.hold(sp, i, 32)

            @block.scalar
            def _(act):
                copied.open(act)
                with act.Fori(0, NG) as i:
                    projected.wait(act, i)
                    nc.scalar.activation(xs[:], k.XT[:, :, bass.ds(i * GC, GC)], ACT.Copy).then_inc(copied.sem, 1)

            @block.tensor
            def _(pe):
                projected.open(pe)
                pe.wait_ge(weights, 80)
                with pe.Fori(0, NG) as i:
                    copied.wait(pe, i, 1)
                    rows_ready.wait(pe, i)
                    for t in range(GT):
                        for c in range(KD):
                            last = nc.tensor.matmul(pr[:, t, :], xs[:, c, t * P:(t + 1) * P], w[:, c, :],
                                                    start=c == 0, stop=c == KD - 1)
                    last.then_inc(projected.sem, 1)

            @block.vector
            def _(dve):
                rows_ready.open(dve)
                dve.wait_ge(weights, 80)
                chain = Chain(dve, order)
                with dve.Fori(0, NG) as i:
                    chain.fresh()
                    projected.wait(dve, i, 1)
                    stored.wait(dve, i)
                    for side, out in ((0, left[:]), (1, row[:, :, D:R0])):
                        chain(nc.vector.tensor_tensor(prod[:], pr[:, 0:GT, :], at[:, side:side + 1, :].to_broadcast((P, GT, D)), ALU.mult))
                        chain(nc.vector.tensor_reduce(out, prod[:].rearrange("p t (h c) -> p t h c", h=H0), AX.X, ALU.add))
                    nc.vector.tensor_copy(row[:, :, 0:D], pr[:, 0:GT, :]).then_inc(rows_ready.sem, 1)

        idx = s.sb("idx", [P, 2, GT], I32)
        got = s.sb("got", [P, GT, R0])
        gotl = s.sb("gotl", [P, GT, H0])
        al = s.sb("al", [P, 2, GT, H0])
        mx = s.sb("mx", [P, 2, GT])
        mix = s.sb("mix", [P, GT, C0])
        indexed = s.tally("indexed", 1)
        gathered = [s.pool_dma_tally(f"gathered{t}", 32) for t in range(GT)]
        consumed = s.tally("consumed", 1)
        logits = s.tally("logits", 1)
        exps = s.tally("exps", 1)
        with nc.Block() as block:
            @block.gpsimd
            def _(pool):
                with pool.Fori(0, NG) as i:
                    indexed.hold(pool, i, 1)
                    for t in range(GT):
                        nc.gpsimd.indirect_dma_start(got[:, t, :], None, table, bass.IndirectOffsetOnAxis(ap=idx[:, 1, t:t + 1], axis=0)).then_inc(gathered[t].sem, 16)
                        nc.gpsimd.indirect_dma_start(gotl[:, t, :], None, ltable, bass.IndirectOffsetOnAxis(ap=idx[:, 0, t:t + 1], axis=0)).then_inc(gathered[t].sem, 16)

            @block.scalar
            def _(act):
                exps.open(act)
                with act.Fori(0, NG) as i:
                    logits.wait(act, i, 1)
                    nc.scalar.activation(al[:, 0], al[:, 0], ACT.Exp).then_inc(exps.sem, 1)

            @block.vector
            def _(dve):
                indexed.open(dve)
                logits.open(dve)
                chain = Chain(dve, order)
                chain.fresh()
                with dve.Fori(0, NG) as i:
                    chain.fresh()
                    nc.vector.tensor_copy(idx[:], iall[:, :, bass.ds(i * GT, GT)]).then_inc(indexed.sem, 1)
                    for t in range(GT):
                        gathered[t].wait(dve, i, 32)
                    v, wt = al[:, 0], al[:, 1]
                    chain(nc.vector.tensor_tensor(v, gotl[:], got[:, :, D:R0], ALU.add))
                    chain(nc.vector.scalar_tensor_tensor(v, v, 0.01, v, ALU.mult, ALU.max))
                    chain(nc.vector.tensor_reduce(mx[:, 0, :], v, AX.X, ALU.max))
                    nc.vector.tensor_tensor(v, v, mx[:, 0, :].unsqueeze(2).to_broadcast((P, GT, H0)), ALU.subtract).then_inc(logits.sem, 1)
                    exps.wait(dve, i, 1)
                    chain(nc.vector.tensor_reduce(mx[:, 1, :], v, AX.X, ALU.add))
                    chain(nc.vector.reciprocal(mx[:, 1, :], mx[:, 1, :]))
                    chain(nc.vector.tensor_tensor(wt, v, mx[:, 1, :].unsqueeze(2).to_broadcast((P, GT, H0)), ALU.mult))
                    chain(nc.vector.tensor_tensor(prod[:].rearrange("p t (h c) -> p t h c", h=H0),
                                                  got[:, :, 0:D].rearrange("p t (h c) -> p t h c", h=H0),
                                                  wt.unsqueeze(3).to_broadcast((P, GT, H0, C0)), ALU.mult))
                    chain(nc.vector.tensor_reduce(mix[:], prod[:].rearrange("p t (h c) -> p t c h", h=H0), AX.X, ALU.add))
                    x = k.X[:, bass.ds(i * GT, GT), :].rearrange("p t (h c) -> p t h c", h=H0)
                    chain(nc.vector.tensor_tensor(x, x, mix[:].unsqueeze(2).to_broadcast((P, GT, H0, C0)), ALU.add))


def mixer_phase(nc, k, a, ball):
    with ExitStack() as es:
        s = Scope(nc, es, "mix")
        wq = s.sb("wq", [P, KD, QC * P])
        col = s.sb("col", [P, 3, QC])
        pw = s.sb("pw", [P, QC, P])
        stats = s.sb("stats", [P, QC, 2 * NG, 6])
        mv = s.sb("mv", [P, QC, 2])
        bn = s.sb("bn", [P, 6, QC])
        ph = s.ps("ph", [P, 8, 512])
        loaded, order, aorder = s.sem("loaded"), s.sem("order"), s.sem("aorder")
        zeroed = s.sem("zeroed")
        product = s.tally("product", QC)
        counted = s.tally("counted", QC)
        var_ready, sd_ready = s.sem("var_ready"), s.sem("sd_ready")
        with nc.Block() as block:
            @block.sync
            def _(sp):
                sp.dma_start(wq[:], a["mix_wq"].rearrange("(k p) c -> p k c", p=P)).then_inc(loaded, 16)
                sp.dma_start(col[:], a["mix_col"].rearrange("j (c p) -> p j c", p=P), allow_slow_non_contiguous=True).then_inc(loaded, 16)
                sp.wait_ge(zeroed, 1)
                for b in range(4):
                    sp.dma_start(pw[b * 32:(b + 1) * 32, :, b * 32:(b + 1) * 32],
                                 a["mix_pw"].rearrange("(c b i) o -> b i c o", b=4, i=32)[b]).then_inc(loaded, 16)
                sp.wait_ge(loaded, 96)

            @block.gpsimd
            def _(pool):
                nc.gpsimd.memset(pw[:], 0.0).then_inc(zeroed, 1)

            @block.tensor
            def _(pe):
                product.open(pe)
                pe.wait_ge(loaded, 96)
                with pe.Fori(0, 2 * NG) as i:
                    for c in range(QC):
                        counted.wait(pe, i)
                        for kk in range(KD):
                            last = nc.tensor.matmul(ph[:, c, 0:HC], wq[:, kk, c * P:(c + 1) * P],
                                                    ball[:, kk, bass.ds(i * HC, HC)], start=kk == 0, stop=kk == KD - 1)
                        last.then_inc(product.sem, 1)

            @block.vector
            def _(dve):
                counted.open(dve)
                chain = Chain(dve, order)
                with dve.Fori(0, 2 * NG) as i:
                    for c in range(QC):
                        product.wait(dve, i, c + 1)
                        nc.vector.bn_stats(stats[:, c, bass.ds(i, 1), :].rearrange("p o s -> p (o s)"), ph[:, c, 0:HC]).then_inc(counted.sem, 1)
                dve.wait_ge(loaded, 96)
                counted.wait(dve, 2 * NG)
                for c in range(QC):
                    last = nc.vector.bn_aggr(mv[:, c, :], stats[:, c].rearrange("p i s -> p (i s)"))
                chain(last)
                mean, ex2, m2, var = (bn[:, j, :] for j in range(4))
                ratio = float(NP) / N
                chain(nc.vector.tensor_tensor(ex2, mv[:, :, 0], mv[:, :, 0], ALU.mult))
                chain(nc.vector.tensor_tensor(ex2, ex2, mv[:, :, 1], ALU.add))
                chain(nc.vector.tensor_scalar(mean, mv[:, :, 0], ratio, None, ALU.mult))
                chain(nc.vector.tensor_tensor(m2, mean, mean, ALU.mult))
                chain(nc.vector.scalar_tensor_tensor(var, ex2, ratio, m2, ALU.mult, ALU.subtract))
                nc.vector.tensor_scalar_max(var, var, 0.0).then_inc(var_ready, 1)
                dve.wait_ge(sd_ready, 1)
                chain(nc.vector.reciprocal(bn[:, 4, :], bn[:, 4, :]))
                chain(nc.vector.tensor_tensor(bn[:, 4, :], bn[:, 4, :], col[:, 0, :], ALU.mult))
                chain(nc.vector.tensor_tensor(mean, mean, bn[:, 4, :], ALU.mult))
                chain(nc.vector.tensor_tensor(bn[:, 5, :], col[:, 1, :], mean, ALU.subtract))
                chain(nc.vector.tensor_tensor(pw[:], pw[:], col[:, 2, :].unsqueeze(2).to_broadcast((P, QC, P)), ALU.mult))

            @block.scalar
            def _(act):
                act.wait_ge(var_ready, 1)
                nc.scalar.activation(bn[:, 4, :], bn[:, 3, :], ACT.Sqrt, bias=k.eps[:, 0:1]).then_inc(sd_ready, 1)

        wr = s.sb("wr", [P, 4, D])
        br = s.sb("br", [P, D])
        blk = s.sb("blk", [P, P])
        work = k.XT[:].rearrange("p k n -> p (k n)")[:, 0:28 * HC].rearrange("p (c n) -> p c n", n=HC)
        U, V = [work[:, 0:4], work[:, 4:8]], [work[:, 8:12], work[:, 12:16]]
        UK, VK, sq, tmp_u = work[:, 16:18], work[:, 18:20], work[:, 20:26], work[:, 26:28]
        tmp_v = s.sb("tmp_v", [P, 2, HC])
        ks = s.sb("ks", [P, 4, HC])
        O = s.sb("O", [P, 4, GC])
        g = s.sb("g", [P, 3, HC])
        node = s.sb("node", [P, 4, GT])
        ft = s.sb("ft", [P, GT, D])
        junk = s.sb("junk", [P, D])
        made = s.sem("made")
        h_done, u_ready = s.tally("h_done", QC), s.tally("u_ready", QC)
        s_done, u_summed, summed, k_summed, o_summed = (s.tally(n, 1) for n in ("s_done", "u_summed", "summed", "k_summed", "o_summed"))
        u_squared, s_ready, ks_ready, root, o_squared, o_root = (s.tally(n, 1) for n in ("u_squared", "s_ready", "ks_ready", "root", "o_squared", "o_root"))
        bounded, o_ready, o_scaled = (s.tally(n, 1) for n in ("bounded", "o_ready", "o_scaled"))
        ft_done, ft_copied, row_norms, ft_ready = (s.tally(n, 1) for n in ("ft_done", "ft_copied", "row_norms", "ft_ready"))

        def groups(eng, group):
            group(0, first=True)
            with eng.Fori(1, NG - 1) as i:
                group(i)
            group(NG - 1, last=True)

        with nc.Block() as block:
            @block.sync
            def _(sp):
                sp.dma_start(wr[:], a["L0_mix_w_res"]).then_inc(loaded, 16)
                sp.dma_start(br[:], a["L0_mix_b_res"].partition_broadcast(P)).then_inc(loaded, 16)
                sp.wait_ge(loaded, 128)

            @block.gpsimd
            def _(pool):
                nc.gpsimd.memset(blk[:], 0.0).then_inc(made, 1)
                pool.wait_ge(made, 1)
                for b in range(4):
                    nc.gpsimd.memset(blk[32 * b:32 * b + 32, 32 * b:32 * b + 32], 1.0).then_inc(made, 1)

            @block.tensor
            def _(pe):
                for x in (h_done, s_done, u_summed, summed, k_summed, o_summed, ft_done):
                    x.open(pe)
                pe.wait_ge(loaded, 128)
                pe.wait_ge(made, 5)

                def front(i, j):
                    f = i * 2 + j
                    ks_ready.wait(pe, f)
                    for c in range(QC):
                        for kk in range(KD):
                            last = nc.tensor.matmul(ph[:, c, 0:HC], wq[:, kk, c * P:(c + 1) * P],
                                                    ball[:, kk, bass.ds(i * GC + j * HC, HC)], start=kk == 0, stop=kk == KD - 1)
                        last.then_inc(h_done.sem, 1)
                    for c in range(QC):
                        u_ready.wait(pe, f, c + 1)
                        last = nc.tensor.matmul(ph[:, c, 0:HC], pw[:, c, :], U[j][:, c, :] if c < 4 else UK[:, c - 4, :], start=True, stop=True)
                    last.then_inc(s_done.sem, 1)
                    u_squared.wait(pe, f, 1)
                    bounded.wait(pe, f)
                    for c in range(QC):
                        last = nc.tensor.matmul(ph[:, 6, 0:HC], k.ones[:], sq[:, c, :], start=c == 0, stop=False)
                    last.then_inc(u_summed.sem, 1)
                    s_ready.wait(pe, f, 1)
                    for c in range(QC):
                        last = nc.tensor.matmul(ph[:, 6, 0:HC], k.ones[:], sq[:, c, :], start=False, stop=c == QC - 1)
                    last.then_inc(summed.sem, 1)
                    for m in range(4):
                        last = nc.tensor.matmul(ph[:, m, 0:HC], blk[:], UK[:, m, :] if m < 2 else VK[:, m - 2, :], start=True, stop=True)
                    last.then_inc(k_summed.sem, 1)

                def back(i, j):
                    f = i * 2 + j
                    o_squared.wait(pe, f, 1)
                    o_root.wait(pe, f)
                    for m in range(4):
                        last = nc.tensor.matmul(ph[:, 7, 0:HC], k.ones[:], U[j][:, m, :], start=m == 0, stop=m == 3)
                    last.then_inc(o_summed.sem, 1)

                def group(i, first=False, last=False):
                    if not first:
                        ft_copied.wait(pe, i)
                    front(i, 1)
                    back(i, 0)
                    if not last:
                        front(i + 1, 0)
                    back(i, 1)
                    o_scaled.wait(pe, i * 2, 2)
                    ks_ready.wait(pe, i * 2, 2 if last else 3)
                    for t in range(GT):
                        for m in range(4):
                            mm = nc.tensor.matmul(ph[:, t // 2, (t % 2) * D:(t % 2 + 1) * D], O[:, m, t * P:(t + 1) * P],
                                                  wr[:, m, :], start=m == 0, stop=m == 3)
                    mm.then_inc(ft_done.sem, 1)

                front(0, 0)
                groups(pe, group)

            @block.scalar
            def _(act):
                for x in (u_ready, u_squared, s_ready, ks_ready, root, o_squared, o_root, ft_copied, row_norms):
                    x.open(act)
                chain = Chain(act, aorder)

                def front(i, j):
                    f = i * 2 + j
                    o_summed.wait(act, max(f - 1, 0) if isinstance(f, int) else f - 1)
                    for c in range(QC):
                        h_done.wait(act, f, c + 1)
                        nc.scalar.activation(U[j][:, c, :] if c < 4 else UK[:, c - 4, :], ph[:, c, 0:HC], ACT.Relu,
                                             bias=bn[:, 5, c:c + 1], scale=bn[:, 4, c:c + 1]).then_inc(u_ready.sem, 1)
                    u_ready.wait(act, f, QC)
                    nc.scalar.activation(sq[:, 0:4, :], U[j], ACT.Square)
                    nc.scalar.activation(sq[:, 4:6, :], UK, ACT.Square).then_inc(u_squared.sem, 1)
                    s_done.wait(act, f, 1)
                    nc.scalar.activation(V[j][:, 0:2, :], ph[:, 0:2, 0:HC], ACT.Relu)
                    nc.scalar.activation(V[j][:, 2:4, :], ph[:, 2:4, 0:HC], ACT.Copy)
                    nc.scalar.activation(VK, ph[:, 4:6, 0:HC], ACT.Relu)
                    u_summed.wait(act, f, 1)
                    nc.scalar.activation(sq, ph[:, 0:6, 0:HC], ACT.Square).then_inc(s_ready.sem, 1)

                def k_sums(i, j):
                    f = i * 2 + j
                    k_summed.wait(act, f, 1)
                    o_ready.wait(act, f)
                    nc.scalar.activation(ks[:], ph[:, 0:4, 0:HC], ACT.Copy).then_inc(ks_ready.sem, 1)

                def norm(i, j):
                    bounded.wait(act, i * 2 + j, 1)
                    nc.scalar.activation(g[:, 1, :], g[:, 0, :], ACT.Sqrt).then_inc(root.sem, 1)

                def output_norm(i, j):
                    f = i * 2 + j
                    o_ready.wait(act, f, 1)
                    nc.scalar.activation(U[j][:, 0:2, :], tmp_u, ACT.Square)
                    nc.scalar.activation(U[j][:, 2:4, :], tmp_v[:], ACT.Square).then_inc(o_squared.sem, 1)
                    o_summed.wait(act, f, 1)
                    nc.scalar.activation(g[:, 2, :], ph[:, 7, 0:HC], ACT.Sqrt, scale=ATANH_MAX ** -2).then_inc(o_root.sem, 1)

                def rows(i):
                    ft_ready.wait(act, i, 1)
                    for t in range(GT):
                        chain(nc.scalar.activation(junk[:], ft[:, t, :], ACT.Square, accum_out=node[:, 0, t:t + 1]))
                    chain(nc.scalar.activation(node[:, 1, :], node[:, 0, :], ACT.Sqrt))
                    nc.scalar.activation(node[:, 2, :], node[:, 1, :], ACT.Tanh).then_inc(row_norms.sem, 1)

                def group(i, first=False, last=False):
                    chain.fresh()
                    norm(i, 0)
                    front(i, 1)
                    if not first:
                        rows(i - 1)
                    output_norm(i, 0)
                    k_sums(i, 1)
                    norm(i, 1)
                    if not last:
                        front(i + 1, 0)
                    output_norm(i, 1)
                    if not last:
                        k_sums(i + 1, 0)
                    ft_done.wait(act, i, 1)
                    nc.scalar.activation(ft[:], ph[:, 0:4, :].rearrange("p b c -> p (b c)")[:, 0:GT * D].rearrange("p (t c) -> p t c", c=D),
                                         ACT.Copy).then_inc(ft_copied.sem, 1)
                    if last:
                        rows(i)

                front(0, 0)
                k_sums(0, 0)
                groups(act, group)

            @block.vector
            def _(dve):
                for x in (bounded, o_ready, o_scaled, ft_ready):
                    x.open(dve)
                chain = Chain(dve, order)
                chain.fresh()
                dve.wait_ge(loaded, 128)

                def bias(i):
                    ft_copied.wait(dve, i, 1)
                    nc.vector.tensor_tensor(ft[:], ft[:], br[:].unsqueeze(1).to_broadcast((P, GT, D)), ALU.add).then_inc(ft_ready.sem, 1)

                def finish(i):
                    row_norms.wait(dve, i, 1)
                    chain(nc.vector.tensor_scalar_max(node[:, 1, :], node[:, 1, :], MIN_NORM))
                    chain(nc.vector.reciprocal(node[:, 1, :], node[:, 1, :]))
                    chain(nc.vector.scalar_tensor_tensor(node[:, 3, :], node[:, 2, :], MAXNORM, node[:, 1, :], ALU.min, ALU.mult))
                    for t in range(GT):
                        x = k.X[:, i * GT + t, :] if isinstance(i, int) else tile_of(k.X, i * GT + t)
                        last = nc.vector.scalar_tensor_tensor(x, ft[:, t, :], node[:, 3, t:t + 1], x, ALU.mult, ALU.add)
                    chain(last)

                def half(i, j, meanwhile):
                    f = i * 2 + j
                    q_v = ((tmp_u, U[j]), (tmp_v[:], V[j]))
                    summed.wait(dve, f, 1)
                    nc.vector.tensor_scalar(g[:, 0, :], ph[:, 6, 0:HC], ATANH_MAX ** -2, 1.0, ALU.mult, ALU.max).then_inc(bounded.sem, 1)
                    root.wait(dve, f, 1)
                    for x, qv in q_v:
                        last = nc.vector.scalar_tensor_tensor(x, g[:, 1:2, :].to_broadcast((P, 2, HC)), ATT_EPS, qv[:, 2:4], ALU.mult, ALU.add)
                    chain(last)
                    for x, qv in q_v:
                        last = nc.vector.reciprocal(x, x)
                    chain(last)
                    for c in (2, 0):
                        for x, qv in q_v:
                            last = nc.vector.tensor_tensor(x, x, qv[:, c:c + 2], ALU.mult)
                        chain(last)
                    if meanwhile:
                        bias(i - 1)
                    ks_ready.wait(dve, f, 1)
                    nc.vector.tensor_tensor(tmp_u, tmp_u, ks[:, 0:2], ALU.mult)
                    nc.vector.tensor_tensor(tmp_v[:], tmp_v[:], ks[:, 2:4], ALU.mult).then_inc(o_ready.sem, 1)
                    if meanwhile:
                        finish(i - 1)
                    o_root.wait(dve, f, 1)
                    chain(nc.vector.tensor_tensor(g[:, 2, :], g[:, 2, :], g[:, 0, :], ALU.max))
                    chain(nc.vector.reciprocal(g[:, 2, :], g[:, 2, :]))
                    ft_done.wait(dve, i)
                    scale = g[:, 2:3, :].to_broadcast((P, 2, HC))
                    nc.vector.tensor_tensor(O[:, 0:2, j * HC:(j + 1) * HC], tmp_u, scale, ALU.mult)
                    nc.vector.tensor_tensor(O[:, 2:4, j * HC:(j + 1) * HC], tmp_v[:], scale, ALU.mult).then_inc(o_scaled.sem, 1)
                    o_scaled.wait(dve, f, 1)

                def group(i, first=False, last=False):
                    chain.fresh()
                    half(i, 0, not first)
                    half(i, 1, False)
                    if last:
                        bias(i)
                        finish(i)

                groups(dve, group)


def leaky(chain, dve, x, slope):
    chain(dve.scalar_tensor_tensor(x, x, slope, x, ALU.mult, ALU.max))


def gate_phase(nc, k, a, gates):
    with ExitStack() as es:
        s = Scope(nc, es, "gate")
        wg = s.sb("wg", [P, KD, GW])
        att = s.sb("att", [P, 4, GW])
        bg = s.sb("bg", [P, GW])
        hs = s.sb("hs", [P, NT, MW])
        td = s.sb("td", [P, NT, 2 * GH])
        own = s.sb("own", [P, NT, MW])
        ew = s.sb("ew", [P, NT, GW])
        si = s.sb("si", [P, S0 + 2 * U0], I32)
        di = s.sb("di", [P, S0 + 2 * U0], I32)
        lo = s.sb("lo", [P, S0])
        hi = s.sb("hi", [P, S0])
        ti = s.sb("ti", [P, S0], I32)
        small = s.sb("small", [P, 16])
        stable, dtable = k.dram("gate_stable", (NP, MW)), k.dram("gate_dtable", (NP, 2 * GH))
        loaded, order = s.sem("loaded"), s.sem("order")
        tables_ready, stored = s.sem("tables_ready"), s.sem("stored")
        top = s.sem("top")
        es2 = ExitStack()
        with es2:
            s2 = Scope(nc, es2, "gate1")
            xs = s2.sb("xs", [P, KD, GC])
            pg = s2.ps("pg", [P, 3, 512])
            copied, projected, taken = s2.tally("copied", 1), s2.tally("projected", 1), s2.tally("taken", 1)
            logits, exps = s2.sem("logits"), s2.sem("exps")
            with nc.Block() as block:
                @block.sync
                def _(sp):
                    sp.dma_start(wg[:], a["L0_ffn_W_gat"].rearrange("(k p) c -> p k c", p=P)).then_inc(loaded, 16)
                    sp.dma_start(att[:, 0, :], a["L0_ffn_att_src"].rearrange("h e -> (h e)").partition_broadcast(P)).then_inc(loaded, 16)
                    sp.dma_start(att[:, 1, :], a["L0_ffn_att_dst"].rearrange("h e -> (h e)").partition_broadcast(P)).then_inc(loaded, 16)
                    sp.dma_start(att[:, 2, :], a["L0_ffn_ln_gamma"].partition_broadcast(P)).then_inc(loaded, 16)
                    sp.dma_start(att[:, 3, :], a["L0_ffn_ln_beta"].partition_broadcast(P)).then_inc(loaded, 16)
                    sp.dma_start(bg[:], a["L0_ffn_b_gat"].partition_broadcast(P)).then_inc(loaded, 16)
                    sp.dma_start(si[:, 0:S0], a["L0_ffn_edge_index"][0]).then_inc(loaded, 16)
                    sp.dma_start(di[:, 0:S0], a["L0_ffn_edge_index"][1]).then_inc(loaded, 16)
                    sp.wait_ge(loaded, 128)
                    sp.wait_ge(tables_ready, 1)
                    sp.dma_start(stable.rearrange("(t p) c -> p t c", p=P), hs[:]).then_inc(stored, 16)
                    sp.dma_start(dtable.rearrange("(t p) c -> p t c", p=P), td[:]).then_inc(stored, 16)
                    sp.wait_ge(stored, 32)

                @block.scalar
                def _(act):
                    copied.open(act)
                    with act.Fori(0, NG) as i:
                        projected.wait(act, i)
                        nc.scalar.activation(xs[:], k.XT[:, :, bass.ds(i * GC, GC)], ACT.Copy).then_inc(copied.sem, 1)
                    act.wait_ge(logits, 1)
                    nc.scalar.activation(own[:, :, GW:MW], own[:, :, GW:MW], ACT.Exp).then_inc(exps, 1)

                @block.tensor
                def _(pe):
                    projected.open(pe)
                    pe.wait_ge(loaded, 128)
                    with pe.Fori(0, NG) as i:
                        copied.wait(pe, i, 1)
                        taken.wait(pe, i)
                        for t in range(GT):
                            for c in range(KD):
                                last = nc.tensor.matmul(pg[:, 0, t * GW:(t + 1) * GW], xs[:, c, t * P:(t + 1) * P], wg[:, c, :],
                                                        start=c == 0, stop=c == KD - 1)
                        last.then_inc(projected.sem, 1)
                    pe.wait_ge(top, 1)
                    nc.tensor.transpose(pg[0:GH, 1, 0:P], small[:, 0:GH], k.ident[:]).then_inc(top, 1)
                    pe.wait_ge(top, 3)
                    nc.tensor.matmul(pg[:, 2, 0:GH], k.ones[0:GH, :], small[0:GH, 8:8 + GH], start=True, stop=True).then_inc(top, 1)

                @block.vector
                def _(dve):
                    taken.open(dve)
                    chain = Chain(dve, order)
                    dve.wait_ge(loaded, 128)
                    with dve.Fori(0, NG) as i:
                        projected.wait(dve, i, 1)
                        nc.vector.tensor_copy(hs[:, bass.ds(i * GT, GT), 0:GW], pg[:, 0, 0:GT * GW].rearrange("p (t c) -> p t c", c=GW)).then_inc(taken.sem, 1)
                    taken.wait(dve, NG)
                    h = hs[:, :, 0:GW]
                    for side, out in ((0, hs[:, :, GW:MW]), (1, td[:, :, 0:GH])):
                        chain(nc.vector.tensor_tensor(ew[:], h, att[:, side:side + 1, :].to_broadcast((P, NT, GW)), ALU.mult))
                        chain(nc.vector.tensor_reduce(out, ew[:].rearrange("p t (h e) -> p t h e", e=E0), AX.X, ALU.add))
                    chain(nc.vector.tensor_scalar(ew[:, :, 4], k.valid[:], BIG, -BIG, ALU.mult, ALU.add))
                    chain(nc.vector.tensor_tensor(ew[:, :, 0:GH], hs[:, :, GW:MW], ew[:, :, 4:5].to_broadcast((P, NT, GH)), ALU.add))
                    nc.vector.tensor_reduce(small[:, 0:GH], ew[:, :, 0:GH].rearrange("p t h -> p h t"), AX.X, ALU.max).then_inc(top, 1)
                    chain(nc.vector.tensor_single_scalar(ti[:], di[:, 0:S0], 7, ALU.arith_shift_right))
                    chain(nc.vector.tensor_copy(hi[:], ti[:]))
                    chain(nc.vector.tensor_single_scalar(ti[:], di[:, 0:S0], P - 1, ALU.bitwise_and))
                    chain(nc.vector.tensor_copy(lo[:], ti[:]))
                    nc.vector.memset(si[:, S0:], 0)
                    nc.vector.memset(di[:, S0:], 0)
                    chain(nc.vector.tensor_scalar_min(si[:, 0:S0], si[:, 0:S0], N - 1))
                    chain(nc.vector.tensor_scalar_min(di[:, 0:S0], di[:, 0:S0], N - 1))
                    dve.wait_ge(top, 2)
                    chain(nc.vector.tensor_reduce(small[0:GH, 4:5], pg[0:GH, 1, 0:P], AX.X, ALU.max))
                    nc.vector.tensor_scalar(small[0:GH, 8:8 + GH], k.ident[0:GH, 0:GH], small[0:GH, 4:5], None, ALU.mult).then_inc(top, 1)
                    dve.wait_ge(top, 4)
                    shift, e = td[:, :, GH:2 * GH], own[:, :, GW:MW]
                    chain(nc.vector.tensor_copy(small[:, 12:16], pg[:, 2, 0:GH]))
                    chain(nc.vector.tensor_tensor(shift, td[:, :, 0:GH], small[:, 12:16].unsqueeze(1).to_broadcast((P, NT, GH)), ALU.add))
                    leaky(chain, nc.vector, shift, 0.2)
                    dve.sem_inc(tables_ready, 1)
                    chain(nc.vector.tensor_tensor(e, hs[:, :, GW:MW], td[:, :, 0:GH], ALU.add))
                    leaky(chain, nc.vector, e, 0.2)
                    nc.vector.tensor_tensor(e, e, shift, ALU.subtract).then_inc(logits, 1)
                    dve.wait_ge(exps, 1)
                    chain(nc.vector.tensor_tensor(own[:, :, 0:GW].rearrange("p t (h e) -> p t h e", e=E0),
                                                  h.rearrange("p t (h e) -> p t h e", e=E0),
                                                  e.unsqueeze(3).to_broadcast((P, NT, GH, E0)), ALU.mult))

        B0 = (NT // 2 + 1) * MW
        iota_lo = s.sb("iota_lo", [P, P])
        iota_hi = s.sb("iota_hi", [P, NT])
        zero = s.sb("zero", [P, 512])
        sums = s.ps("sums", [P, 2, 512])
        with ExitStack() as es2:
            s2 = Scope(nc, es2, "gate2")
            idx = s2.sb("idx", [P, 2, 2, U0], I32)
            gs = s2.sb("gs", [P, 2, U0, MW])
            gd = s2.sb("gd", [P, 2, U0, 2 * GH])
            msg = s2.sb("msg", [P, U0, MW])
            hot = s2.sb("hot", [P, U0, NT])
            pick = s2.sb("pick", [P, 2, 4, P])
            wide = s2.sb("wide", [P, 2, 4, NT * MW])
            made = s2.sem("made")
            indexed = s2.tally("indexed", 2)
            gathered = [s2.pool_dma_tally(f"gathered{b}", 32 * U0) for b in range(2)]
            logits, exps = s2.tally("logits", 2), s2.tally("exps", 2)
            expanded, summed = s2.tally("expanded", 4), s2.tally("summed", 4)
            with nc.Block() as block:
                @block.gpsimd
                def _(pool):
                    nc.gpsimd.memset(zero[:], 0.0).then_inc(made, 1)
                    nc.gpsimd.iota(iota_lo[:], pattern=[[1, P]], base=0, channel_multiplier=0, allow_small_or_imprecise_dtypes=True).then_inc(made, 1)
                    nc.gpsimd.iota(iota_hi[:], pattern=[[1, NT]], base=0, channel_multiplier=0, allow_small_or_imprecise_dtypes=True).then_inc(made, 1)
                    with pool.Fori(0, S0 // (2 * U0)) as i:
                        for b in range(2):
                            indexed.hold(pool, i, b + 1)
                            for u in range(U0):
                                nc.gpsimd.indirect_dma_start(gs[:, b, u, :], None, stable, bass.IndirectOffsetOnAxis(ap=idx[:, 0, b, u:u + 1], axis=0)).then_inc(gathered[b].sem, 16)
                                nc.gpsimd.indirect_dma_start(gd[:, b, u, :], None, dtable, bass.IndirectOffsetOnAxis(ap=idx[:, 1, b, u:u + 1], axis=0)).then_inc(gathered[b].sem, 16)

                @block.scalar
                def _(act):
                    exps.open(act)
                    with act.Fori(0, S0 // (2 * U0)) as i:
                        for b in range(2):
                            logits.wait(act, i, b + 1)
                            nc.scalar.activation(msg[:, :, GW:MW], msg[:, :, GW:MW], ACT.Exp).then_inc(exps.sem, 1)

                @block.vector
                def _(dve):
                    for x in (indexed, logits, expanded):
                        x.open(dve)
                    dve.wait_ge(made, 3)
                    chain = Chain(dve, order)
                    chain.fresh()

                    def index(step, b):
                        nc.vector.tensor_copy(idx[:, 0, b, :], si[:, bass.ds(step, U0)])
                        nc.vector.tensor_copy(idx[:, 1, b, :], di[:, bass.ds(step, U0)]).then_inc(indexed.sem, 1)

                    index(0, 0)
                    index(U0, 1)
                    with dve.Fori(0, S0 // (2 * U0)) as i:
                        chain.fresh()
                        for b in range(2):
                            step = i * (2 * U0) + b * U0
                            gathered[b].wait(dve, i, 32 * U0)
                            e = msg[:, :, GW:MW]
                            chain(nc.vector.tensor_tensor(e, gs[:, b, :, GW:MW], gd[:, b, :, 0:GH], ALU.add))
                            leaky(chain, nc.vector, e, 0.2)
                            nc.vector.tensor_tensor(e, e, gd[:, b, :, GH:2 * GH], ALU.subtract).then_inc(logits.sem, 1)
                            chain(nc.vector.tensor_tensor(hot[:], iota_hi[:].unsqueeze(1).to_broadcast((P, U0, NT)),
                                                          hi[:, bass.ds(step, U0)].unsqueeze(2).to_broadcast((P, U0, NT)), ALU.is_equal))
                            exps.wait(dve, i, b + 1)
                            chain(nc.vector.tensor_tensor(msg[:, :, 0:GW].rearrange("p u (h e) -> p u h e", e=E0),
                                                          gs[:, b, :, 0:GW].rearrange("p u (h e) -> p u h e", e=E0),
                                                          e.unsqueeze(3).to_broadcast((P, U0, GH, E0)), ALU.mult))
                            nc.vector.tensor_copy(idx[:, 0, b, :], si[:, bass.ds((i * (2 * U0) + (b + 2) * U0), U0)])
                            nc.vector.tensor_copy(idx[:, 1, b, :], di[:, bass.ds((i * (2 * U0) + (b + 2) * U0), U0)]).then_inc(indexed.sem, 1)
                            for q in range(2):
                                summed.wait(dve, i, 2 * b + q - 1)
                                u0 = 4 * q
                                nc.vector.tensor_tensor(pick[:, q], iota_lo[:].unsqueeze(1).to_broadcast((P, 4, P)),
                                                        lo[:, bass.ds(step + u0, 4)].unsqueeze(2).to_broadcast((P, 4, P)), ALU.is_equal)
                                nc.vector.tensor_tensor(wide[:, q].rearrange("p u (n c) -> p u n c", c=MW),
                                                        hot[:, u0:u0 + 4, :].unsqueeze(3).to_broadcast((P, 4, NT, MW)),
                                                        msg[:, u0:u0 + 4, :].unsqueeze(2).to_broadcast((P, 4, NT, MW)), ALU.mult).then_inc(expanded.sem, 1)
                            expanded.wait(dve, i, 2 * b + 2)

                @block.tensor
                def _(pe):
                    summed.open(pe)
                    pe.wait_ge(made, 3)
                    for c, w in ((0, B0), (1, NT * MW - B0)):
                        nc.tensor.matmul(sums[:, c, 0:w], zero[:, 0:P], zero[:, 0:w], start=True, stop=False)
                    with pe.Fori(0, S0 // (2 * U0)) as i:
                        for j in range(4):
                            expanded.wait(pe, i, j + 1)
                            for u in range(4):
                                nc.tensor.matmul(sums[:, 0, 0:B0], pick[:, j % 2, u, :], wide[:, j % 2, u, 0:B0], start=False, stop=False)
                                last = nc.tensor.matmul(sums[:, 1, 0:NT * MW - B0], pick[:, j % 2, u, :], wide[:, j % 2, u, B0:], start=False, stop=False)
                            last.then_inc(summed.sem, 1)
                    for c, w in ((0, B0), (1, NT * MW - B0)):
                        nc.tensor.matmul(sums[:, c, 0:w], zero[:, 0:P], zero[:, 0:w], start=False, stop=True)

        with ExitStack() as es2:
            s2 = Scope(nc, es2, "gate3")
            agg = s2.sb("agg", [P, NT, GW])
            t4 = s2.sb("t4", [P, 6, NT, E0])
            t1 = s2.sb("t1", [P, 3, NT])
            steps, asteps = s2.sem("steps"), s2.sem("asteps")
            with nc.Block() as block:
                @block.vector
                def _(dve):
                    chain = Chain(dve, order)
                    chain.fresh()

                    def over(x, w):
                        return x.unsqueeze(2).to_broadcast((P, NT, w))

                    n0 = B0 // MW
                    nc.vector.tensor_tensor(own[:, 0:n0, :], own[:, 0:n0, :], sums[:, 0, 0:B0].rearrange("p (t c) -> p t c", c=MW), ALU.add)
                    chain(nc.vector.tensor_tensor(own[:, n0:, :], own[:, n0:, :], sums[:, 1, 0:NT * MW - B0].rearrange("p (t c) -> p t c", c=MW), ALU.add))
                    chain(nc.vector.reciprocal(own[:, :, GW:MW], own[:, :, GW:MW]))
                    chain(nc.vector.tensor_tensor(agg[:].rearrange("p t (h e) -> p t h e", e=E0),
                                                  own[:, :, 0:GW].rearrange("p t (h e) -> p t h e", e=E0),
                                                  own[:, :, GW:MW].unsqueeze(3).to_broadcast((P, NT, GH, E0)), ALU.mult))
                    chain(nc.vector.tensor_tensor(agg[:], agg[:], bg[:].unsqueeze(1).to_broadcast((P, NT, GW)), ALU.add))
                    mean, var, r = (t1[:, j, :] for j in range(3))
                    chain(nc.vector.tensor_reduce(mean, agg[:], AX.X, ALU.add))
                    chain(nc.vector.tensor_scalar(mean, mean, 1.0 / GW, None, ALU.mult))
                    chain(nc.vector.tensor_tensor(agg[:], agg[:], over(mean, GW), ALU.subtract))
                    chain(nc.vector.tensor_tensor(ew[:], agg[:], agg[:], ALU.mult))
                    chain(nc.vector.tensor_reduce(var, ew[:], AX.X, ALU.add))
                    nc.vector.tensor_scalar(var, var, 1.0 / GW, None, ALU.mult).then_inc(steps, 1)
                    dve.wait_ge(asteps, 1)
                    chain(nc.vector.reciprocal(r, r))
                    chain(nc.vector.tensor_tensor(agg[:], agg[:], over(r, GW), ALU.mult))
                    chain(nc.vector.tensor_tensor(agg[:], agg[:], att[:, 2:3, :].to_broadcast((P, NT, GW)), ALU.mult))
                    chain(nc.vector.tensor_tensor(agg[:], agg[:], att[:, 3:4, :].to_broadcast((P, NT, GW)), ALU.add))
                    score, rank, ge, ex = (t4[:, j] for j in range(4))
                    chain(nc.vector.tensor_reduce(score, agg[:].rearrange("p t (h e) -> p t e h", e=E0), AX.X, ALU.add))
                    chain(nc.vector.tensor_scalar(score, score, 1.0 / GH, None, ALU.mult))
                    chain(nc.vector.memset(rank, 0.0))
                    for e in range(E0):
                        for o in range(E0):
                            if o != e:
                                chain(nc.vector.tensor_tensor(ge[:, :, 0], score[:, :, o], score[:, :, e], ALU.is_ge if o < e else ALU.is_gt))
                                chain(nc.vector.tensor_tensor(rank[:, :, e], rank[:, :, e], ge[:, :, 0], ALU.add))
                    chain(nc.vector.tensor_scalar(rank, rank, 1.5, None, ALU.is_lt))
                    chain(nc.vector.tensor_reduce(mean, score, AX.X, ALU.max))
                    nc.vector.tensor_tensor(ex, score, over(mean, E0), ALU.subtract).then_inc(steps, 1)
                    dve.wait_ge(asteps, 2)
                    chain(nc.vector.tensor_tensor(ex, ex, rank, ALU.mult))
                    chain(nc.vector.tensor_reduce(var, ex, AX.X, ALU.add))
                    chain(nc.vector.reciprocal(var, var))
                    chain(nc.vector.tensor_tensor(gates[:], ex, over(var, E0), ALU.mult))

                @block.scalar
                def _(act):
                    act.wait_ge(steps, 1)
                    nc.scalar.activation(t1[:, 2, :], t1[:, 1, :], ACT.Sqrt, bias=k.eps[:, 0:1]).then_inc(asteps, 1)
                    act.wait_ge(steps, 2)
                    nc.scalar.activation(t4[:, 3], t4[:, 3], ACT.Exp).then_inc(asteps, 1)


def experts_phase(nc, k, name, w1d, b1d, w2d, b2d, parts, gate, dst):
    FC = F0 // P
    with ExitStack() as es:
        s = Scope(nc, es, name)
        w1 = s.sb("w1", [P, parts, KD, F0])
        w2 = s.sb("w2", [P, parts, FC, D])
        b1 = s.sb("b1", [P, parts, FC])
        b2 = s.sb("b2", [1, parts, D])
        hid = s.sb("hid", [P, 2, FC, GC])
        ph = s.ps("ph", [P, FC, 512])
        py = s.ps("py", [P, 8, D])
        loaded = s.sem("loaded")
        h_done, gelus = s.tally("h_done", parts * 2 * FC), s.tally("gelus", parts * 2 * FC)
        y_done, added = s.tally("y_done", parts), s.tally("added", parts)
        with nc.Block() as block:
            @block.sync
            def _(sp):
                for e in range(parts):
                    sp.dma_start(w1[:, e], w1d[e].rearrange("(k p) f -> p k f", p=P)).then_inc(loaded, 16)
                    sp.dma_start(w2[:, e], w2d[e].rearrange("(k p) f -> p k f", p=P)).then_inc(loaded, 16)
                sp.dma_start(b1[:], b1d.rearrange("e (f p) -> p e f", p=P), allow_slow_non_contiguous=True).then_inc(loaded, 16)
                sp.dma_start(b2[:], b2d.rearrange("(o e) d -> o e d", o=1)).then_inc(loaded, 16)
                sp.wait_ge(loaded, 32 * parts + 32)

            @block.tensor
            def _(pe):
                h_done.open(pe)
                y_done.open(pe)
                pe.wait_ge(loaded, 32 * parts + 32)
                with pe.Fori(0, NG) as i:
                    def hidden(e):
                        for j in range(2):
                            for f in range(FC):
                                gelus.wait(pe, i, max((e * 2 + j - 1) * FC + f + 1, 0))
                                for c in range(KD):
                                    last = nc.tensor.matmul(ph[:, f, 0:HC], w1[:, e, c, f * P:(f + 1) * P],
                                                            k.XT[:, c, bass.ds(i * GC + j * HC, HC)], start=c == 0, stop=c == KD - 1)
                                last.then_inc(h_done.sem, 1)

                    def down(e):
                        gelus.wait(pe, i, (e + 1) * 2 * FC)
                        added.wait(pe, i, e)
                        for t in range(GT):
                            nc.tensor.matmul(py[:, t, :], k.ones[0:1, :], b2[0:1, e, :], start=True, stop=False)
                            for f in range(FC):
                                last = nc.tensor.matmul(py[:, t, :], hid[:, e % 2, f, t * P:(t + 1) * P], w2[:, e, f, :],
                                                        start=False, stop=f == FC - 1)
                        last.then_inc(y_done.sem, 1)

                    hidden(0)
                    for e in range(1, parts):
                        hidden(e)
                        down(e - 1)
                    down(parts - 1)

            @block.scalar
            def _(act):
                gelus.open(act)
                act.wait_ge(loaded, 32 * parts + 32)
                with act.Fori(0, NG) as i:
                    for e in range(parts):
                        y_done.wait(act, i, max(e - 1, 0))
                        for j in range(2):
                            for f in range(FC):
                                h_done.wait(act, i, (e * 2 + j) * FC + f + 1)
                                nc.scalar.activation(hid[:, e % 2, f, j * HC:(j + 1) * HC], ph[:, f, 0:HC], ACT.Gelu,
                                                     bias=b1[:, e, f:f + 1]).then_inc(gelus.sem, 1)

            @block.vector
            def _(dve):
                added.open(dve)
                with dve.Fori(0, NG) as i:
                    for e in range(parts):
                        y_done.wait(dve, i, e + 1)
                        for t in range(GT):
                            x = tile_of(dst, i * GT + t)
                            last = nc.vector.scalar_tensor_tensor(x, py[:, t, :], gate(e, i * GT + t), x, ALU.mult, ALU.add)
                        last.then_inc(added.sem, 1)
                        added.wait(dve, i, e + 1)


def tables_phase(nc, k, a, qtable, ktable, atable):
    KW = D + H1 * VW
    with ExitStack() as es:
        s = Scope(nc, es, "tab")
        w = s.sb("w", [P, KD, 3 * D])
        b = s.sb("b", [P, 3 * D])
        be = s.sb("be", [P, D1])
        xs = s.sb("xs", [P, KD, GC])
        qrow = s.sb("qrow", [P, D])
        krow = s.sb("krow", [P, KW])
        blank = s.sb("blank", [P, AW])
        pr = s.ps("pr", [P, 2, 1024])
        loaded, order, made = s.sem("loaded"), s.sem("order"), s.sem("made")
        copied = s.tally("copied", 1)
        projected, rows_ready = s.tally("projected", GT), s.tally("rows_ready", GT)
        stored = s.tally("stored", 48 * GT)
        with nc.Block() as block:
            @block.gpsimd
            def _(pool):
                nc.gpsimd.memset(blank[:, 0:H1 * VW], 0.0)
                nc.gpsimd.memset(blank[:, H1 * VW:], -BIG)
                nc.gpsimd.memset(krow[:], 1.0).then_inc(made, 1)

            @block.sync
            def _(sp):
                for j, n in enumerate("qkv"):
                    sp.dma_start(w[:, :, j * D:(j + 1) * D], a[f"L1_gnn_W{n}"].rearrange("(k p) c -> p k c", p=P)).then_inc(loaded, 16)
                    sp.dma_start(b[:, j * D:(j + 1) * D], a[f"L1_gnn_b{n}"].partition_broadcast(P)).then_inc(loaded, 16)
                sp.dma_start(be[:], a["L1_gnn_be"].partition_broadcast(P)).then_inc(loaded, 16)
                sp.wait_ge(loaded, 112)
                sp.wait_ge(made, 1)
                stored.open(sp)
                with sp.Fori(0, NG) as i:
                    for t in range(GT):
                        rows_ready.hold(sp, i, t + 1)
                        sp.dma_start(qtable[bass.ds(i * GC + t * P, P), :], qrow[:]).then_inc(stored.sem, 16)
                        sp.dma_start(ktable[bass.ds(i * GC + t * P, P), :], krow[:]).then_inc(stored.sem, 16)
                        sp.dma_start(atable[bass.ds(i * GC + t * P, P), :], blank[:]).then_inc(stored.sem, 16)
                        stored.hold(sp, i, 48 * (t + 1))

            @block.scalar
            def _(act):
                copied.open(act)
                with act.Fori(0, NG) as i:
                    projected.wait(act, i)
                    nc.scalar.activation(xs[:], k.XT[:, :, bass.ds(i * GC, GC)], ACT.Copy).then_inc(copied.sem, 1)

            @block.tensor
            def _(pe):
                projected.open(pe)
                pe.wait_ge(loaded, 112)
                with pe.Fori(0, NG) as i:
                    copied.wait(pe, i, 1)
                    for t in range(GT):
                        rows_ready.wait(pe, i, max(t - 1, 0))
                        for n0, n1 in ((0, 512), (512, 3 * D)):
                            for c in range(KD):
                                last = nc.tensor.matmul(pr[:, t % 2, n0:n1], xs[:, c, t * P:(t + 1) * P], w[:, c, n0:n1],
                                                        start=c == 0, stop=c == KD - 1)
                        last.then_inc(projected.sem, 1)

            @block.vector
            def _(dve):
                rows_ready.open(dve)
                dve.wait_ge(loaded, 112)
                dve.wait_ge(made, 1)
                chain = Chain(dve, order)
                chain(nc.vector.tensor_tensor(b[:, D:2 * D].rearrange("p (h c) -> p h c", h=H1), b[:, D:2 * D].rearrange("p (h c) -> p h c", h=H1),
                                              be[:].unsqueeze(1).to_broadcast((P, H1, D1)), ALU.add))
                with dve.Fori(0, NG) as i:
                    for t in range(GT):
                        projected.wait(dve, i, t + 1)
                        stored.wait(dve, i, 48 * t)
                        nc.vector.tensor_tensor(qrow[:], pr[:, t % 2, 0:D], b[:, 0:D], ALU.add)
                        nc.vector.tensor_tensor(krow[:, 0:D], pr[:, t % 2, D:2 * D], b[:, D:2 * D], ALU.add)
                        nc.vector.tensor_tensor(krow[:, D:].rearrange("p (h c) -> p h c", c=VW)[:, :, 0:D1],
                                                pr[:, t % 2, 2 * D:3 * D].rearrange("p (h c) -> p h c", c=D1),
                                                b[:, 2 * D:].rearrange("p (h c) -> p h c", c=D1), ALU.add).then_inc(rows_ready.sem, 1)


def edges_and_linear_phase(nc, k, a, qtable, ktable, atable, xtable, dst):
    KW = D + H1 * VW
    HALF = U1 // 2
    HS, SW = HALF // W, S1 // W
    VS = H1 * VW
    NOWHERE = 1 << 20
    NPASS = S1 // U1
    MID = NPASS // 2
    assert MID == 2 * NT
    scale = float(D1) ** 0.25
    NCH = (PD - 1) * D1 // P
    Q4 = H1 // 4
    NB = H1 + 1
    with ExitStack() as es:
        s = Scope(nc, es, "edge")
        flat = k.XT[:].rearrange("p k n -> p (k n)")
        kv = flat[:, 0:2 * HALF * KW].rearrange("p (b u c) -> p b u c", b=2, c=KW)
        o = 2 * HALF * KW
        df, free = (flat[:, j * S1:(j + 1) * S1].rearrange("p (w s) -> p w s", w=W) for j in range(2))
        q = flat[:, o:o + 2 * HALF * D].rearrange("p (b u c) -> p b u c", b=2, c=D)
        o += 2 * HALF * D
        hist = flat[:, o:o + 4 * HALF * AW].rearrange("p (b u c) -> p b u c", b=4, c=AW)
        o += 4 * HALF * AW
        prod = flat[:, o:o + HALF * D].rearrange("p (u c) -> p u c", c=D)
        o += HALF * D
        assert o <= KD * NP
        si = s.sb("si", [P, W, SW + HALF], I32)
        di = s.sb("di", [P, W, SW + HALF], I32)
        ends = s.sb("ends", [P, W, SW], I32)
        reset = s.sb("reset", [P, W, SW])
        ew = s.sb("ew", [P, W, SW])
        last_dst = s.sb("last_dst", [P, W])
        we = s.sb("we", [ED, D1])
        attr = s.sb("attr", [ED, 2, HALF, P])
        idx = s.sb("idx", [P, 2, 2, HALF], I32)
        eidx = s.sb("eidx", [P, 4, HALF], I32)
        sc = s.sb("sc", [P, HALF, H1])
        ex = s.sb("ex", [P, 2, HALF, H1])
        tmp = s.sb("tmp", [P, W, VS])
        loaded, order, ready, made = s.sem("loaded"), s.sem("order"), s.sem("ready"), s.sem("made")
        indexed = s.tally("indexed", 2)
        gathered = [s.pool_dma_tally(f"gathered{b}", 32 * HALF) for b in range(2)]
        scattered = [s.pool_dma_tally(f"scattered{j}", 16 * HALF) for j in range(4)]
        features = [s.tally(f"features{b}", 16) for b in range(2)]
        projected, logits = s.tally("projected", 2), s.tally("logits", 2)
        shifted, exps, summed = s.tally("shifted", 2), s.tally("exps", 2), s.tally("summed", 2)

        eq = ExitStack()
        es.enter_context(eq)
        sl = Scope(nc, eq, "lin")
        w = sl.sb("w", [P, KD, 3 * D])
        bias = sl.sb("bias", [P, 3 * D])
        wp = sl.sb("wp", [P, KD, D])
        bp = sl.sb("bp", [P, D])
        temp = sl.sb("temp", [P, H1])
        blk = sl.sb("blk", [P, 4, VW])
        coef = sl.sb("coef", [P, 1])
        xs = sl.sb("xs", [P, KD, P])
        row = sl.sb("row", [P, 2 * D])
        sqr = sl.sb("sqr", [P, D])
        nrm = sl.sb("nrm", [P, 3, H1])
        twice = sl.sb("twice", [P, H1, 2 * D1])
        feat = sl.sb("feat", [P, H1, (PD - 1) * D1])
        last_d = sl.sb("last_d", [P, H1 * D1])
        once = sl.sb("once", [P, H1 * D1])
        v1 = sl.sb("v1", [P, VS])
        S = sl.sb("S", [P, H1, NCH, VW])
        Sl = sl.sb("Sl", [P, 2, Q4, 4, VW])
        Sf = sl.sb("Sf", [P, VS])
        xs_loaded = sl.tally("xs_loaded", 16)
        pe_ = s.ps("ep", [P, 512])
        H_A = 3

        def normalise(chain, x, factor):
            f3 = x.rearrange("p (h c) -> p h c", c=D1)
            chain(nc.vector.tensor_tensor(twice[:, :, 0:D1], f3, factor, ALU.mult))
            nc.vector.tensor_copy(twice[:, :, D1:], twice[:, :, 0:D1])
            chain(nc.vector.tensor_copy(once[:].rearrange("p (h c) -> p h c", c=D1), twice[:, :, 0:D1]))
            nc.vector.tensor_tensor(last_d[:].rearrange("p (h c) -> p h c", c=D1), twice[:, :, 0:D1], twice[:, :, D1 // 2:D1 // 2 + D1], ALU.mult)

        def pair_features(h0, h1):
            window = bass.AP(tensor=twice[:].tensor, offset=twice[:].offset + h0 * 2 * D1,
                             ap=[list(twice[:].ap[0]), [2 * D1, h1 - h0], [1, PD - 1], [1, D1]])
            return nc.vector.tensor_tensor(feat[:, h0:h1].rearrange("p h (d c) -> p h d c", c=D1),
                                           twice[:, h0:h1, 0:D1].unsqueeze(2).to_broadcast((P, h1 - h0, PD - 1, D1)), window, ALU.mult)


        def load_features(sp, first):
            with sp.Fori(first, first + MID) as i:
                for b in range(2):
                    projected.hold(sp, i, b)
                    if b == 0:
                        features[0].hold(sp, i)
                    sp.dma_start(attr[:, b].rearrange("e (w u) p -> e w u p", w=W),
                                 a["edge_attr"].rearrange("e (w s) p -> e w s p", w=W)[:, :, bass.ds(i * (2 * HS) + b * HS, HS), :]).then_inc(features[b].sem, 16)

        def project_features(pe, i, b):
            features[b].wait(pe, i, 16)
            logits.wait(pe, i, b)
            for u in range(HALF):
                last = nc.tensor.matmul(pe_[:, (b * HALF + u) * D1:(b * HALF + u + 1) * D1], attr[:, b, u, :], we[:], start=True, stop=True)
            last.then_inc(projected.sem, 1)

        def gathers(b):
            for u in range(HALF):
                nc.gpsimd.indirect_dma_start(kv[:, b, u, :], None, ktable, bass.IndirectOffsetOnAxis(ap=idx[:, 0, b, u:u + 1], axis=0)).then_inc(gathered[b].sem, 16)
                nc.gpsimd.indirect_dma_start(q[:, b, u, :], None, qtable, bass.IndirectOffsetOnAxis(ap=idx[:, 1, b, u:u + 1], axis=0)).then_inc(gathered[b].sem, 16)

        def scatters(j):
            for u in range(HALF):
                nc.gpsimd.indirect_dma_start(atable, bass.IndirectOffsetOnAxis(ap=eidx[:, j, u:u + 1], axis=0), hist[:, j, u, :], None,
                                             bounds_check=NP - 1, oob_is_err=False).then_inc(scattered[j].sem, 16)

        def move_rows(pool, first):
            with pool.Fori(0, NT) as i:
                for j in range(4):
                    i2, b = i * 2 + (first + j // 2), j % 2
                    indexed.hold(pool, i2, b + 2)
                    gathers(1 - b)
                    summed.hold(pool, i2, b)
                    scatters((j - 1) % 4)

        def exponentials(act, i, b):
            shifted.wait(act, i, b + 1)
            nc.scalar.activation(ex[:], ex[:], ACT.Exp).then_inc(exps.sem, 1)

        def edge_set(dve, chain, tile, j):
            i, b = tile * 2 + j // 2, j % 2
            step = i * (2 * HS) + b * HS

            def by_walk(x):
                return x.rearrange("p (w u) -> p w u", w=W)

            states, last_states = (hist[:, n].rearrange("p (w u) c -> p w u c", w=W) for n in (j, (j - 1) % 4))
            gathered[b].wait(dve, i, 32 * HALF)
            projected.wait(dve, i, b + 1)
            p4 = prod.rearrange("p u (h c) -> p u h c", c=D1)
            chain(nc.vector.tensor_tensor(p4, kv[:, b, :, 0:D].rearrange("p u (h c) -> p u h c", c=D1),
                                          pe_[:, b * HALF * D1:(b + 1) * HALF * D1].rearrange("p (u c) -> p u c", c=D1).unsqueeze(2).to_broadcast((P, HALF, H1, D1)), ALU.add))
            dve.sem_inc(logits.sem, 1)
            chain(nc.vector.tensor_tensor(prod, prod, q[:, b], ALU.mult))
            chain(nc.vector.tensor_reduce(sc[:], p4, AX.X, ALU.add))
            sc4, keep = (x.rearrange("p (w u) h -> p w u h", w=W) for x in (sc[:], ex[:, 0]))
            chain(nc.vector.tensor_tensor(sc4, sc4, ew[:, :, bass.ds(step, HS)].unsqueeze(3).to_broadcast((P, W, HS, H1)), ALU.mult))
            scattered[j].wait(dve, tile, 16 * HALF)
            for u in range(HS):
                before = states[:, :, u - 1, VS:] if u else last_states[:, :, HS - 1, VS:]
                r = reset[:, :, bass.ds(step + u, 1)].to_broadcast((P, W, H1))
                chain(nc.vector.tensor_tensor(keep[:, :, u, :], before, r, ALU.add))
                chain(nc.vector.tensor_tensor(states[:, :, u, VS:], keep[:, :, u, :], sc4[:, :, u, :], ALU.max))
            nc.vector.tensor_tensor(ex[:, 0], ex[:, 0], hist[:, j, :, VS:], ALU.subtract)
            nc.vector.tensor_tensor(ex[:, 1], sc[:], hist[:, j, :, VS:], ALU.subtract).then_inc(shifted.sem, 1)
            nc.vector.tensor_copy(by_walk(eidx[:, j, :]), ends[:, :, bass.ds(step, HS)])
            exps.wait(dve, i, b + 1)
            chain(nc.vector.tensor_tensor(hist[:, j, :, 0:VS].rearrange("p u (h c) -> p u h c", c=VW),
                                          kv[:, b, :, D:].rearrange("p u (h c) -> p u h c", c=VW),
                                          ex[:, 1].unsqueeze(3).to_broadcast((P, HALF, H1, VW)), ALU.mult))
            nc.vector.tensor_copy(by_walk(idx[:, 0, b, :]), si[:, :, bass.ds(step + 2 * HS, HS)])
            nc.vector.tensor_copy(by_walk(idx[:, 1, b, :]), di[:, :, bass.ds(step + 2 * HS, HS)]).then_inc(indexed.sem, 1)
            for u in range(HS):
                before = states[:, :, u - 1, 0:VS] if u else last_states[:, :, HS - 1, 0:VS]
                now = states[:, :, u, 0:VS]
                chain(nc.vector.tensor_tensor(tmp[:].rearrange("p w (h c) -> p w h c", c=VW), before.rearrange("p w (h c) -> p w h c", c=VW),
                                              keep[:, :, u, :].unsqueeze(3).to_broadcast((P, W, H1, VW)), ALU.mult))
                chain(nc.vector.tensor_tensor(now, now, tmp[:], ALU.add))
            dve.sem_inc(summed.sem, 1)

        es2 = ExitStack()
        with es2:
            s2 = Scope(nc, es2, "kv")
            pk = s2.ps("pk", [P, 512])
            pS = s2.ps("pS", [P, 3, 512])
            pL = s2.ps("pL", [P, 2, 512])
            pF = s2.ps("pF", [P, 512])
            k_done, norms, roots, sums_done = (s2.tally(n, 1) for n in ("k_done", "norms", "roots", "sums_done"))
            pairs = s2.tally("pairs", 2)
            zero = feat[:].rearrange("p h c -> p (h c)")
            banks = [pS[:, 0], pS[:, 1], pS[:, 2], pL[:, 0], pL[:, 1], pF[:]]
            with nc.Block() as block:
                @block.sync
                def _(sp):
                    sp.dma_start(si[:, :, 0:SW], a["edge_src"].rearrange("p (w s) -> p w s", w=W)).then_inc(loaded, 16)
                    sp.dma_start(di[:, :, 0:SW], a["edge_dst"].rearrange("p (w s) -> p w s", w=W)).then_inc(loaded, 16)
                    sp.dma_start(ew[:], a["edge_weight"].rearrange("p (w s) -> p w s", w=W)).then_inc(loaded, 16)
                    sp.dma_start(we[:], a["L1_gnn_We"]).then_inc(loaded, 16)
                    sp.dma_start(w[:], a["lin_w"].rearrange("(k p) c -> p k c", p=P)).then_inc(loaded, 16)
                    sp.dma_start(bias[:], a["L1_mix_bqkv"].partition_broadcast(P)).then_inc(loaded, 16)
                    sp.dma_start(wp[:], a["lin_wp"].rearrange("(k p) c -> p k c", p=P)).then_inc(loaded, 16)
                    sp.dma_start(bp[:], a["L1_mix_bproj"].partition_broadcast(P)).then_inc(loaded, 16)
                    sp.dma_start(temp[:], a["lin_temp"].partition_broadcast(P)).then_inc(loaded, 16)
                    sp.wait_ge(loaded, 144)
                    for f in features:
                        f.open(sp)
                    load_features(sp, 0)

                @block.tensor
                def _(pe):
                    for x in (projected, k_done, sums_done):
                        x.open(pe)
                    pe.wait_ge(loaded, 144)
                    pe.wait_ge(made, 1)
                    for bank in banks:
                        nc.tensor.matmul(bank, zero[:, 0:P], zero[:, 0:512], start=True, stop=False)

                    def project_row(i):
                        xs_loaded.wait(pe, i, 16)
                        norms.wait(pe, i)
                        for c in range(KD):
                            last = nc.tensor.matmul(pk[:], xs[:, c, :], w[:, c, D:3 * D], start=c == 0, stop=c == KD - 1)
                        last.then_inc(k_done.sem, 1)

                    def sum_pairs(h):
                        for c in range(NCH):
                            o = (h % 3) * NCH * VW + c * VW
                            nc.tensor.matmul(pS[:, h // 3, o:o + VW], feat[:, h, c * P:(c + 1) * P], v1[:, h * VW:(h + 1) * VW], start=False, stop=False)

                    project_row(0)
                    with pe.Fori(0, NT) as i:
                        project_features(pe, i * 2, 0)
                        project_features(pe, i * 2, 1)
                        project_row(i + 1)
                        project_features(pe, i * 2 + 1, 0)
                        pairs.wait(pe, i, 1)
                        for h in range(H_A):
                            sum_pairs(h)
                        for g in range(Q4):
                            vg = v1[:, 4 * g * VW:4 * (g + 1) * VW]
                            nc.tensor.matmul(pL[:, 0, 4 * g * VW:4 * (g + 1) * VW], once[:, g * P:(g + 1) * P], vg, start=False, stop=False)
                            nc.tensor.matmul(pL[:, 1, 4 * g * VW:4 * (g + 1) * VW], last_d[:, g * P:(g + 1) * P], vg, start=False, stop=False)
                        project_features(pe, i * 2 + 1, 1)
                        pairs.wait(pe, i, 2)
                        for h in range(H_A, H1):
                            sum_pairs(h)
                        nc.tensor.matmul(pF[:, 0:VS], k.ones[:], v1[:], start=False, stop=False).then_inc(sums_done.sem, 1)
                    pe.wait_ge(made, 7)
                    for bank in banks:
                        last = nc.tensor.matmul(bank, zero[:, 0:P], zero[:, 0:512], start=False, stop=True)
                    last.then_inc(made, 1)

                @block.gpsimd
                def _(pool):
                    nc.gpsimd.memset(feat[:], 0.0).then_inc(made, 1)
                    nc.gpsimd.memset(blk[:], 1.0).then_inc(made, 1)
                    nc.gpsimd.memset(coef[:], 1.0).then_inc(made, 1)
                    pool.wait_ge(made, 3)
                    nc.gpsimd.affine_select(out=blk[:], in_=blk[:], compare_op=ALU.is_ge, fill=0.0, base=0,
                                            pattern=[[-D1, 4], [0, VW]], channel_multiplier=1).then_inc(made, 1)
                    pool.wait_ge(made, 4)
                    nc.gpsimd.affine_select(out=blk[:], in_=blk[:], compare_op=ALU.is_ge, fill=0.0, base=D1 - 1,
                                            pattern=[[D1, 4], [0, VW]], channel_multiplier=-1).then_inc(made, 1)
                    nc.gpsimd.affine_select(out=coef[:], in_=coef[:], compare_op=ALU.is_ge, fill=0.5, base=-D1,
                                            pattern=[[0, 1]], channel_multiplier=1).then_inc(made, 1)
                    pool.wait_ge(ready, 1)
                    for j in range(3):
                        scatters(j)
                    indexed.hold(pool, 0, 1)
                    gathers(0)
                    move_rows(pool, 0)

                @block.scalar
                def _(act):
                    for x in (exps, roots, xs_loaded):
                        x.open(act)
                    act.dma_start(xs[:], xtable[0]).then_inc(xs_loaded.sem, 16)
                    with act.Fori(0, NT) as i:
                        k_done.hold(act, i, 1)
                        act.dma_start(xs[:], xtable[bass.ds(i + 1, 1)].rearrange("o p k n -> p (o k) n")).then_inc(xs_loaded.sem, 16)
                        norms.wait(act, i, 1)
                        nc.scalar.activation(nrm[:, 1, :], nrm[:, 0, :], ACT.Sqrt).then_inc(roots.sem, 1)
                        exponentials(act, i * 2, 0)
                        exponentials(act, i * 2, 1)
                        exponentials(act, i * 2 + 1, 0)
                        exponentials(act, i * 2 + 1, 1)
                    xs_loaded.wait(act, NT, 16)

                @block.vector
                def _(dve):
                    for x in (indexed, logits, shifted, summed, norms, pairs):
                        x.open(dve)
                    chain = Chain(dve, order)
                    chain(nc.vector.memset(eidx[:], NOWHERE))
                    nc.vector.memset(hist[:, :, :, 0:VS], 0.0)
                    nc.vector.memset(hist[:, :, :, VS:], -BIG).then_inc(ready, 1)
                    dve.wait_ge(loaded, 144)
                    nc.vector.memset(si[:, :, SW:], 0)
                    chain(nc.vector.memset(di[:, :, SW:], 0))
                    chain(nc.vector.tensor_copy(df, di[:, :, 0:SW]))
                    chain(nc.vector.tensor_copy(last_dst[:], df[:, :, SW - 1]))
                    chain(nc.vector.tensor_scalar(ew[:], ew[:], float(D1) ** -0.5, None, ALU.mult))
                    chain(nc.vector.memset(reset[:, :, 0:1], -BIG))
                    chain(nc.vector.tensor_tensor(reset[:, :, 1:], df[:, :, 1:], df[:, :, 0:SW - 1], ALU.not_equal))
                    chain(nc.vector.tensor_scalar(free[:, :, 0:SW - 1], reset[:, :, 1:], -float(NOWHERE), float(NOWHERE), ALU.mult, ALU.add))
                    chain(nc.vector.tensor_tensor(free[:, :, 0:SW - 1], free[:, :, 0:SW - 1], df[:, :, 0:SW - 1], ALU.add))
                    chain(nc.vector.tensor_copy(ends[:, :, 0:SW - 1], free[:, :, 0:SW - 1]))
                    chain(nc.vector.memset(ends[:, :, SW - 1:], NOWHERE))
                    chain(nc.vector.tensor_scalar(reset[:, :, 1:], reset[:, :, 1:], -BIG, None, ALU.mult))
                    for b in range(2):
                        for t, x in enumerate((si, di)):
                            last = nc.vector.tensor_copy(idx[:, t, b, :].rearrange("p (w u) -> p w u", w=W), x[:, :, b * HS:(b + 1) * HS])
                        last.then_inc(indexed.sem, 1)
                    dve.wait_ge(made, 6)
                    with dve.Fori(0, NT) as i:
                        chain.fresh()
                        k_done.wait(dve, i, 1)
                        chain(nc.vector.tensor_tensor(row[:], pk[:], bias[:, D:3 * D], ALU.add))
                        chain(nc.vector.tensor_tensor(sqr[:], row[:, 0:D], row[:, 0:D], ALU.mult))
                        nc.vector.tensor_reduce(nrm[:, 0, :], sqr[:].rearrange("p (h c) -> p h c", c=D1), AX.X, ALU.add).then_inc(norms.sem, 1)
                        edge_set(dve, chain, i, 0)
                        roots.wait(dve, i, 1)
                        chain(nc.vector.tensor_scalar_max(nrm[:, 1, :], nrm[:, 1, :], 1e-12))
                        chain(nc.vector.reciprocal(nrm[:, 1, :], nrm[:, 1, :]))
                        chain(nc.vector.tensor_scalar(nrm[:, 2, :], nrm[:, 1, :], scale, None, ALU.mult))
                        sums_done.wait(dve, i)
                        m = k.valid[:, bass.ds(i, 1)]
                        v3 = v1[:].rearrange("p (h c) -> p h c", c=VW)
                        nc.vector.tensor_copy(v3[:, :, 0], m.to_broadcast((P, H1)))
                        nc.vector.tensor_scalar(v3[:, :, 1:], row[:, D:2 * D].rearrange("p (h c) -> p h c", c=D1), m, None, ALU.mult)
                        normalise(chain, row[:, 0:D], nrm[:, 2, :].unsqueeze(2).to_broadcast((P, H1, D1)))
                        pair_features(0, H_A).then_inc(pairs.sem, 1)
                        edge_set(dve, chain, i, 1)
                        pair_features(H_A, H1).then_inc(pairs.sem, 1)
                        edge_set(dve, chain, i, 2)
                        edge_set(dve, chain, i, 3)
                    sums_done.wait(dve, NT)
                    chain.fresh()
                    nc.vector.memset(feat[:, 0, :], 0.0).then_inc(made, 1)
                    dve.wait_ge(made, 8)
                    for h in range(H1):
                        o = (h % 3) * NCH * VW
                        nc.vector.tensor_scalar(S[:, h].rearrange("p c e -> p (c e)"), pS[:, h // 3, o:o + NCH * VW], 1.0 / N, None, ALU.mult)
                    for g in range(Q4):
                        for j, f in ((0, scale ** 2 / N), (1, 0.5 / N)):
                            nc.vector.scalar_tensor_tensor(Sl[:, j, g].rearrange("p m e -> p (m e)"), pL[:, j, 4 * g * VW:4 * (g + 1) * VW],
                                                           f, blk[:].rearrange("p m e -> p (m e)"), ALU.mult, ALU.mult)
                    chain(nc.vector.tensor_scalar(Sf[:], pF[:, 0:VS], scale ** 4 / N, None, ALU.mult))
                    chain(nc.vector.tensor_scalar(S[:, :, 0, :], S[:, :, 0, :], coef[:, 0:1], None, ALU.mult))

        es2 = ExitStack()
        with es2:
            s2 = Scope(nc, es2, "q")
            RING = 3
            pqp = s2.ps("pqp", [P, 2, 512])
            pq, pp = pqp[:, 0, 0:D], pqp[:, 1, 0:D]
            pt = s2.ps("pt", [P, RING, 512])
            py = s2.ps("py", [P, 512])
            ppt = s2.ps("ppt", [P, 512])
            fT = s2.sb("fT", [P, RING, 512])
            y = s2.sb("y", [P, VS])
            r = s2.sb("r", [P, H1])
            on = s2.sb("on", [P, D])
            oT = s2.sb("oT", [P, D])
            res = s2.sb("res", [P, D])
            tq = s2.sb("tq", [P, H1])
            q_done, norms, roots = (s2.tally(n, 1) for n in ("q_done", "norms", "roots"))
            pairs = s2.tally("pairs", 2)
            turned, evacuated, met = (s2.tally(n, NB) for n in ("turned", "evacuated", "met"))
            normed, o_turned, o_evacuated, out_done, added = (s2.tally(n, 1) for n in ("normed", "o_turned", "o_evacuated", "out_done", "added"))
            xs_again = s2.tally("xs_again", 16)
            with nc.Block() as block:
                @block.sync
                def _(sp):
                    load_features(sp, MID)

                @block.gpsimd
                def _(pool):
                    move_rows(pool, MID)
                    gathered[0].wait(pool, NPASS, 32 * HALF)
                    summed.hold(pool, NPASS)
                    scatters(3)
                    for x in scattered:
                        x.wait(pool, 2 * NT, 16 * HALF)

                @block.scalar
                def _(act):
                    for x in (roots, evacuated, o_evacuated, xs_again):
                        x.open(act)

                    def evacuate(i, b):
                        turned.wait(act, i, b + 1)
                        met.wait(act, i, max(b - RING + 1, 0))
                        nc.scalar.activation(fT[:, b % RING], pt[:, b % RING], ACT.Copy).then_inc(evacuated.sem, 1)

                    act.dma_start(xs[:], xtable[0]).then_inc(xs_again.sem, 16)
                    with act.Fori(0, NT) as i:
                        q_done.hold(act, i, 1)
                        act.dma_start(xs[:], xtable[bass.ds(i + 1, 1)].rearrange("o p k n -> p (o k) n")).then_inc(xs_again.sem, 16)
                        norms.wait(act, i, 1)
                        nc.scalar.activation(nrm[:, 1, :], nrm[:, 0, :], ACT.Sqrt).then_inc(roots.sem, 1)
                        exponentials(act, i * 2 + MID, 0)
                        for b in range(3):
                            evacuate(i, b)
                        exponentials(act, i * 2 + MID, 1)
                        for b in range(3, 7):
                            evacuate(i, b)
                        exponentials(act, i * 2 + (MID + 1), 0)
                        for b in range(7, NB):
                            evacuate(i, b)
                        exponentials(act, i * 2 + (MID + 1), 1)
                        o_turned.wait(act, i, 1)
                        nc.scalar.activation(oT[:], ppt[:, 0:D], ACT.Copy).then_inc(o_evacuated.sem, 1)
                    xs_again.wait(act, NT, 16)

                @block.tensor
                def _(pe):
                    for x in (q_done, turned, met, o_turned, out_done):
                        x.open(pe)

                    def project_row(i):
                        xs_again.wait(pe, i, 16)
                        norms.wait(pe, i)
                        for c in range(KD):
                            last = nc.tensor.matmul(pq, xs[:, c, :], w[:, c, 0:D], start=c == 0, stop=c == KD - 1)
                        last.then_inc(q_done.sem, 1)

                    def turn(i, b):
                        evacuated.wait(pe, i, max(b - RING + 1, 0))
                        for c in range(4):
                            if b:
                                src = feat[:, b - 1, c * P:(c + 1) * P]
                            else:
                                src = (once if c < Q4 else last_d)[:, (c % Q4) * P:(c % Q4 + 1) * P]
                            last = nc.tensor.transpose(pt[:, b % RING, c * P:(c + 1) * P], src, k.ident[:])
                        last.then_inc(turned.sem, 1)

                    def meet(i, b):
                        evacuated.wait(pe, i, b + 1)
                        part = fT[:, b % RING]
                        if b == 0:
                            normed.wait(pe, i)
                            for g in range(Q4):
                                o = py[:, 4 * g * VW:4 * (g + 1) * VW]
                                nc.tensor.matmul(o, part[:, g * P:(g + 1) * P], Sl[:, 0, g].rearrange("p m e -> p (m e)"),
                                                 start=g == 0, stop=False, skip_group_check=True)
                                last = nc.tensor.matmul(o, part[:, (Q4 + g) * P:(Q4 + g + 1) * P], Sl[:, 1, g].rearrange("p m e -> p (m e)"),
                                                        start=False, stop=False, skip_group_check=True)
                        else:
                            for c in range(NCH):
                                last = nc.tensor.matmul(py[:, (b - 1) * VW:b * VW], part[:, c * P:(c + 1) * P], S[:, b - 1, c, :],
                                                        start=False, stop=c == NCH - 1, skip_group_check=True)
                        last.then_inc(met.sem, 1)

                    def meet_banks(i, b0, b1):
                        for b in range(b0, min(b0 + RING, b1)):
                            turn(i, b)
                        for b in range(b0, b1):
                            meet(i, b)
                            if b + RING < b1:
                                turn(i, b + RING)

                    project_row(0)
                    with pe.Fori(0, NT) as i:
                        project_features(pe, i * 2 + MID, 0)
                        project_features(pe, i * 2 + MID, 1)
                        project_row(i + 1)
                        project_features(pe, i * 2 + (MID + 1), 0)
                        pairs.wait(pe, i, 1)
                        meet_banks(i, 0, H_A + 1)
                        project_features(pe, i * 2 + (MID + 1), 1)
                        pairs.wait(pe, i, 2)
                        meet_banks(i, H_A + 1, NB)
                        normed.wait(pe, i, 1)
                        for c in range(KD):
                            last = nc.tensor.transpose(ppt[:, c * P:(c + 1) * P], on[:, c * P:(c + 1) * P], k.ident[:])
                        last.then_inc(o_turned.sem, 1)
                        o_evacuated.wait(pe, i, 1)
                        added.wait(pe, i)
                        for c in range(KD):
                            last = nc.tensor.matmul(pp, oT[:, c * P:(c + 1) * P], wp[:, c, :], start=c == 0, stop=c == KD - 1)
                        last.then_inc(out_done.sem, 1)

                @block.vector
                def _(dve):
                    for x in (norms, pairs, normed, added):
                        x.open(dve)
                    chain = Chain(dve, order)
                    chain.fresh()
                    chain(nc.vector.tensor_scalar(tq[:], temp[:], scale * scale, None, ALU.mult))

                    def finish(i):
                        out_done.wait(dve, i, 1)
                        chain(nc.vector.tensor_tensor(res[:], pp, bp[:], ALU.add))
                        x = dst[:, i, :] if isinstance(i, int) else tile_of(dst, i)
                        nc.vector.tensor_tensor(x, x, res[:], ALU.add).then_inc(added.sem, 1)
                        added.wait(dve, i, 1)

                    def tile(i, first=False):
                        chain.fresh()
                        q_done.wait(dve, i, 1)
                        chain(nc.vector.tensor_tensor(row[:, 0:D], pq, bias[:, 0:D], ALU.add))
                        chain(nc.vector.tensor_tensor(sqr[:], row[:, 0:D], row[:, 0:D], ALU.mult))
                        nc.vector.tensor_reduce(nrm[:, 0, :], sqr[:].rearrange("p (h c) -> p h c", c=D1), AX.X, ALU.add).then_inc(norms.sem, 1)
                        edge_set(dve, chain, i + NT, 0)
                        if not first:
                            finish(i - 1)
                        roots.wait(dve, i, 1)
                        chain(nc.vector.tensor_scalar(nrm[:, 1, :], nrm[:, 1, :], scale, 1e-12, ALU.mult, ALU.max))
                        chain(nc.vector.reciprocal(nrm[:, 1, :], nrm[:, 1, :]))
                        chain(nc.vector.tensor_tensor(nrm[:, 2, :], nrm[:, 1, :], tq[:], ALU.mult))
                        turned.wait(dve, i)
                        normalise(chain, row[:, 0:D], nrm[:, 2, :].unsqueeze(2).to_broadcast((P, H1, D1)))
                        pair_features(0, H_A).then_inc(pairs.sem, 1)
                        edge_set(dve, chain, i + NT, 1)
                        pair_features(H_A, H1).then_inc(pairs.sem, 1)
                        edge_set(dve, chain, i + NT, 2)
                        edge_set(dve, chain, i + NT, 3)
                        met.wait(dve, i, NB)
                        chain(nc.vector.tensor_tensor(y[:], py[:, 0:VS], Sf[:], ALU.add))
                        y3 = y[:].rearrange("p (h c) -> p h c", c=VW)
                        chain(nc.vector.reciprocal(r[:], y3[:, :, 0]))
                        chain(nc.vector.tensor_tensor(on[:].rearrange("p (h c) -> p h c", c=D1), y3[:, :, 1:],
                                                      r[:].unsqueeze(2).to_broadcast((P, H1, D1)), ALU.mult))
                        dve.sem_inc(normed.sem, 1)

                    tile(0, first=True)
                    with dve.Fori(1, NT) as i:
                        tile(i)
                    chain.fresh()
                    finish(NT - 1)
        eq.close()

        for n in range(W):
            tail = hist[:, 3, n * HS + HS - 1, :]
            es2 = ExitStack()
            with es2:
                s2 = Scope(nc, es2, f"join{n}")
                same = s2.sb("same", [P, P])
                off = s2.sb("off", [P, P])
                later = s2.sb("later", [P, P])
                diag = s2.sb("diag", [P, H1, P])
                col = s2.sb("col", [P, 4])
                ti = s2.sb("ti", [P, 1], I32)
                held = s2.sb("held", [P, AW])
                joined = s2.sb("joined", [P, AW])
                part = s2.sb("part", [P, VS])
                mx = s2.sb("mx", [P, 3, H1])
                pj = s2.ps("pj", [P, 4, 512])
                v, p_, e_, g_ = (s2.sem(n) for n in ("v", "p", "e", "g"))
                got, put = s2.pool_dma_sem(f"got{n}"), s2.pool_dma_sem(f"put{n}")
                with nc.Block() as block:
                    @block.tensor
                    def _(pe):
                        pe.wait_ge(v, 1)
                        nc.tensor.matmul(pj[:, 0, 0:P], k.ones[:], same[:], start=True, stop=True)
                        for c in range(2):
                            last = nc.tensor.matmul(pj[:, 1 + c, :], k.ones[:], diag[:, 4 * c:4 * c + 4, :].rearrange("p h c -> p (h c)"), start=True, stop=True)
                        last.then_inc(p_, 1)
                        pe.wait_ge(v, 3)
                        nc.tensor.matmul(pj[:, 3, 0:VS], same[:], part[:], start=True, stop=True).then_inc(p_, 1)

                    @block.gpsimd
                    def _(pool):
                        pool.wait_ge(v, 1)
                        nc.gpsimd.indirect_dma_start(held[:], None, atable, bass.IndirectOffsetOnAxis(ap=ti[:], axis=0)).then_inc(got, 16)
                        pool.wait_ge(v, 2)
                        nc.gpsimd.affine_select(out=later[:], in_=same[:], compare_op=ALU.is_gt, fill=0.0, base=0,
                                                pattern=[[1, P]], channel_multiplier=-1).then_inc(g_, 1)
                        pool.wait_ge(v, 4)
                        nc.gpsimd.indirect_dma_start(atable, bass.IndirectOffsetOnAxis(ap=ti[:], axis=0), joined[:], None,
                                                     bounds_check=NP - 1, oob_is_err=False).then_inc(put, 16)
                        pool.wait_ge(put, 16)

                    @block.scalar
                    def _(act):
                        act.wait_ge(v, 3 - 1)
                        act.wait_ge(e_, 1)
                        nc.scalar.activation(mx[:, 1:3, :], mx[:, 1:3, :], ACT.Exp).then_inc(e_, 1)

                    @block.vector
                    def _(dve):
                        chain = Chain(dve, order)
                        chain.fresh()
                        chain(nc.vector.tensor_copy(col[:, 0:1], last_dst[:, n:n + 1]))
                        chain(nc.vector.tensor_copy(ti[:], di[:, n, SW - 1:SW]))
                        nc.vector.tensor_scalar(same[:], k.ident[:], col[:, 0:1], None, ALU.mult)
                        nc.vector.tensor_tensor(diag[:], k.ident[:].unsqueeze(1).to_broadcast((P, H1, P)), tail[:, VS:].unsqueeze(2).to_broadcast((P, H1, P)), ALU.mult).then_inc(v, 1)
                        dve.wait_ge(p_, 1)
                        nc.vector.tensor_scalar(same[:], pj[:, 0, 0:P], col[:, 0:1], None, ALU.is_equal).then_inc(v, 1)
                        dve.wait_ge(v, 2)
                        chain(nc.vector.tensor_scalar(off[:], same[:], BIG, -BIG, ALU.mult, ALU.add))
                        for c in range(2):
                            last = nc.vector.tensor_tensor(diag[:, 4 * c:4 * c + 4, :], pj[:, 1 + c, :].rearrange("p (h c) -> p h c", c=P),
                                                           off[:].unsqueeze(1).to_broadcast((P, 4, P)), ALU.add)
                        chain(last)
                        chain(nc.vector.tensor_reduce(mx[:, 0, :], diag[:], AX.X, ALU.max))
                        dve.wait_ge(got, 16)
                        chain(nc.vector.tensor_tensor(mx[:, 0, :], mx[:, 0, :], held[:, VS:], ALU.max))
                        nc.vector.tensor_tensor(mx[:, 1, :], tail[:, VS:], mx[:, 0, :], ALU.subtract)
                        nc.vector.tensor_tensor(mx[:, 2, :], held[:, VS:], mx[:, 0, :], ALU.subtract).then_inc(e_, 1)
                        dve.wait_ge(e_, 2)
                        nc.vector.tensor_tensor(part[:].rearrange("p (h c) -> p h c", c=VW), tail[:, 0:VS].rearrange("p (h c) -> p h c", c=VW),
                                                mx[:, 1, :].unsqueeze(2).to_broadcast((P, H1, VW)), ALU.mult).then_inc(v, 1)
                        chain(nc.vector.tensor_tensor(joined[:, 0:VS].rearrange("p (h c) -> p h c", c=VW), held[:, 0:VS].rearrange("p (h c) -> p h c", c=VW),
                                                      mx[:, 2, :].unsqueeze(2).to_broadcast((P, H1, VW)), ALU.mult))
                        dve.wait_ge(g_, 1)
                        chain(nc.vector.tensor_reduce(col[:, 1:2], later[:], AX.X, ALU.max))
                        chain(nc.vector.scalar_tensor_tensor(col[:, 2:3], col[:, 1:2], float(NOWHERE), col[:, 0:1], ALU.mult, ALU.add))
                        chain(nc.vector.tensor_copy(joined[:, VS:], mx[:, 0, :]))
                        chain(nc.vector.tensor_copy(ti[:], col[:, 2:3]))
                        dve.wait_ge(p_, 2)
                        nc.vector.tensor_tensor(joined[:, 0:VS], joined[:, 0:VS], pj[:, 3, 0:VS], ALU.add).then_inc(v, 1)


def attention_out_phase(nc, k, a, atable, dst):
    VS = H1 * VW
    with ExitStack() as es:
        s = Scope(nc, es, "aout")
        wo = s.sb("wo", [P, KD, D])
        bo = s.sb("bo", [P, D])
        alpha = s.sb("alpha", [P, 1])
        rows = s.sb("rows", [P, GT, AW])
        r = s.sb("r", [P, GT, H1])
        on = s.sb("on", [P, GT, D])
        oT = s.sb("oT", [P, KD, GC])
        pt = s.ps("pt", [P, KD, 1024])
        py = s.ps("py", [P, 8, D])
        loaded, order = s.sem("loaded"), s.sem("order")
        fetched, normed, transposed, evacuated, projected, added = (s.tally(n, c) for n, c in (
            ("fetched", 16), ("normed", 1), ("transposed", 1), ("evacuated", 1), ("projected", 1), ("added", 1)))
        with nc.Block() as block:
            @block.sync
            def _(sp):
                sp.dma_start(wo[:], a["L1_gnn_Wo"].rearrange("(k p) c -> p k c", p=P)).then_inc(loaded, 16)
                sp.dma_start(bo[:], a["L1_gnn_bo"].partition_broadcast(P)).then_inc(loaded, 16)
                sp.dma_start(alpha[:], a["L1_gnn_alpha"].partition_broadcast(P)).then_inc(loaded, 16)
                sp.wait_ge(loaded, 48)
                fetched.open(sp)
                with sp.Fori(0, NG) as i:
                    normed.hold(sp, i)
                    sp.dma_start(rows[:], atable[bass.ds(i * GC, GC), :].rearrange("(t p) c -> p t c", p=P)).then_inc(fetched.sem, 16)

            @block.vector
            def _(dve):
                normed.open(dve)
                added.open(dve)
                dve.wait_ge(loaded, 48)
                chain = Chain(dve, order)
                chain.fresh()
                with dve.Fori(0, NG) as i:
                    chain.fresh()
                    fetched.wait(dve, i, 16)
                    acc = rows[:, :, 0:VS].rearrange("p t (h c) -> p t h c", c=VW)
                    chain(nc.vector.tensor_scalar_max(r[:], acc[:, :, :, D1], 1e-30))
                    chain(nc.vector.reciprocal(r[:], r[:]))
                    transposed.wait(dve, i)
                    nc.vector.tensor_tensor(on[:].rearrange("p t (h c) -> p t h c", c=D1), acc[:, :, :, 0:D1],
                                            r[:].unsqueeze(3).to_broadcast((P, GT, H1, D1)), ALU.mult).then_inc(normed.sem, 1)
                    normed.wait(dve, i, 1)
                    projected.wait(dve, i, 1)
                    chain(nc.vector.tensor_tensor(on[:], py[:, 0:GT, :], bo[:].unsqueeze(1).to_broadcast((P, GT, D)), ALU.add))
                    x = dst[:, bass.ds(i * GT, GT), :]
                    nc.vector.scalar_tensor_tensor(x, on[:], alpha[:, 0:1], x, ALU.mult, ALU.add).then_inc(added.sem, 1)
                    added.wait(dve, i, 1)

            @block.tensor
            def _(pe):
                transposed.open(pe)
                projected.open(pe)
                pe.wait_ge(loaded, 48)
                with pe.Fori(0, NG) as i:
                    normed.wait(pe, i, 1)
                    evacuated.wait(pe, i)
                    for c in range(KD):
                        for t in range(GT):
                            last = nc.tensor.transpose(pt[:, c, t * P:(t + 1) * P], on[:, t, c * P:(c + 1) * P], k.ident[:])
                    last.then_inc(transposed.sem, 1)
                    evacuated.wait(pe, i, 1)
                    added.wait(pe, i)
                    for t in range(GT):
                        for c in range(KD):
                            last = nc.tensor.matmul(py[:, t, :], oT[:, c, t * P:(t + 1) * P], wo[:, c, :], start=c == 0, stop=c == KD - 1)
                    last.then_inc(projected.sem, 1)

            @block.scalar
            def _(act):
                evacuated.open(act)
                with act.Fori(0, NG) as i:
                    transposed.wait(act, i, 1)
                    projected.wait(act, i)
                    nc.scalar.activation(oT[:], pt[:, :, 0:GC], ACT.Copy).then_inc(evacuated.sem, 1)


def top1_phase(nc, k, a, B, out):
    SLOTS = E1 * CS
    NOSLOT = 1 << 20
    buf, ybuf = k.dram("slots_in", (SLOTS, D)), k.dram("slots_out", (SLOTS, D))
    with ExitStack() as es:
        s = Scope(nc, es, "top1")
        slot = s.sb("slot", [P, 2, NT], I32)
        prob = s.sb("prob", [P, NT])
        loaded, order = s.sem("loaded"), s.sem("order")
        es2 = ExitStack()
        with es2:
            s2 = Scope(nc, es2, "route")
            gw = s2.sb("gw", [P, KD, E1])
            gb = s2.sb("gb", [P, E1])
            tri = s2.sb("tri", [P, P])
            zero = s2.sb("zero", [P, 2048])
            xs = s2.sb("xs", [P, KD, GC])
            L = s2.sb("L", [P, NT, E1])
            H = s2.sb("H", [P, NT, E1])
            C = s2.sb("C", [P, NT, E1])
            T = s2.sb("T", [P, NT + 1, E1])
            io = s2.sb("io", [P, E1])
            t1 = s2.sb("t1", [P, 6, NT])
            one = s2.sb("one", [P, NT])
            pl = s2.ps("pl", [P, 512])
            pc = s2.ps("pc", [P, 2, 512])
            made, steps, exps, counted, cleared = (s2.sem(n) for n in ("made", "steps", "exps", "counted", "cleared"))
            copied, projected, taken = (s2.tally(n, 1) for n in ("copied", "projected", "taken"))
            with nc.Block() as block:
                @block.gpsimd
                def _(pool):
                    nc.gpsimd.memset(zero[:], 0.0).then_inc(made, 1)
                    nc.gpsimd.iota(io[:], pattern=[[1, E1]], base=0, channel_multiplier=0, allow_small_or_imprecise_dtypes=True).then_inc(made, 1)
                    nc.gpsimd.memset(one[:], 1.0).then_inc(made, 1)
                    nc.gpsimd.affine_select(out=tri[:], in_=k.ones[:], compare_op=ALU.is_ge, fill=0.0, base=0,
                                            pattern=[[1, P]], channel_multiplier=-1).then_inc(made, 1)

                @block.sync
                def _(sp):
                    sp.dma_start(gw[:], a["L1_ffn_gate_w"].rearrange("(k p) c -> p k c", p=P)).then_inc(loaded, 16)
                    sp.dma_start(gb[:], a["L1_ffn_gate_b"].partition_broadcast(P)).then_inc(loaded, 16)
                    sp.wait_ge(made, 4)
                    for e in range(E1):
                        sp.dma_start(buf[e * CS:(e + 1) * CS, :].rearrange("(p r) c -> p (r c)", p=P), zero[:]).then_inc(cleared, 16)
                    sp.wait_ge(loaded, 32)
                    sp.wait_ge(cleared, 16 * E1)

                @block.scalar
                def _(act):
                    copied.open(act)
                    with act.Fori(0, NG) as i:
                        projected.wait(act, i)
                        nc.scalar.activation(xs[:], k.XT[:, :, bass.ds(i * GC, GC)], ACT.Copy).then_inc(copied.sem, 1)
                    act.wait_ge(steps, 1)
                    nc.scalar.activation(L[:], L[:], ACT.Exp).then_inc(exps, 1)

                @block.tensor
                def _(pe):
                    projected.open(pe)
                    pe.wait_ge(loaded, 32)
                    with pe.Fori(0, NG) as i:
                        copied.wait(pe, i, 1)
                        taken.wait(pe, i)
                        for t in range(GT):
                            for c in range(KD):
                                last = nc.tensor.matmul(pl[:, t * E1:(t + 1) * E1], xs[:, c, t * P:(t + 1) * P], gw[:, c, :],
                                                        start=c == 0, stop=c == KD - 1)
                        last.then_inc(projected.sem, 1)
                    pe.wait_ge(made, 4)
                    pe.wait_ge(steps, 2)
                    h = H[:].rearrange("p t e -> p (t e)")
                    nc.tensor.matmul(pc[:, 0, 0:NT * E1], tri[:], h, start=True, stop=True)
                    nc.tensor.matmul(pc[:, 1, 0:NT * E1], k.ones[:], h, start=True, stop=True).then_inc(counted, 1)

                @block.vector
                def _(dve):
                    taken.open(dve)
                    dve.wait_ge(loaded, 32)
                    dve.wait_ge(made, 4)
                    chain = Chain(dve, order)
                    with dve.Fori(0, NG) as i:
                        projected.wait(dve, i, 1)
                        nc.vector.tensor_tensor(L[:, bass.ds(i * GT, GT), :], pl[:, 0:GT * E1].rearrange("p (t e) -> p t e", e=E1),
                                                gb[:].unsqueeze(1).to_broadcast((P, GT, E1)), ALU.add).then_inc(taken.sem, 1)
                    taken.wait(dve, NG)
                    mx, tot, idx, pos, kept, base = (t1[:, j, :] for j in range(6))

                    def over(x):
                        return x.unsqueeze(2).to_broadcast((P, NT, E1))

                    iob = io[:].unsqueeze(1).to_broadcast((P, NT, E1))
                    chain(nc.vector.tensor_reduce(mx, L[:], AX.X, ALU.max))
                    nc.vector.tensor_tensor(L[:], L[:], over(mx), ALU.subtract).then_inc(steps, 1)
                    dve.wait_ge(exps, 1)
                    chain(nc.vector.tensor_reduce(tot, L[:], AX.X, ALU.add))
                    chain(nc.vector.reciprocal(tot, tot))
                    chain(nc.vector.tensor_tensor(L[:], L[:], over(tot), ALU.mult))
                    chain(nc.vector.tensor_reduce(mx, L[:], AX.X, ALU.max))
                    chain(nc.vector.tensor_tensor(H[:], L[:], over(mx), ALU.is_equal))
                    chain(nc.vector.tensor_scalar(io[:], io[:], -1.0, float(E1), ALU.mult, ALU.add))
                    chain(nc.vector.tensor_tensor(H[:], H[:], iob, ALU.mult))
                    chain(nc.vector.tensor_reduce(idx, H[:], AX.X, ALU.max))
                    chain(nc.vector.tensor_tensor(H[:], over(idx), iob, ALU.is_equal))
                    nc.vector.tensor_tensor(H[:], H[:], over(k.valid[:]), ALU.mult).then_inc(steps, 1)
                    dve.wait_ge(counted, 1)
                    chain(nc.vector.memset(T[:, 0, :], 0.0))
                    for e in range(E1):
                        last = nc.vector.tensor_tensor_scan(T[:, 1:, e], one[:], pc[:, 1, 0:NT * E1].rearrange("p (t e) -> p t e", e=E1)[:, :, e],
                                                            0.0, ALU.mult, ALU.add)
                    chain(last)
                    chain(nc.vector.tensor_tensor(C[:], pc[:, 0, 0:NT * E1].rearrange("p (t e) -> p t e", e=E1), T[:, 0:NT, :], ALU.add))
                    chain(nc.vector.tensor_tensor(C[:], C[:], H[:], ALU.mult))
                    chain(nc.vector.tensor_reduce(pos, C[:], AX.X, ALU.add))
                    chain(nc.vector.tensor_scalar(kept, pos, float(CAP), None, ALU.is_le))
                    chain(nc.vector.tensor_tensor(kept, kept, k.valid[:], ALU.mult))
                    chain(nc.vector.tensor_tensor(prob[:], mx, kept, ALU.mult))
                    chain(nc.vector.tensor_scalar(base, idx, -float(CS), float(E1 * CS - 1), ALU.mult, ALU.add))
                    chain(nc.vector.tensor_tensor(base, base, pos, ALU.add))
                    chain(nc.vector.tensor_tensor(base, base, kept, ALU.mult))
                    chain(nc.vector.tensor_copy(slot[:, 1, :], base))
                    chain(nc.vector.tensor_scalar(kept, kept, -float(NOSLOT), float(NOSLOT), ALU.mult, ALU.add))
                    chain(nc.vector.tensor_tensor(base, base, kept, ALU.add))
                    chain(nc.vector.tensor_copy(slot[:, 0, :], base))

        with ExitStack() as es2:
            s2 = Scope(nc, es2, "send")
            rows = s2.sb("rows", [P, GT, D])
            idx = s2.sb("idx", [P, GT], I32)
            sent = s2.pool_dma_tally("sent", 16 * GT)
            ready, free = s2.tally("ready", 1), s2.tally("free", 1)
            with nc.Block() as block:
                @block.vector
                def _(dve):
                    ready.open(dve)
                    with dve.Fori(0, NG) as i:
                        free.wait(dve, i)
                        nc.vector.tensor_copy(rows[:], B[:, bass.ds(i * GT, GT), :])
                        nc.vector.tensor_copy(idx[:], slot[:, 0, bass.ds(i * GT, GT)]).then_inc(ready.sem, 1)

                @block.gpsimd
                def _(pool):
                    free.open(pool)
                    with pool.Fori(0, NG) as i:
                        ready.hold(pool, i, 1)
                        for t in range(GT):
                            nc.gpsimd.indirect_dma_start(buf, bass.IndirectOffsetOnAxis(ap=idx[:, t:t + 1], axis=0), rows[:, t, :], None,
                                                         bounds_check=SLOTS - 1, oob_is_err=False).then_inc(sent.sem, 16)
                        sent.wait(pool, i, 16 * GT)
                        pool.sem_inc(free.sem, 1)

        with ExitStack() as es2:
            s2 = Scope(nc, es2, "ex1")
            FC = F1 // P
            w1 = s2.sb("w1", [P, KD, F1])
            w2 = s2.sb("w2", [P, FC, D])
            b1 = s2.sb("b1", [P, E1, FC])
            bias = s2.sb("bias", [P, FC])
            b2 = s2.sb("b2", [1, E1, D])
            rows = s2.sb("rows", [P, CT, D])
            flat = B[:].rearrange("p t c -> p (t c)")
            XE = flat[:, 0:KD * CS].rearrange("p (k n) -> p k n", k=KD)
            hid = flat[:, KD * CS:KD * CS + FC * CS].rearrange("p (f n) -> p f n", n=CS)
            Y = k.XT[:].rearrange("p k n -> p (k n)")[:, 0:CT * D].rearrange("p (t c) -> p t c", c=D)
            pa = s2.ps("pa", [P, 4, 512])
            py = s2.ps("py", [P, 8, D])
            biases, aorder = s2.sem("biases"), s2.sem("aorder")
            fetched = s2.tally("fetched", 48)
            turned, evacuated = s2.tally("turned", 4), s2.tally("evacuated", 4)
            h_done, relus = s2.tally("h_done", 2 * FC), s2.tally("relus", 2 * FC)
            y_done, copied = s2.tally("y_done", 1), s2.tally("copied", 1)
            stored, written = s2.pool_dma_tally("stored", 16), s2.tally("written", 1)
            with nc.Block() as block:
                @block.sync
                def _(sp):
                    sp.dma_start(b1[:], a["L1_ffn_b1"].rearrange("e (f p) -> p e f", p=P), allow_slow_non_contiguous=True).then_inc(biases, 16)
                    sp.dma_start(b2[:], a["L1_ffn_b2"].rearrange("(o e) d -> o e d", o=1)).then_inc(biases, 16)
                    sp.wait_ge(biases, 32)
                    fetched.open(sp)
                    with sp.Fori(0, E1) as i:
                        y_done.hold(sp, i)
                        sp.dma_start(w1[:], a["L1_ffn_w1"][bass.ds(i, 1)].rearrange("o (k p) f -> p (o k) f", p=P)).then_inc(fetched.sem, 16)
                        sp.dma_start(w2[:], a["L1_ffn_w2"][bass.ds(i, 1)].rearrange("o (k p) f -> p (o k) f", p=P)).then_inc(fetched.sem, 16)
                        sp.dma_start(rows[:], buf[bass.ds(i * CS, CS), :].rearrange("(t p) c -> p t c", p=P)).then_inc(fetched.sem, 16)

                @block.gpsimd
                def _(pool):
                    with pool.Fori(0, E1) as i:
                        copied.hold(pool, i, 1)
                        pool.dma_start(ybuf[bass.ds(i * CS, CS), :].rearrange("(t p) c -> p t c", p=P), Y).then_inc(stored.sem, 16)
                        stored.wait(pool, i, 16)
                        pool.sem_inc(written.sem, 1)

                @block.tensor
                def _(pe):
                    for x in (turned, h_done, y_done):
                        x.open(pe)
                    pe.wait_ge(biases, 32)
                    with pe.Fori(0, E1) as i:
                        fetched.wait(pe, i, 48)
                        for j in range(4):
                            if j == 0:
                                relus.wait(pe, i)
                            for t in range(4):
                                last = nc.tensor.transpose(pa[:, j, t * P:(t + 1) * P], rows[:, j % 2 * 4 + t, j // 2 * P:(j // 2 + 1) * P], k.ident[:])
                            last.then_inc(turned.sem, 1)
                        evacuated.wait(pe, i, 4)
                        for f in range(FC):
                            for j in range(2):
                                n = 2 * f + j
                                if n >= 4:
                                    relus.wait(pe, i, n - 3)
                                for c in range(KD):
                                    last = nc.tensor.matmul(pa[:, n % 4, :], w1[:, c, f * P:(f + 1) * P], XE[:, c, j * 512:(j + 1) * 512],
                                                            start=c == 0, stop=c == KD - 1)
                                last.then_inc(h_done.sem, 1)
                        relus.wait(pe, i, 2 * FC)
                        copied.wait(pe, i)
                        bb = b2[0:1, bass.ds(i, 1), :].rearrange("p o c -> p (o c)")
                        for t in range(CT):
                            nc.tensor.matmul(py[:, t, :], k.ones[0:1, :], bb, start=True, stop=False)
                            for f in range(FC):
                                last = nc.tensor.matmul(py[:, t, :], hid[:, f, t * P:(t + 1) * P], w2[:, f, :], start=False, stop=f == FC - 1)
                        last.then_inc(y_done.sem, 1)

                @block.scalar
                def _(act):
                    for x in (evacuated, relus):
                        x.open(act)
                    act.wait_ge(biases, 32)
                    chain = Chain(act, aorder)
                    with act.Fori(0, E1) as i:
                        chain.fresh()
                        relus.wait(act, i)
                        chain(nc.scalar.activation(bias[:], b1[:, bass.ds(i, 1), :].rearrange("p o f -> p (o f)"), ACT.Copy))
                        for j in range(4):
                            turned.wait(act, i, j + 1)
                            nc.scalar.activation(XE[:, j // 2, j % 2 * 512:(j % 2 + 1) * 512], pa[:, j, :], ACT.Copy).then_inc(evacuated.sem, 1)
                        y_done.wait(act, i)
                        for f in range(FC):
                            for j in range(2):
                                h_done.wait(act, i, 2 * f + j + 1)
                                nc.scalar.activation(hid[:, f, j * 512:(j + 1) * 512], pa[:, (2 * f + j) % 4, :], ACT.Relu,
                                                     bias=bias[:, f:f + 1]).then_inc(relus.sem, 1)


                @block.vector
                def _(dve):
                    copied.open(dve)
                    dve.sem_inc(written.sem, 1)
                    with dve.Fori(0, E1) as i:
                        y_done.wait(dve, i, 1)
                        written.wait(dve, i)
                        nc.vector.tensor_copy(Y, py[:]).then_inc(copied.sem, 1)

        with ExitStack() as es2:
            s2 = Scope(nc, es2, "back")
            idx = s2.sb("idx", [P, GT], I32)
            y = s2.sb("y", [P, GT, D])
            mask = s2.sb("mask", [P, GT * D], I32)
            const = s2.sb("const", [P, 3, 256])
            made = s2.sem("made")
            indexed = s2.tally("indexed", 1)
            got = s2.pool_dma_tally("got", 16 * GT)
            summed = s2.tally("summed", 1)
            stored = s2.sem("stored")
            with nc.Block() as block:
                @block.gpsimd
                def _(pool):
                    for j, v in enumerate((0.0, 1.0e4, -1.0e4)):
                        nc.gpsimd.memset(const[:, j], v).then_inc(made, 1)
                    with pool.Fori(0, NG) as i:
                        indexed.hold(pool, i, 1)
                        for t in range(GT):
                            nc.gpsimd.indirect_dma_start(y[:, t, :], None, ybuf, bass.IndirectOffsetOnAxis(ap=idx[:, t:t + 1], axis=0)).then_inc(got.sem, 16)

                @block.vector
                def _(dve):
                    indexed.open(dve)
                    summed.open(dve)
                    dve.wait_ge(made, 3)
                    chain = Chain(dve, order)
                    chain.fresh()
                    m3 = mask[:].rearrange("p (t c) -> p t c", c=D)

                    def filled(j):
                        return const[:, j:j + 1, 0:D].to_broadcast((P, GT, D))

                    with dve.Fori(0, NG) as i:
                        chain.fresh()
                        nc.vector.tensor_copy(idx[:], slot[:, 1, bass.ds(i * GT, GT)]).then_inc(indexed.sem, 1)
                        got.wait(dve, i, 16 * GT)
                        pr = prob[:, bass.ds(i * GT, GT)].unsqueeze(2).to_broadcast((P, GT, D))
                        chain(nc.vector.tensor_tensor(y[:], y[:], pr, ALU.mult))
                        chain(nc.vector.tensor_tensor(m3, y[:], y[:], ALU.not_equal))
                        chain(nc.vector.copy_predicated(y[:], m3, filled(0)))
                        chain(nc.vector.tensor_scalar(mask[:], y[:].rearrange("p t c -> p (t c)"), FLT_MAX, None, ALU.is_gt))
                        chain(nc.vector.copy_predicated(y[:], m3, filled(1)))
                        chain(nc.vector.tensor_scalar(mask[:], y[:].rearrange("p t c -> p (t c)"), -FLT_MAX, None, ALU.is_lt))
                        chain(nc.vector.copy_predicated(y[:], m3, filled(2)))
                        x = k.X[:, bass.ds(i * GT, GT), :]
                        nc.vector.tensor_tensor(x, x, y[:], ALU.add).then_inc(summed.sem, 1)
                        summed.wait(dve, i, 1)

                @block.sync
                def _(sp):
                    stored_t = Tally(stored, 16)
                    stored_t.open(sp)
                    with sp.Fori(0, NG) as i:
                        summed.hold(sp, i, 1)
                        sp.dma_start(out[bass.ds(i * GC, GC), :].rearrange("(t p) c -> p t c", p=P), k.X[:, bass.ds(i * GT, GT), :]).then_inc(stored, 16)
                    stored_t.wait(sp, NG)


FLT_MAX = float(np.finfo(np.float32).max)


def arrays(inputs):
    a = {n: np.asarray(v) for n, v in inputs.items()}
    out = {n: v for n, v in a.items() if n not in RESHAPED}

    def padded(v, n):
        return np.concatenate([v, np.zeros((n - v.shape[0],) + v.shape[1:], v.dtype)])

    def by_role(v):
        return v.reshape((8, 3, 32) + v.shape[1:])[:, [0, 2, 1]].transpose((1, 0, 2) + tuple(range(3, v.ndim + 2))).reshape(v.shape)

    out["x"] = padded(a["x"], NP)
    out["first_src"] = padded(a["src"][:N], NP).reshape(NT, P).T
    out["first_dst"] = padded(a["dst"][:N], NP).reshape(NT, P).T
    out["mix_wq"] = by_role(a["L0_mix_w_qkv"][:, :, 2]).T
    out["mix_col"] = np.stack([by_role(a["L0_mix_bn_gamma"]), by_role(a["L0_mix_bn_beta"]), by_role(a["L0_mix_w_dw"][:, 0, 2])])
    out["mix_pw"] = by_role(a["L0_mix_w_pw"][:, :, 0].reshape(24, 32, 32).transpose(0, 2, 1).reshape(QC * P, 32))
    for n in ("src", "dst", "weight"):
        v = a["edge_weight" if n == "weight" else n]
        fill = N if n == "dst" else 0
        out["edge_" + n] = np.concatenate([v, np.full(EP - E_EDGES, fill, v.dtype)]).reshape(P, S1)
    out["edge_attr"] = padded(a["edge_attr_64"], EP).reshape(P, S1, ED).transpose(2, 1, 0)
    out["ff_w1"] = a["L1_gnn_W1"].reshape(D, 2, F0).transpose(1, 0, 2)
    out["ff_b1"] = a["L1_gnn_b1"].reshape(2, F0)
    out["ff_w2"] = a["L1_gnn_W2"].reshape(2, F0, D)
    out["ff_b2"] = padded(a["L1_gnn_b2"][None], 2)
    out["lin_w"] = a["L1_mix_Wqkv"].T
    out["lin_wp"] = a["L1_mix_Wproj"].T
    out["lin_temp"] = a["L1_mix_temperature"].reshape(H1)
    out["L0_ffn_edge_index"] = a["L0_ffn_edge_index"].reshape(2, P, S0)
    out["L0_mix_w_res"] = a["L0_mix_w_res"][:, :, 0].T.reshape(4, P, D).transpose(1, 0, 2)
    return {n: np.ascontiguousarray(v) for n, v in out.items()}


RESHAPED = ("x", "src", "dst", "edge_attr_64", "edge_weight", "L0_mix_w_qkv", "L0_mix_bn_gamma", "L0_mix_bn_beta",
            "L0_mix_w_dw", "L0_mix_w_pw", "L0_mix_w_res", "L0_ffn_edge_index",
            "L1_gnn_W1", "L1_gnn_b1", "L1_gnn_W2", "L1_gnn_b2", "L1_mix_Wqkv", "L1_mix_Wproj", "L1_mix_temperature")


class Kept:

    def __init__(self, nc, es):
        self.nc = nc
        Scope.lasting = es
        s = Scope(nc, es, "kept")
        Tally.held = s.sem("held")
        self.X = s.sb("X", [P, NT, D])
        self.XT = s.sb("XT", [P, KD, NP])
        self.ident = s.sb("ident", [P, P])
        self.ones = s.sb("ones", [P, P])
        self.eps = s.sb("eps", [P, 1])
        self.valid = s.sb("valid", [P, NT])

    def dram(self, name, shape, dt=F32):
        return self.nc.dram_tensor(name, shape, dt, kind="Internal").ap()


def layer1_graph(nc, k, a):
    KW = D + H1 * VW
    qtable, ktable, atable = k.dram("qtable", (NP, D)), k.dram("ktable", (NP, KW)), k.dram("atable", (NP, AW))
    xtable = k.dram("xtable", (NT + 1, P, KD, P))
    xrows = k.dram("xrows", (P, NT, D))
    es = ExitStack()
    with es:
        s = Scope(nc, es, "l1")
        chan = s.sb("chan", [P, 4, KD])
        beta = s.sb("beta", [P, 1])
        loaded, order, kept = s.sem("loaded"), s.sem("order"), s.sem("kept")
        es2 = ExitStack()
        with es2:
            B = Scope(nc, es2, "rows").sb("B", [P, NT, D])
            layernorm_phase(nc, k, "ln2", k.X, keep=B)
            with nc.Block() as block:
                @block.sync
                def _(sp):
                    for j, n in enumerate(("ln1_g", "ln1_b", "ln2_g", "ln2_b")):
                        sp.dma_start(chan[:, j, :], a[f"L1_gnn_{n}"].rearrange("(k p) -> p k", p=P), allow_slow_non_contiguous=True).then_inc(loaded, 16)
                    sp.dma_start(beta[:], a["L1_gnn_beta"].partition_broadcast(P)).then_inc(loaded, 16)
                    for c in range(KD):
                        sp.dma_start(xtable[0:NT, :, c, :].rearrange("t p n -> p t n"), k.XT[:, c, :].rearrange("p (t n) -> p t n", n=P)).then_inc(kept, 16)
                    sp.dma_start(xtable[NT], k.XT[:, :, 0:P]).then_inc(kept, 16)
                    sp.dma_start(xrows, B[:]).then_inc(kept, 16)
                    sp.wait_ge(loaded, 80)
                    sp.wait_ge(kept, 16 * (KD + 2))
            layernorm_phase(nc, k, "ln3", B, scale=chan[:, 0, :], shift=chan[:, 1, :])
            tables_phase(nc, k, a, qtable, ktable, atable)
        edges_and_linear_phase(nc, k, a, qtable, ktable, atable, xtable, k.X)
        es2 = ExitStack()
        with es2:
            B = Scope(nc, es2, "rows2").sb("B", [P, NT, D])
            with nc.Block() as block:
                @block.sync
                def _(sp):
                    sp.dma_start(B[:], xrows).then_inc(loaded, 16)
                    sp.wait_ge(loaded, 96)
            attention_out_phase(nc, k, a, atable, B)
            layernorm_phase(nc, k, "ln4", B, scale=chan[:, 2, :], shift=chan[:, 3, :])
            experts_phase(nc, k, "ff1", a["ff_w1"], a["ff_b1"], a["ff_w2"], a["ff_b2"], 2, lambda e, t: beta[:, 0:1], B)
            with nc.Block() as block:
                @block.vector
                def _(dve):
                    nc.vector.tensor_tensor(k.X[:], k.X[:], B[:], ALU.add).then_inc(order, 1)
                    dve.wait_ge(order, 1)


def program(nc, a, out, phases=("L0a", "L0b", "L1a", "L1b")):
    with ExitStack() as es:
        k = Kept(nc, es)
        setup_phase(nc, a, k)
        if "L0a" in phases:
            with ExitStack() as es0:
                ball = Scope(nc, es0, "L0").sb("ball", [P, KD, NP])
                layernorm_phase(nc, k, "ln0", k.X, ball=ball)
                gather_phase(nc, k, a)
                mixer_phase(nc, k, a, ball)
        if "L0b" in phases:
            with ExitStack() as es0:
                gates = Scope(nc, es0, "L0").sb("gates", [P, NT, E0])
                layernorm_phase(nc, k, "ln1", k.X)
                gate_phase(nc, k, a, gates)
                experts_phase(nc, k, "moe0", a["L0_ffn_W1"], a["L0_ffn_b1"], a["L0_ffn_W2"], a["L0_ffn_b2"], E0,
                              lambda e, t: gates[:, bass.ds(t, 1), e], k.X)
        if "L1a" in phases:
            layer1_graph(nc, k, a)
        es1 = ExitStack()
        with es1:
            B = Scope(nc, es1, "last").sb("B", [P, NT, D])
            if "L1b" in phases:
                layernorm_phase(nc, k, "ln5", k.X, keep=B)
                top1_phase(nc, k, a, B, out)
                return
        with ExitStack() as es1:
            stored = Scope(nc, es1, "end").sem("stored")
            with nc.Block() as block:
                @block.sync
                def _(sp):
                    sp.dma_start(out.rearrange("(t p) c -> p t c", p=P), k.X[:]).then_inc(stored, 16)
                    sp.wait_ge(stored, 16)


def kernel(**inputs):
    import concourse.bacc as bacc
    from concourse.bass_utils import run_bass_kernel_spmd

    nc = bacc.Bacc("TRN2", target_bir_lowering=False, num_devices=1)
    host = arrays(inputs)
    a = {n: nc.dram_tensor(f"in_{n}", v.shape, mybir.dt.from_np(v.dtype), kind="ExternalInput").ap() for n, v in host.items()}
    out = nc.dram_tensor("out", (NP, D), F32, kind="ExternalOutput").ap()
    program(nc, a, out)
    r = run_bass_kernel_spmd(nc, [{f"in_{n}": v for n, v in host.items()}], core_ids=[0])
    return r.results[0]["out"][:N]
```

```python
import numpy as np
import concourse.bass as bass
from concourse import mybir
from concourse.alu_op_type import AluOpType as ALU
from contextlib import ExitStack

F32 = mybir.dt.float32
I32 = mybir.dt.int32
ACT = mybir.ActivationFunctionType
AX = mybir.AxisListType

P = 128
N = 6250
D = 256
KD = D // P
NT = -(-N // P)
GT = 7
NG = NT // GT
GC = GT * P
HC = GC // 2
NP = NT * P
BIG = 1.0e30
LN_EPS = 1e-05

H0, C0 = 4, 64
R0 = D + H0
QC = 6
MAXNORM = 1.0 - 1e-05
ATANH_MAX = float(np.arctanh(np.float64(np.float32(MAXNORM))))
MIN_NORM = 1e-15
ATT_EPS = 1e-15
E0, F0, GH = 4, 512, 4
GW = GH * E0
MW = GW + GH
E0_EDGES = 131072
S0 = E0_EDGES // P
U0 = 8

E_EDGES = 200000
H1, D1, ED = 8, 32, 64
U1 = 8
W = 2
S1 = -(-E_EDGES // (P * U1)) * U1
EP = S1 * P
AW = D + 2 * H1
FF = 1024
VW = D1 + 1
PD = D1 // 2 + 1
PR = PD * D1
PC = -(-PR // P)
E1, F1 = 8, 1024
CAP = -(-5 * N // (4 * E1))
CS = 1024
CT = CS // P


class Chain:

    def __init__(self, eng, sem):
        self.eng, self.sem, self.n = eng, sem, 0

    def __call__(self, ins):
        self.n += 1
        ins.then_inc(self.sem, 1)
        self.eng.wait_ge(self.sem, self.n)

    def start(self, ins):
        self.n += 1
        ins.then_inc(self.sem, 1)
        return self.n

    def until(self, n):
        self.eng.wait_ge(self.sem, n)

    def fresh(self):
        self.eng.sem_clear(self.sem)
        self.n = 0


class Tally:

    held = None

    def __init__(self, sem, per_pass, credit=1):
        self.sem, self.per_pass, self.credit = sem, per_pass, credit

    def open(self, eng):
        eng.sem_inc(self.sem, self.credit)

    def wait(self, eng, i, n=0):
        eng.wait_ge(self.sem, i * self.per_pass + (self.credit + n))

    def hold(self, eng, i, n=0):
        self.wait(eng, i, n)
        eng.sem_inc(self.held, 1)


class Scope:

    lasting = None

    def __init__(self, nc, es, name):
        self.nc, self.es, self.name, self.sems = nc, es, name, []
        es.callback(self.clear)

    def clear(self):
        if self.sems:
            with self.nc.Block() as block:
                @block.sync
                def _(sp):
                    for sem in self.sems:
                        sp.sem_clear(sem)

    def sb(self, name, shape, dt=F32):
        return self.es.enter_context(self.nc.sbuf_tensor(f"{self.name}_{name}", shape, dt))

    def ps(self, name, shape):
        return self.es.enter_context(self.nc.psum_tensor(f"{self.name}_{name}", shape, F32))

    def sem(self, name):
        self.sems.append(self.es.enter_context(self.nc.semaphore(f"{self.name}_{name}")))
        return self.sems[-1]

    def pool_dma_sem(self, name):
        return Scope.lasting.enter_context(self.nc.semaphore(f"{self.name}_{name}"))

    def tally(self, name, per_pass, credit=1):
        return Tally(self.sem(name), per_pass, credit)

    def pool_dma_tally(self, name, per_pass):
        return Tally(self.pool_dma_sem(name), per_pass, 0)


def tile_of(x, t):
    return x[:, bass.ds(t, 1), :].rearrange("p o c -> p (o c)")


def setup_phase(nc, a, k):
    with ExitStack() as es:
        s = Scope(nc, es, "setup")
        loaded, made = s.sem("loaded"), s.sem("made")
        with nc.Block() as block:
            @block.sync
            def _(sp):
                sp.dma_start(k.X[:], a["x"].rearrange("(t p) c -> p t c", p=P)).then_inc(loaded, 16)
                sp.wait_ge(loaded, 16)

            @block.gpsimd
            def _(pool):
                chain = Chain(pool, made)
                nc.gpsimd.memset(k.ones[:], 1.0)
                nc.gpsimd.memset(k.eps[:], LN_EPS)
                nc.gpsimd.memset(k.valid[:], 1.0)
                chain(nc.gpsimd.memset(k.ident[:], 0.0))
                nc.gpsimd.affine_select(out=k.ident[:], in_=k.ident[:], compare_op=ALU.not_equal, fill=1.0,
                                        base=0, pattern=[[-1, P]], channel_multiplier=1)
                chain(nc.gpsimd.affine_select(out=k.valid[:], in_=k.valid[:], compare_op=ALU.is_ge, fill=0.0,
                                              base=N - 1, pattern=[[-P, NT]], channel_multiplier=-1))


def layernorm_phase(nc, k, name, src, keep=None, scale=None, shift=None, ball=None):
    with ExitStack() as es:
        s = Scope(nc, es, name)
        stats = s.sb("stats", [P, GT, 6])
        mv = s.sb("mv", [P, GT, 2])
        sd = s.sb("sd", [P, GT])
        rows = s.sb("rows", [P, GT, D])
        pt = s.ps("pt", [P, KD, 1024])
        nsets = 2 if ball is not None else 1
        stats_ready = s.tally("stats_ready", 1)
        sd_ready = s.tally("sd_ready", 1)
        rows_ready = s.tally("rows_ready", nsets)
        transposed = s.tally("transposed", KD * nsets)
        evacuated = s.tally("evacuated", KD * nsets)
        kept = s.tally("kept", 1)
        order = s.sem("order")
        aorder = s.sem("aorder")
        if ball is not None:
            sq = s.sb("sq", [P, D])
            n2 = s.sb("n2", [P, GT])
            nrm = s.sb("nrm", [P, GT])
            z = s.sb("z", [P, 8, GT])
            norms_ready = s.tally("norms_ready", 2)
            ratio_ready = s.tally("ratio_ready", 1)

        with nc.Block() as block:
            @block.vector
            def _(dve):
                stats_ready.open(dve)
                rows_ready.open(dve)
                chain = Chain(dve, order)
                if ball is not None:
                    ratio_ready.open(dve)
                with dve.Fori(0, NG) as i:
                    chain.fresh()
                    for t in range(GT):
                        last = nc.vector.bn_stats(stats[:, t, :], tile_of(src, i * GT + t))
                    chain(last)
                    for t in range(GT):
                        last = nc.vector.bn_aggr(mv[:, t, :], stats[:, t, :])
                    last.then_inc(stats_ready.sem, 1)
                    sd_ready.wait(dve, i, 1)
                    chain(nc.vector.reciprocal(sd[:], sd[:]))
                    transposed.wait(dve, i)
                    if keep is not None:
                        kept.wait(dve, i)
                    for t in range(GT):
                        last = nc.vector.tensor_scalar(rows[:, t, :], tile_of(src, i * GT + t), mv[:, t, 0:1],
                                                       sd[:, t:t + 1], ALU.subtract, ALU.mult)
                    last.then_inc(rows_ready.sem, 1)
                    if ball is not None:
                        c, c2, top, r, ser, m = (z[:, j, :] for j in range(6))
                        norms_ready.wait(dve, i, 1)
                        chain(nc.vector.tensor_scalar_min(c, nrm[:], MAXNORM))
                        chain(nc.vector.tensor_scalar(r, c, -1.0, 1.0, ALU.mult, ALU.add))
                        chain(nc.vector.reciprocal(r, r))
                        chain(nc.vector.scalar_tensor_tensor(top, c, 1.0, r, ALU.add, ALU.mult))
                        nc.vector.tensor_tensor(c2, c, c, ALU.mult).then_inc(ratio_ready.sem, 1)
                        norms_ready.wait(dve, i, 2)
                        chain(nc.vector.tensor_scalar_max(r, nrm[:], MIN_NORM))
                        chain(nc.vector.reciprocal(r, r))
                        chain(nc.vector.scalar_tensor_tensor(top, z[:, 6, :], 0.5, r, ALU.mult, ALU.mult))
                        chain(nc.vector.tensor_scalar(ser, c2, 1.0 / 7, 1.0 / 5, ALU.mult, ALU.add))
                        chain(nc.vector.tensor_tensor(ser, ser, c2, ALU.mult))
                        chain(nc.vector.scalar_tensor_tensor(ser, ser, 1.0 / 3, c2, ALU.add, ALU.mult))
                        chain(nc.vector.tensor_scalar(m, c, 0.05, None, ALU.is_lt))
                        chain(nc.vector.scalar_tensor_tensor(ser, ser, 1.0, top, ALU.add, ALU.subtract))
                        chain(nc.vector.tensor_tensor(ser, ser, m, ALU.mult))
                        chain(nc.vector.tensor_tensor(top, ser, top, ALU.add))
                        transposed.wait(dve, i, KD)
                        for t in range(GT):
                            last = nc.vector.tensor_scalar(rows[:, t, :], rows[:, t, :], top[:, t:t + 1], None, ALU.mult)
                        last.then_inc(rows_ready.sem, 1)

            @block.scalar
            def _(act):
                sd_ready.open(act)
                evacuated.open(act)
                if ball is not None:
                    norms_ready.open(act)
                chain = Chain(act, aorder)
                with act.Fori(0, NG) as i:
                    chain.fresh()
                    stats_ready.wait(act, i, 1)
                    nc.scalar.activation(sd[:], mv[:, :, 1], ACT.Sqrt, bias=k.eps[:, 0:1]).then_inc(sd_ready.sem, 1)
                    if ball is not None:
                        rows_ready.wait(act, i, 1)
                        for t in range(GT):
                            chain(nc.scalar.activation(sq[:], rows[:, t, :], ACT.Square, accum_out=n2[:, t:t + 1]))
                        nc.scalar.activation(nrm[:], n2[:], ACT.Sqrt).then_inc(norms_ready.sem, 1)
                    for j in range(nsets):
                        if j:
                            ratio_ready.wait(act, i, 1)
                            nc.scalar.activation(z[:, 6, :], z[:, 2, :], ACT.Ln).then_inc(norms_ready.sem, 1)
                        for c in range(KD):
                            transposed.wait(act, i, KD * j + c + 1)
                            out = (ball if j else k.XT)[:, c, bass.ds(i * GC, GC)]
                            if scale is not None:
                                ins = nc.scalar.activation(out, pt[:, c, 0:GC], ACT.Identity,
                                                           bias=shift[:, c:c + 1], scale=scale[:, c:c + 1])
                            else:
                                ins = nc.scalar.activation(out, pt[:, c, 0:GC], ACT.Copy)
                            ins.then_inc(evacuated.sem, 1)

            @block.tensor
            def _(pe):
                transposed.open(pe)
                with pe.Fori(0, NG) as i:
                    for j in range(nsets):
                        rows_ready.wait(pe, i, j + 1)
                        for c in range(KD):
                            evacuated.wait(pe, i, c + 1 if j else 0)
                            for t in range(GT):
                                last = nc.tensor.transpose(pt[:, c, t * P:(t + 1) * P], rows[:, t, c * P:(c + 1) * P],
                                                           k.ident[:])
                            last.then_inc(transposed.sem, 1)

            if keep is not None:
                @block.gpsimd
                def _(pool):
                    kept.open(pool)
                    with pool.Fori(0, NG) as i:
                        rows_ready.hold(pool, i, 1)
                        nc.gpsimd.tensor_copy(keep[:, bass.ds(i * GT, GT), :], rows[:]).then_inc(kept.sem, 1)


def gather_phase(nc, k, a):
    with ExitStack() as es:
        s = Scope(nc, es, "g0")
        w = s.sb("w", [P, KD, D])
        at = s.sb("at", [P, 2, D])
        xs = s.sb("xs", [P, 2, KD, GC])
        pr = s.ps("pr", [P, 2, 8, D])
        row = s.sb("row", [P, 2, GT, R0])
        left = s.sb("left", [P, 2, GT, H0])
        prod = s.sb("prod", [P, 2, GT, D])
        iall = s.sb("iall", [P, 2, NT], I32)
        table, ltable = k.dram("g0_table", (NP, R0)), k.dram("g0_left_logits", (NP, H0))
        weights = s.sem("weights")
        copied, projected, rows_ready = ([s.tally(f"{x}{b}", 1) for b in range(2)] for x in ("copied", "projected", "rows_ready"))
        stored = [s.tally(f"stored{b}", 32) for b in range(2)]
        order = s.sem("order")

        def groups(eng, group):
            with eng.Fori(0, NG // 2) as n:
                group(n, 0, n * 2)
                group(n, 1, n * 2 + 1)
            group(NG // 2, 0, NG - 1)

        assert NG % 2 == 1
        with nc.Block() as block:
            @block.sync
            def _(sp):
                sp.dma_start(w[:], a["L0_gnn_weight"].rearrange("(k p) c -> p k c", p=P)).then_inc(weights, 16)
                sp.dma_start(at[:, 0, :], a["L0_gnn_attn_l"].rearrange("h c -> (h c)").partition_broadcast(P)).then_inc(weights, 16)
                sp.dma_start(at[:, 1, :], a["L0_gnn_attn_r"].rearrange("h c -> (h c)").partition_broadcast(P)).then_inc(weights, 16)
                sp.dma_start(iall[:, 0, :], a["first_src"]).then_inc(weights, 16)
                sp.dma_start(iall[:, 1, :], a["first_dst"]).then_inc(weights, 16)
                sp.wait_ge(weights, 80)
                for x in stored:
                    x.open(sp)

                def group(n, b, g):
                    rows_ready[b].hold(sp, n, 1)
                    sp.dma_start(table[bass.ds(g * GC, GC), :].rearrange("(t p) c -> p t c", p=P), row[:, b]).then_inc(stored[b].sem, 16)
                    sp.dma_start(ltable[bass.ds(g * GC, GC), :].rearrange("(t p) c -> p t c", p=P), left[:, b]).then_inc(stored[b].sem, 16)

                groups(sp, group)
                stored[0].wait(sp, NG // 2 + 1)
                stored[1].wait(sp, NG // 2)

            @block.scalar
            def _(act):
                for x in copied:
                    x.open(act)

                def group(n, b, g):
                    projected[b].wait(act, n)
                    nc.scalar.activation(xs[:, b], k.XT[:, :, bass.ds(g * GC, GC)], ACT.Copy).then_inc(copied[b].sem, 1)

                groups(act, group)

            @block.tensor
            def _(pe):
                for x in projected:
                    x.open(pe)
                pe.wait_ge(weights, 80)

                def group(n, b, g):
                    copied[b].wait(pe, n, 1)
                    rows_ready[b].wait(pe, n)
                    for t in range(GT):
                        for c in range(KD):
                            last = nc.tensor.matmul(pr[:, b, t, :], xs[:, b, c, t * P:(t + 1) * P], w[:, c, :],
                                                    start=c == 0, stop=c == KD - 1)
                    last.then_inc(projected[b].sem, 1)

                groups(pe, group)

            @block.vector
            def _(dve):
                for x in rows_ready:
                    x.open(dve)
                dve.wait_ge(weights, 80)
                chain = Chain(dve, order)

                def group(n, b, g):
                    if b == 0:
                        chain.fresh()
                    projected[b].wait(dve, n, 1)
                    stored[b].wait(dve, n)
                    for side in range(2):
                        last = nc.vector.tensor_tensor(prod[:, side], pr[:, b, 0:GT, :], at[:, side:side + 1, :].to_broadcast((P, GT, D)), ALU.mult)
                    chain(last)
                    for side, out in ((0, left[:, b]), (1, row[:, b, :, D:R0])):
                        nc.vector.tensor_reduce(out, prod[:, side].rearrange("p t (h c) -> p t h c", h=H0), AX.X, ALU.add)
                    nc.vector.tensor_copy(row[:, b, :, 0:D], pr[:, b, 0:GT, :]).then_inc(rows_ready[b].sem, 1)
                    rows_ready[b].wait(dve, n, 1)

                groups(dve, group)

        got, gotl = row, left
        al = s.sb("al", [P, 2, GT, H0])
        mx = s.sb("mx", [P, 2, GT])
        mix = s.sb("mix", [P, GT, C0])
        gathered = [s.pool_dma_sem(f"gathered{b}") for b in range(2)]
        used, logits, exps = (s.sem(n) for n in ("used", "logits", "exps"))
        with nc.Block() as block:
            @block.gpsimd
            def _(pool):
                for i in range(NG):
                    if i >= 2:
                        pool.wait_ge(used, i - 1)
                        pool.sem_inc(Tally.held, 1)
                    for t in range(GT):
                        n = i * GT + t
                        nc.gpsimd.indirect_dma_start(got[:, i % 2, t, :], None, table, bass.IndirectOffsetOnAxis(ap=iall[:, 1, n:n + 1], axis=0)).then_inc(gathered[i % 2], 16)
                        nc.gpsimd.indirect_dma_start(gotl[:, i % 2, t, :], None, ltable, bass.IndirectOffsetOnAxis(ap=iall[:, 0, n:n + 1], axis=0)).then_inc(gathered[i % 2], 16)

            @block.scalar
            def _(act):
                for i in range(NG):
                    act.wait_ge(logits, i + 1)
                    nc.scalar.activation(al[:, 0], al[:, 0], ACT.Exp).then_inc(exps, 1)

            @block.vector
            def _(dve):
                chain = Chain(dve, order)
                chain.fresh()
                for i in range(NG):
                    rows = got[:, i % 2]
                    dve.wait_ge(gathered[i % 2], (i // 2 + 1) * 32 * GT)
                    v, wt = al[:, 0], al[:, 1]
                    chain(nc.vector.tensor_tensor(v, gotl[:, i % 2], rows[:, :, D:R0], ALU.add))
                    chain(nc.vector.scalar_tensor_tensor(v, v, 0.01, v, ALU.mult, ALU.max))
                    chain(nc.vector.tensor_reduce(mx[:, 0, :], v, AX.X, ALU.max))
                    nc.vector.tensor_tensor(v, v, mx[:, 0, :].unsqueeze(2).to_broadcast((P, GT, H0)), ALU.subtract).then_inc(logits, 1)
                    dve.wait_ge(exps, i + 1)
                    chain(nc.vector.tensor_reduce(mx[:, 1, :], v, AX.X, ALU.add))
                    chain(nc.vector.reciprocal(mx[:, 1, :], mx[:, 1, :]))
                    chain(nc.vector.tensor_tensor(wt, v, mx[:, 1, :].unsqueeze(2).to_broadcast((P, GT, H0)), ALU.mult))
                    product = prod[:, 0]
                    chain(nc.vector.tensor_tensor(product.rearrange("p t (h c) -> p t h c", h=H0),
                                                  rows[:, :, 0:D].rearrange("p t (h c) -> p t h c", h=H0),
                                                  wt.unsqueeze(3).to_broadcast((P, GT, H0, C0)), ALU.mult))
                    dve.sem_inc(used, 1)
                    chain(nc.vector.tensor_reduce(mix[:], product.rearrange("p t (h c) -> p t c h", h=H0), AX.X, ALU.add))
                    x = k.X[:, i * GT:(i + 1) * GT, :].rearrange("p t (h c) -> p t h c", h=H0)
                    chain(nc.vector.tensor_tensor(x, x, mix[:].unsqueeze(2).to_broadcast((P, GT, H0, C0)), ALU.add))


def mixer_phase(nc, k, a, ball):
    with ExitStack() as es:
        s = Scope(nc, es, "mix")
        wq = s.sb("wq", [P, KD, QC * P])
        col = s.sb("col", [P, 3, QC])
        pw = s.sb("pw", [P, QC, P])
        stats = s.sb("stats", [P, QC, 2 * NG, 6])
        mv = s.sb("mv", [P, QC, 2])
        bn = s.sb("bn", [P, 6, QC])
        ph = s.ps("ph", [P, 8, 512])
        loaded, order, aorder = s.sem("loaded"), s.sem("order"), s.sem("aorder")
        zeroed = s.sem("zeroed")
        product = s.tally("product", QC)
        counted = s.tally("counted", QC)
        var_ready, sd_ready = s.sem("var_ready"), s.sem("sd_ready")
        with nc.Block() as block:
            @block.sync
            def _(sp):
                sp.dma_start(wq[:], a["mix_wq"].rearrange("(k p) c -> p k c", p=P)).then_inc(loaded, 16)
                sp.dma_start(col[:], a["mix_col"].rearrange("j (c p) -> p j c", p=P), allow_slow_non_contiguous=True).then_inc(loaded, 16)
                sp.wait_ge(zeroed, 1)
                for b in range(4):
                    sp.dma_start(pw[b * 32:(b + 1) * 32, :, b * 32:(b + 1) * 32],
                                 a["mix_pw"].rearrange("(c b i) o -> b i c o", b=4, i=32)[b]).then_inc(loaded, 16)
                sp.wait_ge(loaded, 96)

            @block.gpsimd
            def _(pool):
                nc.gpsimd.memset(pw[:], 0.0).then_inc(zeroed, 1)

            @block.tensor
            def _(pe):
                product.open(pe)
                pe.wait_ge(loaded, 96)
                with pe.Fori(0, 2 * NG) as i:
                    for c in range(QC):
                        counted.wait(pe, i)
                        for kk in range(KD):
                            last = nc.tensor.matmul(ph[:, c, 0:HC], wq[:, kk, c * P:(c + 1) * P],
                                                    ball[:, kk, bass.ds(i * HC, HC)], start=kk == 0, stop=kk == KD - 1)
                        last.then_inc(product.sem, 1)

            @block.vector
            def _(dve):
                counted.open(dve)
                chain = Chain(dve, order)
                with dve.Fori(0, 2 * NG) as i:
                    for c in range(QC):
                        product.wait(dve, i, c + 1)
                        nc.vector.bn_stats(stats[:, c, bass.ds(i, 1), :].rearrange("p o s -> p (o s)"), ph[:, c, 0:HC]).then_inc(counted.sem, 1)
                dve.wait_ge(loaded, 96)
                counted.wait(dve, 2 * NG)
                for c in range(QC):
                    last = nc.vector.bn_aggr(mv[:, c, :], stats[:, c].rearrange("p i s -> p (i s)"))
                chain(last)
                mean, ex2, m2, var = (bn[:, j, :] for j in range(4))
                ratio = float(NP) / N
                chain(nc.vector.tensor_tensor(ex2, mv[:, :, 0], mv[:, :, 0], ALU.mult))
                chain(nc.vector.tensor_tensor(ex2, ex2, mv[:, :, 1], ALU.add))
                chain(nc.vector.tensor_scalar(mean, mv[:, :, 0], ratio, None, ALU.mult))
                chain(nc.vector.tensor_tensor(m2, mean, mean, ALU.mult))
                chain(nc.vector.scalar_tensor_tensor(var, ex2, ratio, m2, ALU.mult, ALU.subtract))
                nc.vector.tensor_scalar_max(var, var, 0.0).then_inc(var_ready, 1)
                dve.wait_ge(sd_ready, 1)
                chain(nc.vector.reciprocal(bn[:, 4, :], bn[:, 4, :]))
                chain(nc.vector.tensor_tensor(bn[:, 4, :], bn[:, 4, :], col[:, 0, :], ALU.mult))
                chain(nc.vector.tensor_tensor(mean, mean, bn[:, 4, :], ALU.mult))
                chain(nc.vector.tensor_tensor(bn[:, 5, :], col[:, 1, :], mean, ALU.subtract))
                chain(nc.vector.tensor_tensor(pw[:], pw[:], col[:, 2, :].unsqueeze(2).to_broadcast((P, QC, P)), ALU.mult))

            @block.scalar
            def _(act):
                act.wait_ge(var_ready, 1)
                nc.scalar.activation(bn[:, 4, :], bn[:, 3, :], ACT.Sqrt, bias=k.eps[:, 0:1]).then_inc(sd_ready, 1)

        wr = s.sb("wr", [P, 4, D])
        br = s.sb("br", [P, D])
        blk = s.sb("blk", [P, P])
        work = k.XT[:].rearrange("p k n -> p (k n)")[:, 0:28 * HC].rearrange("p (c n) -> p c n", n=HC)
        U, V = [work[:, 0:4], work[:, 4:8]], [work[:, 8:12], work[:, 12:16]]
        UK, VK, sq, tmp_u = work[:, 16:18], work[:, 18:20], work[:, 20:26], work[:, 26:28]
        tmp_v = s.sb("tmp_v", [P, 2, HC])
        ks = s.sb("ks", [P, 4, HC])
        O = s.sb("O", [P, 4, GC])
        g = s.sb("g", [P, 3, HC])
        node = s.sb("node", [P, 4, GT])
        ft = s.sb("ft", [P, GT, D])
        junk = s.sb("junk", [P, D])
        made = s.sem("made")
        h_done, u_ready = s.tally("h_done", QC), s.tally("u_ready", QC)
        s_done, u_summed, summed, k_summed, o_summed = (s.tally(n, 1) for n in ("s_done", "u_summed", "summed", "k_summed", "o_summed"))
        u_squared, s_ready, ks_ready, root, o_squared, o_root = (s.tally(n, 1) for n in ("u_squared", "s_ready", "ks_ready", "root", "o_squared", "o_root"))
        bounded, o_ready, o_scaled = (s.tally(n, 1) for n in ("bounded", "o_ready", "o_scaled"))
        ft_done, ft_copied, row_norms, ft_ready = (s.tally(n, 1) for n in ("ft_done", "ft_copied", "row_norms", "ft_ready"))

        def groups(eng, group):
            group(0, first=True)
            with eng.Fori(1, NG - 1) as i:
                group(i)
            group(NG - 1, last=True)

        with nc.Block() as block:
            @block.sync
            def _(sp):
                sp.dma_start(wr[:], a["L0_mix_w_res"]).then_inc(loaded, 16)
                sp.dma_start(br[:], a["L0_mix_b_res"].partition_broadcast(P)).then_inc(loaded, 16)
                sp.wait_ge(loaded, 128)

            @block.gpsimd
            def _(pool):
                nc.gpsimd.memset(blk[:], 0.0).then_inc(made, 1)
                pool.wait_ge(made, 1)
                for b in range(4):
                    nc.gpsimd.memset(blk[32 * b:32 * b + 32, 32 * b:32 * b + 32], 1.0).then_inc(made, 1)

            @block.tensor
            def _(pe):
                for x in (h_done, s_done, u_summed, summed, k_summed, o_summed, ft_done):
                    x.open(pe)
                pe.wait_ge(loaded, 128)
                pe.wait_ge(made, 5)

                def front(i, j):
                    f = i * 2 + j
                    ks_ready.wait(pe, f)
                    for c in range(QC):
                        for kk in range(KD):
                            last = nc.tensor.matmul(ph[:, c, 0:HC], wq[:, kk, c * P:(c + 1) * P],
                                                    ball[:, kk, bass.ds(i * GC + j * HC, HC)], start=kk == 0, stop=kk == KD - 1)
                        last.then_inc(h_done.sem, 1)
                    for c in range(QC):
                        u_ready.wait(pe, f, c + 1)
                        last = nc.tensor.matmul(ph[:, c, 0:HC], pw[:, c, :], U[j][:, c, :] if c < 4 else UK[:, c - 4, :], start=True, stop=True)
                    last.then_inc(s_done.sem, 1)
                    u_squared.wait(pe, f, 1)
                    bounded.wait(pe, f)
                    for c in range(QC):
                        last = nc.tensor.matmul(ph[:, 6, 0:HC], k.ones[:], sq[:, c, :], start=c == 0, stop=False)
                    last.then_inc(u_summed.sem, 1)
                    s_ready.wait(pe, f, 1)
                    for c in range(QC):
                        last = nc.tensor.matmul(ph[:, 6, 0:HC], k.ones[:], sq[:, c, :], start=False, stop=c == QC - 1)
                    last.then_inc(summed.sem, 1)
                    for m in range(4):
                        last = nc.tensor.matmul(ph[:, m, 0:HC], blk[:], UK[:, m, :] if m < 2 else VK[:, m - 2, :], start=True, stop=True)
                    last.then_inc(k_summed.sem, 1)

                def back(i, j):
                    f = i * 2 + j
                    o_squared.wait(pe, f, 1)
                    o_root.wait(pe, f)
                    for m in range(4):
                        last = nc.tensor.matmul(ph[:, 7, 0:HC], k.ones[:], U[j][:, m, :], start=m == 0, stop=m == 3)
                    last.then_inc(o_summed.sem, 1)

                def group(i, first=False, last=False):
                    if not first:
                        ft_copied.wait(pe, i)
                    front(i, 1)
                    back(i, 0)
                    if not last:
                        front(i + 1, 0)
                    back(i, 1)
                    o_scaled.wait(pe, i * 2, 2)
                    ks_ready.wait(pe, i * 2, 2 if last else 3)
                    for t in range(GT):
                        for m in range(4):
                            mm = nc.tensor.matmul(ph[:, t // 2, (t % 2) * D:(t % 2 + 1) * D], O[:, m, t * P:(t + 1) * P],
                                                  wr[:, m, :], start=m == 0, stop=m == 3)
                    mm.then_inc(ft_done.sem, 1)

                front(0, 0)
                groups(pe, group)

            @block.scalar
            def _(act):
                for x in (u_ready, u_squared, s_ready, ks_ready, root, o_squared, o_root, ft_copied, row_norms):
                    x.open(act)
                chain = Chain(act, aorder)

                def front(i, j):
                    f = i * 2 + j
                    o_summed.wait(act, max(f - 1, 0) if isinstance(f, int) else f - 1)
                    for c in range(QC):
                        h_done.wait(act, f, c + 1)
                        nc.scalar.activation(U[j][:, c, :] if c < 4 else UK[:, c - 4, :], ph[:, c, 0:HC], ACT.Relu,
                                             bias=bn[:, 5, c:c + 1], scale=bn[:, 4, c:c + 1]).then_inc(u_ready.sem, 1)
                    u_ready.wait(act, f, QC)
                    nc.scalar.activation(sq[:, 0:4, :], U[j], ACT.Square)
                    nc.scalar.activation(sq[:, 4:6, :], UK, ACT.Square).then_inc(u_squared.sem, 1)
                    s_done.wait(act, f, 1)
                    nc.scalar.activation(V[j][:, 0:2, :], ph[:, 0:2, 0:HC], ACT.Relu)
                    nc.scalar.activation(V[j][:, 2:4, :], ph[:, 2:4, 0:HC], ACT.Copy)
                    nc.scalar.activation(VK, ph[:, 4:6, 0:HC], ACT.Relu)
                    u_summed.wait(act, f, 1)
                    nc.scalar.activation(sq, ph[:, 0:6, 0:HC], ACT.Square).then_inc(s_ready.sem, 1)

                def k_sums(i, j):
                    f = i * 2 + j
                    k_summed.wait(act, f, 1)
                    o_ready.wait(act, f)
                    nc.scalar.activation(ks[:], ph[:, 0:4, 0:HC], ACT.Copy).then_inc(ks_ready.sem, 1)

                def norm(i, j):
                    bounded.wait(act, i * 2 + j, 1)
                    nc.scalar.activation(g[:, 1, :], g[:, 0, :], ACT.Sqrt).then_inc(root.sem, 1)

                def output_norm(i, j):
                    f = i * 2 + j
                    o_ready.wait(act, f, 1)
                    nc.scalar.activation(U[j][:, 0:2, :], tmp_u, ACT.Square)
                    nc.scalar.activation(U[j][:, 2:4, :], tmp_v[:], ACT.Square).then_inc(o_squared.sem, 1)
                    o_summed.wait(act, f, 1)
                    nc.scalar.activation(g[:, 2, :], ph[:, 7, 0:HC], ACT.Sqrt, scale=ATANH_MAX ** -2).then_inc(o_root.sem, 1)

                def rows(i):
                    ft_ready.wait(act, i, 1)
                    for t in range(GT):
                        chain(nc.scalar.activation(junk[:], ft[:, t, :], ACT.Square, accum_out=node[:, 0, t:t + 1]))
                    chain(nc.scalar.activation(node[:, 1, :], node[:, 0, :], ACT.Sqrt))
                    nc.scalar.activation(node[:, 2, :], node[:, 1, :], ACT.Tanh).then_inc(row_norms.sem, 1)

                def group(i, first=False, last=False):
                    chain.fresh()
                    norm(i, 0)
                    front(i, 1)
                    if not first:
                        rows(i - 1)
                    output_norm(i, 0)
                    k_sums(i, 1)
                    norm(i, 1)
                    if not last:
                        front(i + 1, 0)
                    output_norm(i, 1)
                    if not last:
                        k_sums(i + 1, 0)
                    ft_done.wait(act, i, 1)
                    nc.scalar.activation(ft[:], ph[:, 0:4, :].rearrange("p b c -> p (b c)")[:, 0:GT * D].rearrange("p (t c) -> p t c", c=D),
                                         ACT.Copy).then_inc(ft_copied.sem, 1)
                    if last:
                        rows(i)

                front(0, 0)
                k_sums(0, 0)
                groups(act, group)

            @block.vector
            def _(dve):
                for x in (bounded, o_ready, o_scaled, ft_ready):
                    x.open(dve)
                chain = Chain(dve, order)
                chain.fresh()
                dve.wait_ge(loaded, 128)

                def bias(i):
                    ft_copied.wait(dve, i, 1)
                    nc.vector.tensor_tensor(ft[:], ft[:], br[:].unsqueeze(1).to_broadcast((P, GT, D)), ALU.add).then_inc(ft_ready.sem, 1)

                def finish(i):
                    row_norms.wait(dve, i, 1)
                    chain(nc.vector.tensor_scalar_max(node[:, 1, :], node[:, 1, :], MIN_NORM))
                    chain(nc.vector.reciprocal(node[:, 1, :], node[:, 1, :]))
                    chain(nc.vector.scalar_tensor_tensor(node[:, 3, :], node[:, 2, :], MAXNORM, node[:, 1, :], ALU.min, ALU.mult))
                    for t in range(GT):
                        x = k.X[:, i * GT + t, :] if isinstance(i, int) else tile_of(k.X, i * GT + t)
                        last = nc.vector.scalar_tensor_tensor(x, ft[:, t, :], node[:, 3, t:t + 1], x, ALU.mult, ALU.add)
                    chain(last)

                def half(i, j, meanwhile):
                    f = i * 2 + j
                    q_v = ((tmp_u, U[j]), (tmp_v[:], V[j]))
                    summed.wait(dve, f, 1)
                    nc.vector.tensor_scalar(g[:, 0, :], ph[:, 6, 0:HC], ATANH_MAX ** -2, 1.0, ALU.mult, ALU.max).then_inc(bounded.sem, 1)
                    root.wait(dve, f, 1)
                    for x, qv in q_v:
                        last = nc.vector.scalar_tensor_tensor(x, g[:, 1:2, :].to_broadcast((P, 2, HC)), ATT_EPS, qv[:, 2:4], ALU.mult, ALU.add)
                    chain(last)
                    for x, qv in q_v:
                        last = nc.vector.reciprocal(x, x)
                    chain(last)
                    for c in (2, 0):
                        for x, qv in q_v:
                            last = nc.vector.tensor_tensor(x, x, qv[:, c:c + 2], ALU.mult)
                        chain(last)
                    if meanwhile:
                        bias(i - 1)
                    ks_ready.wait(dve, f, 1)
                    nc.vector.tensor_tensor(tmp_u, tmp_u, ks[:, 0:2], ALU.mult)
                    nc.vector.tensor_tensor(tmp_v[:], tmp_v[:], ks[:, 2:4], ALU.mult).then_inc(o_ready.sem, 1)
                    if meanwhile:
                        finish(i - 1)
                    o_root.wait(dve, f, 1)
                    chain(nc.vector.tensor_tensor(g[:, 2, :], g[:, 2, :], g[:, 0, :], ALU.max))
                    chain(nc.vector.reciprocal(g[:, 2, :], g[:, 2, :]))
                    ft_done.wait(dve, i)
                    scale = g[:, 2:3, :].to_broadcast((P, 2, HC))
                    nc.vector.tensor_tensor(O[:, 0:2, j * HC:(j + 1) * HC], tmp_u, scale, ALU.mult)
                    nc.vector.tensor_tensor(O[:, 2:4, j * HC:(j + 1) * HC], tmp_v[:], scale, ALU.mult).then_inc(o_scaled.sem, 1)
                    o_scaled.wait(dve, f, 1)

                def group(i, first=False, last=False):
                    chain.fresh()
                    half(i, 0, not first)
                    half(i, 1, False)
                    if last:
                        bias(i)
                        finish(i)

                groups(dve, group)


def leaky(chain, dve, x, slope):
    chain(dve.scalar_tensor_tensor(x, x, slope, x, ALU.mult, ALU.max))


def gate_phase(nc, k, a, gates, early):
    with ExitStack() as es:
        s = Scope(nc, es, "gate")
        wg = s.sb("wg", [P, KD, GW])
        att = s.sb("att", [P, 4, GW])
        bg = s.sb("bg", [P, GW])
        hs = s.sb("hs", [P, NT, MW])
        td = s.sb("td", [P, NT, 2 * GH])
        own = s.sb("own", [P, NT, MW])
        ew = s.sb("ew", [P, NT, GW])
        si = s.sb("si", [P, S0 + 2 * U0], I32)
        di = s.sb("di", [P, S0 + 2 * U0], I32)
        lo = s.sb("lo", [P, S0])
        hi = s.sb("hi", [P, S0])
        ti = s.sb("ti", [P, S0], I32)
        small = s.sb("small", [P, 16])
        stable, dtable = k.dram("gate_stable", (NP, MW)), k.dram("gate_dtable", (NP, 2 * GH))
        loaded, order = s.sem("loaded"), s.sem("order")
        tables_ready, stored = s.sem("tables_ready"), s.sem("stored")
        top = s.sem("top")
        es2 = ExitStack()
        with es2:
            s2 = Scope(nc, es2, "gate1")
            xs = s2.sb("xs", [P, KD, GC])
            pg = s2.ps("pg", [P, 3, 512])
            copied, projected, taken = s2.tally("copied", 1), s2.tally("projected", 1), s2.tally("taken", 1)
            logits, exps = s2.sem("logits"), s2.sem("exps")
            with nc.Block() as block:
                @block.sync
                def _(sp):
                    sp.dma_start(wg[:], a["L0_ffn_W_gat"].rearrange("(k p) c -> p k c", p=P)).then_inc(loaded, 16)
                    sp.dma_start(att[:, 0, :], a["L0_ffn_att_src"].rearrange("h e -> (h e)").partition_broadcast(P)).then_inc(loaded, 16)
                    sp.dma_start(att[:, 1, :], a["L0_ffn_att_dst"].rearrange("h e -> (h e)").partition_broadcast(P)).then_inc(loaded, 16)
                    sp.dma_start(att[:, 2, :], a["L0_ffn_ln_gamma"].partition_broadcast(P)).then_inc(loaded, 16)
                    sp.dma_start(att[:, 3, :], a["L0_ffn_ln_beta"].partition_broadcast(P)).then_inc(loaded, 16)
                    sp.dma_start(bg[:], a["L0_ffn_b_gat"].partition_broadcast(P)).then_inc(loaded, 16)
                    sp.dma_start(si[:, 0:S0], a["L0_ffn_edge_index"][0]).then_inc(loaded, 16)
                    sp.dma_start(di[:, 0:S0], a["L0_ffn_edge_index"][1]).then_inc(loaded, 16)
                    sp.wait_ge(loaded, 128)
                    sp.wait_ge(tables_ready, 1)
                    sp.dma_start(stable.rearrange("(t p) c -> p t c", p=P), hs[:]).then_inc(stored, 16)
                    sp.dma_start(dtable.rearrange("(t p) c -> p t c", p=P), td[:]).then_inc(stored, 16)
                    sp.wait_ge(stored, 32)

                @block.scalar
                def _(act):
                    copied.open(act)
                    with act.Fori(0, NG) as i:
                        projected.wait(act, i)
                        nc.scalar.activation(xs[:], k.XT[:, :, bass.ds(i * GC, GC)], ACT.Copy).then_inc(copied.sem, 1)
                    act.wait_ge(logits, 1)
                    nc.scalar.activation(own[:, :, GW:MW], own[:, :, GW:MW], ACT.Exp).then_inc(exps, 1)

                @block.tensor
                def _(pe):
                    projected.open(pe)
                    pe.wait_ge(loaded, 128)
                    with pe.Fori(0, NG) as i:
                        copied.wait(pe, i, 1)
                        taken.wait(pe, i)
                        for t in range(GT):
                            for c in range(KD):
                                last = nc.tensor.matmul(pg[:, 0, t * GW:(t + 1) * GW], xs[:, c, t * P:(t + 1) * P], wg[:, c, :],
                                                        start=c == 0, stop=c == KD - 1)
                        last.then_inc(projected.sem, 1)
                    pe.wait_ge(top, 1)
                    nc.tensor.transpose(pg[0:GH, 1, 0:P], small[:, 0:GH], k.ident[:]).then_inc(top, 1)
                    pe.wait_ge(top, 3)
                    nc.tensor.matmul(pg[:, 2, 0:GH], k.ones[0:GH, :], small[0:GH, 8:8 + GH], start=True, stop=True).then_inc(top, 1)

                @block.vector
                def _(dve):
                    taken.open(dve)
                    chain = Chain(dve, order)
                    dve.wait_ge(loaded, 128)
                    with dve.Fori(0, NG) as i:
                        projected.wait(dve, i, 1)
                        nc.vector.tensor_copy(hs[:, bass.ds(i * GT, GT), 0:GW], pg[:, 0, 0:GT * GW].rearrange("p (t c) -> p t c", c=GW)).then_inc(taken.sem, 1)
                    taken.wait(dve, NG)
                    h = hs[:, :, 0:GW]
                    for side, out in ((0, hs[:, :, GW:MW]), (1, td[:, :, 0:GH])):
                        chain(nc.vector.tensor_tensor(ew[:], h, att[:, side:side + 1, :].to_broadcast((P, NT, GW)), ALU.mult))
                        chain(nc.vector.tensor_reduce(out, ew[:].rearrange("p t (h e) -> p t h e", e=E0), AX.X, ALU.add))
                    chain(nc.vector.tensor_scalar(ew[:, :, 4], k.valid[:], BIG, -BIG, ALU.mult, ALU.add))
                    chain(nc.vector.tensor_tensor(ew[:, :, 0:GH], hs[:, :, GW:MW], ew[:, :, 4:5].to_broadcast((P, NT, GH)), ALU.add))
                    nc.vector.tensor_reduce(small[:, 0:GH], ew[:, :, 0:GH].rearrange("p t h -> p h t"), AX.X, ALU.max).then_inc(top, 1)
                    chain(nc.vector.tensor_single_scalar(ti[:], di[:, 0:S0], 7, ALU.arith_shift_right))
                    chain(nc.vector.tensor_copy(hi[:], ti[:]))
                    chain(nc.vector.tensor_single_scalar(ti[:], di[:, 0:S0], P - 1, ALU.bitwise_and))
                    chain(nc.vector.tensor_copy(lo[:], ti[:]))
                    nc.vector.memset(si[:, S0:], 0)
                    nc.vector.memset(di[:, S0:], 0)
                    chain(nc.vector.tensor_scalar_min(si[:, 0:S0], si[:, 0:S0], N - 1))
                    chain(nc.vector.tensor_scalar_min(di[:, 0:S0], di[:, 0:S0], N - 1))
                    dve.wait_ge(top, 2)
                    chain(nc.vector.tensor_reduce(small[0:GH, 4:5], pg[0:GH, 1, 0:P], AX.X, ALU.max))
                    nc.vector.tensor_scalar(small[0:GH, 8:8 + GH], k.ident[0:GH, 0:GH], small[0:GH, 4:5], None, ALU.mult).then_inc(top, 1)
                    dve.wait_ge(top, 4)
                    shift, e = td[:, :, GH:2 * GH], own[:, :, GW:MW]
                    chain(nc.vector.tensor_copy(small[:, 12:16], pg[:, 2, 0:GH]))
                    chain(nc.vector.tensor_tensor(shift, td[:, :, 0:GH], small[:, 12:16].unsqueeze(1).to_broadcast((P, NT, GH)), ALU.add))
                    leaky(chain, nc.vector, shift, 0.2)
                    dve.sem_inc(tables_ready, 1)
                    chain(nc.vector.tensor_tensor(e, hs[:, :, GW:MW], td[:, :, 0:GH], ALU.add))
                    leaky(chain, nc.vector, e, 0.2)
                    nc.vector.tensor_tensor(e, e, shift, ALU.subtract).then_inc(logits, 1)
                    dve.wait_ge(exps, 1)
                    chain(nc.vector.tensor_tensor(own[:, :, 0:GW].rearrange("p t (h e) -> p t h e", e=E0),
                                                  h.rearrange("p t (h e) -> p t h e", e=E0),
                                                  e.unsqueeze(3).to_broadcast((P, NT, GH, E0)), ALU.mult))

        B0 = (NT // 2 + 1) * MW
        iota_lo = s.sb("iota_lo", [P, P])
        iota_hi = s.sb("iota_hi", [P, NT])
        zero = s.sb("zero", [P, 512])
        sums = s.ps("sums", [P, 2, 512])
        with ExitStack() as es2:
            s2 = Scope(nc, es2, "gate2")
            idx = s2.sb("idx", [P, 2, 2, U0], I32)
            gs = s2.sb("gs", [P, 2, U0, MW])
            gd = s2.sb("gd", [P, 2, U0, 2 * GH])
            msg = s2.sb("msg", [P, U0, MW])
            hot = s2.sb("hot", [P, U0, NT])
            pick = s2.sb("pick", [P, 2, 4, P])
            wide = s2.sb("wide", [P, 2, 4, NT * MW])
            made = s2.sem("made")
            indexed = s2.tally("indexed", 2)
            gathered = [s2.pool_dma_tally(f"gathered{b}", 32 * U0) for b in range(2)]
            logits, exps = s2.tally("logits", 2), s2.tally("exps", 2)
            expanded, summed = s2.tally("expanded", 4), s2.tally("summed", 4)
            FC = F0 // P
            w1 = s2.sb("w1", [P, 2, KD, F0])
            w2 = s2.sb("w2", [P, 2, FC, D])
            b1 = s2.sb("b1", [P, 2, FC])
            hid = s2.sb("hid", [P, 2, FC, P])
            y = s2.sb("y", [P, 2, D])
            eh = s2.ps("eh", [P, 2, 512])
            ey = s2.ps("ey", [P, 2, D])
            weights = s2.sem("weights")
            h_done, gelus = s2.tally("h_done", 2), s2.tally("gelus", 2)
            y_done, y_ready, y_stored = s2.tally("y_done", 1), s2.tally("y_ready", 1), s2.tally("y_stored", 16)
            PASSES = S0 // (2 * U0)
            assert PASSES > NT

            def passes(eng, body):
                with eng.Fori(0, NT) as i:
                    body(i, True)
                with eng.Fori(NT, PASSES) as i:
                    body(i, False)
            with nc.Block() as block:
                @block.gpsimd
                def _(pool):
                    nc.gpsimd.memset(zero[:], 0.0).then_inc(made, 1)
                    nc.gpsimd.iota(iota_lo[:], pattern=[[1, P]], base=0, channel_multiplier=0, allow_small_or_imprecise_dtypes=True).then_inc(made, 1)
                    nc.gpsimd.iota(iota_hi[:], pattern=[[1, NT]], base=0, channel_multiplier=0, allow_small_or_imprecise_dtypes=True).then_inc(made, 1)
                    with pool.Fori(0, S0 // (2 * U0)) as i:
                        for b in range(2):
                            indexed.hold(pool, i, b + 1)
                            for u in range(U0):
                                nc.gpsimd.indirect_dma_start(gs[:, b, u, :], None, stable, bass.IndirectOffsetOnAxis(ap=idx[:, 0, b, u:u + 1], axis=0)).then_inc(gathered[b].sem, 16)
                                nc.gpsimd.indirect_dma_start(gd[:, b, u, :], None, dtable, bass.IndirectOffsetOnAxis(ap=idx[:, 1, b, u:u + 1], axis=0)).then_inc(gathered[b].sem, 16)

                @block.scalar
                def _(act):
                    for x in (exps, gelus, y_ready):
                        x.open(act)
                    act.wait_ge(weights, 96)

                    def body(i, tile):
                        for b in range(2):
                            logits.wait(act, i, b + 1)
                            nc.scalar.activation(msg[:, :, GW:MW], msg[:, :, GW:MW], ACT.Exp).then_inc(exps.sem, 1)
                            if tile and b == 0:
                                y_done.wait(act, i)
                                for e in range(2):
                                    h_done.wait(act, i, e + 1)
                                    for f in range(FC):
                                        last = nc.scalar.activation(hid[:, e, f, :], eh[:, e, f * P:(f + 1) * P], ACT.Gelu, bias=b1[:, e, f:f + 1])
                                    last.then_inc(gelus.sem, 1)
                        if tile:
                            y_done.wait(act, i, 1)
                            y_stored.wait(act, i)
                            nc.scalar.activation(y[:], ey[:], ACT.Copy).then_inc(y_ready.sem, 1)

                    passes(act, body)

                @block.sync
                def _(sp):
                    y_stored.open(sp)
                    for e in range(2):
                        sp.dma_start(w1[:, e], a["L0_ffn_W1"][e].rearrange("(k p) f -> p k f", p=P)).then_inc(weights, 16)
                        sp.dma_start(w2[:, e], a["L0_ffn_W2"][e].rearrange("(k p) f -> p k f", p=P)).then_inc(weights, 16)
                        sp.dma_start(b1[:, e, :], a["L0_ffn_b1"][e].rearrange("(f p) -> p f", p=P), allow_slow_non_contiguous=True).then_inc(weights, 16)
                    with sp.Fori(0, NT) as i:
                        y_ready.hold(sp, i, 1)
                        sp.dma_start(early[:, bass.ds(i * P, P), :].rearrange("e p d -> p e d"), y[:]).then_inc(y_stored.sem, 16)
                    y_stored.wait(sp, NT)

                @block.vector
                def _(dve):
                    for x in (indexed, logits, expanded):
                        x.open(dve)
                    dve.wait_ge(made, 3)
                    chain = Chain(dve, order)
                    chain.fresh()

                    def index(step, b):
                        nc.vector.tensor_copy(idx[:, 0, b, :], si[:, bass.ds(step, U0)])
                        nc.vector.tensor_copy(idx[:, 1, b, :], di[:, bass.ds(step, U0)]).then_inc(indexed.sem, 1)

                    index(0, 0)
                    index(U0, 1)
                    with dve.Fori(0, S0 // (2 * U0)) as i:
                        chain.fresh()
                        for b in range(2):
                            step = i * (2 * U0) + b * U0
                            gathered[b].wait(dve, i, 32 * U0)
                            e = msg[:, :, GW:MW]
                            chain(nc.vector.tensor_tensor(e, gs[:, b, :, GW:MW], gd[:, b, :, 0:GH], ALU.add))
                            leaky(chain, nc.vector, e, 0.2)
                            nc.vector.tensor_tensor(e, e, gd[:, b, :, GH:2 * GH], ALU.subtract).then_inc(logits.sem, 1)
                            chain(nc.vector.tensor_tensor(hot[:], iota_hi[:].unsqueeze(1).to_broadcast((P, U0, NT)),
                                                          hi[:, bass.ds(step, U0)].unsqueeze(2).to_broadcast((P, U0, NT)), ALU.is_equal))
                            exps.wait(dve, i, b + 1)
                            chain(nc.vector.tensor_tensor(msg[:, :, 0:GW].rearrange("p u (h e) -> p u h e", e=E0),
                                                          gs[:, b, :, 0:GW].rearrange("p u (h e) -> p u h e", e=E0),
                                                          e.unsqueeze(3).to_broadcast((P, U0, GH, E0)), ALU.mult))
                            nc.vector.tensor_copy(idx[:, 0, b, :], si[:, bass.ds((i * (2 * U0) + (b + 2) * U0), U0)])
                            nc.vector.tensor_copy(idx[:, 1, b, :], di[:, bass.ds((i * (2 * U0) + (b + 2) * U0), U0)]).then_inc(indexed.sem, 1)
                            for q in range(2):
                                summed.wait(dve, i, 2 * b + q - 1)
                                u0 = 4 * q
                                nc.vector.tensor_tensor(pick[:, q], iota_lo[:].unsqueeze(1).to_broadcast((P, 4, P)),
                                                        lo[:, bass.ds(step + u0, 4)].unsqueeze(2).to_broadcast((P, 4, P)), ALU.is_equal)
                                nc.vector.tensor_tensor(wide[:, q].rearrange("p u (n c) -> p u n c", c=MW),
                                                        hot[:, u0:u0 + 4, :].unsqueeze(3).to_broadcast((P, 4, NT, MW)),
                                                        msg[:, u0:u0 + 4, :].unsqueeze(2).to_broadcast((P, 4, NT, MW)), ALU.mult).then_inc(expanded.sem, 1)
                            expanded.wait(dve, i, 2 * b + 2)

                @block.tensor
                def _(pe):
                    for x in (summed, h_done, y_done):
                        x.open(pe)
                    pe.wait_ge(made, 3)
                    pe.wait_ge(weights, 96)
                    for c, w in ((0, B0), (1, NT * MW - B0)):
                        nc.tensor.matmul(sums[:, c, 0:w], zero[:, 0:P], zero[:, 0:w], start=True, stop=False)

                    def hidden(i):
                        for e in range(2):
                            gelus.wait(pe, i)
                            for f in range(FC):
                                for c in range(KD):
                                    last = nc.tensor.matmul(eh[:, e, f * P:(f + 1) * P], w1[:, e, c, f * P:(f + 1) * P],
                                                            k.XT[:, c, bass.ds(i * P, P)], start=c == 0, stop=c == KD - 1)
                            last.then_inc(h_done.sem, 1)

                    def down(i):
                        gelus.wait(pe, i, 2)
                        y_ready.wait(pe, i)
                        for e in range(2):
                            for f in range(FC):
                                last = nc.tensor.matmul(ey[:, e, :], hid[:, e, f, :], w2[:, e, f, :], start=f == 0, stop=f == FC - 1)
                        last.then_inc(y_done.sem, 1)

                    def body(i, tile):
                        if tile:
                            hidden(i)
                        for j in range(4):
                            expanded.wait(pe, i, j + 1)
                            for u in range(4):
                                nc.tensor.matmul(sums[:, 0, 0:B0], pick[:, j % 2, u, :], wide[:, j % 2, u, 0:B0], start=False, stop=False)
                                last = nc.tensor.matmul(sums[:, 1, 0:NT * MW - B0], pick[:, j % 2, u, :], wide[:, j % 2, u, B0:], start=False, stop=False)
                            last.then_inc(summed.sem, 1)
                            if tile and j == 1:
                                down(i)

                    passes(pe, body)
                    for c, w in ((0, B0), (1, NT * MW - B0)):
                        nc.tensor.matmul(sums[:, c, 0:w], zero[:, 0:P], zero[:, 0:w], start=False, stop=True)

        with ExitStack() as es2:
            s2 = Scope(nc, es2, "gate3")
            agg = s2.sb("agg", [P, NT, GW])
            t4 = s2.sb("t4", [P, 6, NT, E0])
            t1 = s2.sb("t1", [P, 3, NT])
            steps, asteps = s2.sem("steps"), s2.sem("asteps")
            with nc.Block() as block:
                @block.vector
                def _(dve):
                    chain = Chain(dve, order)
                    chain.fresh()

                    def over(x, w):
                        return x.unsqueeze(2).to_broadcast((P, NT, w))

                    n0 = B0 // MW
                    nc.vector.tensor_tensor(own[:, 0:n0, :], own[:, 0:n0, :], sums[:, 0, 0:B0].rearrange("p (t c) -> p t c", c=MW), ALU.add)
                    chain(nc.vector.tensor_tensor(own[:, n0:, :], own[:, n0:, :], sums[:, 1, 0:NT * MW - B0].rearrange("p (t c) -> p t c", c=MW), ALU.add))
                    chain(nc.vector.reciprocal(own[:, :, GW:MW], own[:, :, GW:MW]))
                    chain(nc.vector.tensor_tensor(agg[:].rearrange("p t (h e) -> p t h e", e=E0),
                                                  own[:, :, 0:GW].rearrange("p t (h e) -> p t h e", e=E0),
                                                  own[:, :, GW:MW].unsqueeze(3).to_broadcast((P, NT, GH, E0)), ALU.mult))
                    chain(nc.vector.tensor_tensor(agg[:], agg[:], bg[:].unsqueeze(1).to_broadcast((P, NT, GW)), ALU.add))
                    mean, var, r = (t1[:, j, :] for j in range(3))
                    chain(nc.vector.tensor_reduce(mean, agg[:], AX.X, ALU.add))
                    chain(nc.vector.tensor_scalar(mean, mean, 1.0 / GW, None, ALU.mult))
                    chain(nc.vector.tensor_tensor(agg[:], agg[:], over(mean, GW), ALU.subtract))
                    chain(nc.vector.tensor_tensor(ew[:], agg[:], agg[:], ALU.mult))
                    chain(nc.vector.tensor_reduce(var, ew[:], AX.X, ALU.add))
                    nc.vector.tensor_scalar(var, var, 1.0 / GW, None, ALU.mult).then_inc(steps, 1)
                    dve.wait_ge(asteps, 1)
                    chain(nc.vector.reciprocal(r, r))
                    chain(nc.vector.tensor_tensor(agg[:], agg[:], over(r, GW), ALU.mult))
                    chain(nc.vector.tensor_tensor(agg[:], agg[:], att[:, 2:3, :].to_broadcast((P, NT, GW)), ALU.mult))
                    chain(nc.vector.tensor_tensor(agg[:], agg[:], att[:, 3:4, :].to_broadcast((P, NT, GW)), ALU.add))
                    score, rank, ge, ex = (t4[:, j] for j in range(4))
                    chain(nc.vector.tensor_reduce(score, agg[:].rearrange("p t (h e) -> p t e h", e=E0), AX.X, ALU.add))
                    chain(nc.vector.tensor_scalar(score, score, 1.0 / GH, None, ALU.mult))
                    chain(nc.vector.memset(rank, 0.0))
                    for e in range(E0):
                        for o in range(E0):
                            if o != e:
                                chain(nc.vector.tensor_tensor(ge[:, :, 0], score[:, :, o], score[:, :, e], ALU.is_ge if o < e else ALU.is_gt))
                                chain(nc.vector.tensor_tensor(rank[:, :, e], rank[:, :, e], ge[:, :, 0], ALU.add))
                    chain(nc.vector.tensor_scalar(rank, rank, 1.5, None, ALU.is_lt))
                    chain(nc.vector.tensor_reduce(mean, score, AX.X, ALU.max))
                    nc.vector.tensor_tensor(ex, score, over(mean, E0), ALU.subtract).then_inc(steps, 1)
                    dve.wait_ge(asteps, 2)
                    chain(nc.vector.tensor_tensor(ex, ex, rank, ALU.mult))
                    chain(nc.vector.tensor_reduce(var, ex, AX.X, ALU.add))
                    chain(nc.vector.reciprocal(var, var))
                    chain(nc.vector.tensor_tensor(gates[:], ex, over(var, E0), ALU.mult))

                @block.scalar
                def _(act):
                    act.wait_ge(steps, 1)
                    nc.scalar.activation(t1[:, 2, :], t1[:, 1, :], ACT.Sqrt, bias=k.eps[:, 0:1]).then_inc(asteps, 1)
                    act.wait_ge(steps, 2)
                    nc.scalar.activation(t4[:, 3], t4[:, 3], ACT.Exp).then_inc(asteps, 1)


def experts_phase(nc, k, name, w1d, b1d, w2d, b2d, parts, gate, dst, early=None):
    FC = F0 // P
    with ExitStack() as es:
        s = Scope(nc, es, name)
        w1 = s.sb("w1", [P, parts, KD, F0])
        w2 = s.sb("w2", [P, parts, FC, D])
        b1 = s.sb("b1", [P, parts, FC])
        b2 = s.sb("b2", [P, parts, D])
        y = s.sb("y", [P, GT, D])
        hid = s.sb("hid", [P, 2, FC, GC])
        ph = s.ps("ph", [P, FC, 512])
        py = s.ps("py", [P, 8, D])
        loaded, order = s.sem("loaded"), s.sem("order")
        h_done, gelus = s.tally("h_done", parts * 2 * FC), s.tally("gelus", parts * 2 * FC)
        y_done, added = s.tally("y_done", parts), s.tally("added", parts)
        if early:
            edram, eb2d, egate = early
            eb2 = s.sb("eb2", [P, 2, D])
            ey = s.sb("ey", [P, 2, GT, D])
            e_fetched, e_used = s.tally("e_fetched", 32), s.tally("e_used", 1)
        with nc.Block() as block:
            @block.sync
            def _(sp):
                for e in range(parts):
                    sp.dma_start(w1[:, e], w1d[e].rearrange("(k p) f -> p k f", p=P)).then_inc(loaded, 16)
                    sp.dma_start(w2[:, e], w2d[e].rearrange("(k p) f -> p k f", p=P)).then_inc(loaded, 16)
                sp.dma_start(b1[:], b1d.rearrange("e (f p) -> p e f", p=P), allow_slow_non_contiguous=True).then_inc(loaded, 16)
                sp.dma_start(b2[:], b2d.rearrange("e d -> (e d)").partition_broadcast(P)).then_inc(loaded, 16)
                sp.wait_ge(loaded, 32 * parts + 32)
                if early:
                    sp.dma_start(eb2[:], eb2d.rearrange("e d -> (e d)").partition_broadcast(P)).then_inc(loaded, 16)
                    e_fetched.open(sp)
                    with sp.Fori(0, NG) as i:
                        e_used.hold(sp, i)
                        for e in range(2):
                            sp.dma_start(ey[:, e], edram[e, bass.ds(i * GC, GC), :].rearrange("(t p) d -> p t d", p=P)).then_inc(e_fetched.sem, 16)

            @block.tensor
            def _(pe):
                h_done.open(pe)
                y_done.open(pe)
                pe.wait_ge(loaded, 32 * parts + 32)
                with pe.Fori(0, NG) as i:
                    def hidden(e):
                        for j in range(2):
                            for f in range(FC):
                                gelus.wait(pe, i, max((e * 2 + j - 1) * FC + f + 1, 0))
                                for c in range(KD):
                                    last = nc.tensor.matmul(ph[:, f, 0:HC], w1[:, e, c, f * P:(f + 1) * P],
                                                            k.XT[:, c, bass.ds(i * GC + j * HC, HC)], start=c == 0, stop=c == KD - 1)
                                last.then_inc(h_done.sem, 1)

                    def down(e):
                        gelus.wait(pe, i, (e + 1) * 2 * FC)
                        added.wait(pe, i, e)
                        for t in range(GT):
                            for f in range(FC):
                                last = nc.tensor.matmul(py[:, t, :], hid[:, e % 2, f, t * P:(t + 1) * P], w2[:, e, f, :],
                                                        start=f == 0, stop=f == FC - 1)
                        last.then_inc(y_done.sem, 1)

                    hidden(0)
                    for e in range(1, parts):
                        hidden(e)
                        down(e - 1)
                    down(parts - 1)

            @block.scalar
            def _(act):
                gelus.open(act)
                act.wait_ge(loaded, 32 * parts + 32)
                with act.Fori(0, NG) as i:
                    for e in range(parts):
                        y_done.wait(act, i, max(e - 1, 0))
                        for j in range(2):
                            for f in range(FC):
                                h_done.wait(act, i, (e * 2 + j) * FC + f + 1)
                                nc.scalar.activation(hid[:, e % 2, f, j * HC:(j + 1) * HC], ph[:, f, 0:HC], ACT.Gelu,
                                                     bias=b1[:, e, f:f + 1]).then_inc(gelus.sem, 1)

            @block.vector
            def _(dve):
                added.open(dve)
                dve.wait_ge(loaded, 32 * parts + 32 + (16 if early else 0))
                chain = Chain(dve, order)
                if early:
                    e_used.open(dve)
                with dve.Fori(0, NG) as i:
                    chain.fresh()
                    if early:
                        e_fetched.wait(dve, i, 32)
                        chain(nc.vector.tensor_tensor(ey[:], ey[:], eb2[:].unsqueeze(2).to_broadcast((P, 2, GT, D)), ALU.add))
                        for e in range(2):
                            for t in range(GT):
                                x = tile_of(dst, i * GT + t)
                                last = nc.vector.scalar_tensor_tensor(x, ey[:, e, t, :], egate(e, i * GT + t), x, ALU.mult, ALU.add)
                            chain(last)
                        dve.sem_inc(e_used.sem, 1)
                    for e in range(parts):
                        y_done.wait(dve, i, e + 1)
                        nc.vector.tensor_tensor(y[:], py[:, 0:GT, :], b2[:, e:e + 1, :].to_broadcast((P, GT, D)), ALU.add).then_inc(added.sem, 1)
                        added.wait(dve, i, e + 1)
                        for t in range(GT):
                            x = tile_of(dst, i * GT + t)
                            last = nc.vector.scalar_tensor_tensor(x, y[:, t, :], gate(e, i * GT + t), x, ALU.mult, ALU.add)
                        chain(last)


def tables_phase(nc, k, a, qtable, ktable, atable):
    KW = D + H1 * VW
    with ExitStack() as es:
        s = Scope(nc, es, "tab")
        w = s.sb("w", [P, KD, 3 * D])
        b = s.sb("b", [P, 3 * D])
        be = s.sb("be", [P, D1])
        xs = s.sb("xs", [P, KD, GC])
        qrow = s.sb("qrow", [P, 2, D])
        krow = s.sb("krow", [P, 2, KW])
        blank = s.sb("blank", [P, AW])
        pr = s.ps("pr", [P, 2, 1024])
        loaded, order, made = s.sem("loaded"), s.sem("order"), s.sem("made")
        copied = s.tally("copied", 1)
        projected, rows_ready = s.tally("projected", GT), s.tally("rows_ready", GT)
        stored = [s.tally("stored0", 32 * (GT - GT // 2)), s.tally("stored1", 32 * (GT // 2))]
        blanked = s.tally("blanked", 16 * GT)
        with nc.Block() as block:
            @block.gpsimd
            def _(pool):
                nc.gpsimd.memset(blank[:, 0:H1 * VW], 0.0)
                nc.gpsimd.memset(blank[:, H1 * VW:], -BIG)
                nc.gpsimd.memset(krow[:], 1.0).then_inc(made, 1)

            @block.sync
            def _(sp):
                for j, n in enumerate("qkv"):
                    sp.dma_start(w[:, :, j * D:(j + 1) * D], a[f"L1_gnn_W{n}"].rearrange("(k p) c -> p k c", p=P)).then_inc(loaded, 16)
                    sp.dma_start(b[:, j * D:(j + 1) * D], a[f"L1_gnn_b{n}"].partition_broadcast(P)).then_inc(loaded, 16)
                sp.dma_start(be[:], a["L1_gnn_be"].partition_broadcast(P)).then_inc(loaded, 16)
                sp.wait_ge(loaded, 112)
                sp.wait_ge(made, 1)
                for x in (*stored, blanked):
                    x.open(sp)
                with sp.Fori(0, NG) as i:
                    for t in range(GT):
                        sp.dma_start(atable[bass.ds(i * GC + t * P, P), :], blank[:]).then_inc(blanked.sem, 16)
                        rows_ready.hold(sp, i, t + 1)
                        sp.dma_start(qtable[bass.ds(i * GC + t * P, P), :], qrow[:, t % 2]).then_inc(stored[t % 2].sem, 16)
                        sp.dma_start(ktable[bass.ds(i * GC + t * P, P), :], krow[:, t % 2]).then_inc(stored[t % 2].sem, 16)
                for x in (*stored, blanked):
                    x.wait(sp, NG)

            @block.scalar
            def _(act):
                copied.open(act)
                with act.Fori(0, NG) as i:
                    projected.wait(act, i)
                    nc.scalar.activation(xs[:], k.XT[:, :, bass.ds(i * GC, GC)], ACT.Copy).then_inc(copied.sem, 1)

            @block.tensor
            def _(pe):
                projected.open(pe)
                pe.wait_ge(loaded, 112)
                with pe.Fori(0, NG) as i:
                    copied.wait(pe, i, 1)
                    for t in range(GT):
                        rows_ready.wait(pe, i, max(t - 1, 0))
                        for n0, n1 in ((0, 512), (512, 3 * D)):
                            for c in range(KD):
                                last = nc.tensor.matmul(pr[:, t % 2, n0:n1], xs[:, c, t * P:(t + 1) * P], w[:, c, n0:n1],
                                                        start=c == 0, stop=c == KD - 1)
                        last.then_inc(projected.sem, 1)

            @block.vector
            def _(dve):
                rows_ready.open(dve)
                dve.wait_ge(loaded, 112)
                dve.wait_ge(made, 1)
                chain = Chain(dve, order)
                chain(nc.vector.tensor_tensor(b[:, D:2 * D].rearrange("p (h c) -> p h c", h=H1), b[:, D:2 * D].rearrange("p (h c) -> p h c", h=H1),
                                              be[:].unsqueeze(1).to_broadcast((P, H1, D1)), ALU.add))
                with dve.Fori(0, NG) as i:
                    for t in range(GT):
                        projected.wait(dve, i, t + 1)
                        stored[t % 2].wait(dve, i, 32 * (t // 2))
                        nc.vector.tensor_tensor(qrow[:, t % 2], pr[:, t % 2, 0:D], b[:, 0:D], ALU.add)
                        nc.vector.tensor_tensor(krow[:, t % 2, 0:D], pr[:, t % 2, D:2 * D], b[:, D:2 * D], ALU.add)
                        nc.vector.tensor_tensor(krow[:, t % 2, D:].rearrange("p (h c) -> p h c", c=VW)[:, :, 0:D1],
                                                pr[:, t % 2, 2 * D:3 * D].rearrange("p (h c) -> p h c", c=D1),
                                                b[:, 2 * D:].rearrange("p (h c) -> p h c", c=D1), ALU.add).then_inc(rows_ready.sem, 1)


def edges_and_linear_phase(nc, k, a, qtable, ktable, atable, xtable, dst):
    KW = D + H1 * VW
    HALF = U1 // 2
    HS, SW = HALF // W, S1 // W
    VS = H1 * VW
    NOWHERE = 1 << 20
    NPASS = S1 // U1
    MID = NPASS // 2
    assert MID == 2 * NT
    scale = float(D1) ** 0.25
    NCH = (PD - 1) * D1 // P
    Q4 = H1 // 4
    NB = H1 + 1
    with ExitStack() as es:
        s = Scope(nc, es, "edge")
        flat = k.XT[:].rearrange("p k n -> p (k n)")
        kv = flat[:, 0:2 * HALF * KW].rearrange("p (b u c) -> p b u c", b=2, c=KW)
        o = 2 * HALF * KW
        df, free = (flat[:, j * S1:(j + 1) * S1].rearrange("p (w s) -> p w s", w=W) for j in range(2))
        q = flat[:, o:o + 2 * HALF * D].rearrange("p (b u c) -> p b u c", b=2, c=D)
        o += 2 * HALF * D
        hist = flat[:, o:o + 4 * HALF * AW].rearrange("p (b u c) -> p b u c", b=4, c=AW)
        o += 4 * HALF * AW
        prod = flat[:, o:o + HALF * D].rearrange("p (u c) -> p u c", c=D)
        o += HALF * D
        assert o <= KD * NP
        si = s.sb("si", [P, W, SW + HALF], I32)
        di = s.sb("di", [P, W, SW + HALF], I32)
        ends = s.sb("ends", [P, W, SW], I32)
        reset = s.sb("reset", [P, W, SW])
        ew = s.sb("ew", [P, W, SW])
        last_dst = s.sb("last_dst", [P, W])
        we = s.sb("we", [ED, D1])
        attr = s.sb("attr", [ED, 2, HALF, P])
        idx = s.sb("idx", [P, 2, 2, HALF], I32)
        eidx = s.sb("eidx", [P, 4, HALF], I32)
        sc = s.sb("sc", [P, HALF, H1])
        ex = s.sb("ex", [P, 2, HALF, H1])
        tmp = s.sb("tmp", [P, W, VS])
        loaded, order, ready, made = s.sem("loaded"), s.sem("order"), s.sem("ready"), s.sem("made")
        indexed = s.tally("indexed", 2)
        gathered = [s.pool_dma_tally(f"gathered{b}", 32 * HALF) for b in range(2)]
        scattered = [s.pool_dma_tally(f"scattered{j}", 16 * HALF) for j in range(4)]
        features = [s.tally(f"features{b}", 16) for b in range(2)]
        projected, logits = s.tally("projected", 2), s.tally("logits", 2)
        shifted, exps, summed = s.tally("shifted", 2), s.tally("exps", 2), s.tally("summed", 2)

        eq = ExitStack()
        es.enter_context(eq)
        sl = Scope(nc, eq, "lin")
        w = sl.sb("w", [P, KD, 3 * D])
        bias = sl.sb("bias", [P, 3 * D])
        wp = sl.sb("wp", [P, KD, D])
        bp = sl.sb("bp", [P, D])
        temp = sl.sb("temp", [P, H1])
        blk = sl.sb("blk", [P, 4, VW])
        coef = sl.sb("coef", [P, 1])
        xs = sl.sb("xs", [P, KD, P])
        row = sl.sb("row", [P, 2 * D])
        sqr = sl.sb("sqr", [P, D])
        nrm = sl.sb("nrm", [P, 3, H1])
        twice = sl.sb("twice", [P, H1, 2 * D1])
        feat = sl.sb("feat", [P, H1, (PD - 1) * D1])
        last_d = sl.sb("last_d", [P, H1 * D1])
        once = sl.sb("once", [P, H1 * D1])
        v1 = sl.sb("v1", [P, VS])
        S = sl.sb("S", [P, H1, NCH, VW])
        Sl = sl.sb("Sl", [P, 2, Q4, 4, VW])
        Sf = sl.sb("Sf", [P, VS])
        xs_loaded = sl.tally("xs_loaded", 16)
        pe_ = s.ps("ep", [P, 512])
        heads = ((0, 2), (2, 6), (6, 8))

        def normalise(chain, x, factor):
            f3 = x.rearrange("p (h c) -> p h c", c=D1)
            chain(nc.vector.tensor_tensor(twice[:, :, 0:D1], f3, factor, ALU.mult))
            nc.vector.tensor_copy(twice[:, :, D1:], twice[:, :, 0:D1])
            chain(nc.vector.tensor_copy(once[:].rearrange("p (h c) -> p h c", c=D1), twice[:, :, 0:D1]))
            nc.vector.tensor_tensor(last_d[:].rearrange("p (h c) -> p h c", c=D1), twice[:, :, 0:D1], twice[:, :, D1 // 2:D1 // 2 + D1], ALU.mult)

        def pair_features(h0, h1):
            window = bass.AP(tensor=twice[:].tensor, offset=twice[:].offset + h0 * 2 * D1,
                             ap=[list(twice[:].ap[0]), [2 * D1, h1 - h0], [1, PD - 1], [1, D1]])
            return nc.vector.tensor_tensor(feat[:, h0:h1].rearrange("p h (d c) -> p h d c", c=D1),
                                           twice[:, h0:h1, 0:D1].unsqueeze(2).to_broadcast((P, h1 - h0, PD - 1, D1)), window, ALU.mult)


        def load_features(sp, first):
            with sp.Fori(first, first + MID) as i:
                for b in range(2):
                    projected.hold(sp, i, b)
                    if b == 0:
                        features[0].hold(sp, i)
                    sp.dma_start(attr[:, b].rearrange("e (w u) p -> e w u p", w=W),
                                 a["edge_attr"].rearrange("e (w s) p -> e w s p", w=W)[:, :, bass.ds(i * (2 * HS) + b * HS, HS), :]).then_inc(features[b].sem, 16)

        def project_features(pe, i, b):
            features[b].wait(pe, i, 16)
            logits.wait(pe, i, b)
            for u in range(HALF):
                last = nc.tensor.matmul(pe_[:, (b * HALF + u) * D1:(b * HALF + u + 1) * D1], attr[:, b, u, :], we[:], start=True, stop=True)
            last.then_inc(projected.sem, 1)

        def gathers(b):
            for u in range(HALF):
                nc.gpsimd.indirect_dma_start(kv[:, b, u, :], None, ktable, bass.IndirectOffsetOnAxis(ap=idx[:, 0, b, u:u + 1], axis=0)).then_inc(gathered[b].sem, 16)
                nc.gpsimd.indirect_dma_start(q[:, b, u, :], None, qtable, bass.IndirectOffsetOnAxis(ap=idx[:, 1, b, u:u + 1], axis=0)).then_inc(gathered[b].sem, 16)

        def scatters(j):
            for u in range(HALF):
                nc.gpsimd.indirect_dma_start(atable, bass.IndirectOffsetOnAxis(ap=eidx[:, j, u:u + 1], axis=0), hist[:, j, u, :], None,
                                             bounds_check=NP - 1, oob_is_err=False).then_inc(scattered[j].sem, 16)

        def move_rows(pool, first):
            with pool.Fori(0, NT) as i:
                for j in range(4):
                    i2, b = i * 2 + (first + j // 2), j % 2
                    indexed.hold(pool, i2, b + 2)
                    gathers(1 - b)
                    summed.hold(pool, i2, b)
                    scatters((j - 1) % 4)

        def exponentials(act, i, b):
            shifted.wait(act, i, b + 1)
            nc.scalar.activation(ex[:], ex[:], ACT.Exp).then_inc(exps.sem, 1)

        def edge_set(dve, chain, tile, j, meanwhile=None):
            i, b = tile * 2 + j // 2, j % 2
            step = i * (2 * HS) + b * HS

            def by_walk(x):
                return x.rearrange("p (w u) -> p w u", w=W)

            states, last_states = (hist[:, n].rearrange("p (w u) c -> p w u c", w=W) for n in (j, (j - 1) % 4))
            gathered[b].wait(dve, i, 32 * HALF)
            projected.wait(dve, i, b + 1)
            p4 = prod.rearrange("p u (h c) -> p u h c", c=D1)
            ep = pe_[:, b * HALF * D1:(b + 1) * HALF * D1].rearrange("p (u c) -> p u c", c=D1)
            walks = [slice(w * HS, (w + 1) * HS) for w in range(W)]
            sums = [chain.start(nc.vector.tensor_tensor(p4[:, x], kv[:, b, x, 0:D].rearrange("p u (h c) -> p u h c", c=D1),
                                                        ep[:, x].unsqueeze(2).to_broadcast((P, HS, H1, D1)), ALU.add)) for x in walks]
            products = []
            for x, n in zip(walks, sums):
                chain.until(n)
                products.append(chain.start(nc.vector.tensor_tensor(prod[:, x], prod[:, x], q[:, b, x], ALU.mult)))
            dve.sem_inc(logits.sem, 1)
            for x, n in zip(walks, products):
                chain.until(n)
                last = chain.start(nc.vector.tensor_reduce(sc[:, x], p4[:, x], AX.X, ALU.add))
            chain.until(last)
            sc4, keep = (x.rearrange("p (w u) h -> p w u h", w=W) for x in (sc[:], ex[:, 0]))
            chain(nc.vector.tensor_tensor(sc4, sc4, ew[:, :, bass.ds(step, HS)].unsqueeze(3).to_broadcast((P, W, HS, H1)), ALU.mult))
            scattered[j].wait(dve, tile, 16 * HALF)
            for u in range(HS):
                before = states[:, :, u - 1, VS:] if u else last_states[:, :, HS - 1, VS:]
                r = reset[:, :, bass.ds(step + u, 1)].to_broadcast((P, W, H1))
                chain(nc.vector.tensor_tensor(keep[:, :, u, :], before, r, ALU.add))
                chain(nc.vector.tensor_tensor(states[:, :, u, VS:], keep[:, :, u, :], sc4[:, :, u, :], ALU.max))
            nc.vector.tensor_tensor(ex[:, 0], ex[:, 0], hist[:, j, :, VS:], ALU.subtract)
            nc.vector.tensor_tensor(ex[:, 1], sc[:], hist[:, j, :, VS:], ALU.subtract).then_inc(shifted.sem, 1)
            nc.vector.tensor_copy(by_walk(eidx[:, j, :]), ends[:, :, bass.ds(step, HS)])
            if meanwhile:
                meanwhile()
            exps.wait(dve, i, b + 1)
            chain(nc.vector.tensor_tensor(hist[:, j, :, 0:VS].rearrange("p u (h c) -> p u h c", c=VW),
                                          kv[:, b, :, D:].rearrange("p u (h c) -> p u h c", c=VW),
                                          ex[:, 1].unsqueeze(3).to_broadcast((P, HALF, H1, VW)), ALU.mult))
            nc.vector.tensor_copy(by_walk(idx[:, 0, b, :]), si[:, :, bass.ds(step + 2 * HS, HS)])
            nc.vector.tensor_copy(by_walk(idx[:, 1, b, :]), di[:, :, bass.ds(step + 2 * HS, HS)]).then_inc(indexed.sem, 1)
            for u in range(HS):
                before = states[:, :, u - 1, 0:VS] if u else last_states[:, :, HS - 1, 0:VS]
                now = states[:, :, u, 0:VS]
                chain(nc.vector.tensor_tensor(tmp[:].rearrange("p w (h c) -> p w h c", c=VW), before.rearrange("p w (h c) -> p w h c", c=VW),
                                              keep[:, :, u, :].unsqueeze(3).to_broadcast((P, W, H1, VW)), ALU.mult))
                chain(nc.vector.tensor_tensor(now, now, tmp[:], ALU.add))
            dve.sem_inc(summed.sem, 1)

        es2 = ExitStack()
        with es2:
            s2 = Scope(nc, es2, "kv")
            pk = s2.ps("pk", [P, 512])
            pS = s2.ps("pS", [P, 3, 512])
            pL = s2.ps("pL", [P, 2, 512])
            pF = s2.ps("pF", [P, 512])
            k_done, norms, roots, sums_done = (s2.tally(n, 1) for n in ("k_done", "norms", "roots", "sums_done"))
            pairs = s2.tally("pairs", len(heads))
            zero = feat[:].rearrange("p h c -> p (h c)")
            banks = [pS[:, 0], pS[:, 1], pS[:, 2], pL[:, 0], pL[:, 1], pF[:]]
            with nc.Block() as block:
                @block.sync
                def _(sp):
                    sp.dma_start(si[:, :, 0:SW], a["edge_src"].rearrange("p (w s) -> p w s", w=W)).then_inc(loaded, 16)
                    sp.dma_start(di[:, :, 0:SW], a["edge_dst"].rearrange("p (w s) -> p w s", w=W)).then_inc(loaded, 16)
                    sp.dma_start(ew[:], a["edge_weight"].rearrange("p (w s) -> p w s", w=W)).then_inc(loaded, 16)
                    sp.dma_start(we[:], a["L1_gnn_We"]).then_inc(loaded, 16)
                    sp.dma_start(w[:], a["lin_w"].rearrange("(k p) c -> p k c", p=P)).then_inc(loaded, 16)
                    sp.dma_start(bias[:], a["L1_mix_bqkv"].partition_broadcast(P)).then_inc(loaded, 16)
                    sp.dma_start(wp[:], a["lin_wp"].rearrange("(k p) c -> p k c", p=P)).then_inc(loaded, 16)
                    sp.dma_start(bp[:], a["L1_mix_bproj"].partition_broadcast(P)).then_inc(loaded, 16)
                    sp.dma_start(temp[:], a["lin_temp"].partition_broadcast(P)).then_inc(loaded, 16)
                    sp.wait_ge(loaded, 144)
                    for f in features:
                        f.open(sp)
                    load_features(sp, 0)

                @block.tensor
                def _(pe):
                    for x in (projected, k_done, sums_done):
                        x.open(pe)
                    pe.wait_ge(loaded, 144)
                    pe.wait_ge(made, 1)
                    for bank in banks:
                        nc.tensor.matmul(bank, zero[:, 0:P], zero[:, 0:512], start=True, stop=False)

                    def project_row(i):
                        xs_loaded.wait(pe, i, 16)
                        norms.wait(pe, i)
                        for c in range(KD):
                            last = nc.tensor.matmul(pk[:], xs[:, c, :], w[:, c, D:3 * D], start=c == 0, stop=c == KD - 1)
                        last.then_inc(k_done.sem, 1)

                    def sum_pairs(h):
                        for c in range(NCH):
                            o = (h % 3) * NCH * VW + c * VW
                            nc.tensor.matmul(pS[:, h // 3, o:o + VW], feat[:, h, c * P:(c + 1) * P], v1[:, h * VW:(h + 1) * VW], start=False, stop=False)

                    project_row(0)
                    with pe.Fori(0, NT) as i:
                        project_features(pe, i * 2, 0)
                        project_features(pe, i * 2, 1)
                        project_row(i + 1)
                        project_features(pe, i * 2 + 1, 0)
                        pairs.wait(pe, i, 1)
                        for h in range(*heads[0]):
                            sum_pairs(h)
                        for g in range(Q4):
                            vg = v1[:, 4 * g * VW:4 * (g + 1) * VW]
                            nc.tensor.matmul(pL[:, 0, 4 * g * VW:4 * (g + 1) * VW], once[:, g * P:(g + 1) * P], vg, start=False, stop=False)
                            nc.tensor.matmul(pL[:, 1, 4 * g * VW:4 * (g + 1) * VW], last_d[:, g * P:(g + 1) * P], vg, start=False, stop=False)
                        project_features(pe, i * 2 + 1, 1)
                        for n in (1, 2):
                            pairs.wait(pe, i, n + 1)
                            for h in range(*heads[n]):
                                sum_pairs(h)
                        nc.tensor.matmul(pF[:, 0:VS], k.ones[:], v1[:], start=False, stop=False).then_inc(sums_done.sem, 1)
                    pe.wait_ge(made, 7)
                    for bank in banks:
                        last = nc.tensor.matmul(bank, zero[:, 0:P], zero[:, 0:512], start=False, stop=True)
                    last.then_inc(made, 1)

                @block.gpsimd
                def _(pool):
                    nc.gpsimd.memset(feat[:], 0.0).then_inc(made, 1)
                    nc.gpsimd.memset(blk[:], 1.0).then_inc(made, 1)
                    nc.gpsimd.memset(coef[:], 1.0).then_inc(made, 1)
                    pool.wait_ge(made, 3)
                    nc.gpsimd.affine_select(out=blk[:], in_=blk[:], compare_op=ALU.is_ge, fill=0.0, base=0,
                                            pattern=[[-D1, 4], [0, VW]], channel_multiplier=1).then_inc(made, 1)
                    pool.wait_ge(made, 4)
                    nc.gpsimd.affine_select(out=blk[:], in_=blk[:], compare_op=ALU.is_ge, fill=0.0, base=D1 - 1,
                                            pattern=[[D1, 4], [0, VW]], channel_multiplier=-1).then_inc(made, 1)
                    nc.gpsimd.affine_select(out=coef[:], in_=coef[:], compare_op=ALU.is_ge, fill=0.5, base=-D1,
                                            pattern=[[0, 1]], channel_multiplier=1).then_inc(made, 1)
                    pool.wait_ge(ready, 1)
                    for j in range(3):
                        scatters(j)
                    indexed.hold(pool, 0, 1)
                    gathers(0)
                    move_rows(pool, 0)

                @block.scalar
                def _(act):
                    for x in (exps, roots, xs_loaded):
                        x.open(act)
                    act.dma_start(xs[:], xtable[0]).then_inc(xs_loaded.sem, 16)
                    with act.Fori(0, NT) as i:
                        k_done.hold(act, i, 1)
                        act.dma_start(xs[:], xtable[bass.ds(i + 1, 1)].rearrange("o p k n -> p (o k) n")).then_inc(xs_loaded.sem, 16)
                        norms.wait(act, i, 1)
                        nc.scalar.activation(nrm[:, 1, :], nrm[:, 0, :], ACT.Sqrt).then_inc(roots.sem, 1)
                        exponentials(act, i * 2, 0)
                        exponentials(act, i * 2, 1)
                        exponentials(act, i * 2 + 1, 0)
                        exponentials(act, i * 2 + 1, 1)
                    xs_loaded.wait(act, NT, 16)

                @block.vector
                def _(dve):
                    for x in (indexed, logits, shifted, summed, norms, pairs):
                        x.open(dve)
                    chain = Chain(dve, order)
                    chain(nc.vector.memset(eidx[:], NOWHERE))
                    nc.vector.memset(hist[:, :, :, 0:VS], 0.0)
                    nc.vector.memset(hist[:, :, :, VS:], -BIG).then_inc(ready, 1)
                    dve.wait_ge(loaded, 144)
                    nc.vector.memset(si[:, :, SW:], 0)
                    chain(nc.vector.memset(di[:, :, SW:], 0))
                    chain(nc.vector.tensor_copy(df, di[:, :, 0:SW]))
                    chain(nc.vector.tensor_copy(last_dst[:], df[:, :, SW - 1]))
                    chain(nc.vector.tensor_scalar(ew[:], ew[:], float(D1) ** -0.5, None, ALU.mult))
                    chain(nc.vector.memset(reset[:, :, 0:1], -BIG))
                    chain(nc.vector.tensor_tensor(reset[:, :, 1:], df[:, :, 1:], df[:, :, 0:SW - 1], ALU.not_equal))
                    chain(nc.vector.tensor_scalar(free[:, :, 0:SW - 1], reset[:, :, 1:], -float(NOWHERE), float(NOWHERE), ALU.mult, ALU.add))
                    chain(nc.vector.tensor_tensor(free[:, :, 0:SW - 1], free[:, :, 0:SW - 1], df[:, :, 0:SW - 1], ALU.add))
                    chain(nc.vector.tensor_copy(ends[:, :, 0:SW - 1], free[:, :, 0:SW - 1]))
                    chain(nc.vector.memset(ends[:, :, SW - 1:], NOWHERE))
                    chain(nc.vector.tensor_scalar(reset[:, :, 1:], reset[:, :, 1:], -BIG, None, ALU.mult))
                    for b in range(2):
                        for t, x in enumerate((si, di)):
                            last = nc.vector.tensor_copy(idx[:, t, b, :].rearrange("p (w u) -> p w u", w=W), x[:, :, b * HS:(b + 1) * HS])
                        last.then_inc(indexed.sem, 1)
                    dve.wait_ge(made, 6)
                    def take_row(i):
                        k_done.wait(dve, i, 1)
                        chain(nc.vector.tensor_tensor(row[:], pk[:], bias[:, D:3 * D], ALU.add))
                        chain(nc.vector.tensor_tensor(sqr[:], row[:, 0:D], row[:, 0:D], ALU.mult))
                        nc.vector.tensor_reduce(nrm[:, 0, :], sqr[:].rearrange("p (h c) -> p h c", c=D1), AX.X, ALU.add).then_inc(norms.sem, 1)

                    take_row(0)
                    with dve.Fori(0, NT) as i:
                        chain.fresh()
                        edge_set(dve, chain, i, 0)
                        roots.wait(dve, i, 1)
                        chain(nc.vector.tensor_scalar_max(nrm[:, 1, :], nrm[:, 1, :], 1e-12))
                        chain(nc.vector.reciprocal(nrm[:, 1, :], nrm[:, 1, :]))
                        chain(nc.vector.tensor_scalar(nrm[:, 2, :], nrm[:, 1, :], scale, None, ALU.mult))
                        sums_done.wait(dve, i)
                        m = k.valid[:, bass.ds(i, 1)]
                        v3 = v1[:].rearrange("p (h c) -> p h c", c=VW)
                        nc.vector.tensor_copy(v3[:, :, 0], m.to_broadcast((P, H1)))
                        nc.vector.tensor_scalar(v3[:, :, 1:], row[:, D:2 * D].rearrange("p (h c) -> p h c", c=D1), m, None, ALU.mult)
                        normalise(chain, row[:, 0:D], nrm[:, 2, :].unsqueeze(2).to_broadcast((P, H1, D1)))
                        pair_features(0, 2).then_inc(pairs.sem, 1)
                        edge_set(dve, chain, i, 1, lambda: pair_features(2, 4))
                        pair_features(4, 6).then_inc(pairs.sem, 1)
                        edge_set(dve, chain, i, 2, lambda: pair_features(6, 8).then_inc(pairs.sem, 1))
                        take_row(i + 1)
                        edge_set(dve, chain, i, 3)
                    sums_done.wait(dve, NT)
                    chain.fresh()
                    nc.vector.memset(feat[:, 0, :], 0.0).then_inc(made, 1)
                    dve.wait_ge(made, 8)
                    for h in range(H1):
                        o = (h % 3) * NCH * VW
                        nc.vector.tensor_scalar(S[:, h].rearrange("p c e -> p (c e)"), pS[:, h // 3, o:o + NCH * VW], 1.0 / N, None, ALU.mult)
                    for g in range(Q4):
                        for j, f in ((0, scale ** 2 / N), (1, 0.5 / N)):
                            nc.vector.scalar_tensor_tensor(Sl[:, j, g].rearrange("p m e -> p (m e)"), pL[:, j, 4 * g * VW:4 * (g + 1) * VW],
                                                           f, blk[:].rearrange("p m e -> p (m e)"), ALU.mult, ALU.mult)
                    chain(nc.vector.tensor_scalar(Sf[:], pF[:, 0:VS], scale ** 4 / N, None, ALU.mult))
                    chain(nc.vector.tensor_scalar(S[:, :, 0, :], S[:, :, 0, :], coef[:, 0:1], None, ALU.mult))

        es2 = ExitStack()
        with es2:
            s2 = Scope(nc, es2, "q")
            RING = 3
            pqp = s2.ps("pqp", [P, 2, 512])
            pq, pp = pqp[:, 0, 0:D], pqp[:, 1, 0:D]
            pt = s2.ps("pt", [P, RING, 512])
            py = s2.ps("py", [P, 512])
            ppt = s2.ps("ppt", [P, 512])
            fT = s2.sb("fT", [P, RING, 512])
            y = s2.sb("y", [P, VS])
            r = s2.sb("r", [P, H1])
            on = s2.sb("on", [P, D])
            oT = s2.sb("oT", [P, D])
            res = s2.sb("res", [P, D])
            tq = s2.sb("tq", [P, H1])
            q_done, norms, roots = (s2.tally(n, 1) for n in ("q_done", "norms", "roots"))
            pairs = s2.tally("pairs", len(heads))
            turned, evacuated, met = (s2.tally(n, NB) for n in ("turned", "evacuated", "met"))
            normed, o_turned, o_evacuated, out_done, added = (s2.tally(n, 1) for n in ("normed", "o_turned", "o_evacuated", "out_done", "added"))
            xs_again = s2.tally("xs_again", 16)
            with nc.Block() as block:
                @block.sync
                def _(sp):
                    load_features(sp, MID)

                @block.gpsimd
                def _(pool):
                    move_rows(pool, MID)
                    gathered[0].wait(pool, NPASS, 32 * HALF)
                    summed.hold(pool, NPASS)
                    scatters(3)
                    for x in scattered:
                        x.wait(pool, 2 * NT, 16 * HALF)

                @block.scalar
                def _(act):
                    for x in (roots, evacuated, o_evacuated, xs_again):
                        x.open(act)

                    def evacuate(i, b):
                        turned.wait(act, i, b + 1)
                        met.wait(act, i, max(b - RING + 1, 0))
                        nc.scalar.activation(fT[:, b % RING], pt[:, b % RING], ACT.Copy).then_inc(evacuated.sem, 1)

                    act.dma_start(xs[:], xtable[0]).then_inc(xs_again.sem, 16)
                    with act.Fori(0, NT) as i:
                        q_done.hold(act, i, 1)
                        act.dma_start(xs[:], xtable[bass.ds(i + 1, 1)].rearrange("o p k n -> p (o k) n")).then_inc(xs_again.sem, 16)
                        norms.wait(act, i, 1)
                        nc.scalar.activation(nrm[:, 1, :], nrm[:, 0, :], ACT.Sqrt).then_inc(roots.sem, 1)
                        exponentials(act, i * 2 + MID, 0)
                        for b in range(2):
                            evacuate(i, b)
                        exponentials(act, i * 2 + MID, 1)
                        for b in range(2, 6):
                            evacuate(i, b)
                        exponentials(act, i * 2 + (MID + 1), 0)
                        for b in range(6, NB):
                            evacuate(i, b)
                        exponentials(act, i * 2 + (MID + 1), 1)
                        o_turned.wait(act, i, 1)
                        nc.scalar.activation(oT[:], ppt[:, 0:D], ACT.Copy).then_inc(o_evacuated.sem, 1)
                    xs_again.wait(act, NT, 16)

                @block.tensor
                def _(pe):
                    for x in (q_done, turned, met, o_turned, out_done):
                        x.open(pe)

                    def project_row(i):
                        xs_again.wait(pe, i, 16)
                        norms.wait(pe, i)
                        for c in range(KD):
                            last = nc.tensor.matmul(pq, xs[:, c, :], w[:, c, 0:D], start=c == 0, stop=c == KD - 1)
                        last.then_inc(q_done.sem, 1)

                    def turn(i, b):
                        evacuated.wait(pe, i, max(b - RING + 1, 0))
                        for c in range(4):
                            if b:
                                src = feat[:, b - 1, c * P:(c + 1) * P]
                            else:
                                src = (once if c < Q4 else last_d)[:, (c % Q4) * P:(c % Q4 + 1) * P]
                            last = nc.tensor.transpose(pt[:, b % RING, c * P:(c + 1) * P], src, k.ident[:])
                        last.then_inc(turned.sem, 1)

                    def meet(i, b):
                        evacuated.wait(pe, i, b + 1)
                        part = fT[:, b % RING]
                        if b == 0:
                            normed.wait(pe, i)
                            for g in range(Q4):
                                o = py[:, 4 * g * VW:4 * (g + 1) * VW]
                                nc.tensor.matmul(o, part[:, g * P:(g + 1) * P], Sl[:, 0, g].rearrange("p m e -> p (m e)"),
                                                 start=g == 0, stop=False, skip_group_check=True)
                                last = nc.tensor.matmul(o, part[:, (Q4 + g) * P:(Q4 + g + 1) * P], Sl[:, 1, g].rearrange("p m e -> p (m e)"),
                                                        start=False, stop=False, skip_group_check=True)
                        else:
                            for c in range(NCH):
                                last = nc.tensor.matmul(py[:, (b - 1) * VW:b * VW], part[:, c * P:(c + 1) * P], S[:, b - 1, c, :],
                                                        start=False, stop=c == NCH - 1, skip_group_check=True)
                        last.then_inc(met.sem, 1)

                    def meet_banks(i, b0, b1):
                        for b in range(b0, min(b0 + RING, b1)):
                            turn(i, b)
                        for b in range(b0, b1):
                            meet(i, b)
                            if b + RING < b1:
                                turn(i, b + RING)

                    project_row(0)
                    with pe.Fori(0, NT) as i:
                        project_features(pe, i * 2 + MID, 0)
                        project_features(pe, i * 2 + MID, 1)
                        project_row(i + 1)
                        project_features(pe, i * 2 + (MID + 1), 0)
                        pairs.wait(pe, i, 1)
                        meet_banks(i, 0, heads[0][1] + 1)
                        project_features(pe, i * 2 + (MID + 1), 1)
                        for n in (1, 2):
                            pairs.wait(pe, i, n + 1)
                            meet_banks(i, heads[n][0] + 1, heads[n][1] + 1)
                        normed.wait(pe, i, 1)
                        for c in range(KD):
                            last = nc.tensor.transpose(ppt[:, c * P:(c + 1) * P], on[:, c * P:(c + 1) * P], k.ident[:])
                        last.then_inc(o_turned.sem, 1)
                        o_evacuated.wait(pe, i, 1)
                        added.wait(pe, i)
                        for c in range(KD):
                            last = nc.tensor.matmul(pp, oT[:, c * P:(c + 1) * P], wp[:, c, :], start=c == 0, stop=c == KD - 1)
                        last.then_inc(out_done.sem, 1)

                @block.vector
                def _(dve):
                    for x in (norms, pairs, normed, added):
                        x.open(dve)
                    chain = Chain(dve, order)
                    chain.fresh()
                    chain(nc.vector.tensor_scalar(tq[:], temp[:], scale * scale, None, ALU.mult))

                    def finish(i):
                        out_done.wait(dve, i, 1)
                        chain(nc.vector.tensor_tensor(res[:], pp, bp[:], ALU.add))
                        x = dst[:, i, :] if isinstance(i, int) else tile_of(dst, i)
                        nc.vector.tensor_tensor(x, x, res[:], ALU.add).then_inc(added.sem, 1)
                        added.wait(dve, i, 1)

                    def take_row(i):
                        q_done.wait(dve, i, 1)
                        chain(nc.vector.tensor_tensor(row[:, 0:D], pq, bias[:, 0:D], ALU.add))
                        chain(nc.vector.tensor_tensor(sqr[:], row[:, 0:D], row[:, 0:D], ALU.mult))
                        nc.vector.tensor_reduce(nrm[:, 0, :], sqr[:].rearrange("p (h c) -> p h c", c=D1), AX.X, ALU.add).then_inc(norms.sem, 1)

                    def attend(i):
                        met.wait(dve, i, NB)
                        chain(nc.vector.tensor_tensor(y[:], py[:, 0:VS], Sf[:], ALU.add))
                        y3 = y[:].rearrange("p (h c) -> p h c", c=VW)
                        chain(nc.vector.reciprocal(r[:], y3[:, :, 0]))
                        chain(nc.vector.tensor_tensor(on[:].rearrange("p (h c) -> p h c", c=D1), y3[:, :, 1:],
                                                      r[:].unsqueeze(2).to_broadcast((P, H1, D1)), ALU.mult))
                        dve.sem_inc(normed.sem, 1)

                    def tile(i, first=False):
                        chain.fresh()
                        edge_set(dve, chain, i + NT, 0, None if first else lambda: finish(i - 1))
                        roots.wait(dve, i, 1)
                        chain(nc.vector.tensor_scalar(nrm[:, 1, :], nrm[:, 1, :], scale, 1e-12, ALU.mult, ALU.max))
                        chain(nc.vector.reciprocal(nrm[:, 1, :], nrm[:, 1, :]))
                        chain(nc.vector.tensor_tensor(nrm[:, 2, :], nrm[:, 1, :], tq[:], ALU.mult))
                        turned.wait(dve, i)
                        normalise(chain, row[:, 0:D], nrm[:, 2, :].unsqueeze(2).to_broadcast((P, H1, D1)))
                        pair_features(0, 2).then_inc(pairs.sem, 1)
                        edge_set(dve, chain, i + NT, 1, lambda: pair_features(2, 4))
                        pair_features(4, 6).then_inc(pairs.sem, 1)
                        edge_set(dve, chain, i + NT, 2, lambda: pair_features(6, 8).then_inc(pairs.sem, 1))
                        take_row(i + 1)
                        edge_set(dve, chain, i + NT, 3, lambda: attend(i))

                    take_row(0)
                    tile(0, first=True)
                    with dve.Fori(1, NT) as i:
                        tile(i)
                    chain.fresh()
                    finish(NT - 1)
        eq.close()

        for n in range(W):
            tail = hist[:, 3, n * HS + HS - 1, :]
            es2 = ExitStack()
            with es2:
                s2 = Scope(nc, es2, f"join{n}")
                same = s2.sb("same", [P, P])
                off = s2.sb("off", [P, P])
                later = s2.sb("later", [P, P])
                diag = s2.sb("diag", [P, H1, P])
                col = s2.sb("col", [P, 4])
                ti = s2.sb("ti", [P, 1], I32)
                held = s2.sb("held", [P, AW])
                joined = s2.sb("joined", [P, AW])
                part = s2.sb("part", [P, VS])
                mx = s2.sb("mx", [P, 3, H1])
                pj = s2.ps("pj", [P, 4, 512])
                v, p_, e_, g_ = (s2.sem(n) for n in ("v", "p", "e", "g"))
                got, put = s2.pool_dma_sem(f"got{n}"), s2.pool_dma_sem(f"put{n}")
                with nc.Block() as block:
                    @block.tensor
                    def _(pe):
                        pe.wait_ge(v, 1)
                        nc.tensor.matmul(pj[:, 0, 0:P], k.ones[:], same[:], start=True, stop=True)
                        for c in range(2):
                            last = nc.tensor.matmul(pj[:, 1 + c, :], k.ones[:], diag[:, 4 * c:4 * c + 4, :].rearrange("p h c -> p (h c)"), start=True, stop=True)
                        last.then_inc(p_, 1)
                        pe.wait_ge(v, 3)
                        nc.tensor.matmul(pj[:, 3, 0:VS], same[:], part[:], start=True, stop=True).then_inc(p_, 1)

                    @block.gpsimd
                    def _(pool):
                        pool.wait_ge(v, 1)
                        nc.gpsimd.indirect_dma_start(held[:], None, atable, bass.IndirectOffsetOnAxis(ap=ti[:], axis=0)).then_inc(got, 16)
                        pool.wait_ge(v, 2)
                        nc.gpsimd.affine_select(out=later[:], in_=same[:], compare_op=ALU.is_gt, fill=0.0, base=0,
                                                pattern=[[1, P]], channel_multiplier=-1).then_inc(g_, 1)
                        pool.wait_ge(v, 4)
                        nc.gpsimd.indirect_dma_start(atable, bass.IndirectOffsetOnAxis(ap=ti[:], axis=0), joined[:], None,
                                                     bounds_check=NP - 1, oob_is_err=False).then_inc(put, 16)
                        pool.wait_ge(put, 16)

                    @block.scalar
                    def _(act):
                        act.wait_ge(v, 3 - 1)
                        act.wait_ge(e_, 1)
                        nc.scalar.activation(mx[:, 1:3, :], mx[:, 1:3, :], ACT.Exp).then_inc(e_, 1)

                    @block.vector
                    def _(dve):
                        chain = Chain(dve, order)
                        chain.fresh()
                        chain(nc.vector.tensor_copy(col[:, 0:1], last_dst[:, n:n + 1]))
                        chain(nc.vector.tensor_copy(ti[:], di[:, n, SW - 1:SW]))
                        nc.vector.tensor_scalar(same[:], k.ident[:], col[:, 0:1], None, ALU.mult)
                        nc.vector.tensor_tensor(diag[:], k.ident[:].unsqueeze(1).to_broadcast((P, H1, P)), tail[:, VS:].unsqueeze(2).to_broadcast((P, H1, P)), ALU.mult).then_inc(v, 1)
                        dve.wait_ge(p_, 1)
                        nc.vector.tensor_scalar(same[:], pj[:, 0, 0:P], col[:, 0:1], None, ALU.is_equal).then_inc(v, 1)
                        dve.wait_ge(v, 2)
                        chain(nc.vector.tensor_scalar(off[:], same[:], BIG, -BIG, ALU.mult, ALU.add))
                        for c in range(2):
                            last = nc.vector.tensor_tensor(diag[:, 4 * c:4 * c + 4, :], pj[:, 1 + c, :].rearrange("p (h c) -> p h c", c=P),
                                                           off[:].unsqueeze(1).to_broadcast((P, 4, P)), ALU.add)
                        chain(last)
                        chain(nc.vector.tensor_reduce(mx[:, 0, :], diag[:], AX.X, ALU.max))
                        dve.wait_ge(got, 16)
                        chain(nc.vector.tensor_tensor(mx[:, 0, :], mx[:, 0, :], held[:, VS:], ALU.max))
                        nc.vector.tensor_tensor(mx[:, 1, :], tail[:, VS:], mx[:, 0, :], ALU.subtract)
                        nc.vector.tensor_tensor(mx[:, 2, :], held[:, VS:], mx[:, 0, :], ALU.subtract).then_inc(e_, 1)
                        dve.wait_ge(e_, 2)
                        nc.vector.tensor_tensor(part[:].rearrange("p (h c) -> p h c", c=VW), tail[:, 0:VS].rearrange("p (h c) -> p h c", c=VW),
                                                mx[:, 1, :].unsqueeze(2).to_broadcast((P, H1, VW)), ALU.mult).then_inc(v, 1)
                        chain(nc.vector.tensor_tensor(joined[:, 0:VS].rearrange("p (h c) -> p h c", c=VW), held[:, 0:VS].rearrange("p (h c) -> p h c", c=VW),
                                                      mx[:, 2, :].unsqueeze(2).to_broadcast((P, H1, VW)), ALU.mult))
                        dve.wait_ge(g_, 1)
                        chain(nc.vector.tensor_reduce(col[:, 1:2], later[:], AX.X, ALU.max))
                        chain(nc.vector.scalar_tensor_tensor(col[:, 2:3], col[:, 1:2], float(NOWHERE), col[:, 0:1], ALU.mult, ALU.add))
                        chain(nc.vector.tensor_copy(joined[:, VS:], mx[:, 0, :]))
                        chain(nc.vector.tensor_copy(ti[:], col[:, 2:3]))
                        dve.wait_ge(p_, 2)
                        nc.vector.tensor_tensor(joined[:, 0:VS], joined[:, 0:VS], pj[:, 3, 0:VS], ALU.add).then_inc(v, 1)


def attention_out_phase(nc, k, a, atable, dst):
    VS = H1 * VW
    with ExitStack() as es:
        s = Scope(nc, es, "aout")
        wo = s.sb("wo", [P, KD, D])
        bo = s.sb("bo", [P, D])
        alpha = s.sb("alpha", [P, 1])
        rows = s.sb("rows", [P, GT, AW])
        r = s.sb("r", [P, GT, H1])
        on = s.sb("on", [P, GT, D])
        y = s.sb("y", [P, GT, D])
        oT = s.sb("oT", [P, KD, GC])
        pt = s.ps("pt", [P, KD, 1024])
        py = s.ps("py", [P, 8, D])
        loaded, order = s.sem("loaded"), s.sem("order")
        fetched, normed, transposed, evacuated, projected, added = (s.tally(n, c) for n, c in (
            ("fetched", 16), ("normed", 1), ("transposed", 1), ("evacuated", 1), ("projected", 1), ("added", 1)))
        with nc.Block() as block:
            @block.sync
            def _(sp):
                sp.dma_start(wo[:], a["L1_gnn_Wo"].rearrange("(k p) c -> p k c", p=P)).then_inc(loaded, 16)
                sp.dma_start(bo[:], a["L1_gnn_bo"].partition_broadcast(P)).then_inc(loaded, 16)
                sp.dma_start(alpha[:], a["L1_gnn_alpha"].partition_broadcast(P)).then_inc(loaded, 16)
                sp.wait_ge(loaded, 48)
                fetched.open(sp)
                with sp.Fori(0, NG) as i:
                    normed.hold(sp, i)
                    sp.dma_start(rows[:], atable[bass.ds(i * GC, GC), :].rearrange("(t p) c -> p t c", p=P)).then_inc(fetched.sem, 16)

            @block.vector
            def _(dve):
                normed.open(dve)
                added.open(dve)
                dve.wait_ge(loaded, 48)
                chain = Chain(dve, order)
                chain.fresh()

                def normalise(i):
                    fetched.wait(dve, i, 16)
                    acc = rows[:, :, 0:VS].rearrange("p t (h c) -> p t h c", c=VW)
                    chain(nc.vector.tensor_scalar_max(r[:], acc[:, :, :, D1], 1e-30))
                    chain(nc.vector.reciprocal(r[:], r[:]))
                    transposed.wait(dve, i)
                    nc.vector.tensor_tensor(on[:].rearrange("p t (h c) -> p t h c", c=D1), acc[:, :, :, 0:D1],
                                            r[:].unsqueeze(3).to_broadcast((P, GT, H1, D1)), ALU.mult).then_inc(normed.sem, 1)

                def add(i):
                    projected.wait(dve, i, 1)
                    chain(nc.vector.tensor_tensor(y[:], py[:, 0:GT, :], bo[:].unsqueeze(1).to_broadcast((P, GT, D)), ALU.add))
                    x = dst[:, bass.ds(i * GT, GT), :]
                    nc.vector.scalar_tensor_tensor(x, y[:], alpha[:, 0:1], x, ALU.mult, ALU.add).then_inc(added.sem, 1)
                    added.wait(dve, i, 1)

                normalise(0)
                with dve.Fori(0, NG - 1) as i:
                    chain.fresh()
                    normalise(i + 1)
                    add(i)
                add(NG - 1)

            @block.tensor
            def _(pe):
                transposed.open(pe)
                projected.open(pe)
                pe.wait_ge(loaded, 48)

                def transpose(i):
                    normed.wait(pe, i, 1)
                    evacuated.wait(pe, i)
                    for c in range(KD):
                        for t in range(GT):
                            last = nc.tensor.transpose(pt[:, c, t * P:(t + 1) * P], on[:, t, c * P:(c + 1) * P], k.ident[:])
                    last.then_inc(transposed.sem, 1)

                def project(i):
                    evacuated.wait(pe, i, 1)
                    added.wait(pe, i)
                    for t in range(GT):
                        for c in range(KD):
                            last = nc.tensor.matmul(py[:, t, :], oT[:, c, t * P:(t + 1) * P], wo[:, c, :], start=c == 0, stop=c == KD - 1)
                    last.then_inc(projected.sem, 1)

                transpose(0)
                with pe.Fori(0, NG - 1) as i:
                    project(i)
                    transpose(i + 1)
                project(NG - 1)

            @block.scalar
            def _(act):
                evacuated.open(act)
                with act.Fori(0, NG) as i:
                    transposed.wait(act, i, 1)
                    projected.wait(act, i)
                    nc.scalar.activation(oT[:], pt[:, :, 0:GC], ACT.Copy).then_inc(evacuated.sem, 1)


def top1_phase(nc, k, a, B, out):
    SLOTS = E1 * CS
    NOSLOT = 1 << 20
    buf, ybuf = k.dram("slots_in", (SLOTS, D)), k.dram("slots_out", (SLOTS, D))
    with ExitStack() as es:
        s = Scope(nc, es, "top1")
        slot = s.sb("slot", [P, 2, NT], I32)
        prob = s.sb("prob", [P, NT])
        loaded, order = s.sem("loaded"), s.sem("order")
        es2 = ExitStack()
        with es2:
            s2 = Scope(nc, es2, "route")
            gw = s2.sb("gw", [P, KD, E1])
            gb = s2.sb("gb", [P, E1])
            tri = s2.sb("tri", [P, P])
            zero = s2.sb("zero", [P, 2048])
            xs = s2.sb("xs", [P, KD, GC])
            L = s2.sb("L", [P, NT, E1])
            H = s2.sb("H", [P, NT, E1])
            C = s2.sb("C", [P, NT, E1])
            T = s2.sb("T", [P, NT + 1, E1])
            io = s2.sb("io", [P, E1])
            t1 = s2.sb("t1", [P, 6, NT])
            one = s2.sb("one", [P, NT])
            pl = s2.ps("pl", [P, 512])
            pc = s2.ps("pc", [P, 2, 512])
            made, steps, exps, counted, cleared = (s2.sem(n) for n in ("made", "steps", "exps", "counted", "cleared"))
            copied, projected, taken = (s2.tally(n, 1) for n in ("copied", "projected", "taken"))
            with nc.Block() as block:
                @block.gpsimd
                def _(pool):
                    nc.gpsimd.memset(zero[:], 0.0).then_inc(made, 1)
                    nc.gpsimd.iota(io[:], pattern=[[1, E1]], base=0, channel_multiplier=0, allow_small_or_imprecise_dtypes=True).then_inc(made, 1)
                    nc.gpsimd.memset(one[:], 1.0).then_inc(made, 1)
                    nc.gpsimd.affine_select(out=tri[:], in_=k.ones[:], compare_op=ALU.is_ge, fill=0.0, base=0,
                                            pattern=[[1, P]], channel_multiplier=-1).then_inc(made, 1)

                @block.sync
                def _(sp):
                    sp.dma_start(gw[:], a["L1_ffn_gate_w"].rearrange("(k p) c -> p k c", p=P)).then_inc(loaded, 16)
                    sp.dma_start(gb[:], a["L1_ffn_gate_b"].partition_broadcast(P)).then_inc(loaded, 16)
                    sp.wait_ge(made, 4)
                    for e in range(E1):
                        sp.dma_start(buf[e * CS:(e + 1) * CS, :].rearrange("(p r) c -> p (r c)", p=P), zero[:]).then_inc(cleared, 16)
                    sp.wait_ge(loaded, 32)
                    sp.wait_ge(cleared, 16 * E1)

                @block.scalar
                def _(act):
                    copied.open(act)
                    with act.Fori(0, NG) as i:
                        projected.wait(act, i)
                        nc.scalar.activation(xs[:], k.XT[:, :, bass.ds(i * GC, GC)], ACT.Copy).then_inc(copied.sem, 1)
                    act.wait_ge(steps, 1)
                    nc.scalar.activation(L[:], L[:], ACT.Exp).then_inc(exps, 1)

                @block.tensor
                def _(pe):
                    projected.open(pe)
                    pe.wait_ge(loaded, 32)
                    with pe.Fori(0, NG) as i:
                        copied.wait(pe, i, 1)
                        taken.wait(pe, i)
                        for t in range(GT):
                            for c in range(KD):
                                last = nc.tensor.matmul(pl[:, t * E1:(t + 1) * E1], xs[:, c, t * P:(t + 1) * P], gw[:, c, :],
                                                        start=c == 0, stop=c == KD - 1)
                        last.then_inc(projected.sem, 1)
                    pe.wait_ge(made, 4)
                    pe.wait_ge(steps, 2)
                    h = H[:].rearrange("p t e -> p (t e)")
                    nc.tensor.matmul(pc[:, 0, 0:NT * E1], tri[:], h, start=True, stop=True)
                    nc.tensor.matmul(pc[:, 1, 0:NT * E1], k.ones[:], h, start=True, stop=True).then_inc(counted, 1)

                @block.vector
                def _(dve):
                    taken.open(dve)
                    dve.wait_ge(loaded, 32)
                    dve.wait_ge(made, 4)
                    chain = Chain(dve, order)
                    with dve.Fori(0, NG) as i:
                        projected.wait(dve, i, 1)
                        nc.vector.tensor_tensor(L[:, bass.ds(i * GT, GT), :], pl[:, 0:GT * E1].rearrange("p (t e) -> p t e", e=E1),
                                                gb[:].unsqueeze(1).to_broadcast((P, GT, E1)), ALU.add).then_inc(taken.sem, 1)
                    taken.wait(dve, NG)
                    mx, tot, idx, pos, kept, base = (t1[:, j, :] for j in range(6))

                    def over(x):
                        return x.unsqueeze(2).to_broadcast((P, NT, E1))

                    iob = io[:].unsqueeze(1).to_broadcast((P, NT, E1))
                    chain(nc.vector.tensor_reduce(mx, L[:], AX.X, ALU.max))
                    nc.vector.tensor_tensor(L[:], L[:], over(mx), ALU.subtract).then_inc(steps, 1)
                    dve.wait_ge(exps, 1)
                    chain(nc.vector.tensor_reduce(tot, L[:], AX.X, ALU.add))
                    chain(nc.vector.reciprocal(tot, tot))
                    chain(nc.vector.tensor_tensor(L[:], L[:], over(tot), ALU.mult))
                    chain(nc.vector.tensor_reduce(mx, L[:], AX.X, ALU.max))
                    chain(nc.vector.tensor_tensor(H[:], L[:], over(mx), ALU.is_equal))
                    chain(nc.vector.tensor_scalar(io[:], io[:], -1.0, float(E1), ALU.mult, ALU.add))
                    chain(nc.vector.tensor_tensor(H[:], H[:], iob, ALU.mult))
                    chain(nc.vector.tensor_reduce(idx, H[:], AX.X, ALU.max))
                    chain(nc.vector.tensor_tensor(H[:], over(idx), iob, ALU.is_equal))
                    nc.vector.tensor_tensor(H[:], H[:], over(k.valid[:]), ALU.mult).then_inc(steps, 1)
                    dve.wait_ge(counted, 1)
                    chain(nc.vector.memset(T[:, 0, :], 0.0))
                    for e in range(E1):
                        last = nc.vector.tensor_tensor_scan(T[:, 1:, e], one[:], pc[:, 1, 0:NT * E1].rearrange("p (t e) -> p t e", e=E1)[:, :, e],
                                                            0.0, ALU.mult, ALU.add)
                    chain(last)
                    chain(nc.vector.tensor_tensor(C[:], pc[:, 0, 0:NT * E1].rearrange("p (t e) -> p t e", e=E1), T[:, 0:NT, :], ALU.add))
                    chain(nc.vector.tensor_tensor(C[:], C[:], H[:], ALU.mult))
                    chain(nc.vector.tensor_reduce(pos, C[:], AX.X, ALU.add))
                    chain(nc.vector.tensor_scalar(kept, pos, float(CAP), None, ALU.is_le))
                    chain(nc.vector.tensor_tensor(kept, kept, k.valid[:], ALU.mult))
                    chain(nc.vector.tensor_tensor(prob[:], mx, kept, ALU.mult))
                    chain(nc.vector.tensor_scalar(base, idx, -float(CS), float(E1 * CS - 1), ALU.mult, ALU.add))
                    chain(nc.vector.tensor_tensor(base, base, pos, ALU.add))
                    chain(nc.vector.tensor_tensor(base, base, kept, ALU.mult))
                    chain(nc.vector.tensor_copy(slot[:, 1, :], base))
                    chain(nc.vector.tensor_scalar(kept, kept, -float(NOSLOT), float(NOSLOT), ALU.mult, ALU.add))
                    chain(nc.vector.tensor_tensor(base, base, kept, ALU.add))
                    chain(nc.vector.tensor_copy(slot[:, 0, :], base))

        with ExitStack() as es2:
            s2 = Scope(nc, es2, "send")
            sent = s2.pool_dma_sem("sent")
            with nc.Block() as block:
                @block.gpsimd
                def _(pool):
                    for t in range(NT):
                        nc.gpsimd.indirect_dma_start(buf, bass.IndirectOffsetOnAxis(ap=slot[:, 0, t:t + 1], axis=0), B[:, t, :], None,
                                                     bounds_check=SLOTS - 1, oob_is_err=False).then_inc(sent, 16)
                    pool.wait_ge(sent, 16 * NT)

        with ExitStack() as es2:
            s2 = Scope(nc, es2, "ex1")
            FC = F1 // P
            b1 = s2.sb("b1", [P, E1, FC])
            bias = s2.sb("bias", [P, FC])
            b2 = s2.sb("b2", [P, E1, D])
            rows = s2.sb("rows", [P, CT, D])
            flat = B[:].rearrange("p t c -> p (t c)")
            XE = flat[:, 0:KD * CS].rearrange("p (k n) -> p k n", k=KD)
            hid = flat[:, KD * CS:KD * CS + FC * CS].rearrange("p (f n) -> p f n", n=CS)
            flat = k.XT[:].rearrange("p k n -> p (k n)")
            w1 = flat[:, 0:2 * KD * F1].rearrange("p (b k f) -> p b k f", b=2, k=KD)
            o = 2 * KD * F1
            w2 = flat[:, o:o + 2 * FC * D].rearrange("p (b k f) -> p b k f", b=2, k=FC)
            o += 2 * FC * D
            Y = flat[:, o:o + CT * D].rearrange("p (t c) -> p t c", c=D)
            assert o + CT * D <= KD * NP
            pa = s2.ps("pa", [P, 4, 512])
            py = s2.ps("py", [P, 8, D])
            biases, aorder = s2.sem("biases"), s2.sem("aorder")
            rows_in = s2.tally("rows_in", 16)
            weights = [s2.tally(f"weights{b}", 32) for b in range(2)]
            turned, evacuated = s2.tally("turned", 4), s2.tally("evacuated", 4)
            h_done, relus = s2.tally("h_done", 2 * FC), s2.tally("relus", 2 * FC)
            y_done, copied = s2.tally("y_done", 1, credit=2), s2.tally("copied", 1)
            stored, written = s2.pool_dma_tally("stored", 16), s2.tally("written", 1)
            with nc.Block() as block:
                @block.sync
                def _(sp):
                    sp.dma_start(b1[:], a["L1_ffn_b1"].rearrange("e (f p) -> p e f", p=P), allow_slow_non_contiguous=True).then_inc(biases, 16)
                    sp.dma_start(b2[:], a["L1_ffn_b2"].rearrange("e d -> (e d)").partition_broadcast(P)).then_inc(biases, 16)
                    sp.wait_ge(biases, 32)
                    for x in (rows_in, *weights):
                        x.open(sp)
                    with sp.Fori(0, E1 // 2) as i:
                        for b in range(2):
                            e = i * 2 + b
                            turned.hold(sp, e)
                            sp.dma_start(rows[:], buf[bass.ds(e * CS, CS), :].rearrange("(t p) c -> p t c", p=P)).then_inc(rows_in.sem, 16)
                            if b == 0:
                                weights[0].hold(sp, i)
                            y_done.hold(sp, e - 1)
                            sp.dma_start(w1[:, b], a["L1_ffn_w1"][bass.ds(e, 1)].rearrange("o (k p) f -> p (o k) f", p=P)).then_inc(weights[b].sem, 16)
                            sp.dma_start(w2[:, b], a["L1_ffn_w2"][bass.ds(e, 1)].rearrange("o (k p) f -> p (o k) f", p=P)).then_inc(weights[b].sem, 16)

                @block.gpsimd
                def _(pool):
                    with pool.Fori(0, E1) as i:
                        copied.hold(pool, i, 1)
                        pool.dma_start(ybuf[bass.ds(i * CS, CS), :].rearrange("(t p) c -> p t c", p=P), Y).then_inc(stored.sem, 16)
                        stored.wait(pool, i, 16)
                        pool.sem_inc(written.sem, 1)

                @block.tensor
                def _(pe):
                    for x in (turned, h_done, y_done):
                        x.open(pe)
                    pe.wait_ge(biases, 32)

                    def expert(i, b):
                        e = i * 2 + b
                        rows_in.wait(pe, e, 16)
                        for j in range(4):
                            if j == 0:
                                relus.wait(pe, e)
                            for t in range(4):
                                last = nc.tensor.transpose(pa[:, j, t * P:(t + 1) * P], rows[:, j % 2 * 4 + t, j // 2 * P:(j // 2 + 1) * P], k.ident[:])
                            last.then_inc(turned.sem, 1)
                        evacuated.wait(pe, e, 4)
                        weights[b].wait(pe, i, 32)
                        for f in range(FC):
                            for j in range(2):
                                n = 2 * f + j
                                if n >= 4:
                                    relus.wait(pe, e, n - 3)
                                for c in range(KD):
                                    last = nc.tensor.matmul(pa[:, n % 4, :], w1[:, b, c, f * P:(f + 1) * P], XE[:, c, j * 512:(j + 1) * 512],
                                                            start=c == 0, stop=c == KD - 1)
                                last.then_inc(h_done.sem, 1)
                        relus.wait(pe, e, 2 * FC)
                        copied.wait(pe, e)
                        for t in range(CT):
                            for f in range(FC):
                                last = nc.tensor.matmul(py[:, t, :], hid[:, f, t * P:(t + 1) * P], w2[:, b, f, :], start=f == 0, stop=f == FC - 1)
                        last.then_inc(y_done.sem, 1)

                    with pe.Fori(0, E1 // 2) as i:
                        expert(i, 0)
                        expert(i, 1)

                @block.scalar
                def _(act):
                    for x in (evacuated, relus):
                        x.open(act)
                    act.wait_ge(biases, 32)
                    chain = Chain(act, aorder)
                    with act.Fori(0, E1) as i:
                        chain.fresh()
                        relus.wait(act, i)
                        chain(nc.scalar.activation(bias[:], b1[:, bass.ds(i, 1), :].rearrange("p o f -> p (o f)"), ACT.Copy))
                        for j in range(4):
                            turned.wait(act, i, j + 1)
                            nc.scalar.activation(XE[:, j // 2, j % 2 * 512:(j % 2 + 1) * 512], pa[:, j, :], ACT.Copy).then_inc(evacuated.sem, 1)
                        y_done.wait(act, i)
                        for f in range(FC):
                            for j in range(2):
                                h_done.wait(act, i, 2 * f + j + 1)
                                nc.scalar.activation(hid[:, f, j * 512:(j + 1) * 512], pa[:, (2 * f + j) % 4, :], ACT.Relu,
                                                     bias=bias[:, f:f + 1]).then_inc(relus.sem, 1)


                @block.vector
                def _(dve):
                    copied.open(dve)
                    dve.sem_inc(written.sem, 1)
                    dve.wait_ge(biases, 32)
                    with dve.Fori(0, E1) as i:
                        y_done.wait(dve, i, 1)
                        written.wait(dve, i)
                        nc.vector.tensor_tensor(Y, py[:], b2[:, bass.ds(i, 1), :].to_broadcast((P, CT, D)), ALU.add).then_inc(copied.sem, 1)

        with ExitStack() as es2:
            s2 = Scope(nc, es2, "back")
            y2 = s2.sb("y", [P, 2, GT, D])
            mask = s2.sb("mask", [P, GT * D], I32)
            const = s2.sb("const", [P, 3, 256])
            made = s2.sem("made")
            got = [s2.pool_dma_sem(f"got{b}") for b in range(2)]
            summed = s2.tally("summed", 1)
            stored = s2.sem("stored")
            with nc.Block() as block:
                @block.gpsimd
                def _(pool):
                    for j, v in enumerate((0.0, 1.0e4, -1.0e4)):
                        nc.gpsimd.memset(const[:, j], v).then_inc(made, 1)
                    for i in range(NG):
                        if i >= 2:
                            summed.hold(pool, i - 1)
                        for t in range(GT):
                            nc.gpsimd.indirect_dma_start(y2[:, i % 2, t, :], None, ybuf,
                                                         bass.IndirectOffsetOnAxis(ap=slot[:, 1, i * GT + t:i * GT + t + 1], axis=0)).then_inc(got[i % 2], 16)

                @block.vector
                def _(dve):
                    summed.open(dve)
                    dve.wait_ge(made, 3)
                    chain = Chain(dve, order)
                    chain.fresh()
                    m3 = mask[:].rearrange("p (t c) -> p t c", c=D)

                    def filled(j):
                        return const[:, j:j + 1, 0:D].to_broadcast((P, GT, D))

                    for i in range(NG):
                        y = y2[:, i % 2]
                        dve.wait_ge(got[i % 2], (i // 2 + 1) * 16 * GT)
                        pr = prob[:, i * GT:(i + 1) * GT].unsqueeze(2).to_broadcast((P, GT, D))
                        chain(nc.vector.tensor_tensor(y, y, pr, ALU.mult))
                        chain(nc.vector.tensor_tensor(m3, y, y, ALU.not_equal))
                        chain(nc.vector.copy_predicated(y, m3, filled(0)))
                        chain(nc.vector.tensor_scalar(mask[:], y.rearrange("p t c -> p (t c)"), FLT_MAX, None, ALU.is_gt))
                        chain(nc.vector.copy_predicated(y, m3, filled(1)))
                        chain(nc.vector.tensor_scalar(mask[:], y.rearrange("p t c -> p (t c)"), -FLT_MAX, None, ALU.is_lt))
                        chain(nc.vector.copy_predicated(y, m3, filled(2)))
                        x = k.X[:, i * GT:(i + 1) * GT, :]
                        nc.vector.tensor_tensor(x, x, y, ALU.add).then_inc(summed.sem, 1)
                        summed.wait(dve, i, 1)

                @block.sync
                def _(sp):
                    stored_t = Tally(stored, 16)
                    stored_t.open(sp)
                    with sp.Fori(0, NG) as i:
                        summed.hold(sp, i, 1)
                        sp.dma_start(out[bass.ds(i * GC, GC), :].rearrange("(t p) c -> p t c", p=P), k.X[:, bass.ds(i * GT, GT), :]).then_inc(stored, 16)
                    stored_t.wait(sp, NG)


FLT_MAX = float(np.finfo(np.float32).max)


def arrays(inputs):
    a = {n: np.asarray(v) for n, v in inputs.items()}
    out = {n: v for n, v in a.items() if n not in RESHAPED}

    def padded(v, n):
        return np.concatenate([v, np.zeros((n - v.shape[0],) + v.shape[1:], v.dtype)])

    def by_role(v):
        return v.reshape((8, 3, 32) + v.shape[1:])[:, [0, 2, 1]].transpose((1, 0, 2) + tuple(range(3, v.ndim + 2))).reshape(v.shape)

    out["x"] = padded(a["x"], NP)
    out["first_src"] = padded(a["src"][:N], NP).reshape(NT, P).T
    out["first_dst"] = padded(a["dst"][:N], NP).reshape(NT, P).T
    out["mix_wq"] = by_role(a["L0_mix_w_qkv"][:, :, 2]).T
    out["mix_col"] = np.stack([by_role(a["L0_mix_bn_gamma"]), by_role(a["L0_mix_bn_beta"]), by_role(a["L0_mix_w_dw"][:, 0, 2])])
    out["mix_pw"] = by_role(a["L0_mix_w_pw"][:, :, 0].reshape(24, 32, 32).transpose(0, 2, 1).reshape(QC * P, 32))
    for n in ("src", "dst", "weight"):
        v = a["edge_weight" if n == "weight" else n]
        fill = N if n == "dst" else 0
        out["edge_" + n] = np.concatenate([v, np.full(EP - E_EDGES, fill, v.dtype)]).reshape(P, S1)
    out["edge_attr"] = padded(a["edge_attr_64"], EP).reshape(P, S1, ED).transpose(2, 1, 0)
    out["ff_w1"] = a["L1_gnn_W1"].reshape(D, 2, F0).transpose(1, 0, 2)
    out["ff_b1"] = a["L1_gnn_b1"].reshape(2, F0)
    out["ff_w2"] = a["L1_gnn_W2"].reshape(2, F0, D)
    out["ff_b2"] = padded(a["L1_gnn_b2"][None], 2)
    out["lin_w"] = a["L1_mix_Wqkv"].T
    out["lin_wp"] = a["L1_mix_Wproj"].T
    out["lin_temp"] = a["L1_mix_temperature"].reshape(H1)
    out["L0_ffn_edge_index"] = a["L0_ffn_edge_index"].reshape(2, P, S0)
    out["L0_mix_w_res"] = a["L0_mix_w_res"][:, :, 0].T.reshape(4, P, D).transpose(1, 0, 2)
    return {n: np.ascontiguousarray(v) for n, v in out.items()}


RESHAPED = ("x", "src", "dst", "edge_attr_64", "edge_weight", "L0_mix_w_qkv", "L0_mix_bn_gamma", "L0_mix_bn_beta",
            "L0_mix_w_dw", "L0_mix_w_pw", "L0_mix_w_res", "L0_ffn_edge_index",
            "L1_gnn_W1", "L1_gnn_b1", "L1_gnn_W2", "L1_gnn_b2", "L1_mix_Wqkv", "L1_mix_Wproj", "L1_mix_temperature")


class Kept:

    def __init__(self, nc, es):
        self.nc = nc
        Scope.lasting = es
        s = Scope(nc, es, "kept")
        Tally.held = s.sem("held")
        self.X = s.sb("X", [P, NT, D])
        self.XT = s.sb("XT", [P, KD, NP])
        self.ident = s.sb("ident", [P, P])
        self.ones = s.sb("ones", [P, P])
        self.eps = s.sb("eps", [P, 1])
        self.valid = s.sb("valid", [P, NT])

    def dram(self, name, shape, dt=F32):
        return self.nc.dram_tensor(name, shape, dt, kind="Internal").ap()


def layer1_graph(nc, k, a):
    KW = D + H1 * VW
    qtable, ktable, atable = k.dram("qtable", (NP, D)), k.dram("ktable", (NP, KW)), k.dram("atable", (NP, AW))
    xtable = k.dram("xtable", (NT + 1, P, KD, P))
    xrows = k.dram("xrows", (P, NT, D))
    es = ExitStack()
    with es:
        s = Scope(nc, es, "l1")
        chan = s.sb("chan", [P, 4, KD])
        beta = s.sb("beta", [P, 1])
        loaded, order, kept = s.sem("loaded"), s.sem("order"), s.sem("kept")
        es2 = ExitStack()
        with es2:
            B = Scope(nc, es2, "rows").sb("B", [P, NT, D])
            layernorm_phase(nc, k, "ln2", k.X, keep=B)
            with nc.Block() as block:
                @block.sync
                def _(sp):
                    for j, n in enumerate(("ln1_g", "ln1_b", "ln2_g", "ln2_b")):
                        sp.dma_start(chan[:, j, :], a[f"L1_gnn_{n}"].rearrange("(k p) -> p k", p=P), allow_slow_non_contiguous=True).then_inc(loaded, 16)
                    sp.dma_start(beta[:], a["L1_gnn_beta"].partition_broadcast(P)).then_inc(loaded, 16)
                    for c in range(KD):
                        sp.dma_start(xtable[0:NT, :, c, :].rearrange("t p n -> p t n"), k.XT[:, c, :].rearrange("p (t n) -> p t n", n=P)).then_inc(kept, 16)
                    sp.dma_start(xtable[NT], k.XT[:, :, 0:P]).then_inc(kept, 16)
                    sp.dma_start(xrows, B[:]).then_inc(kept, 16)
                    sp.wait_ge(loaded, 80)
                    sp.wait_ge(kept, 16 * (KD + 2))
            layernorm_phase(nc, k, "ln3", B, scale=chan[:, 0, :], shift=chan[:, 1, :])
            tables_phase(nc, k, a, qtable, ktable, atable)
        edges_and_linear_phase(nc, k, a, qtable, ktable, atable, xtable, k.X)
        es2 = ExitStack()
        with es2:
            B = Scope(nc, es2, "rows2").sb("B", [P, NT, D])
            with nc.Block() as block:
                @block.sync
                def _(sp):
                    sp.dma_start(B[:], xrows).then_inc(loaded, 16)
                    sp.wait_ge(loaded, 96)
            attention_out_phase(nc, k, a, atable, B)
            layernorm_phase(nc, k, "ln4", B, scale=chan[:, 2, :], shift=chan[:, 3, :])
            experts_phase(nc, k, "ff1", a["ff_w1"], a["ff_b1"], a["ff_w2"], a["ff_b2"], 2, lambda e, t: beta[:, 0:1], B)
            with nc.Block() as block:
                @block.vector
                def _(dve):
                    nc.vector.tensor_tensor(k.X[:], k.X[:], B[:], ALU.add).then_inc(order, 1)
                    dve.wait_ge(order, 1)


def program(nc, a, out, phases=("L0a", "L0b", "L1a", "L1b")):
    with ExitStack() as es:
        k = Kept(nc, es)
        setup_phase(nc, a, k)
        if "L0a" in phases:
            with ExitStack() as es0:
                ball = Scope(nc, es0, "L0").sb("ball", [P, KD, NP])
                layernorm_phase(nc, k, "ln0", k.X, ball=ball)
                gather_phase(nc, k, a)
                mixer_phase(nc, k, a, ball)
        if "L0b" in phases:
            with ExitStack() as es0:
                gates = Scope(nc, es0, "L0").sb("gates", [P, NT, E0])
                layernorm_phase(nc, k, "ln1", k.X)
                early = k.dram("early_experts", (2, NP, D))
                gate_phase(nc, k, a, gates, early)
                w1, b1, w2, b2 = (a["L0_ffn_" + n] for n in ("W1", "b1", "W2", "b2"))
                experts_phase(nc, k, "moe0", w1[2:], b1[2:], w2[2:], b2[2:], E0 - 2, lambda e, t: gates[:, bass.ds(t, 1), e + 2], k.X,
                              early=(early, b2[0:2], lambda e, t: gates[:, bass.ds(t, 1), e]))
        if "L1a" in phases:
            layer1_graph(nc, k, a)
        es1 = ExitStack()
        with es1:
            B = Scope(nc, es1, "last").sb("B", [P, NT, D])
            if "L1b" in phases:
                layernorm_phase(nc, k, "ln5", k.X, keep=B)
                top1_phase(nc, k, a, B, out)
                return
        with ExitStack() as es1:
            stored = Scope(nc, es1, "end").sem("stored")
            with nc.Block() as block:
                @block.sync
                def _(sp):
                    sp.dma_start(out.rearrange("(t p) c -> p t c", p=P), k.X[:]).then_inc(stored, 16)
                    sp.wait_ge(stored, 16)


def kernel(**inputs):
    import concourse.bacc as bacc
    from concourse.bass_utils import run_bass_kernel_spmd

    nc = bacc.Bacc("TRN2", target_bir_lowering=False, num_devices=1)
    host = arrays(inputs)
    a = {n: nc.dram_tensor(f"in_{n}", v.shape, mybir.dt.from_np(v.dtype), kind="ExternalInput").ap() for n, v in host.items()}
    out = nc.dram_tensor("out", (NP, D), F32, kind="ExternalOutput").ap()
    program(nc, a, out)
    r = run_bass_kernel_spmd(nc, [{f"in_{n}": v for n, v in host.items()}], core_ids=[0])
    return r.results[0]["out"][:N]
```
